# Optimizing a Trainium2 kernel written in Bass

```python
import numpy as np
import jax
import jax.numpy as jnp

def _softmax(x, axis=-1):
    return jax.nn.softmax(x, axis=axis)

def _gelu(x):
    return jax.nn.gelu(x, approximate=True)

def _silu(x):
    return jax.nn.silu(x)

def _sigmoid(x):
    return jax.nn.sigmoid(x)

def _layernorm(x, axis=-1, eps=1e-05):
    m = jnp.mean(x, axis=axis, keepdims=True)
    v = jnp.var(x, axis=axis, keepdims=True)
    return (x - m) / jnp.sqrt(v + eps)

def _scatter_add(tgt, idx, src, axis=0):
    return tgt.at[idx].add(src)

def _segment_sum(src, seg, n):
    return jax.ops.segment_sum(src, seg, n)
kernel_name = 'mk_decoder_preln_d4_seqx_r8_89abc4'

def setup_inputs(seed: int=0):
    np.random.seed(seed)
    _w = jnp.asarray

    def _rec_inputs():
        import jax
        import jax.numpy as jnp
        _rk = jax.random.key(seed)
        x = 7.22e-05 + 1 * jax.random.normal(jax.random.fold_in(_rk, 1), (8, 256, 128), jnp.float32)
        _lenS = 256 - jax.random.randint(jax.random.fold_in(_rk, 7), (8,), 0, max(1, 256 // 4) + 1, jnp.int32)
        _lenS2 = 512 - jax.random.randint(jax.random.fold_in(_rk, 8), (8,), 0, max(1, 512 // 4) + 1, jnp.int32)
        _ctx_768P = jax.random.normal(jax.random.fold_in(_rk, 11), (8, 16, 96), jnp.float32)
        _ctx_768c = jax.random.dirichlet(jax.random.fold_in(_rk, 511), 0.3 * jnp.ones((16,), jnp.float32), (8, 512))
        _ctx_768t = jnp.einsum('bsk,bkd->bsd', _ctx_768c, _ctx_768P)
        _ctx_768t = _ctx_768t * jax.lax.rsqrt(jnp.mean(jnp.square(_ctx_768t)) + 1e-12) * 0.953939
        ctx_768 = -0.000191848 + 0.999787 * (_ctx_768t + 0.3 * jax.random.normal(jax.random.fold_in(_rk, 611), (8, 512, 96), jnp.float32))
        return (x, ctx_768)
    x, ctx_768 = _rec_inputs()

    def _L0_attn_setup():
        import jax, jax.numpy as jnp
        import numpy as np
        DIM = 128
        HEADS = 16
        HDIM = DIM // HEADS
        CHUNK = 64
        RES_SCALE = float(1.0 / np.sqrt(2.0))
        EPS_FP32 = float(np.finfo(np.float32).eps)

        def _rms(x, eps):
            return x * jax.lax.rsqrt(jnp.mean(x * x, axis=-1, keepdims=True) + eps)

        def _mixer(x, in_proj_w, out_proj_w):
            B, S, D = x.shape
            proj = x @ in_proj_w.T
            q, k, v, a, g = jnp.split(proj, 5, axis=-1)
            rs = lambda t: t.reshape(B, S, HEADS, HDIM)
            q, k, v, a, g = map(rs, (q, k, v, a, g))
            q = _rms(q, EPS_FP32)
            k = jnp.tanh(k)
            a = jnp.clip(jax.nn.sigmoid(a + 2.0), 0.6, 0.9995)
            u = k * v
            nC = S // CHUNK
            a_c = jnp.moveaxis(a.reshape(B, nC, CHUNK, HEADS, HDIM), 1, 0)
            u_c = jnp.moveaxis(u.reshape(B, nC, CHUNK, HEADS, HDIM), 1, 0)

            def step(state, inp):
                ac, uc = inp
                prefix = jnp.cumprod(ac, axis=1)
                acc = jnp.cumsum(uc / jnp.maximum(prefix, 1e-06), axis=1)
                states = prefix * (state[:, None] + acc)
                return (states[:, -1], states)
            state0 = jnp.zeros((B, HEADS, HDIM), jnp.float32)
            _, states = jax.lax.scan(step, state0, (a_c, u_c))
            memory = jnp.moveaxis(states, 0, 1).reshape(B, S, HEADS, HDIM)
            gate = jax.nn.sigmoid(g)
            y = gate * (q * memory) + (1.0 - gate) * v
            return y.reshape(B, S, D) @ out_proj_w.T
        key = jax.random.key(seed)
        ks = jax.random.split(key, 5)
        s = 0.02
        return {'x': jax.random.normal(ks[0], (2, 512, DIM), jnp.float32), 'norm1_w': jnp.ones((DIM,), jnp.float32), 'norm2_w': jnp.ones((DIM,), jnp.float32), 'in_proj_w': jax.random.normal(ks[1], (5 * DIM, DIM), jnp.float32) * s, 'out_proj_w': jax.random.normal(ks[2], (DIM, DIM), jnp.float32) * s, 'fc_w': jax.random.normal(ks[3], (512, DIM), jnp.float32) * s, 'proj_w': jax.random.normal(ks[4], (DIM, 512), jnp.float32) * s}
    _L0_attn_all = _L0_attn_setup()
    _L0_attn_in = {k: v for k, v in _L0_attn_all.items() if k in ('norm1_w', 'norm2_w', 'in_proj_w', 'out_proj_w', 'fc_w', 'proj_w')}
    del _L0_attn_all

    def _L0_xattn_setup():
        import jax, jax.numpy as jnp
        import numpy as np
        NUM_HEADS = 16
        CLAMP = 10000.0
        key = jax.random.key(seed)
        ks = jax.random.split(key, 8)
        B, Nq, Nkv, Cq, Ckv = (4, 256, 256, 128, 96)
        s_q = 1.0 / np.sqrt(Cq)
        s_kv = 1.0 / np.sqrt(Ckv)
        return {'query': jax.random.normal(ks[0], (B, Nq, Cq), jnp.float32), 'key_value': jax.random.normal(ks[1], (B, Nkv, Ckv), jnp.float32), 'Wq': jax.random.normal(ks[2], (Cq, Cq), jnp.float32) * s_q, 'bq': jnp.zeros((Cq,), jnp.float32), 'Wk': jax.random.normal(ks[3], (Ckv, Cq), jnp.float32) * s_kv, 'bk': jnp.zeros((Cq,), jnp.float32), 'Wv': jax.random.normal(ks[4], (Ckv, Cq), jnp.float32) * s_kv, 'bv': jnp.zeros((Cq,), jnp.float32), 'Wo': jax.random.normal(ks[5], (Cq, Cq), jnp.float32) * s_q, 'bo': jnp.zeros((Cq,), jnp.float32)}
    _L0_xattn_all = _L0_xattn_setup()
    _L0_xattn_in = {k: v for k, v in _L0_xattn_all.items() if k in ('Wq', 'bq', 'Wk', 'bk', 'Wv', 'bv', 'Wo', 'bo')}
    del _L0_xattn_all

    def _L0_ffn_setup():
        import jax, jax.numpy as jnp
        import numpy as np
        TOP_K = 8
        key = jax.random.key(seed)
        ks = jax.random.split(key, 6)
        B, S, D, F, E = (2, 128, 128, 64, 64)
        x = jax.random.normal(ks[0], (B, S, D), dtype=jnp.float32)
        centroids = jax.random.normal(ks[1], (E, D), dtype=jnp.float32) * 0.05
        expert_biases = jnp.zeros((E,), dtype=jnp.float32)
        Ws_up = jax.random.normal(ks[2], (D, F), dtype=jnp.float32) / np.sqrt(D)
        Ws_down = jax.random.normal(ks[3], (F, D), dtype=jnp.float32) / np.sqrt(F)
        W_up = jax.random.normal(ks[4], (E, D, F), dtype=jnp.float32) / np.sqrt(D)
        W_down = jax.random.normal(ks[5], (E, F, D), dtype=jnp.float32) / np.sqrt(F)
        return {'x': x, 'centroids': centroids, 'expert_biases': expert_biases, 'Ws_up': Ws_up, 'Ws_down': Ws_down, 'W_up': W_up, 'W_down': W_down}
    _L0_ffn_all = _L0_ffn_setup()
    _L0_ffn_in = {k: v for k, v in _L0_ffn_all.items() if k in ('centroids', 'expert_biases', 'Ws_up', 'Ws_down', 'W_up', 'W_down')}
    del _L0_ffn_all

    def _L1_attn_setup():
        import jax, jax.numpy as jnp
        import numpy as np
        B, T, E, H = (4, 256, 128, 16)
        S = E // H
        key = jax.random.key(seed)
        ks = jax.random.split(key, 4)
        x = jax.random.normal(ks[0], (B, T, E), dtype=jnp.float32)
        Wk = jax.random.normal(ks[1], (E, E), dtype=jnp.float32) * E ** (-0.5)
        Wq = jax.random.normal(ks[2], (E, E), dtype=jnp.float32) * E ** (-0.5)
        Wo = jax.random.normal(ks[3], (E, E), dtype=jnp.float32) * E ** (-0.5)
        bo = jnp.zeros((E,), dtype=jnp.float32)
        return {'x': x, 'Wk': Wk, 'Wq': Wq, 'Wo': Wo, 'bo': bo}
    _L1_attn_all = _L1_attn_setup()
    _L1_attn_in = {k: v for k, v in _L1_attn_all.items() if k in ('Wk', 'Wq', 'Wo', 'bo')}
    del _L1_attn_all

    def _L1_xattn_setup():
        import jax, jax.numpy as jnp
        import numpy as np
        N_HEADS = 8
        D_EMBED = 128
        D_CROSS = 96
        D_HEAD = D_EMBED // N_HEADS
        key = jax.random.key(seed)
        ks = jax.random.split(key, 10)
        B, Lq, Lkv = (16, 512, 77)
        s_e = 1.0 / np.sqrt(D_EMBED)
        s_c = 1.0 / np.sqrt(D_CROSS)
        return {'x': jax.random.normal(ks[0], (B, Lq, D_EMBED), jnp.float32), 'y': jax.random.normal(ks[1], (B, Lkv, D_CROSS), jnp.float32), 'Wq': jax.random.normal(ks[2], (D_EMBED, D_EMBED), jnp.float32) * s_e, 'bq': jnp.zeros((D_EMBED,), jnp.float32), 'Wk': jax.random.normal(ks[3], (D_CROSS, D_EMBED), jnp.float32) * s_c, 'bk': jnp.zeros((D_EMBED,), jnp.float32), 'Wv': jax.random.normal(ks[4], (D_CROSS, D_EMBED), jnp.float32) * s_c, 'bv': jnp.zeros((D_EMBED,), jnp.float32), 'Wo': jax.random.normal(ks[5], (D_EMBED, D_EMBED), jnp.float32) * s_e, 'bo': jnp.zeros((D_EMBED,), jnp.float32)}
    _L1_xattn_all = _L1_xattn_setup()
    _L1_xattn_in = {k: v for k, v in _L1_xattn_all.items() if k in ('Wq', 'bq', 'Wk', 'bk', 'Wv', 'bv', 'Wo', 'bo')}
    del _L1_xattn_all

    def _L1_ffn_setup():
        import jax, jax.numpy as jnp
        import numpy as np
        BLOCK = 16
        _GRID = jnp.array([0.0, 0.5, 1.0, 1.5, 2.0, 3.0, 4.0, 6.0], dtype=jnp.float32)
        _MID = jnp.array([0.25, 0.75, 1.25, 1.75, 2.5, 3.5, 5.0], dtype=jnp.float32)

        def fp4_quant_dequant(x):
            shape = x.shape
            xb = x.reshape(shape[:-1] + (shape[-1] // BLOCK, BLOCK))
            scale = jnp.max(jnp.abs(xb), axis=-1, keepdims=True) / 6.0
            scale = jnp.maximum(scale, jnp.float32(1e-12))
            xn = xb / scale
            idx = jnp.searchsorted(_MID, jnp.abs(xn))
            q = _GRID[idx] * jnp.sign(xn) * scale
            return q.reshape(shape)

        def fp4_linear(x, w):
            xq = fp4_quant_dequant(x)
            wq = fp4_quant_dequant(w)
            return jnp.einsum('bsk,nk->bsn', xq, wq)
        key = jax.random.key(seed)
        k1, k2, k3, k4 = jax.random.split(key, 4)
        H, I = (128, 352)
        x = jax.random.normal(k1, (4, 512, H), dtype=jnp.float32)
        w_gate = jax.random.normal(k2, (I, H), dtype=jnp.float32) * 0.02
        w_up = jax.random.normal(k3, (I, H), dtype=jnp.float32) * 0.02
        w_down = jax.random.normal(k4, (H, I), dtype=jnp.float32) * 0.02
        return {'x': x, 'w_gate': w_gate, 'w_up': w_up, 'w_down': w_down}
    _L1_ffn_all = _L1_ffn_setup()
    _L1_ffn_in = {k: v for k, v in _L1_ffn_all.items() if k in ('w_gate', 'w_up', 'w_down')}
    del _L1_ffn_all

    def _L2_attn_setup():
        import jax, jax.numpy as jnp
        import numpy as np
        HEADS = 16
        DIM_HEAD = 64
        EPS = 1e-08
        key = jax.random.key(seed)
        ks = jax.random.split(key, 5)
        B, N, D = (2, 256, 128)
        inner = HEADS * DIM_HEAD
        return {'x': jax.random.normal(ks[0], (B, N, D), jnp.float32), 'Wq': jax.random.normal(ks[1], (D, inner), jnp.float32) * D ** (-0.5), 'Wkv': jax.random.normal(ks[2], (D, 2 * inner), jnp.float32) * D ** (-0.5), 'Wo': jax.random.normal(ks[3], (inner, D), jnp.float32) * inner ** (-0.5), 'bo': jax.random.normal(ks[4], (D,), jnp.float32) * 0.02}
    _L2_attn_all = _L2_attn_setup()
    _L2_attn_in = {k: v for k, v in _L2_attn_all.items() if k in ('Wq', 'Wkv', 'Wo', 'bo')}
    del _L2_attn_all

    def _L2_xattn_setup():
        import jax, jax.numpy as jnp
        import numpy as np
        EPS = 1e-05

        def layernorm(x, g, b):
            mu = jnp.mean(x, axis=-1, keepdims=True)
            var = jnp.mean(jnp.square(x - mu), axis=-1, keepdims=True)
            return (x - mu) * jax.lax.rsqrt(var + EPS) * g + b
        key = jax.random.key(seed)
        ks = jax.random.split(key, 12)
        B, L1, L2 = (8, 256, 256)
        D1, D2, E = (128, 96, 128)
        s1, s2, se = (D1 ** (-0.5), D2 ** (-0.5), E ** (-0.5))
        return {'modality1': jax.random.normal(ks[0], (B, L1, D1), jnp.float32), 'modality2': jax.random.normal(ks[1], (B, L2, D2), jnp.float32), 'ln1_g': jnp.ones((D1,), jnp.float32), 'ln1_b': jnp.zeros((D1,), jnp.float32), 'ln2_g': jnp.ones((D2,), jnp.float32), 'ln2_b': jnp.zeros((D2,), jnp.float32), 'Wq': jax.random.normal(ks[2], (D1, E), jnp.float32) * s1, 'bq': jax.random.normal(ks[3], (E,), jnp.float32) * 0.01, 'Wk': jax.random.normal(ks[4], (D2, E), jnp.float32) * s2, 'bk': jax.random.normal(ks[5], (E,), jnp.float32) * 0.01, 'Wv': jax.random.normal(ks[6], (D2, E), jnp.float32) * s2, 'bv': jax.random.normal(ks[7], (E,), jnp.float32) * 0.01, 'Wo': jax.random.normal(ks[8], (E, D1), jnp.float32) * se, 'bo': jax.random.normal(ks[9], (D1,), jnp.float32) * 0.01}
    _L2_xattn_all = _L2_xattn_setup()
    _L2_xattn_in = {k: v for k, v in _L2_xattn_all.items() if k in ('ln1_g', 'ln1_b', 'ln2_g', 'ln2_b', 'Wq', 'bq', 'Wk', 'bk', 'Wv', 'bv', 'Wo', 'bo')}
    del _L2_xattn_all

    def _L2_ffn_setup():
        import jax, jax.numpy as jnp
        import numpy as np
        EPS = 1e-05

        def _ln(x, g, b):
            mu = jnp.mean(x, axis=-1, keepdims=True)
            var = jnp.mean(jnp.square(x - mu), axis=-1, keepdims=True)
            return (x - mu) * jax.lax.rsqrt(var + EPS) * g + b

        def _forward(x, index_b, index_t, sw1, sb1, sw2, sb2, sw3, sb3, s_ln_g, s_ln_b, sg_w, sg_b, eg_w, eg_b, exp_bias, ew1, eb1, ew2, eb2, ew3, eb3, sel_ln_g, sel_ln_b):
            x1 = jnp.einsum('btd,hd->bth', x, sw1) + sb1
            x2 = jnp.einsum('btd,hd->bth', x, sw2) + sb2
            sh = _ln(jax.nn.silu(x1) * x2, s_ln_g, s_ln_b)
            shared_out = jnp.einsum('bth,dh->btd', sh, sw3) + sb3
            x_moe = x[index_b, index_t]
            shared_scores = jax.nn.sigmoid(x_moe @ sg_w.T + sg_b)
            expert_scores = jax.nn.sigmoid(x_moe @ eg_w.T + eg_b)
            top1_idx = jnp.argmax(expert_scores + exp_bias, axis=-1)
            top1_score = jnp.take_along_axis(expert_scores, top1_idx[:, None], axis=-1)
            weights = jax.nn.softmax(jnp.concatenate([shared_scores, top1_score], axis=-1), axis=-1)
            shared_w, expert_w = (weights[:, 0], weights[:, 1])
            shared_moe_out = shared_out[index_b, index_t] * shared_w[:, None]
            h1 = jnp.einsum('md,ehd->meh', x_moe, ew1) + eb1
            h2 = jnp.einsum('md,ehd->meh', x_moe, ew2) + eb2
            z = _ln(jax.nn.silu(h1) * h2, sel_ln_g, sel_ln_b)
            out_all = jnp.einsum('meh,edh->med', z, ew3) + eb3
            expert_out = jnp.take_along_axis(out_all, top1_idx[:, None, None], axis=1)[:, 0]
            expert_moe_out = expert_out * expert_w[:, None]
            final_out = shared_out.at[index_b, index_t].set(shared_moe_out + expert_moe_out)
            return final_out
        B, T, D, E, H, M = (2, 256, 128, 8, 64, 256)
        key = jax.random.key(seed)
        ks = jax.random.split(key, 24)
        s = 0.02
        inp = {}
        inp['x'] = jax.random.normal(ks[0], (B, T, D), jnp.float32)
        flat = jnp.arange(M, dtype=jnp.int32) * 2
        inp['index_b'] = flat // T
        inp['index_t'] = flat % T
        inp['sw1'] = jax.random.normal(ks[1], (H, D), jnp.float32) * s
        inp['sb1'] = jnp.zeros((H,), jnp.float32)
        inp['sw2'] = jax.random.normal(ks[2], (H, D), jnp.float32) * s
        inp['sb2'] = jnp.zeros((H,), jnp.float32)
        inp['sw3'] = jax.random.normal(ks[3], (D, H), jnp.float32) * s
        inp['sb3'] = jnp.zeros((D,), jnp.float32)
        inp['s_ln_g'] = jnp.ones((H,), jnp.float32)
        inp['s_ln_b'] = jnp.zeros((H,), jnp.float32)
        inp['sg_w'] = jax.random.normal(ks[4], (1, D), jnp.float32) * s
        inp['sg_b'] = jnp.zeros((1,), jnp.float32)
        inp['eg_w'] = jax.random.normal(ks[5], (E, D), jnp.float32) * s
        inp['eg_b'] = jnp.zeros((E,), jnp.float32)
        inp['exp_bias'] = jnp.zeros((E,), jnp.float32)
        inp['ew1'] = jax.random.normal(ks[6], (E, H, D), jnp.float32) * s
        inp['eb1'] = jnp.zeros((E, H), jnp.float32)
        inp['ew2'] = jax.random.normal(ks[7], (E, H, D), jnp.float32) * s
        inp['eb2'] = jnp.zeros((E, H), jnp.float32)
        inp['ew3'] = jax.random.normal(ks[8], (E, D, H), jnp.float32) * s
        inp['eb3'] = jnp.zeros((E, D), jnp.float32)
        inp['sel_ln_g'] = jnp.ones((H,), jnp.float32)
        inp['sel_ln_b'] = jnp.zeros((H,), jnp.float32)
        return inp
    _L2_ffn_all = _L2_ffn_setup()
    _L2_ffn_in = {k: v for k, v in _L2_ffn_all.items() if k in ('index_b', 'index_t', 'sw1', 'sb1', 'sw2', 'sb2', 'sw3', 'sb3', 's_ln_g', 's_ln_b', 'sg_w', 'sg_b', 'eg_w', 'eg_b', 'exp_bias', 'ew1', 'eb1', 'ew2', 'eb2', 'ew3', 'eb3', 'sel_ln_g', 'sel_ln_b')}
    del _L2_ffn_all

    def _L3_attn_setup():
        import jax, jax.numpy as jnp
        import numpy as np
        B, S, D = (2, 256, 128)
        H, DH = (16, 64)
        DQL, DKVL = (64, 64)
        DR = 64
        TOPK = 64
        LN_EPS = 1e-05
        ROPE_BASE = 10000.0

        def _rope_tables(seq_len, dim):
            inv_freq = 1.0 / ROPE_BASE ** (np.arange(0, dim, 2, dtype=np.float32) / dim)
            t = np.arange(seq_len, dtype=np.float32)
            freqs = np.outer(t, inv_freq)
            cos = np.concatenate([np.cos(freqs), np.cos(freqs)], -1)[:, ::2]
            sin = np.concatenate([np.sin(freqs), np.sin(freqs)], -1)[:, ::2]
            return (jnp.asarray(cos), jnp.asarray(sin))

        def _apply_rope_subspace(x, d_rope):
            s = x.shape[-2]
            cos, sin = _rope_tables(s, d_rope)
            xr, xp = (x[..., :d_rope], x[..., d_rope:])
            e, o = (xr[..., 0::2], xr[..., 1::2])
            rot = jnp.stack([e * cos - o * sin, e * sin + o * cos], axis=-1).reshape(xr.shape)
            return jnp.concatenate([rot, xp], axis=-1)

        def _reference_tuple_inner(x, w_down_q, w_down_kv, w_up_q, w_up_k, w_up_v, w_out, ln_scale, ln_bias):
            b, s, d = x.shape
            residual = x
            mu = jnp.mean(x, axis=-1, keepdims=True)
            var = jnp.mean((x - mu) ** 2, axis=-1, keepdims=True)
            h = (x - mu) * jax.lax.rsqrt(var + LN_EPS) * ln_scale + ln_bias
            c_q = h @ w_down_q.T
            c_kv = h @ w_down_kv.T
            q = (c_q @ w_up_q.T).reshape(b, s, H, DH).transpose(0, 2, 1, 3)
            k = (c_kv @ w_up_k.T).reshape(b, s, H, DH).transpose(0, 2, 1, 3)
            v = (c_kv @ w_up_v.T).reshape(b, s, H, DH).transpose(0, 2, 1, 3)
            q = _apply_rope_subspace(q, DR)
            k = _apply_rope_subspace(k, DR)
            scale = 1.0 / np.sqrt(DH).astype(np.float32)
            scores = jnp.einsum('bhqd,bhkd->bhqk', q, k) * scale
            _, indices = jax.lax.top_k(scores, min(TOPK, s))
            attn = jax.nn.softmax(scores, axis=-1)
            out = jnp.einsum('bhqk,bhkd->bhqd', attn, v)
            out = out.transpose(0, 2, 1, 3).reshape(b, s, H * DH)
            out = out @ w_out.T + residual
            return (out, indices.astype(jnp.int64))
        key = jax.random.key(seed)
        ks = jax.random.split(key, 7)
        init = lambda k, shape: jax.random.normal(k, shape, jnp.float32) * 0.02
        return {'x': jax.random.normal(ks[0], (B, S, D), jnp.float32), 'w_down_q': init(ks[1], (DQL, D)), 'w_down_kv': init(ks[2], (DKVL, D)), 'w_up_q': init(ks[3], (H * DH, DQL)), 'w_up_k': init(ks[4], (H * DH, DKVL)), 'w_up_v': init(ks[5], (H * DH, DKVL)), 'w_out': init(ks[6], (D, H * DH)), 'ln_scale': jnp.ones((D,), jnp.float32), 'ln_bias': jnp.zeros((D,), jnp.float32)}
    _L3_attn_all = _L3_attn_setup()
    _L3_attn_in = {k: v for k, v in _L3_attn_all.items() if k in ('w_down_q', 'w_down_kv', 'w_up_q', 'w_up_k', 'w_up_v', 'w_out', 'ln_scale', 'ln_bias')}
    del _L3_attn_all

    def _L3_xattn_setup():
        import jax, jax.numpy as jnp
        import numpy as np
        import math
        B, L, E = (16, 512, 128)
        LC, EC = (77, 96)
        H = 16
        DH = E // H
        key = jax.random.key(seed)
        ks = jax.random.split(key, 10)
        s = 0.02
        return {'x': jax.random.normal(ks[0], (B, L, E), jnp.float32), 'cross': jax.random.normal(ks[1], (B, LC, EC), jnp.float32), 'q_w': jax.random.normal(ks[2], (E, E), jnp.float32) * s, 'q_b': jax.random.normal(ks[3], (E,), jnp.float32) * s, 'k_w': jax.random.normal(ks[4], (E, EC), jnp.float32) * s, 'k_b': jax.random.normal(ks[5], (E,), jnp.float32) * s, 'v_w': jax.random.normal(ks[6], (E, EC), jnp.float32) * s, 'v_b': jax.random.normal(ks[7], (E,), jnp.float32) * s, 'o_w': jax.random.normal(ks[8], (E, E), jnp.float32) * s, 'o_b': jax.random.normal(ks[9], (E,), jnp.float32) * s}
    _L3_xattn_all = _L3_xattn_setup()
    _L3_xattn_in = {k: v for k, v in _L3_xattn_all.items() if k in ('q_w', 'q_b', 'k_w', 'k_b', 'v_w', 'v_b', 'o_w', 'o_b')}
    del _L3_xattn_all

    def _L3_ffn_setup():
        import jax, jax.numpy as jnp
        import numpy as np
        MAX_VAL = 100.0
        key = jax.random.key(seed)
        k1, k2, k3 = jax.random.split(key, 3)
        B, S, D_IN, D_OUT = (4, 1024, 128, 128)
        x = jax.random.normal(k1, (B, S, D_IN), dtype=jnp.float32)
        weights = jax.random.normal(k2, (D_OUT, D_IN), dtype=jnp.float32)
        scale = jnp.ones((D_OUT,), dtype=jnp.float32)
        bias = jax.random.normal(k3, (D_OUT,), dtype=jnp.float32)
        return {'x': x, 'weights': weights, 'scale': scale, 'bias': bias}
    _L3_ffn_all = _L3_ffn_setup()
    _L3_ffn_in = {k: v for k, v in _L3_ffn_all.items() if k in ('weights', 'scale', 'bias')}
    del _L3_ffn_all
    return {'x': x, 'ctx_768': ctx_768, 'L0_attn_norm1_w': _L0_attn_in['norm1_w'], 'L0_attn_norm2_w': _L0_attn_in['norm2_w'], 'L0_attn_in_proj_w': _L0_attn_in['in_proj_w'], 'L0_attn_out_proj_w': _L0_attn_in['out_proj_w'], 'L0_attn_fc_w': _L0_attn_in['fc_w'], 'L0_attn_proj_w': _L0_attn_in['proj_w'], 'L0_xattn_Wq': _L0_xattn_in['Wq'], 'L0_xattn_bq': _L0_xattn_in['bq'], 'L0_xattn_Wk': _L0_xattn_in['Wk'], 'L0_xattn_bk': _L0_xattn_in['bk'], 'L0_xattn_Wv': _L0_xattn_in['Wv'], 'L0_xattn_bv': _L0_xattn_in['bv'], 'L0_xattn_Wo': _L0_xattn_in['Wo'], 'L0_xattn_bo': _L0_xattn_in['bo'], 'L0_ffn_centroids': _L0_ffn_in['centroids'], 'L0_ffn_expert_biases': _L0_ffn_in['expert_biases'], 'L0_ffn_Ws_up': _L0_ffn_in['Ws_up'], 'L0_ffn_Ws_down': _L0_ffn_in['Ws_down'], 'L0_ffn_W_up': _L0_ffn_in['W_up'], 'L0_ffn_W_down': _L0_ffn_in['W_down'], 'L1_attn_Wk': _L1_attn_in['Wk'], 'L1_attn_Wq': _L1_attn_in['Wq'], 'L1_attn_Wo': _L1_attn_in['Wo'], 'L1_attn_bo': _L1_attn_in['bo'], 'L1_xattn_Wq': _L1_xattn_in['Wq'], 'L1_xattn_bq': _L1_xattn_in['bq'], 'L1_xattn_Wk': _L1_xattn_in['Wk'], 'L1_xattn_bk': _L1_xattn_in['bk'], 'L1_xattn_Wv': _L1_xattn_in['Wv'], 'L1_xattn_bv': _L1_xattn_in['bv'], 'L1_xattn_Wo': _L1_xattn_in['Wo'], 'L1_xattn_bo': _L1_xattn_in['bo'], 'L1_ffn_w_gate': _L1_ffn_in['w_gate'], 'L1_ffn_w_up': _L1_ffn_in['w_up'], 'L1_ffn_w_down': _L1_ffn_in['w_down'], 'L2_attn_Wq': _L2_attn_in['Wq'], 'L2_attn_Wkv': _L2_attn_in['Wkv'], 'L2_attn_Wo': _L2_attn_in['Wo'], 'L2_attn_bo': _L2_attn_in['bo'], 'L2_xattn_ln1_g': _L2_xattn_in['ln1_g'], 'L2_xattn_ln1_b': _L2_xattn_in['ln1_b'], 'L2_xattn_ln2_g': _L2_xattn_in['ln2_g'], 'L2_xattn_ln2_b': _L2_xattn_in['ln2_b'], 'L2_xattn_Wq': _L2_xattn_in['Wq'], 'L2_xattn_bq': _L2_xattn_in['bq'], 'L2_xattn_Wk': _L2_xattn_in['Wk'], 'L2_xattn_bk': _L2_xattn_in['bk'], 'L2_xattn_Wv': _L2_xattn_in['Wv'], 'L2_xattn_bv': _L2_xattn_in['bv'], 'L2_xattn_Wo': _L2_xattn_in['Wo'], 'L2_xattn_bo': _L2_xattn_in['bo'], 'L2_ffn_index_b': _L2_ffn_in['index_b'], 'L2_ffn_index_t': _L2_ffn_in['index_t'], 'L2_ffn_sw1': _L2_ffn_in['sw1'], 'L2_ffn_sb1': _L2_ffn_in['sb1'], 'L2_ffn_sw2': _L2_ffn_in['sw2'], 'L2_ffn_sb2': _L2_ffn_in['sb2'], 'L2_ffn_sw3': _L2_ffn_in['sw3'], 'L2_ffn_sb3': _L2_ffn_in['sb3'], 'L2_ffn_s_ln_g': _L2_ffn_in['s_ln_g'], 'L2_ffn_s_ln_b': _L2_ffn_in['s_ln_b'], 'L2_ffn_sg_w': _L2_ffn_in['sg_w'], 'L2_ffn_sg_b': _L2_ffn_in['sg_b'], 'L2_ffn_eg_w': _L2_ffn_in['eg_w'], 'L2_ffn_eg_b': _L2_ffn_in['eg_b'], 'L2_ffn_exp_bias': _L2_ffn_in['exp_bias'], 'L2_ffn_ew1': _L2_ffn_in['ew1'], 'L2_ffn_eb1': _L2_ffn_in['eb1'], 'L2_ffn_ew2': _L2_ffn_in['ew2'], 'L2_ffn_eb2': _L2_ffn_in['eb2'], 'L2_ffn_ew3': _L2_ffn_in['ew3'], 'L2_ffn_eb3': _L2_ffn_in['eb3'], 'L2_ffn_sel_ln_g': _L2_ffn_in['sel_ln_g'], 'L2_ffn_sel_ln_b': _L2_ffn_in['sel_ln_b'], 'L3_attn_w_down_q': _L3_attn_in['w_down_q'], 'L3_attn_w_down_kv': _L3_attn_in['w_down_kv'], 'L3_attn_w_up_q': _L3_attn_in['w_up_q'], 'L3_attn_w_up_k': _L3_attn_in['w_up_k'], 'L3_attn_w_up_v': _L3_attn_in['w_up_v'], 'L3_attn_w_out': _L3_attn_in['w_out'], 'L3_attn_ln_scale': _L3_attn_in['ln_scale'], 'L3_attn_ln_bias': _L3_attn_in['ln_bias'], 'L3_xattn_q_w': _L3_xattn_in['q_w'], 'L3_xattn_q_b': _L3_xattn_in['q_b'], 'L3_xattn_k_w': _L3_xattn_in['k_w'], 'L3_xattn_k_b': _L3_xattn_in['k_b'], 'L3_xattn_v_w': _L3_xattn_in['v_w'], 'L3_xattn_v_b': _L3_xattn_in['v_b'], 'L3_xattn_o_w': _L3_xattn_in['o_w'], 'L3_xattn_o_b': _L3_xattn_in['o_b'], 'L3_ffn_weights': _L3_ffn_in['weights'], 'L3_ffn_scale': _L3_ffn_in['scale'], 'L3_ffn_bias': _L3_ffn_in['bias']}

def reference(x, ctx_768, L0_attn_norm1_w, L0_attn_norm2_w, L0_attn_in_proj_w, L0_attn_out_proj_w, L0_attn_fc_w, L0_attn_proj_w, L0_xattn_Wq, L0_xattn_bq, L0_xattn_Wk, L0_xattn_bk, L0_xattn_Wv, L0_xattn_bv, L0_xattn_Wo, L0_xattn_bo, L0_ffn_centroids, L0_ffn_expert_biases, L0_ffn_Ws_up, L0_ffn_Ws_down, L0_ffn_W_up, L0_ffn_W_down, L1_attn_Wk, L1_attn_Wq, L1_attn_Wo, L1_attn_bo, L1_xattn_Wq, L1_xattn_bq, L1_xattn_Wk, L1_xattn_bk, L1_xattn_Wv, L1_xattn_bv, L1_xattn_Wo, L1_xattn_bo, L1_ffn_w_gate, L1_ffn_w_up, L1_ffn_w_down, L2_attn_Wq, L2_attn_Wkv, L2_attn_Wo, L2_attn_bo, L2_xattn_ln1_g, L2_xattn_ln1_b, L2_xattn_ln2_g, L2_xattn_ln2_b, L2_xattn_Wq, L2_xattn_bq, L2_xattn_Wk, L2_xattn_bk, L2_xattn_Wv, L2_xattn_bv, L2_xattn_Wo, L2_xattn_bo, L2_ffn_index_b, L2_ffn_index_t, L2_ffn_sw1, L2_ffn_sb1, L2_ffn_sw2, L2_ffn_sb2, L2_ffn_sw3, L2_ffn_sb3, L2_ffn_s_ln_g, L2_ffn_s_ln_b, L2_ffn_sg_w, L2_ffn_sg_b, L2_ffn_eg_w, L2_ffn_eg_b, L2_ffn_exp_bias, L2_ffn_ew1, L2_ffn_eb1, L2_ffn_ew2, L2_ffn_eb2, L2_ffn_ew3, L2_ffn_eb3, L2_ffn_sel_ln_g, L2_ffn_sel_ln_b, L3_attn_w_down_q, L3_attn_w_down_kv, L3_attn_w_up_q, L3_attn_w_up_k, L3_attn_w_up_v, L3_attn_w_out, L3_attn_ln_scale, L3_attn_ln_bias, L3_xattn_q_w, L3_xattn_q_b, L3_xattn_k_w, L3_xattn_k_b, L3_xattn_v_w, L3_xattn_v_b, L3_xattn_o_w, L3_xattn_o_b, L3_ffn_weights, L3_ffn_scale, L3_ffn_bias):
    import jax
    import jax.numpy as jnp

    def _L0_attn_ref(x, norm1_w, norm2_w, in_proj_w, out_proj_w, fc_w, proj_w):
        import jax, jax.numpy as jnp
        import numpy as np
        DIM = 128
        HEADS = 16
        HDIM = DIM // HEADS
        CHUNK = 64
        RES_SCALE = float(1.0 / np.sqrt(2.0))
        EPS_FP32 = float(np.finfo(np.float32).eps)

        def _rms(x, eps):
            return x * jax.lax.rsqrt(jnp.mean(x * x, axis=-1, keepdims=True) + eps)

        def _mixer(x, in_proj_w, out_proj_w):
            B, S, D = x.shape
            proj = x @ in_proj_w.T
            q, k, v, a, g = jnp.split(proj, 5, axis=-1)
            rs = lambda t: t.reshape(B, S, HEADS, HDIM)
            q, k, v, a, g = map(rs, (q, k, v, a, g))
            q = _rms(q, EPS_FP32)
            k = jnp.tanh(k)
            a = jnp.clip(jax.nn.sigmoid(a + 2.0), 0.6, 0.9995)
            u = k * v
            nC = S // CHUNK
            a_c = jnp.moveaxis(a.reshape(B, nC, CHUNK, HEADS, HDIM), 1, 0)
            u_c = jnp.moveaxis(u.reshape(B, nC, CHUNK, HEADS, HDIM), 1, 0)

            def step(state, inp):
                ac, uc = inp
                prefix = jnp.cumprod(ac, axis=1)
                acc = jnp.cumsum(uc / jnp.maximum(prefix, 1e-06), axis=1)
                states = prefix * (state[:, None] + acc)
                return (states[:, -1], states)
            state0 = jnp.zeros((B, HEADS, HDIM), jnp.float32)
            _, states = jax.lax.scan(step, state0, (a_c, u_c))
            memory = jnp.moveaxis(states, 0, 1).reshape(B, S, HEADS, HDIM)
            gate = jax.nn.sigmoid(g)
            y = gate * (q * memory) + (1.0 - gate) * v
            return y.reshape(B, S, D) @ out_proj_w.T
        h1 = norm1_w * _rms(x, 1e-06)
        x = x + RES_SCALE * _mixer(h1, in_proj_w, out_proj_w)
        h2 = norm2_w * _rms(x, 1e-06)
        mlp = jax.nn.silu(h2 @ fc_w.T) @ proj_w.T
        return x + RES_SCALE * mlp

    def _L0_xattn_ref(query, key_value, Wq, bq, Wk, bk, Wv, bv, Wo, bo):
        import jax, jax.numpy as jnp
        import numpy as np
        NUM_HEADS = 16
        CLAMP = 10000.0
        B, Nq, Cq = query.shape
        Nkv = key_value.shape[1]
        H = NUM_HEADS
        D = Cq // H
        scale = D ** (-0.5)
        q = (query @ Wq + bq).reshape(B, Nq, H, D).transpose(0, 2, 1, 3)
        k = (key_value @ Wk + bk).reshape(B, Nkv, H, D).transpose(0, 2, 1, 3)
        v = (key_value @ Wv + bv).reshape(B, Nkv, H, D).transpose(0, 2, 1, 3)
        attn = jnp.einsum('bhqd,bhkd->bhqk', q, k) * scale
        attn = jnp.clip(attn, -CLAMP, CLAMP)
        attn = jax.nn.softmax(attn, axis=-1)
        attn = jnp.where(jnp.any(jnp.isnan(attn)), jnp.asarray(1.0 / Nkv, attn.dtype), attn)
        x = jnp.einsum('bhqk,bhkd->bqhd', attn, v).reshape(B, Nq, Cq)
        return x @ Wo + bo

    def _L0_ffn_ref(x, centroids, expert_biases, Ws_up, Ws_down, W_up, W_down):
        import jax, jax.numpy as jnp
        import numpy as np
        TOP_K = 8
        B, S, D = x.shape
        E = centroids.shape[0]
        T = B * S
        xf = x.reshape(T, D)
        shared = jax.nn.silu(xf @ Ws_up) @ Ws_down
        aff = xf @ centroids.T
        biased = aff + expert_biases
        _, idx = jax.lax.top_k(biased, TOP_K)
        sel = jnp.take_along_axis(aff, idx, axis=1)
        w = jax.nn.sigmoid(sel)
        w = w / (jnp.sum(w, axis=-1, keepdims=True) + 1e-08)
        cw = jnp.zeros((T, E), dtype=x.dtype).at[jnp.arange(T)[:, None], idx].add(w)
        h = jax.nn.silu(jnp.einsum('td,edf->etf', xf, W_up))
        y = jnp.einsum('etf,efd->etd', h, W_down)
        routed = jnp.einsum('etd,te->td', y, cw)
        return (shared + routed).reshape(B, S, D)

    def _L1_attn_ref(x, Wk, Wq, Wo, bo):
        import jax, jax.numpy as jnp
        import numpy as np
        B, T, E, H = (4, 256, 128, 16)
        S = E // H
        b, t, e = x.shape
        h, s = (H, E // H)
        scale = e ** (-0.25)
        k = (x @ Wk).reshape(b, t, h, s).transpose(0, 2, 1, 3)
        q = (x @ Wq).reshape(b, t, h, s).transpose(0, 2, 1, 3)
        v = (x @ Wk).reshape(b, t, h, s).transpose(0, 2, 1, 3)
        dot = jnp.einsum('bhqd,bhkd->bhqk', q * scale, k * scale)
        attn = jax.nn.softmax(dot, axis=-1)
        out = jnp.einsum('bhqk,bhkd->bhqd', attn, v)
        out = out.transpose(0, 2, 1, 3).reshape(b, t, e)
        return out @ Wo + bo

    def _L1_xattn_ref(x, y, Wq, bq, Wk, bk, Wv, bv, Wo, bo):
        import jax, jax.numpy as jnp
        import numpy as np
        N_HEADS = 8
        D_EMBED = 128
        D_CROSS = 96
        D_HEAD = D_EMBED // N_HEADS
        q = jnp.einsum('bqd,de->bqe', x, Wq) + bq
        k = jnp.einsum('bkc,ce->bke', y, Wk) + bk
        v = jnp.einsum('bkc,ce->bke', y, Wv) + bv
        scale = 1.0 / np.sqrt(D_HEAD)
        scores = jnp.einsum('bqe,bke->bqk', q, k) * scale
        attn = jax.nn.softmax(scores, axis=-1)
        out = jnp.einsum('bqk,bke->bqe', attn, v)
        return jnp.einsum('bqe,ef->bqf', out, Wo) + bo

    def _L1_ffn_ref(x, w_gate, w_up, w_down):
        import jax, jax.numpy as jnp
        import numpy as np
        BLOCK = 16
        _GRID = jnp.array([0.0, 0.5, 1.0, 1.5, 2.0, 3.0, 4.0, 6.0], dtype=jnp.float32)
        _MID = jnp.array([0.25, 0.75, 1.25, 1.75, 2.5, 3.5, 5.0], dtype=jnp.float32)

        def fp4_quant_dequant(x):
            shape = x.shape
            xb = x.reshape(shape[:-1] + (shape[-1] // BLOCK, BLOCK))
            scale = jnp.max(jnp.abs(xb), axis=-1, keepdims=True) / 6.0
            scale = jnp.maximum(scale, jnp.float32(1e-12))
            xn = xb / scale
            idx = jnp.searchsorted(_MID, jnp.abs(xn))
            q = _GRID[idx] * jnp.sign(xn) * scale
            return q.reshape(shape)

        def fp4_linear(x, w):
            xq = fp4_quant_dequant(x)
            wq = fp4_quant_dequant(w)
            return jnp.einsum('bsk,nk->bsn', xq, wq)
        gate = fp4_linear(x, w_gate)
        y = fp4_linear(x, w_up)
        h = jax.nn.silu(gate) * y
        return fp4_linear(h, w_down)

    def _L2_attn_ref(x, Wq, Wkv, Wo, bo):
        import jax, jax.numpy as jnp
        import numpy as np
        HEADS = 16
        DIM_HEAD = 64
        EPS = 1e-08
        B, N, D = x.shape
        H, Dh = (HEADS, DIM_HEAD)
        scale = Dh ** (-0.5)
        q = (x @ Wq).reshape(B, N, H, Dh).transpose(0, 2, 1, 3)
        kv = x @ Wkv
        k = kv[..., :H * Dh].reshape(B, N, H, Dh).transpose(0, 2, 1, 3)
        v = kv[..., H * Dh:].reshape(B, N, H, Dh).transpose(0, 2, 1, 3)
        s = jnp.einsum('bhid,bhjd->bhij', q * scale, k)
        gm = jax.lax.stop_gradient(jnp.max(s, axis=-1, keepdims=True))
        causal_mask = jnp.triu(jnp.ones((N, N), bool), 1)
        p = jnp.where(causal_mask, 0.0, jnp.exp(s - gm))
        num = jnp.einsum('bhij,bhjd->bhid', p, v)
        out = num / (jnp.sum(p, axis=-1, keepdims=True) + EPS)
        out = out.transpose(0, 2, 1, 3).reshape(B, N, H * Dh)
        return out @ Wo + bo

    def _L2_xattn_ref(modality1, modality2, ln1_g, ln1_b, ln2_g, ln2_b, Wq, bq, Wk, bk, Wv, bv, Wo, bo):
        import jax, jax.numpy as jnp
        import numpy as np
        EPS = 1e-05

        def layernorm(x, g, b):
            mu = jnp.mean(x, axis=-1, keepdims=True)
            var = jnp.mean(jnp.square(x - mu), axis=-1, keepdims=True)
            return (x - mu) * jax.lax.rsqrt(var + EPS) * g + b
        E = Wq.shape[1]
        scaling = E ** (-0.5)
        x1 = layernorm(modality1, ln1_g, ln1_b)
        x2 = layernorm(modality2, ln2_g, ln2_b)
        q = x1 @ Wq + bq
        k = x2 @ Wk + bk
        v = x2 @ Wv + bv
        scores = jnp.einsum('bqe,bke->bqk', q, k) * scaling
        attn = jax.nn.softmax(scores, axis=-1)
        ctx = jnp.einsum('bqk,bke->bqe', attn, v)
        return ctx @ Wo + bo

    def _L2_ffn_ref(x, index_b, index_t, sw1, sb1, sw2, sb2, sw3, sb3, s_ln_g, s_ln_b, sg_w, sg_b, eg_w, eg_b, exp_bias, ew1, eb1, ew2, eb2, ew3, eb3, sel_ln_g, sel_ln_b):
        import jax, jax.numpy as jnp
        import numpy as np
        EPS = 1e-05

        def _ln(x, g, b):
            mu = jnp.mean(x, axis=-1, keepdims=True)
            var = jnp.mean(jnp.square(x - mu), axis=-1, keepdims=True)
            return (x - mu) * jax.lax.rsqrt(var + EPS) * g + b

        def _forward(x, index_b, index_t, sw1, sb1, sw2, sb2, sw3, sb3, s_ln_g, s_ln_b, sg_w, sg_b, eg_w, eg_b, exp_bias, ew1, eb1, ew2, eb2, ew3, eb3, sel_ln_g, sel_ln_b):
            x1 = jnp.einsum('btd,hd->bth', x, sw1) + sb1
            x2 = jnp.einsum('btd,hd->bth', x, sw2) + sb2
            sh = _ln(jax.nn.silu(x1) * x2, s_ln_g, s_ln_b)
            shared_out = jnp.einsum('bth,dh->btd', sh, sw3) + sb3
            x_moe = x[index_b, index_t]
            shared_scores = jax.nn.sigmoid(x_moe @ sg_w.T + sg_b)
            expert_scores = jax.nn.sigmoid(x_moe @ eg_w.T + eg_b)
            top1_idx = jnp.argmax(expert_scores + exp_bias, axis=-1)
            top1_score = jnp.take_along_axis(expert_scores, top1_idx[:, None], axis=-1)
            weights = jax.nn.softmax(jnp.concatenate([shared_scores, top1_score], axis=-1), axis=-1)
            shared_w, expert_w = (weights[:, 0], weights[:, 1])
            shared_moe_out = shared_out[index_b, index_t] * shared_w[:, None]
            h1 = jnp.einsum('md,ehd->meh', x_moe, ew1) + eb1
            h2 = jnp.einsum('md,ehd->meh', x_moe, ew2) + eb2
            z = _ln(jax.nn.silu(h1) * h2, sel_ln_g, sel_ln_b)
            out_all = jnp.einsum('meh,edh->med', z, ew3) + eb3
            expert_out = jnp.take_along_axis(out_all, top1_idx[:, None, None], axis=1)[:, 0]
            expert_moe_out = expert_out * expert_w[:, None]
            final_out = shared_out.at[index_b, index_t].set(shared_moe_out + expert_moe_out)
            return final_out
        return _forward(x, index_b, index_t, sw1, sb1, sw2, sb2, sw3, sb3, s_ln_g, s_ln_b, sg_w, sg_b, eg_w, eg_b, exp_bias, ew1, eb1, ew2, eb2, ew3, eb3, sel_ln_g, sel_ln_b)

    def _L3_attn_ref(x, w_down_q, w_down_kv, w_up_q, w_up_k, w_up_v, w_out, ln_scale, ln_bias):
        import jax, jax.numpy as jnp
        import numpy as np
        B, S, D = (2, 256, 128)
        H, DH = (16, 64)
        DQL, DKVL = (64, 64)
        DR = 64
        TOPK = 64
        LN_EPS = 1e-05
        ROPE_BASE = 10000.0

        def _rope_tables(seq_len, dim):
            inv_freq = 1.0 / ROPE_BASE ** (np.arange(0, dim, 2, dtype=np.float32) / dim)
            t = np.arange(seq_len, dtype=np.float32)
            freqs = np.outer(t, inv_freq)
            cos = np.concatenate([np.cos(freqs), np.cos(freqs)], -1)[:, ::2]
            sin = np.concatenate([np.sin(freqs), np.sin(freqs)], -1)[:, ::2]
            return (jnp.asarray(cos), jnp.asarray(sin))

        def _apply_rope_subspace(x, d_rope):
            s = x.shape[-2]
            cos, sin = _rope_tables(s, d_rope)
            xr, xp = (x[..., :d_rope], x[..., d_rope:])
            e, o = (xr[..., 0::2], xr[..., 1::2])
            rot = jnp.stack([e * cos - o * sin, e * sin + o * cos], axis=-1).reshape(xr.shape)
            return jnp.concatenate([rot, xp], axis=-1)

        def _reference_tuple_inner(x, w_down_q, w_down_kv, w_up_q, w_up_k, w_up_v, w_out, ln_scale, ln_bias):
            b, s, d = x.shape
            residual = x
            mu = jnp.mean(x, axis=-1, keepdims=True)
            var = jnp.mean((x - mu) ** 2, axis=-1, keepdims=True)
            h = (x - mu) * jax.lax.rsqrt(var + LN_EPS) * ln_scale + ln_bias
            c_q = h @ w_down_q.T
            c_kv = h @ w_down_kv.T
            q = (c_q @ w_up_q.T).reshape(b, s, H, DH).transpose(0, 2, 1, 3)
            k = (c_kv @ w_up_k.T).reshape(b, s, H, DH).transpose(0, 2, 1, 3)
            v = (c_kv @ w_up_v.T).reshape(b, s, H, DH).transpose(0, 2, 1, 3)
            q = _apply_rope_subspace(q, DR)
            k = _apply_rope_subspace(k, DR)
            scale = 1.0 / np.sqrt(DH).astype(np.float32)
            scores = jnp.einsum('bhqd,bhkd->bhqk', q, k) * scale
            _, indices = jax.lax.top_k(scores, min(TOPK, s))
            attn = jax.nn.softmax(scores, axis=-1)
            out = jnp.einsum('bhqk,bhkd->bhqd', attn, v)
            out = out.transpose(0, 2, 1, 3).reshape(b, s, H * DH)
            out = out @ w_out.T + residual
            return (out, indices.astype(jnp.int64))
        return _reference_tuple_inner(x, w_down_q, w_down_kv, w_up_q, w_up_k, w_up_v, w_out, ln_scale, ln_bias)[0]

    def _L3_xattn_ref(x, cross, q_w, q_b, k_w, k_b, v_w, v_b, o_w, o_b):
        import jax, jax.numpy as jnp
        import numpy as np
        import math
        B, L, E = (16, 512, 128)
        LC, EC = (77, 96)
        H = 16
        DH = E // H
        b, l, e = x.shape
        q = jnp.einsum('ble,fe->blf', x, q_w) + q_b
        k = jnp.einsum('bce,fe->bcf', cross, k_w) + k_b
        v = jnp.einsum('bce,fe->bcf', cross, v_w) + v_b
        q = q.reshape(b, l, H, DH).transpose(0, 2, 1, 3)
        v = v.reshape(b, -1, H, DH).transpose(0, 2, 1, 3)
        scores = jnp.einsum('bhld,bhcd->bhlc', q, v) / math.sqrt(DH)
        attn = jax.nn.softmax(scores, axis=-1)
        qkv = jnp.einsum('bhlc,bhcd->bhld', attn, v)
        qkv = qkv.reshape(b, l, e)
        out = jnp.einsum('ble,fe->blf', qkv, o_w) + o_b
        return out

    def _L3_ffn_ref(x, weights, scale, bias):
        import jax, jax.numpy as jnp
        import numpy as np
        MAX_VAL = 100.0
        w = (weights >= 0.0).astype(x.dtype) * 2.0 - 1.0
        y = jnp.einsum('bsi,oi->bso', x, w)
        y = y * scale + bias
        y = jnp.clip(y, -MAX_VAL, MAX_VAL)
        return y
    x = x + _L0_attn_ref(_layernorm(x, axis=-1), L0_attn_norm1_w, L0_attn_norm2_w, L0_attn_in_proj_w, L0_attn_out_proj_w, L0_attn_fc_w, L0_attn_proj_w)
    x = x + _L0_xattn_ref(_layernorm(x, axis=-1), ctx_768, L0_xattn_Wq, L0_xattn_bq, L0_xattn_Wk, L0_xattn_bk, L0_xattn_Wv, L0_xattn_bv, L0_xattn_Wo, L0_xattn_bo)
    x = x + _L0_ffn_ref(_layernorm(x, axis=-1), L0_ffn_centroids, L0_ffn_expert_biases, L0_ffn_Ws_up, L0_ffn_Ws_down, L0_ffn_W_up, L0_ffn_W_down)
    x = x + _L1_attn_ref(_layernorm(x, axis=-1), L1_attn_Wk, L1_attn_Wq, L1_attn_Wo, L1_attn_bo)
    x = x + _L1_xattn_ref(_layernorm(x, axis=-1), ctx_768, L1_xattn_Wq, L1_xattn_bq, L1_xattn_Wk, L1_xattn_bk, L1_xattn_Wv, L1_xattn_bv, L1_xattn_Wo, L1_xattn_bo)
    x = x + _L1_ffn_ref(_layernorm(x, axis=-1), L1_ffn_w_gate, L1_ffn_w_up, L1_ffn_w_down)
    x = x + _L2_attn_ref(_layernorm(x, axis=-1), L2_attn_Wq, L2_attn_Wkv, L2_attn_Wo, L2_attn_bo)
    x = x + _L2_xattn_ref(_layernorm(x, axis=-1), ctx_768, L2_xattn_ln1_g, L2_xattn_ln1_b, L2_xattn_ln2_g, L2_xattn_ln2_b, L2_xattn_Wq, L2_xattn_bq, L2_xattn_Wk, L2_xattn_bk, L2_xattn_Wv, L2_xattn_bv, L2_xattn_Wo, L2_xattn_bo)
    x = x + _L2_ffn_ref(_layernorm(x, axis=-1), L2_ffn_index_b, L2_ffn_index_t, L2_ffn_sw1, L2_ffn_sb1, L2_ffn_sw2, L2_ffn_sb2, L2_ffn_sw3, L2_ffn_sb3, L2_ffn_s_ln_g, L2_ffn_s_ln_b, L2_ffn_sg_w, L2_ffn_sg_b, L2_ffn_eg_w, L2_ffn_eg_b, L2_ffn_exp_bias, L2_ffn_ew1, L2_ffn_eb1, L2_ffn_ew2, L2_ffn_eb2, L2_ffn_ew3, L2_ffn_eb3, L2_ffn_sel_ln_g, L2_ffn_sel_ln_b)
    x = x + _L3_attn_ref(_layernorm(x, axis=-1), L3_attn_w_down_q, L3_attn_w_down_kv, L3_attn_w_up_q, L3_attn_w_up_k, L3_attn_w_up_v, L3_attn_w_out, L3_attn_ln_scale, L3_attn_ln_bias)
    x = x + _L3_xattn_ref(_layernorm(x, axis=-1), ctx_768, L3_xattn_q_w, L3_xattn_q_b, L3_xattn_k_w, L3_xattn_k_b, L3_xattn_v_w, L3_xattn_v_b, L3_xattn_o_w, L3_xattn_o_b)
    x = x + _L3_ffn_ref(_layernorm(x, axis=-1), L3_ffn_weights, L3_ffn_scale, L3_ffn_bias)
    return x

_drawn_inputs = setup_inputs


def setup_inputs(seed=0):
    import zlib

    import numpy as np

    out = dict(_drawn_inputs(seed))
    spreads = {'L0_attn_norm1_w': (1.0, 0.6),
     'L0_attn_norm2_w': (1.0, 0.6),
     'L0_xattn_bq': (0.0, 0.47),
     'L0_xattn_bk': (0.0, 2.0),
     'L0_xattn_bv': (0.0, 0.1),
     'L0_xattn_bo': (0.0, 0.1),
     'L0_ffn_expert_biases': (0.0, 0.1),
     'L1_attn_bo': (0.0, 0.1),
     'L1_xattn_bq': (0.0, 0.1),
     'L1_xattn_bk': (0.0, 2.0),
     'L1_xattn_bv': (0.0, 0.1),
     'L1_xattn_bo': (0.0, 0.1),
     'L2_xattn_ln1_g': (1.0, 0.6),
     'L2_xattn_ln1_b': (0.0, 0.697),
     'L2_xattn_ln2_g': (1.0, 0.2),
     'L2_xattn_ln2_b': (0.0, 0.1),
     'L2_ffn_sb1': (0.0, 0.412),
     'L2_ffn_sb2': (0.0, 0.282),
     'L2_ffn_sb3': (0.0, 0.1),
     'L2_ffn_s_ln_g': (1.0, 0.6),
     'L2_ffn_s_ln_b': (0.0, 0.8),
     'L2_ffn_eg_b': (0.0, 0.8),
     'L2_ffn_exp_bias': (0.0, 0.612),
     'L2_ffn_eb1': (0.0, 0.8),
     'L2_ffn_eb2': (0.0, 0.8),
     'L2_ffn_eb3': (0.0, 0.8),
     'L2_ffn_sel_ln_g': (1.0, 0.6),
     'L2_ffn_sel_ln_b': (0.0, 0.8),
     'L3_attn_ln_scale': (1.0, 0.6),
     'L3_attn_ln_bias': (0.0, 0.8),
     'L3_ffn_scale': (1.0, 0.2)}
    factors = {'L0_attn_in_proj_w': 4.288,
     'L0_attn_out_proj_w': 4.264,
     'L0_attn_fc_w': 2.711,
     'L0_attn_proj_w': 2.741,
     'L1_ffn_w_gate': 8.0,
     'L1_ffn_w_up': 8.0,
     'L1_ffn_w_down': 8.0,
     'L2_attn_bo': 7.488,
     'L2_xattn_bq': 63.999,
     'L2_xattn_bk': 64.0,
     'L2_xattn_bv': 8.0,
     'L2_xattn_bo': 8.0,
     'L2_ffn_sg_w': 27.747,
     'L2_ffn_eg_w': 5.003,
     'L2_ffn_ew1': 5.815,
     'L2_ffn_ew2': 5.775,
     'L2_ffn_ew3': 5.28,
     'L3_attn_w_down_q': 8.0,
     'L3_attn_w_down_kv': 8.0,
     'L3_attn_w_up_q': 8.0,
     'L3_attn_w_up_k': 8.0,
     'L3_attn_w_up_v': 8.0,
     'L3_attn_w_out': 8.0,
     'L3_xattn_q_w': 8.0,
     'L3_xattn_q_b': 32.124,
     'L3_xattn_v_w': 8.0,
     'L3_xattn_v_b': 31.79,
     'L3_xattn_o_w': 8.0,
     'L3_xattn_o_b': 51.107}
    for name, (base, spread) in spreads.items():
        noise = np.random.default_rng([zlib.crc32(name.encode()), seed]).standard_normal(out[name].shape)
        drawn = base * np.exp(spread * noise) if base else spread * noise
        out[name] = jnp.asarray(drawn.astype(out[name].dtype))
    for name, factor in factors.items():
        out[name] = (out[name] * factor).astype(out[name].dtype)
    return out
```

```python
import numpy as np
import concourse.bass as bass
from concourse import mybir
from contextlib import ExitStack

F32 = mybir.dt.float32
BF16 = mybir.dt.bfloat16
I32 = mybir.dt.int32
ALU = mybir.AluOpType
ACT = mybir.ActivationFunctionType
AX = mybir.AxisListType

LAYERS = [0, 1, 2, 3, 4, 5, 6, 7, 8, 9, 10, 11]

B, S, D = 8, 256, 128
P = 128
TB = S // P
NT = B * TB
SK, DK = 512, 96
KT = SK // P
LN_EPS = 1e-5


class Links:

    def __init__(self, eng, sem, base=0):
        self.eng, self.sem, self.base, self.n = eng, sem, base, 0

    def mark(self, ins):
        ins.then_inc(self.sem, 1)
        self.n += 1

    def wait(self):
        self.eng.wait_ge(self.sem, self.base + self.n)

    def __call__(self, ins):
        self.mark(ins)
        self.wait()


class Model:

    def __init__(self, nc, dram, out, ctx):
        self.nc, self.dram, self.out, self.ctx = nc, dram, out, ctx
        self.x = self.sb("x", [P, B, TB, D], F32)
        self.ident = self.sb("ident", [P, P], F32)
        self.identb = self.sb("identb", [P, P], BF16)
        self.half = self.sb("minus_half", [P, 64], F32)

    def sb(self, name, shape, dt=F32):
        return self.ctx.enter_context(self.nc.sbuf_tensor(name, shape, dt))


def rows(ap):
    return ap.rearrange("(a d) -> a d", a=1)


def setup(m):
    nc = m.nc
    with ExitStack() as es:
        _, _, sem = allocators(nc, es, "setup")
        x_loaded, pool_chain = sem("x_loaded"), sem("pool_chain")
        block = es.enter_context(nc.Block())

        @block.sync
        def _(sp):
            for b in range(B):
                sp.dma_start(m.x[:, b], m.dram["x"][b].rearrange("(t p) d -> p t d", p=P)).then_inc(x_loaded, 16)
            sp.wait_ge(x_loaded, 16 * B)

        @block.gpsimd
        def _(pool):
            link = Links(pool, pool_chain)
            link(nc.gpsimd.memset(m.half[:], -0.5))
            link(nc.gpsimd.memset(m.ident[:], 0.0))
            link(nc.gpsimd.affine_select(out=m.ident[:], in_=m.ident[:], compare_op=ALU.not_equal, fill=1.0,
                                         base=0, pattern=[[-1, P]], channel_multiplier=1))
            link(nc.gpsimd.tensor_copy(m.identb[:], m.ident[:]))


def finish(m):
    nc = m.nc
    with ExitStack() as es:
        _, _, sem = allocators(nc, es, "finish")
        x_stored = sem("x_stored")
        block = es.enter_context(nc.Block())

        @block.sync
        def _(sp):
            for b in range(B):
                sp.dma_start(m.out[b].rearrange("(t p) d -> p t d", p=P), m.x[:, b]).then_inc(x_stored, 16)
            sp.wait_ge(x_stored, 16 * B)


def wait(eng, sem, count):
    if not isinstance(count, int) or count > 0:
        eng.wait_ge(sem, count)


class Norm:

    def __init__(self, sb, tag="", n=TB):
        self.n = n
        self.stats = sb(f"stats{tag}", [P, n, 6])
        self.s, self.d, self.m2, self.q = (sb(f"{v}{tag}", [P, n]) for v in ("msum", "mdif", "m2", "msq"))
        self.mean, self.veps, self.rstd = (sb(f"{v}{tag}", [P, n]) for v in ("mean", "veps", "rstd"))


def dve_moments(nc, link, w, xs, width, eps):
    for t, x in enumerate(xs):
        link.mark(nc.vector.bn_stats(w.stats[:, t], x))
    link.wait()
    n = len(xs)
    me, mo, ve, vo = w.stats[:, 0:n, 1], w.stats[:, 0:n, 4], w.stats[:, 0:n, 2], w.stats[:, 0:n, 5]
    link.mark(nc.vector.tensor_tensor(w.s[:, 0:n], me, mo, ALU.add))
    link.mark(nc.vector.tensor_tensor(w.d[:, 0:n], me, mo, ALU.subtract))
    link(nc.vector.tensor_tensor(w.m2[:, 0:n], ve, vo, ALU.add))
    link.mark(nc.vector.tensor_scalar(w.mean[:, 0:n], w.s[:, 0:n], 0.5, None, ALU.mult))
    link.mark(nc.vector.tensor_tensor(w.q[:, 0:n], w.d[:, 0:n], w.d[:, 0:n], ALU.mult))
    link(nc.vector.tensor_scalar(w.m2[:, 0:n], w.m2[:, 0:n], 1.0 / width, eps, ALU.mult, ALU.add))
    return nc.vector.scalar_tensor_tensor(w.veps[:, 0:n], w.q[:, 0:n], 0.25, w.m2[:, 0:n], ALU.mult, ALU.add)


def dve_square_mean(nc, link, w, xs, width, eps):
    for t, x in enumerate(xs):
        link.mark(nc.vector.bn_stats(w.stats[:, t], x))
    link.wait()
    n = len(xs)
    me, mo, ve, vo = w.stats[:, 0:n, 1], w.stats[:, 0:n, 4], w.stats[:, 0:n, 2], w.stats[:, 0:n, 5]
    link.mark(nc.vector.tensor_tensor(w.s[:, 0:n], me, me, ALU.mult))
    link.mark(nc.vector.tensor_tensor(w.d[:, 0:n], mo, mo, ALU.mult))
    link(nc.vector.tensor_tensor(w.m2[:, 0:n], ve, vo, ALU.add))
    link.mark(nc.vector.tensor_tensor(w.q[:, 0:n], w.s[:, 0:n], w.d[:, 0:n], ALU.add))
    link(nc.vector.tensor_scalar(w.m2[:, 0:n], w.m2[:, 0:n], 1.0 / width, eps, ALU.mult, ALU.add))
    return nc.vector.scalar_tensor_tensor(w.veps[:, 0:n], w.q[:, 0:n], 0.5, w.m2[:, 0:n], ALU.mult, ALU.add)


def pool_rsqrt(nc, m, w, n=TB):
    return nc.gpsimd.tensor_tensor(w.rstd[:, 0:n], w.veps[:, 0:n], m.half[:, 0:n], ALU.pow)


def allocators(nc, es, pre):
    sems = []

    def clear():
        nc.clear_and_free_semaphores(sems)
        nc.all_engine_barrier()

    es.callback(clear)

    def sem(name):
        sems.append(nc.alloc_semaphore(name=f"{pre}_{name}"))
        return sems[-1]

    sb = lambda name, shape, dt=F32: es.enter_context(nc.sbuf_tensor(f"{pre}_{name}", shape, dt))
    ps = lambda name, shape, dt=F32: es.enter_context(nc.psum_tensor(f"{pre}_{name}", shape, dt))
    return sb, ps, sem


def layer_attention_heads64(m, pre, causal):
    nc = m.nc
    d = m.dram
    H, DH, NPAIR, LAT = 16, 64, 8, 64
    VW = DH + 1
    EPS_SUM = 1e-8 if causal else 0.0
    SCALE = DH ** -0.5
    with ExitStack() as es:
        sb, ps, sem = allocators(nc, es, pre)
        KW = D if causal else LAT
        wq, wk, wv = sb("wq", [KW, H * DH]), sb("wk", [KW, H * DH]), sb("wv", [KW, H * DH])
        if not causal:
            wqs, wks = sb("wqs", [KW, H * DH]), sb("wks", [KW, H * DH])
            wdq, wdkv, gain, shift = sb("wdq", [P, LAT]), sb("wdkv", [P, LAT]), sb("gain", [P, 1]), sb("shift", [P, 1])
            cosT, sinT = sb("cosT", [P, S]), sb("sinT", [P, S])
            cT, w2 = sb("cT", [LAT, 2, S]), Norm(sb, "2")
            rotc, rots = sb("rotc", [P, 2, S]), sb("rots", [P, 2, S])
        wo = sb("wo", [P, NPAIR, D])
        bo = sb("bo", [P, D]) if causal else None
        mask = sb("mask", [P, P]) if causal else None
        w = Norm(sb)
        h, hi, hT = [sb(f"hn{i}", [P, TB, D]) for i in range(2)], sb("hi", [P, TB, D]), sb("hT", [P, S])
        qT, kT = [[sb(f"{v}{i}", [P, NPAIR, S]) for i in range(2)] for v in ("q", "k")]
        V = [sb(f"V{i}", [P, TB, H, VW]) for i in range(2)]
        mx, negm = sb("mx", [P, 4, TB]), sb("negm", [P, 4, TB])
        pr = [sb(f"pr{i}", [P, TB, S]) for i in range(3)]
        prT = [sb(f"prT{i}", [P, 2 * S]) for i in range(3)]
        ao, aoT, rinv = sb("ao", [P, TB, H, DH]), sb("aoT", [P, NPAIR, S]), sb("rinv", [P, 4])
        y = sb("y", [P, TB, D])
        psA = [ps(f"psA{i}", [P, 2, S]) for i in range(2)]
        psS, psO = ([ps(f"{v}{i}", [P, TB, S]) for i in range(2)] for v in ("psS", "psO"))
        psT = [ps(f"psT{i}", [P, 2 * S]) for i in range(2)]
        names = ("loaded", "consts", "pool_chain", "dve_chain", "moments", "rstd", "h_ready", "turned", "hT_ready", "c_ready", "cT_ready",
                 "proj_ready", "rotated", "s_ready", "negm_ready", "exp_ready", "masked", "p_turned", "prT_ready", "pv_done",
                 "ao_ready", "ao_turned", "aoT_ready", "out_ready", "x_done", "qk_read", "v_read", "turning")
        (loaded, consts, pool_chain, dve_chain, moments, rstd, h_ready, turned, hT_ready, c_ready, cT_ready,
         proj_ready, rotated, s_ready, negm_ready, exp_ready, masked, p_turned, prT_ready, pv_done,
         ao_ready, ao_turned, aoT_ready, out_ready, x_done, qk_read, v_read, turning) = (sem(n) for n in names)
        block = es.enter_context(nc.Block())
        NMOM = 1 if causal else 2
        NQK = NPAIR * (1 if causal else 2)
        NV = TB * 2
        NPJ = NQK + NV
        blocks = [(0, 0), (0, 1), (1, 1)] if causal else [(0, 0), (0, 1), (1, 0), (1, 1)]
        WB = len(blocks) * P
        loads = []
        if causal:
            loads = [(wq[:], d[f"{pre}_Wq"]), (wk[:], d[f"{pre}_Wkv"][:, 0:H * DH]), (wv[:], d[f"{pre}_Wkv"][:, H * DH:2 * H * DH]),
                     (wo[:], d[f"{pre}_Wo"].rearrange("(n p) c -> p n c", p=P)), (bo[:], rows(d[f"{pre}_bo"]).to_broadcast((P, D)))]
        else:
            loads = [(wq[:], d[f"{pre}_w_up_q"]), (wk[:], d[f"{pre}_w_up_k"]), (wv[:], d[f"{pre}_w_up_v"]),
                     (wo[:], d[f"{pre}_w_out"].rearrange("(n p) c -> p n c", p=P)),
                     (wqs[:], d["up_q_swapped"]), (wks[:], d["up_k_swapped"]), (wdq[:], d[f"{pre}_w_down_q"]), (wdkv[:], d[f"{pre}_w_down_kv"]),
                     (gain[:], d[f"{pre}_ln_scale"].rearrange("(d a) -> d a", a=1)), (shift[:], d[f"{pre}_ln_bias"].rearrange("(d a) -> d a", a=1)),
                     (cosT[:], d["rope_cos"]), (sinT[:], d["rope_sin"])]

        @block.sync
        def _(sp):
            for dst, src in loads:
                sp.dma_start(dst, src).then_inc(loaded, 16)

        @block.gpsimd
        def _(pool):
            link = Links(pool, pool_chain)
            for i in range(2):
                nc.gpsimd.memset(V[i][:], 1.0).then_inc(consts, 1)
            if causal:
                link(nc.gpsimd.memset(mask[:], 1.0))
                nc.gpsimd.affine_select(out=mask[:], in_=mask[:], compare_op=ALU.is_ge, fill=0.0, base=0,
                                        pattern=[[-1, P]], channel_multiplier=1).then_inc(consts, 1)

            def prep(b):
                pool.wait_ge(moments, NMOM * b + 1)
                pool_rsqrt(nc, m, w).then_inc(rstd, 1)
                if not causal:
                    pool.wait_ge(moments, NMOM * b + 2)
                    pool_rsqrt(nc, m, w2).then_inc(rstd, 1)

            def rotate(b):
                for j in range(NPAIR):
                    n = b * NPAIR + j
                    pool.wait_ge(qk_read, 2 * (n + 1))
                    wait(pool, pv_done, H * (b - 1))
                    nc.gpsimd.tensor_tensor(qT[b % 2][:, j], rotc[:, 0], rots[:, 0], ALU.add).then_inc(rotated, 1)
                    nc.gpsimd.tensor_tensor(kT[b % 2][:, j], rotc[:, 1], rots[:, 1], ALU.add).then_inc(rotated, 1)

            def mask_probs(n):
                pool.wait_ge(exp_ready, n + 1)
                for t in range(TB):
                    z = pr[n % 3][:, t, t * P:(t + 1) * P]
                    nc.gpsimd.tensor_tensor(z, z, mask[:], ALU.mult).then_inc(masked, 1)

            if causal:
                pool.wait_ge(consts, 3)
            prep(0)
            if not causal:
                rotate(0)
            for b in range(B):
                if b + 1 < B:
                    prep(b + 1)
                    if not causal:
                        rotate(b + 1)
                if causal:
                    for hd in range(H):
                        mask_probs(b * H + hd)

        @block.vector
        def _(dve):
            link = Links(dve, dve_chain)
            dve.wait_ge(loaded, 16 * len(loads))
            dve.wait_ge(consts, 3 if causal else 2)

            def norm(b):
                xs, hs = [m.x[:, b, t] for t in range(TB)], [h[b % 2][:, t] for t in range(TB)]
                dve_moments(nc, link, w, xs, D, LN_EPS).then_inc(moments, 1)
                dve.wait_ge(rstd, NMOM * b + 1)
                wait(dve, turned, b - 1 if causal else b)
                for t in range(TB):
                    ins = nc.vector.tensor_scalar(hs[t], xs[t], w.mean[:, t:t + 1], w.rstd[:, t:t + 1], ALU.subtract, ALU.mult)
                    if causal:
                        ins.then_inc(h_ready, 1)
                    else:
                        link.mark(ins)
                if not causal:
                    link.wait()
                    dve_moments(nc, link, w2, hs, D, LN_EPS).then_inc(moments, 1)
                    dve.wait_ge(rstd, NMOM * b + 2)
                    for t in range(TB):
                        nc.vector.tensor_scalar(hi[:, t], hs[t], w2.mean[:, t:t + 1], w2.rstd[:, t:t + 1], ALU.subtract, ALU.mult).then_inc(h_ready, 1)

            def project(b, j):
                n = b * NPJ + j
                bank = psA[n % 2]
                dve.wait_ge(proj_ready, n + 1)
                if j < NQK and not causal:
                    pair, swapped = j // 2, j % 2
                    wait(dve, rotated, 2 * (b * NPAIR + pair))
                    dst, tab = (rots, sinT) if swapped else (rotc, cosT)
                    nc.vector.tensor_tensor(dst[:], bank[:], tab[:, None, :].to_broadcast((P, 2, S)), ALU.mult).then_inc(qk_read, 1)
                elif j >= NQK:
                    t, half = (j - NQK) // 2, (j - NQK) % 2
                    wait(dve, pv_done, H * (b - 1))
                    nc.vector.tensor_copy(V[b % 2][:, t, half * 8:half * 8 + 8, 0:DH],
                                          bank[:].rearrange("p a (c e) -> p (a c) e", e=DH)).then_inc(v_read, 1)

            def maximum(n):
                dve.wait_ge(s_ready, n + 1)
                wait(dve, exp_ready, n - 3)
                link(nc.vector.reduce_max(mx[:, n % 4], psS[n % 2][:], AX.X))
                nc.vector.tensor_scalar(negm[:, n % 4], mx[:, n % 4], -SCALE, None, ALU.mult).then_inc(negm_ready, 1)

            def copy_turned(n):
                dve.wait_ge(p_turned, n + 1)
                wait(dve, pv_done, n - 2)
                nc.vector.tensor_copy(prT[n % 3][:, 0:WB], psT[n % 2][:, 0:WB]).then_inc(prT_ready, 1)

            def normalise(n):
                b, hd = n // H, n % H
                dve.wait_ge(pv_done, n + 1)
                if hd == 0:
                    wait(dve, ao_turned, b)
                r = rinv[:, 2 * (n % 2):2 * (n % 2) + 2]
                link(nc.vector.tensor_scalar(r, psO[n % 2][:, :, DH], EPS_SUM, None, ALU.add))
                link(nc.vector.reciprocal(r, r))
                nc.vector.tensor_tensor(ao[:, :, hd], psO[n % 2][:, :, 0:DH], r[:, :, None].to_broadcast((P, TB, DH)), ALU.mult).then_inc(ao_ready, 1)

            def update(b):
                dve.wait_ge(out_ready, b + 1)
                src = psO[0][:, 0].rearrange("p (t d) -> p t d", t=TB)
                other = bo[:, None, :].to_broadcast((P, TB, D)) if causal else h[b % 2][:]
                link(nc.vector.tensor_tensor(y[:], src, other, ALU.add))
                nc.vector.tensor_tensor(m.x[:, b], m.x[:, b], y[:], ALU.add).then_inc(x_done, 1)

            norm(0)
            for j in range(NPJ):
                project(0, j)
            for b in range(B):
                more = b + 1 < B
                if more:
                    norm(b + 1)
                for s in range(H + 3):
                    if s < H:
                        maximum(b * H + s)
                    if 1 <= s < H + 1:
                        copy_turned(b * H + s - 1)
                    if more:
                        for j in range(s * NPJ // (H + 3), (s + 1) * NPJ // (H + 3)):
                            project(b + 1, j)
                    if s >= 2 and s - 2 < H:
                        normalise(b * H + s - 2)
                update(b)

        @block.tensor
        def _(pe):
            pe.wait_ge(loaded, 16 * len(loads))
            pe.wait_ge(consts, 3 if causal else 2)

            def turn(b):
                pe.wait_ge(h_ready, TB * (b + 1))
                wait(pe, v_read, NV * b)
                src = h[b % 2] if causal else hi
                for t in range(TB):
                    ins = nc.tensor.transpose(psA[0][:, 0, t * P:(t + 1) * P], src[:, t], m.ident[:])
                ins.then_inc(turned, 1)
                pe.wait_ge(hT_ready, b + 1)
                if not causal:
                    nc.tensor.matmul(psA[1][0:LAT, 0], wdq[:], hT[:], start=True, stop=True)
                    nc.tensor.matmul(psA[1][0:LAT, 1], wdkv[:], hT[:], start=True, stop=True).then_inc(c_ready, 1)
                    pe.wait_ge(cT_ready, b + 1)

            def project(b, j):
                n = b * NPJ + j
                if n >= 2:
                    bb, jj = (n - 2) // NPJ, (n - 2) % NPJ
                    if jj < NQK:
                        pe.wait_ge(qk_read, bb * NQK + jj + 1)
                    else:
                        pe.wait_ge(v_read, bb * NV + jj - NQK + 1)
                bank = psA[n % 2]
                if j < NQK:
                    pair = j if causal else j // 2
                    c = slice(pair * P, (pair + 1) * P)
                    mats = (wq, wk) if causal or j % 2 == 0 else (wqs, wks)
                    for i, mat in enumerate(mats):
                        ins = nc.tensor.matmul(bank[:, i], mat[:, c], hT[:] if causal else cT[:, i], start=True, stop=True)
                else:
                    t, half = (j - NQK) // 2, (j - NQK) % 2
                    lhs = hT[:, t * P:(t + 1) * P] if causal else cT[:, 1, t * P:(t + 1) * P]
                    ins = nc.tensor.matmul(bank[:].rearrange("p a c -> p (a c)"), lhs, wv[:, half * 512:(half + 1) * 512], start=True, stop=True)
                ins.then_inc(proj_ready, 1)

            def scores(n):
                b, hd = n // H, n % H
                wait(pe, exp_ready, n - 1)
                r = slice((hd % 2) * DH, (hd % 2) * DH + DH)
                for t in range(TB):
                    ins = nc.tensor.matmul(psS[n % 2][:, t], qT[b % 2][r, hd // 2, t * P:(t + 1) * P], kT[b % 2][r, hd // 2], start=True, stop=True)
                ins.then_inc(s_ready, 1)

            def turn_probs(n):
                if n % H == 0:
                    wait(pe, aoT_ready, 4 * (n // H))
                if causal:
                    pe.wait_ge(masked, TB * (n + 1))
                else:
                    pe.wait_ge(exp_ready, n + 1)
                wait(pe, prT_ready, n - 1)
                for i, (k, t) in enumerate(blocks):
                    ins = nc.tensor.transpose(psT[n % 2][:, i * P:(i + 1) * P], pr[n % 3][:, t, k * P:(k + 1) * P], m.ident[:])
                ins.then_inc(p_turned, 1)

            def values(n):
                b, hd = n // H, n % H
                pe.wait_ge(prT_ready, n + 1)
                if hd == 0:
                    pe.wait_ge(v_read, NV * (b + 1))
                    wait(pe, x_done, b)
                wait(pe, ao_ready, n - 1)
                for t in range(TB):
                    mine = [(i, k) for i, (k, tt) in enumerate(blocks) if tt == t]
                    for i, k in mine:
                        ins = nc.tensor.matmul(psO[n % 2][:, t, 0:VW], prT[n % 3][:, i * P:(i + 1) * P], V[b % 2][:, k, hd], start=(i == mine[0][0]), stop=(i == mine[-1][0]))
                ins.then_inc(pv_done, 1)

            def out(b):
                pe.wait_ge(ao_ready, H * (b + 1))
                for q in range(4):
                    wait(pe, aoT_ready, 4 * b + q - 1)
                    for j in range(2):
                        for t in range(TB):
                            pair = 2 * q + j
                            ins = nc.tensor.transpose(psT[q % 2][:, j * S + t * P:j * S + (t + 1) * P], ao[:, t, 2 * pair:2 * pair + 2].rearrange("p h e -> p (h e)"), m.ident[:])
                    ins.then_inc(ao_turned, 1) if q == 3 else ins.then_inc(turning, 1)

            def project_out(b):
                pe.wait_ge(aoT_ready, 4 * (b + 1))
                for t in range(TB):
                    for pair in range(NPAIR):
                        ins = nc.tensor.matmul(psO[0][:, 0, t * D:(t + 1) * D], aoT[:, pair, t * P:(t + 1) * P], wo[:, pair], start=(pair == 0), stop=(pair == NPAIR - 1))
                ins.then_inc(out_ready, 1)

            turn(0)
            for j in range(NPJ):
                project(0, j)
            for b in range(B):
                more = b + 1 < B
                if causal:
                    pe.wait_ge(qk_read, NQK * (b + 1))
                else:
                    pe.wait_ge(rotated, 2 * NPAIR * (b + 1))
                for s in range(H + 3):
                    if s < H:
                        scores(b * H + s)
                    if s == 0 and more:
                        turn(b + 1)
                    if more:
                        for j in range(s * NPJ // (H + 3), (s + 1) * NPJ // (H + 3)):
                            project(b + 1, j)
                    if 1 <= s < H + 1:
                        turn_probs(b * H + s - 1)
                    if 2 <= s < H + 2:
                        values(b * H + s - 2)
                out(b)
                project_out(b)

        @block.scalar
        def _(act):
            act.wait_ge(loaded, 16 * len(loads))

            def copy_h(b):
                act.wait_ge(turned, b + 1)
                if causal:
                    nc.scalar.copy(hT[:], psA[0][:, 0]).then_inc(hT_ready, 1)
                else:
                    nc.scalar.activation(hT[:], psA[0][:, 0], ACT.Identity, bias=shift[:], scale=gain[:]).then_inc(hT_ready, 1)
                    act.wait_ge(c_ready, b + 1)
                    nc.scalar.copy(cT[:], psA[1][0:LAT]).then_inc(cT_ready, 1)

            def project(b, j):
                if causal and j < NQK:
                    n = b * NPJ + j
                    act.wait_ge(proj_ready, n + 1)
                    wait(act, pv_done, H * (b - 1))
                    nc.scalar.copy(qT[b % 2][:, j], psA[n % 2][:, 0]).then_inc(rotated, 1)
                    nc.scalar.copy(kT[b % 2][:, j], psA[n % 2][:, 1]).then_inc(qk_read, 1)

            def exps(n):
                act.wait_ge(negm_ready, n + 1)
                wait(act, p_turned, n - 2)
                for t in range(TB):
                    width = (t + 1) * P if causal else S
                    ins = nc.scalar.activation(pr[n % 3][:, t, 0:width], psS[n % 2][:, t, 0:width], ACT.Exp, bias=negm[:, n % 4, t:t + 1], scale=SCALE)
                ins.then_inc(exp_ready, 1)

            copy_h(0)
            for j in range(NPJ):
                project(0, j)
            for b in range(B):
                more = b + 1 < B
                for s in range(H + 3):
                    if s == 0 and more:
                        copy_h(b + 1)
                    if s < H:
                        exps(b * H + s)
                    if more:
                        for j in range(s * NPJ // (H + 3), (s + 1) * NPJ // (H + 3)):
                            project(b + 1, j)
                for q in range(4):
                    if q < 3:
                        act.wait_ge(turning, 3 * b + q + 1)
                    else:
                        act.wait_ge(ao_turned, b + 1)
                    nc.scalar.copy(aoT[:, 2 * q:2 * q + 2], psT[q % 2][:].rearrange("p (j s) -> p j s", j=2)).then_inc(aoT_ready, 1)


def layer_attention_heads8(m, pre, wq, wk, wv, wo, bq, bk, bv, bo, keys, scale, from_ctx, head_major=False):
    nc = m.nc
    H, DH = 16, 8
    PARTS = 3
    PAIR = PARTS * PARTS * DH
    MAXROW = 96
    NKT = keys // P
    NU = NKT // 2
    HG, HW = 4, 32
    NG = H // HG
    CK = DK if from_ctx else D
    SPB = keys // 256
    NREG = 2 * PARTS * PARTS
    NPS, NPT = 3, 6
    LAST_S = 12
    T_H, T_Q, T_K, T_V, T_O, T_Y, T_M = 2, 3, 4, 5, 8, 9, 13
    s_until = [min(H, (hd + 1) * H // LAST_S) for hd in range(H)]
    s_heads = [range(s_until[hd - 1] if hd else 0, s_until[hd]) for hd in range(H)]
    with ExitStack() as es:
        sb, ps, sem = allocators(nc, es, pre)
        wq_s, wk_s, wv_s, wo_s = sb("wq", [P, D]), sb("wk", [CK, D]), sb("wv", [CK, D]), sb("wo", [P, D])
        bq_s, bk_s = sb("bq", [P, 1]), sb("bk", [P, 1])
        bv_s, bo_s = sb("bv", [P, D]), sb("bo", [P, D])
        ctxT = sb("ctxT", [CK, 2, keys]) if from_ctx else None
        w = Norm(sb)
        h, hT = sb("h", [P, TB, D]), sb("hT", [P, S])
        qf, kf = sb("qf", [P, S]), sb("kf", [P, keys])
        qs, ks = sb("qs", [P, PARTS, S], BF16), sb("ks", [P, PARTS, keys], BF16)
        QR = [sb(f"QR{i}", [P, H, S], BF16) for i in range(3)]
        KR = [sb(f"KR{i}", [P, H, keys], BF16) for i in range(3)]
        V = [sb(f"V{i}", [P, NKT, H, HW]) for i in range(3)]
        mx = sb("mx", [P, TB, H])
        negm, mp = sb("negm", [H, S]), sb("mp", [H, PARTS, S], BF16)
        PT = [sb(f"PT{i}", [P, 2, S]) for i in range(NPT)]
        ot = [sb(f"ot{i}", [P, S]) for i in range(2)]
        rinv, ao, aoT = sb("rinv", [P, TB, HG]), sb("ao", [P, 2, TB, H, DH]), sb("aoT", [P, S])
        ao2 = sb("ao2", [P, TB, D]) if head_major else None
        y = sb("y", [P, TB, D])
        psS = [ps(f"psS{i}", [P, 512]) for i in range(2)]
        psT = [ps(f"psT{i}", [P, 2, S]) for i in range(NPS)]
        psO, psOT, psM = ps("psO", [P, 2, S]), ps("psOT", [P, TB, HG, HW]), ps("psM", [P, 512])
        q_dram = nc.dram_tensor(f"{pre}_q_parts", (PARTS, P, S), BF16, kind="Internal").ap()
        k_dram = nc.dram_tensor(f"{pre}_k_parts", (PARTS, P, keys), BF16, kind="Internal").ap()
        m_dram = nc.dram_tensor(f"{pre}_m_parts", (PARTS, H, S), BF16, kind="Internal").ap()
        o_dram = nc.dram_tensor(f"{pre}_o_heads", (H, S, DH), F32, kind="Internal").ap() if head_major else None
        names = ("loaded", "bias_scaled", "ones_set", "dve_chain", "pool_chain", "var_ready", "rstd_ready", "h_ready", "turned",
                 "hT_ready", "q_proj", "qf_ready", "k_proj", "kf_ready", "v_proj", "v_ready", "q_split", "k_split", "q_staged",
                 "k_staged", "m_staged", "regrouped", "s_ready", "s_used", "mx_turned", "m_split", "m_rows", "st_ready",
                 "exp_ready", "pv_done", "ot_ready", "group_turned", "ao_ready", "o_staged", "ao_back", "ao_turned", "aoT_ready",
                 "out_ready", "x_done")
        (loaded, bias_scaled, ones_set, dve_chain, pool_chain, var_ready, rstd_ready, h_ready, turned,
         hT_ready, q_proj, qf_ready, k_proj, kf_ready, v_proj, v_ready, q_split, k_split, q_staged,
         k_staged, m_staged, regrouped, s_ready, s_used, mx_turned, m_split, m_rows, st_ready,
         exp_ready, pv_done, ot_ready, group_turned, ao_ready, o_staged, ao_back, ao_turned, aoT_ready,
         out_ready, x_done) = (sem(n) for n in names)
        ctx_loaded = [sem("ctx_loaded0"), sem("ctx_loaded1")]
        block = es.enter_context(nc.Block())
        NLOAD = 8 if bq is not None else 5

        @block.sync
        def _(sp):
            loads = [(wq_s[:], m.dram[wq]), (wk_s[:], m.dram[wk]), (wv_s[:], m.dram[wv]), (wo_s[:], m.dram[wo]),
                     (bo_s[:], rows(m.dram[bo]).to_broadcast((P, D)))]
            if bq is not None:
                loads += [(bq_s[:], m.dram[bq].rearrange("(d a) -> d a", a=1)), (bk_s[:], m.dram[bk].rearrange("(d a) -> d a", a=1)),
                          (bv_s[:], rows(m.dram[bv]).to_broadcast((P, D)))]
            for dst, src in loads:
                sp.dma_start(dst, src).then_inc(loaded, 16)

            def load_ctx(b):
                if from_ctx:
                    wait(sp, v_proj, b - 1)
                    sp.dma_start(ctxT[:, b % 2], m.dram["ctx_768"][b]).then_inc(ctx_loaded[b % 2], 16)

            def regroup(b):
                wait(sp, st_ready, NU * H * (b - 2))
                wait(sp, regrouped, 16 * NREG * b)
                if b == 0:
                    sp.wait_ge(ones_set, 9)
                sp.wait_ge(q_split, b + 1)
                sp.dma_start(q_dram.rearrange("i p c -> p i c"), qs[:]).then_inc(q_staged, 16)
                sp.wait_ge(k_split, b + 1)
                sp.dma_start(k_dram.rearrange("i p c -> p i c"), ks[:]).then_inc(k_staged, 16)
                sp.wait_ge(q_staged, 16 * (b + 1))
                for i in range(PARTS):
                    for j in range(PARTS):
                        r = (i * PARTS + j) * DH
                        sp.dma_start(QR[b % 3][r:r + DH], q_dram[i].rearrange("(h d) c -> d h c", d=DH)).then_inc(regrouped, 16)
                sp.wait_ge(k_staged, 16 * (b + 1))
                for i in range(PARTS):
                    for j in range(PARTS):
                        r = (i * PARTS + j) * DH
                        sp.dma_start(KR[b % 3][r:r + DH], k_dram[j].rearrange("(h d) c -> d h c", d=DH)).then_inc(regrouped, 16)

            def max_rows(b):
                sp.wait_ge(m_split, b + 1)
                sp.dma_start(m_dram.rearrange("i h c -> h i c"), mp[:]).then_inc(m_staged, 16)
                sp.wait_ge(m_staged, 16 * (b + 1))
                sp.dma_start(QR[b % 3][MAXROW:MAXROW + PARTS], m_dram).then_inc(m_rows, 16)

            def reread(b):
                if head_major:
                    sp.wait_ge(ao_ready, NG * (b + 1))
                    for t in range(TB):
                        sp.dma_start(o_dram[:, t * P:(t + 1) * P].rearrange("h q d -> q h d"), ao[:, b % 2, t]).then_inc(o_staged, 16)
                    sp.wait_ge(o_staged, 16 * TB * (b + 1))
                    wait(sp, ao_turned, b)
                    flat = o_dram.rearrange("h (l r) d -> (h l) (r d)", r=D // DH)
                    sp.dma_start(ao2[:], flat.rearrange("(t p) c -> p t c", p=P)).then_inc(ao_back, 16)

            load_ctx(0)
            load_ctx(1)
            regroup(0)
            regroup(1)
            max_rows(0)
            for b in range(B):
                if b + 2 < B:
                    load_ctx(b + 2)
                if b >= 1:
                    reread(b - 1)
                if b + 2 < B:
                    regroup(b + 2)
                if b + 1 < B:
                    max_rows(b + 1)
            reread(B - 1)

        @block.gpsimd
        def _(pool):
            link = Links(pool, pool_chain)
            for i in range(3):
                nc.gpsimd.memset(KR[i][:], 1.0).then_inc(ones_set, 1)
                nc.gpsimd.memset(QR[i][:], 0.0).then_inc(ones_set, 1)

            def split(src, parts):
                link(nc.gpsimd.tensor_copy(parts[:, 0], src[:]))
                link(nc.gpsimd.tensor_tensor(src[:], src[:], parts[:, 0], ALU.subtract))
                link(nc.gpsimd.tensor_copy(parts[:, 1], src[:]))
                link(nc.gpsimd.tensor_tensor(src[:], src[:], parts[:, 1], ALU.subtract))
                return nc.gpsimd.tensor_copy(parts[:, 2], src[:])

            for b in range(B):
                pool.wait_ge(var_ready, b + 1)
                pool_rsqrt(nc, m, w).then_inc(rstd_ready, 1)
                pool.wait_ge(qf_ready, b + 1)
                wait(pool, q_staged, 16 * b)
                split(qf, qs).then_inc(q_split, 1)
                pool.wait_ge(kf_ready, b + 1)
                wait(pool, k_staged, 16 * b)
                split(kf, ks).then_inc(k_split, 1)

        @block.vector
        def _(dve):
            link = Links(dve, dve_chain)
            for i in range(3):
                nc.vector.memset(V[i][:], 1.0).then_inc(ones_set, 1)
            dve.wait_ge(loaded, 16 * NLOAD)
            if bq is not None:
                nc.vector.tensor_scalar(bq_s[:], bq_s[:], scale, None, ALU.mult).then_inc(bias_scaled, 1)
            dve.wait_ge(ones_set, 9)

            def norm(b):
                dve_moments(nc, link, w, [m.x[:, b, t] for t in range(TB)], D, LN_EPS).then_inc(var_ready, 1)
                dve.wait_ge(rstd_ready, b + 1)
                wait(dve, turned, b)
                for t in range(TB):
                    nc.vector.tensor_scalar(h[:, t], m.x[:, b, t], w.mean[:, t:t + 1], w.rstd[:, t:t + 1], ALU.subtract, ALU.mult).then_inc(h_ready, 1)

            def values(b):
                dve.wait_ge(v_proj, b + 1)
                wait(dve, pv_done, H * (b - 2))
                for t in range(NKT):
                    src = psM[:, t * D:(t + 1) * D].rearrange("p (h d) -> p h d", d=DH)
                    if bq is not None:
                        nc.vector.tensor_tensor(V[b % 3][:, t, :, 0:DH], src, bv_s[:].rearrange("p (h d) -> p h d", d=DH), ALU.add).then_inc(v_ready, 1)
                    else:
                        nc.vector.tensor_copy(V[b % 3][:, t, :, 0:DH], src).then_inc(v_ready, 1)

            def maxima(b, hd):
                for u in range(SPB):
                    n = (b * H + hd) * SPB + u
                    dve.wait_ge(s_ready, n + 1)
                    if hd == 0 and u == 0:
                        wait(dve, mx_turned, b)
                    if SPB == 2:
                        nc.vector.reduce_max(mx[:, u, hd:hd + 1], psS[n % 2][:], AX.X).then_inc(s_used, 1)
                    else:
                        nc.vector.reduce_max(mx[:, :, hd], psS[n % 2][:].rearrange("p (t k) -> p t k", t=TB), AX.X).then_inc(s_used, 1)

            def split_max(b):
                dve.wait_ge(mx_turned, b + 1)
                wait(dve, m_staged, 16 * b)
                link(nc.vector.tensor_scalar(negm[:], psM[0:H, 0:S], -1.0, None, ALU.mult))
                link(nc.vector.tensor_copy(mp[:, 0], negm[:]))
                link(nc.vector.tensor_tensor(negm[:], negm[:], mp[:, 0], ALU.subtract))
                link(nc.vector.tensor_copy(mp[:, 1], negm[:]))
                link(nc.vector.tensor_tensor(negm[:], negm[:], mp[:, 1], ALU.subtract))
                nc.vector.tensor_copy(mp[:, 2], negm[:]).then_inc(m_split, 1)

            def normalise(g):
                b, hg = g // NG, g % NG
                dve.wait_ge(group_turned, g + 1)
                link(nc.vector.reciprocal(rinv[:], psOT[:, :, :, DH]))
                if hg == 0:
                    if head_major:
                        wait(dve, o_staged, 16 * TB * (b - 1))
                    else:
                        wait(dve, ao_turned, b - 1)
                nc.vector.tensor_tensor(ao[:, b % 2, :, hg * HG:(hg + 1) * HG, :], psOT[:, :, :, 0:DH],
                                        rinv[:][:, :, :, None].to_broadcast((P, TB, HG, DH)), ALU.mult).then_inc(ao_ready, 1)

            def update(b):
                dve.wait_ge(out_ready, b + 1)
                link(nc.vector.tensor_tensor(y[:], psM[:, 0:S].rearrange("p (t d) -> p t d", t=TB), bo_s[:, None, :].to_broadcast((P, TB, D)), ALU.add))
                nc.vector.tensor_tensor(m.x[:, b], m.x[:, b], y[:], ALU.add).then_inc(x_done, 1)

            norm(0)
            values(0)
            norm(1)
            values(1)
            for hd in range(H):
                maxima(0, hd)
            split_max(0)
            for b in range(B):
                for hd in range(H):
                    n = b * H + hd
                    if hd == 0 and b + 2 < B:
                        norm(b + 2)
                    if b + 1 < B:
                        for other in s_heads[hd]:
                            maxima(b + 1, other)
                    if n >= 5 and n % HG == 1:
                        normalise(n // HG - 1)
                    if hd == T_V and b + 2 < B:
                        values(b + 2)
                    if hd == T_Y and b >= 1:
                        update(b - 1)
                    if hd == T_M and b + 1 < B:
                        split_max(b + 1)
            normalise(B * NG - 1)
            update(B - 1)

        @block.tensor
        def _(pe):
            pe.wait_ge(loaded, 16 * NLOAD)

            def turn(b):
                pe.wait_ge(h_ready, TB * (b + 1))
                for t in range(TB):
                    ins = nc.tensor.transpose(psM[:, t * P:(t + 1) * P], h[:, t], m.ident[:])
                ins.then_inc(turned, 1)

            def project_q(b):
                pe.wait_ge(hT_ready, b + 1)
                nc.tensor.matmul(psM[:, 0:S], wq_s[:], hT[:], start=True, stop=True).then_inc(q_proj, 1)

            def kv_source(b):
                return ctxT[:, b % 2] if from_ctx else hT[:]

            def project_k(b):
                if from_ctx:
                    pe.wait_ge(ctx_loaded[b % 2], 16 * (b // 2 + 1))
                pe.wait_ge(qf_ready, b + 1)
                nc.tensor.matmul(psM[:, 0:keys], wk_s[:], kv_source(b), start=True, stop=True).then_inc(k_proj, 1)

            def project_v(b):
                pe.wait_ge(kf_ready, b + 1)
                for t in range(NKT):
                    ins = nc.tensor.matmul(psM[:, t * D:(t + 1) * D], kv_source(b)[:, t * P:(t + 1) * P], wv_s[:], start=True, stop=True)
                ins.then_inc(v_proj, 1)

            def scores(b, hd):
                if hd == 0:
                    pe.wait_ge(regrouped, 16 * NREG * (b + 1))
                for t in range(TB):
                    n = (b * H + hd) * SPB + (t if SPB == 2 else 0)
                    if SPB == 2 or t == 0:
                        wait(pe, s_used, n - 1)
                    at = psS[n % 2][:] if SPB == 2 else psS[n % 2][:, t * keys:(t + 1) * keys]
                    ins = nc.tensor.matmul(at, QR[b % 3][0:MAXROW, hd, t * P:(t + 1) * P], KR[b % 3][0:MAXROW, hd, :], start=True, stop=True)
                    if SPB == 2 or t == 1:
                        ins.then_inc(s_ready, 1)

            def turn_max(b):
                pe.wait_ge(s_used, H * SPB * (b + 1))
                for t in range(TB):
                    ins = nc.tensor.transpose(psM[0:H, t * P:(t + 1) * P], mx[:, t], m.ident[:])
                ins.then_inc(mx_turned, 1)

            def scores_turned(b, hd):
                if hd == 0:
                    pe.wait_ge(m_rows, 16 * (b + 1))
                for u in range(NU):
                    n = (b * H + hd) * NU + u
                    wait(pe, exp_ready, n - NPS + 1)
                    for k in range(2):
                        kt = 2 * u + k
                        ins = nc.tensor.matmul(psT[n % NPS][:, k], KR[b % 3][:, hd, kt * P:(kt + 1) * P], QR[b % 3][:, hd, :], start=True, stop=True)
                    ins.then_inc(st_ready, 1)

            def weigh(b, hd):
                g = (b * H + hd) // HG
                if hd == 0:
                    pe.wait_ge(v_ready, NKT * (b + 1))
                if hd % HG == 0:
                    wait(pe, ot_ready, g - 1)
                for u in range(NU):
                    n = (b * H + hd) * NU + u
                    pe.wait_ge(exp_ready, n + 1)
                    for k in range(2):
                        kt = 2 * u + k
                        r = hd % HG * HW
                        ins = nc.tensor.matmul(psO[r:r + HW, g % 2], V[b % 3][:, kt, hd], PT[n % NPT][:, k], start=(kt == 0), stop=(kt == NKT - 1))
                ins.then_inc(pv_done, 1)

            def turn_group(g):
                pe.wait_ge(ot_ready, g + 1)
                wait(pe, ao_ready, g)
                for t in range(TB):
                    ins = nc.tensor.transpose(psOT[:, t].rearrange("p h w -> p (h w)"), ot[g % 2][:, t * P:(t + 1) * P], m.ident[:])
                ins.then_inc(group_turned, 1)

            def turn_out(b):
                if head_major:
                    pe.wait_ge(ao_back, 16 * (b + 1))
                else:
                    pe.wait_ge(ao_ready, NG * (b + 1))
                for t in range(TB):
                    src = ao2[:, t] if head_major else ao[:, b % 2, t].rearrange("p h d -> p (h d)")
                    ins = nc.tensor.transpose(psM[:, t * P:(t + 1) * P], src, m.ident[:])
                ins.then_inc(ao_turned, 1)

            def project_out(b):
                pe.wait_ge(aoT_ready, b + 1)
                for t in range(TB):
                    ins = nc.tensor.matmul(psM[:, t * D:(t + 1) * D], aoT[:, t * P:(t + 1) * P], wo_s[:], start=True, stop=True)
                ins.then_inc(out_ready, 1)

            for b in range(2):
                wait(pe, v_ready, NKT * b)
                turn(b)
                project_q(b)
                project_k(b)
                project_v(b)
            for hd in range(H):
                scores(0, hd)
            pe.wait_ge(v_ready, NKT * 2)
            turn_max(0)
            for b in range(B):
                for hd in range(H):
                    n = b * H + hd
                    more = b + 2 < B
                    if hd == T_H and more:
                        pe.wait_ge(m_split, b + 1)
                        turn(b + 2)
                    if hd == T_Q and more:
                        project_q(b + 2)
                    if hd == T_K and more:
                        project_k(b + 2)
                    if hd == T_V and more:
                        project_v(b + 2)
                    if hd == T_O and b >= 1:
                        if more:
                            pe.wait_ge(v_ready, NKT * (b + 3))
                        else:
                            pe.wait_ge(m_split, b + 1)
                        turn_out(b - 1)
                    if hd == T_Y and b >= 1:
                        project_out(b - 1)
                    if hd == T_M and b + 1 < B:
                        wait(pe, x_done, b)
                        if b == 0:
                            pe.wait_ge(v_ready, NKT * 3)
                        turn_max(b + 1)
                    if n >= 5 and n % HG == 1:
                        turn_group(n // HG - 1)
                    if b + 1 < B:
                        for other in s_heads[hd]:
                            scores(b + 1, other)
                    scores_turned(b, hd)
                    if n >= 1:
                        weigh((n - 1) // H, (n - 1) % H)
            weigh(B - 1, H - 1)
            turn_group(B * NG - 1)
            turn_out(B - 1)
            project_out(B - 1)

        @block.scalar
        def _(act):
            if bq is not None:
                act.wait_ge(bias_scaled, 1)

            def copy_h(b):
                act.wait_ge(turned, b + 1)
                nc.scalar.copy(hT[:], psM[:, 0:S]).then_inc(hT_ready, 1)

            def copy_q(b):
                act.wait_ge(q_proj, b + 1)
                wait(act, q_split, b)
                nc.scalar.activation(qf[:], psM[:, 0:S], ACT.Identity, bias=bq_s[:] if bq is not None else 0.0, scale=scale).then_inc(qf_ready, 1)

            def copy_k(b):
                act.wait_ge(k_proj, b + 1)
                wait(act, k_split, b)
                nc.scalar.activation(kf[:], psM[:, 0:keys], ACT.Identity, bias=bk_s[:] if bq is not None else 0.0).then_inc(kf_ready, 1)

            def copy_group(g):
                act.wait_ge(pv_done, HG * (g + 1))
                wait(act, group_turned, g - 1)
                nc.scalar.copy(ot[g % 2][:], psO[:, g % 2]).then_inc(ot_ready, 1)

            def copy_out(b):
                act.wait_ge(ao_turned, b + 1)
                nc.scalar.copy(aoT[:], psM[:, 0:S]).then_inc(aoT_ready, 1)

            for b in range(2):
                copy_h(b)
                copy_q(b)
                copy_k(b)
            for b in range(B):
                for hd in range(H):
                    more = b + 2 < B
                    if hd == T_H and more:
                        copy_h(b + 2)
                    if hd == T_Q and more:
                        copy_q(b + 2)
                    if hd == T_K and more:
                        copy_k(b + 2)
                    if hd == T_O and b >= 1:
                        copy_out(b - 1)
                    if (b * H + hd) % HG == 1 and b * H + hd >= 5:
                        copy_group((b * H + hd) // HG - 1)
                    for u in range(NU):
                        n = (b * H + hd) * NU + u
                        act.wait_ge(st_ready, n + 1)
                        wait(act, pv_done, (n - NPT) // NU + 1)
                        nc.scalar.activation(PT[n % NPT][:], psT[n % NPS][:], ACT.Exp).then_inc(exp_ready, 1)
            copy_group(B * NG - 1)
            copy_out(B - 1)


def layer_fp4_mlp(m, pre):
    nc = m.nc
    BLK, FI = 16, 352
    CH = [(0, 128), (128, 128), (256, 96)]
    with ExitStack() as es:
        sb, ps, sem = allocators(nc, es, pre)
        wg, wu, wd = sb("wg", [P, 3, D]), sb("wu", [P, 3, D]), sb("wd", [P, FI])
        wguT, wdT = sb("wguT", [P, 2, FI]), sb("wdT", [P, 3, D])
        w = Norm(sb)
        h, hT = sb("h", [P, TB, D]), sb("hT", [P, S])
        g, f, fT = sb("g", [P, TB, FI]), sb("f", [P, TB, FI]), sb("fT", [P, 3, S])
        WIDE = TB * FI
        mag, lev, c1, sg = sb("mag", [P, WIDE]), sb("lev", [P, WIDE]), sb("c1", [P, WIDE]), sb("sg", [P, WIDE])
        bmax, bscale, binv = sb("bmax", [P, WIDE // BLK]), sb("bscale", [P, WIDE // BLK]), sb("binv", [P, WIDE // BLK])
        psA, psG, psU, psF, psY = ps("psA", [P, 512]), ps("psG", [P, TB, 512]), ps("psU", [P, TB, 512]), ps("psF", [P, 2, 512]), ps("psY", [P, TB, D])
        names = ("loaded", "dve_chain", "w_ready", "w_turned", "wT_ready", "moments", "rstd", "h_ready", "turned", "hT_ready",
                 "gu_ready", "silu_ready", "f_ready", "f_turned", "fT_ready", "y_ready", "x_done")
        (loaded, dve_chain, w_ready, w_turned, wT_ready, moments, rstd, h_ready, turned, hT_ready,
         gu_ready, silu_ready, f_ready, f_turned, fT_ready, y_ready, x_done) = (sem(n) for n in names)
        block = es.enter_context(nc.Block())

        @block.sync
        def _(sp):
            for n, (c, k) in enumerate(CH):
                sp.dma_start(wg[0:k, n], m.dram[f"{pre}_w_gate"][c:c + k]).then_inc(loaded, 16)
                sp.dma_start(wu[0:k, n], m.dram[f"{pre}_w_up"][c:c + k]).then_inc(loaded, 16)
            sp.dma_start(wd[:], m.dram[f"{pre}_w_down"]).then_inc(loaded, 16)

        @block.gpsimd
        def _(pool):
            for b in range(B):
                pool.wait_ge(moments, b + 1)
                pool_rsqrt(nc, m, w).then_inc(rstd, 1)

        @block.vector
        def _(dve):
            link = Links(dve, dve_chain)

            def quantise(a, k, width):
                blocks = lambda v: v[0:k, 0:width].rearrange("p (n e) -> p n e", e=BLK)
                nb = width // BLK
                wide = lambda v: v[0:k, 0:nb][:, :, None].to_broadcast((k, nb, BLK))
                M, L, C, G = mag[0:k, 0:width], lev[0:k, 0:width], c1[0:k, 0:width], sg[0:k, 0:width]
                link.mark(nc.vector.tensor_scalar(C, a, -1.0, None, ALU.mult))
                link.mark(nc.vector.tensor_scalar(G, a, 0.0, None, ALU.is_gt))
                link(nc.vector.tensor_scalar(L, a, 0.0, None, ALU.is_lt))
                link.mark(nc.vector.tensor_tensor(G, G, L, ALU.subtract))
                link(nc.vector.tensor_tensor(M, a, C, ALU.max))
                link(nc.vector.tensor_reduce(bmax[0:k, 0:nb], blocks(mag), AX.X, ALU.max))
                link(nc.vector.tensor_scalar(bscale[0:k, 0:nb], bmax[0:k, 0:nb], 1.0 / 6.0, 1e-12, ALU.mult, ALU.max))
                link(nc.vector.reciprocal(binv[0:k, 0:nb], bscale[0:k, 0:nb]))
                link(nc.vector.tensor_tensor(blocks(mag), blocks(mag), wide(binv), ALU.mult))
                link.mark(nc.vector.tensor_scalar(L, M, 5.0, 2.0, ALU.is_gt, ALU.mult))
                link(nc.vector.tensor_scalar(C, M, 0.25, None, ALU.is_gt))
                link(nc.vector.scalar_tensor_tensor(L, M, 3.5, L, ALU.is_gt, ALU.add))
                link(nc.vector.scalar_tensor_tensor(L, M, 2.5, L, ALU.is_gt, ALU.add))
                link(nc.vector.scalar_tensor_tensor(L, L, 2.0, C, ALU.mult, ALU.add))
                for mid in (0.75, 1.25, 1.75):
                    link(nc.vector.scalar_tensor_tensor(L, M, mid, L, ALU.is_gt, ALU.add))
                link(nc.vector.scalar_tensor_tensor(L, L, 0.5, G, ALU.mult, ALU.mult))
                return nc.vector.tensor_tensor(a.rearrange("p (n e) -> p n e", e=BLK), blocks(lev), wide(bscale), ALU.mult)

            dve.wait_ge(loaded, 16 * 7)
            for mat in (wg, wu):
                link(quantise(mat[:, 0:2].rearrange("p c d -> p (c d)"), P, 2 * D))
                link(quantise(mat[0:96, 2], 96, D))
            quantise(wd[:], P, FI).then_inc(w_ready, 1)
            for b in range(B):
                xs = [m.x[:, b, t] for t in range(TB)]
                dve_moments(nc, link, w, xs, D, LN_EPS).then_inc(moments, 1)
                dve.wait_ge(rstd, b + 1)
                wait(dve, turned, b)
                for t in range(TB):
                    link.mark(nc.vector.tensor_scalar(h[:, t], xs[t], w.mean[:, t:t + 1], w.rstd[:, t:t + 1], ALU.subtract, ALU.mult))
                link.wait()
                quantise(h[:].rearrange("p t d -> p (t d)"), P, TB * D).then_inc(h_ready, 1)
                dve.wait_ge(silu_ready, b + 1)
                link(nc.vector.tensor_tensor(f[:], g[:], psU[:, :, 0:FI], ALU.mult))
                quantise(f[:].rearrange("p t d -> p (t d)"), P, TB * FI).then_inc(f_ready, 1)
                dve.wait_ge(y_ready, b + 1)
                nc.vector.tensor_tensor(m.x[:, b], m.x[:, b], psY[:], ALU.add).then_inc(x_done, 1)

        @block.tensor
        def _(pe):
            pe.wait_ge(w_ready, 1)
            for n, (c, k) in enumerate(CH):
                nc.tensor.transpose(psG[:, 0, c:c + k], wg[0:k, n], m.ident[0:k, 0:k])
                nc.tensor.transpose(psG[:, 1, c:c + k], wu[0:k, n], m.ident[0:k, 0:k])
                ins = nc.tensor.transpose(psU[0:k, 0, n * D:(n + 1) * D], wd[:, c:c + k], m.ident[:])
            ins.then_inc(w_turned, 1)
            pe.wait_ge(wT_ready, 3)
            for b in range(B):
                pe.wait_ge(h_ready, b + 1)
                for t in range(TB):
                    ins = nc.tensor.transpose(psA[:, t * P:(t + 1) * P], h[:, t], m.ident[:])
                ins.then_inc(turned, 1)
                pe.wait_ge(hT_ready, b + 1)
                for t in range(TB):
                    nc.tensor.matmul(psG[:, t, 0:FI], hT[:, t * P:(t + 1) * P], wguT[:, 0], start=True, stop=True)
                    ins = nc.tensor.matmul(psU[:, t, 0:FI], hT[:, t * P:(t + 1) * P], wguT[:, 1], start=True, stop=True)
                ins.then_inc(gu_ready, 1)
                pe.wait_ge(f_ready, b + 1)
                for n, (c, k) in enumerate(CH):
                    for t in range(TB):
                        at = psF[0:k, n // 2, (n % 2) * S + t * P:(n % 2) * S + (t + 1) * P]
                        ins = nc.tensor.transpose(at, f[:, t, c:c + k], m.ident[:])
                ins.then_inc(f_turned, 1)
                pe.wait_ge(fT_ready, 2 * (b + 1))
                for t in range(TB):
                    for n, (c, k) in enumerate(CH):
                        ins = nc.tensor.matmul(psY[:, t], fT[0:k, n, t * P:(t + 1) * P], wdT[0:k, n], start=(n == 0), stop=(n == 2))
                ins.then_inc(y_ready, 1)

        @block.scalar
        def _(act):
            act.wait_ge(w_turned, 1)
            nc.scalar.copy(wguT[:], psG[:, :, 0:FI]).then_inc(wT_ready, 1)
            nc.scalar.copy(wdT[:, 0:2], psU[:, 0, 0:2 * D].rearrange("p (n d) -> p n d", n=2)).then_inc(wT_ready, 1)
            nc.scalar.copy(wdT[0:96, 2], psU[0:96, 0, 2 * D:3 * D]).then_inc(wT_ready, 1)
            for b in range(B):
                act.wait_ge(turned, b + 1)
                nc.scalar.copy(hT[:], psA[:, 0:S]).then_inc(hT_ready, 1)
                act.wait_ge(gu_ready, b + 1)
                nc.scalar.activation(g[:], psG[:, :, 0:FI], ACT.Silu).then_inc(silu_ready, 1)
                act.wait_ge(f_turned, b + 1)
                nc.scalar.copy(fT[:, 0:2], psF[:, 0].rearrange("p (n s) -> p n s", n=2)).then_inc(fT_ready, 1)
                nc.scalar.copy(fT[0:96, 2], psF[0:96, 1, 0:S]).then_inc(fT_ready, 1)


def layer_gated_recurrence(m, pre):
    nc = m.nc
    H, DH, CHUNK, FC = 16, 8, 64, 512
    NC = S // CHUNK
    RES = float(1.0 / np.sqrt(2.0))
    EPS_Q = float(np.finfo(np.float32).eps)
    EPS_X = 1e-6
    with ExitStack() as es:
        sb, ps, sem = allocators(nc, es, pre)
        wi, wo, wf, wp = sb("wi", [P, 5 * D]), sb("wo", [P, D]), sb("wf", [P, FC]), sb("wp", [P, FC // P, D])
        n1, n2 = sb("n1", [P, 1]), sb("n2", [P, 1])
        headsum, headexp = sb("headsum", [P, H]), sb("headexp", [H, P])
        go, begin = sb("go", [P, S]), sb("begin", [P, S])
        w, w1, w3 = Norm(sb), Norm(sb, "1"), Norm(sb, "3")
        h, h1, hT = [sb(f"hn{i}", [P, TB, D]) for i in range(2)], sb("h1", [P, TB, D]), sb("hT", [P, S])
        two = lambda v: [sb(f"{v}{i}", [P, S]) for i in range(2)]
        q, k, v, a, g, q2 = two("q"), two("k"), two("v"), two("a"), two("g"), two("q2")
        two_c = sb("two", [P, 1])
        qms, qrs, qrT = sb("qms", [P, TB * H]), sb("qrs", [P, TB * H]), sb("qrT", [H, S])
        u, a0, a1, pref, rec, acc, st, yT = (sb(n, [P, S]) for n in ("u", "a_go", "a_begin", "pref", "rec", "acc", "st", "yT"))
        hm, h2, h2T, sT, y = sb("hm", [P, TB, D]), sb("h2", [P, TB, D]), sb("h2T", [P, S]), sb("sT", [P, FC // P, S]), sb("y", [P, TB, D])
        psA, psP, psB, psC, psD = ps("psA", [P, 512]), ps("psP", [P, 6, S]), ps("psB", [P, 512]), ps("psC", [P, FC // P, S]), ps("psD", [P, TB, D])
        names = ("loaded", "consts", "pool_chain", "dve_chain", "moments", "rstd", "h_ready", "turned", "hT_ready", "proj_ready", "proj_read",
                 "q2_ready", "qs_ready", "qms_ready", "qrs_ready", "q_turned", "qrT_ready", "q_spread", "clipped", "started",
                 "u_ready", "y_ready", "mix_ready", "m3", "rstd3", "h2_ready", "h2_turned", "h2T_ready", "fc_ready", "silu_ready", "mlp_ready", "x_done",
                 "gates_ready")
        (loaded, consts, pool_chain, dve_chain, moments, rstd, h_ready, turned, hT_ready, proj_ready, proj_read,
         q2_ready, qs_ready, qms_ready, qrs_ready, q_turned, qrT_ready, q_spread, clipped, started,
         u_ready, y_ready, mix_ready, m3, rstd3, h2_ready, h2_turned, h2T_ready, fc_ready, silu_ready, mlp_ready, x_done,
         gates_ready) = (sem(n) for n in names)
        block = es.enter_context(nc.Block())
        NLOAD = 6

        @block.sync
        def _(sp):
            col = lambda ap: ap.rearrange("(d a) -> d a", a=1)
            for dst, src in ((wi[:], m.dram[f"{pre}_in_proj_w"]), (wo[:], m.dram[f"{pre}_out_proj_w"]), (wf[:], m.dram[f"{pre}_fc_w"]),
                             (wp[:], m.dram[f"{pre}_proj_w"].rearrange("(c p) d -> p c d", p=P)),
                             (n1[:], col(m.dram[f"{pre}_norm1_w"])), (n2[:], col(m.dram[f"{pre}_norm2_w"]))):
                sp.dma_start(dst, src).then_inc(loaded, 16)

        @block.gpsimd
        def _(pool):
            link = Links(pool, pool_chain)

            def band(t, keep, steps):
                link(nc.gpsimd.memset(t[:], keep))
                for base, mult, step in steps:
                    link(nc.gpsimd.affine_select(out=t[:], in_=t[:], compare_op=ALU.is_ge, fill=0.0, base=base,
                                                 pattern=[[step, t.shape[1]]], channel_multiplier=mult))

            band(headsum, 1.0 / DH, [(0, 1, -DH), (DH - 1, -1, DH)])
            band(headexp, 1.0, [(0, -DH, 1), (DH - 1, DH, -1)])
            link(nc.gpsimd.memset(two_c[:], 2.0))
            link(nc.gpsimd.memset(go[:], 1.0))
            link(nc.gpsimd.memset(begin[:], 0.0))
            link(nc.gpsimd.memset(go[:, 0:S:CHUNK], 0.0))
            nc.gpsimd.memset(begin[:, 0:S:CHUNK], 1.0).then_inc(consts, 1)
            pool.wait_ge(consts, 1)

            def prep(b):
                pool.wait_ge(moments, 2 * b + 1)
                pool_rsqrt(nc, m, w).then_inc(rstd, 1)
                pool.wait_ge(moments, 2 * b + 2)
                pool_rsqrt(nc, m, w1).then_inc(rstd, 1)

            prep(0)
            for b in range(B):
                i = b % 2
                if b + 1 < B:
                    prep(b + 1)
                pool.wait_ge(gates_ready, 3 * (b + 1))
                pool.wait_ge(proj_read, 2 * (b + 1))
                wait(pool, y_ready, b)
                nc.gpsimd.tensor_tensor(u[:], k[i][:], v[i][:], ALU.mult).then_inc(u_ready, 1)
                pool.wait_ge(clipped, b + 1)
                nc.gpsimd.tensor_tensor(a0[:], a[i][:], go[:], ALU.mult).then_inc(started, 1)
                nc.gpsimd.tensor_tensor(a1[:], a[i][:], begin[:], ALU.mult).then_inc(started, 1)
                pool.wait_ge(qms_ready, b + 1)
                nc.gpsimd.tensor_tensor(qrs[:], qms[:], m.half[:, 0:TB * H], ALU.pow).then_inc(qrs_ready, 1)
                pool.wait_ge(m3, b + 1)
                pool_rsqrt(nc, m, w3).then_inc(rstd3, 1)

        @block.vector
        def _(dve):
            link = Links(dve, dve_chain)
            dve.wait_ge(loaded, 16 * NLOAD)
            dve.wait_ge(consts, 1)

            def prep(b):
                xs, hs = [m.x[:, b, t] for t in range(TB)], [h[b % 2][:, t] for t in range(TB)]
                dve_moments(nc, link, w, xs, D, LN_EPS).then_inc(moments, 1)
                dve.wait_ge(rstd, 2 * b + 1)
                for t in range(TB):
                    link.mark(nc.vector.tensor_scalar(hs[t], xs[t], w.mean[:, t:t + 1], w.rstd[:, t:t + 1], ALU.subtract, ALU.mult))
                link.wait()
                dve_square_mean(nc, link, w1, hs, D, EPS_X).then_inc(moments, 1)
                dve.wait_ge(rstd, 2 * b + 2)
                wait(dve, turned, b)
                for t in range(TB):
                    nc.vector.tensor_scalar(h1[:, t], hs[t], w1.rstd[:, t:t + 1], None, ALU.mult).then_inc(h_ready, 1)

            prep(0)
            for b in range(B):
                i = b % 2
                dve.wait_ge(gates_ready, 3 * (b + 1))
                nc.vector.tensor_scalar(a[i][:], a[i][:], 0.6, 0.9995, ALU.max, ALU.min).then_inc(clipped, 1)
                dve.wait_ge(qs_ready, b + 1)
                nc.vector.tensor_scalar(qms[:], psB[:, 0:TB * H], EPS_Q, None, ALU.add).then_inc(qms_ready, 1)
                if b + 1 < B:
                    prep(b + 1)
                dve.wait_ge(started, 2 * (b + 1))
                link(nc.vector.tensor_tensor_scan(pref[:], a0[:], a1[:], 0.0, ALU.mult, ALU.add))
                link(nc.vector.tensor_scalar(rec[:], pref[:], 1e-6, None, ALU.max))
                link(nc.vector.reciprocal(rec[:], rec[:]))
                dve.wait_ge(u_ready, b + 1)
                link(nc.vector.tensor_tensor(rec[:], u[:], rec[:], ALU.mult))
                link(nc.vector.tensor_tensor_scan(acc[:], go[:], rec[:], 0.0, ALU.mult, ALU.add))
                link(nc.vector.tensor_tensor(st[:, 0:CHUNK], pref[:, 0:CHUNK], acc[:, 0:CHUNK], ALU.mult))
                for c in range(1, NC):
                    z = slice(c * CHUNK, (c + 1) * CHUNK)
                    link(nc.vector.scalar_tensor_tensor(st[:, z], acc[:, z], st[:, c * CHUNK - 1:c * CHUNK], pref[:, z], ALU.add, ALU.mult))
                dve.wait_ge(proj_read, 2 * (b + 1))
                link(nc.vector.tensor_tensor(st[:], st[:], q[i][:], ALU.mult))
                dve.wait_ge(q_spread, b + 1)
                link(nc.vector.tensor_tensor(st[:], st[:], psB[:, 0:S], ALU.mult))
                link(nc.vector.tensor_tensor(st[:], st[:], v[i][:], ALU.subtract))
                link(nc.vector.tensor_tensor(st[:], st[:], g[i][:], ALU.mult))
                nc.vector.tensor_tensor(yT[:], st[:], v[i][:], ALU.add).then_inc(y_ready, 1)
                dve.wait_ge(mix_ready, b + 1)
                link(nc.vector.scalar_tensor_tensor(hm[:], psB[:, 0:S].rearrange("p (t d) -> p t d", t=TB), RES, h[i][:], ALU.mult, ALU.add))
                dve_square_mean(nc, link, w3, [hm[:, t] for t in range(TB)], D, EPS_X).then_inc(m3, 1)
                dve.wait_ge(rstd3, b + 1)
                for t in range(TB):
                    nc.vector.tensor_scalar(h2[:, t], hm[:, t], w3.rstd[:, t:t + 1], None, ALU.mult).then_inc(h2_ready, 1)
                dve.wait_ge(mlp_ready, b + 1)
                link(nc.vector.scalar_tensor_tensor(y[:], psD[:], RES, hm[:], ALU.mult, ALU.add))
                nc.vector.tensor_tensor(m.x[:, b], m.x[:, b], y[:], ALU.add).then_inc(x_done, 1)

        @block.tensor
        def _(pe):
            pe.wait_ge(loaded, 16 * NLOAD)
            pe.wait_ge(consts, 1)

            def prep(b):
                pe.wait_ge(h_ready, TB * (b + 1))
                for t in range(TB):
                    ins = nc.tensor.transpose(psA[:, t * P:(t + 1) * P], h1[:, t], m.ident[:])
                ins.then_inc(turned, 1)
                pe.wait_ge(hT_ready, b + 1)
                wait(pe, proj_read, 2 * b)
                wait(pe, gates_ready, 3 * b)
                wait(pe, q2_ready, b)
                for j in range(5):
                    ins = nc.tensor.matmul(psP[:, j], wi[:, j * D:(j + 1) * D], hT[:], start=True, stop=True)
                ins.then_inc(proj_ready, 1)

            prep(0)
            for b in range(B):
                i = b % 2
                pe.wait_ge(q2_ready, b + 1)
                for t in range(TB):
                    ins = nc.tensor.matmul(psB[:, t * H:(t + 1) * H], q2[i][:, t * P:(t + 1) * P], headsum[:], start=True, stop=True)
                ins.then_inc(qs_ready, 1)
                if b + 1 < B:
                    prep(b + 1)
                pe.wait_ge(qrs_ready, b + 1)
                for t in range(TB):
                    ins = nc.tensor.transpose(psA[0:H, 256 + t * P:256 + (t + 1) * P], qrs[:, t * H:(t + 1) * H], m.ident[:])
                ins.then_inc(q_turned, 1)
                pe.wait_ge(qrT_ready, b + 1)
                nc.tensor.matmul(psB[:, 0:S], headexp[:], qrT[:], start=True, stop=True).then_inc(q_spread, 1)
                pe.wait_ge(y_ready, b + 1)
                for t in range(TB):
                    ins = nc.tensor.matmul(psB[:, t * D:(t + 1) * D], yT[:, t * P:(t + 1) * P], wo[:], start=True, stop=True)
                ins.then_inc(mix_ready, 1)
                pe.wait_ge(h2_ready, TB * (b + 1))
                for t in range(TB):
                    ins = nc.tensor.transpose(psA[:, t * P:(t + 1) * P], h2[:, t], m.ident[:])
                ins.then_inc(h2_turned, 1)
                pe.wait_ge(h2T_ready, b + 1)
                for c in range(FC // P):
                    ins = nc.tensor.matmul(psC[:, c], wf[:, c * P:(c + 1) * P], h2T[:], start=True, stop=True)
                ins.then_inc(fc_ready, 1)
                pe.wait_ge(silu_ready, b + 1)
                for t in range(TB):
                    for c in range(FC // P):
                        ins = nc.tensor.matmul(psD[:, t], sT[:, c, t * P:(t + 1) * P], wp[:, c], start=(c == 0), stop=(c == FC // P - 1))
                ins.then_inc(mlp_ready, 1)

        @block.scalar
        def _(act):
            act.wait_ge(loaded, 16 * NLOAD)
            act.wait_ge(consts, 1)

            def prep(b):
                i = b % 2
                act.wait_ge(turned, b + 1)
                nc.scalar.activation(hT[:], psA[:, 0:S], ACT.Copy, scale=n1[:]).then_inc(hT_ready, 1)
                act.wait_ge(proj_ready, b + 1)
                wait(act, y_ready, b - 1)
                nc.scalar.activation(q2[i][:], psP[:, 0], ACT.Square).then_inc(q2_ready, 1)
                nc.scalar.activation(k[i][:], psP[:, 1], ACT.Tanh).then_inc(gates_ready, 1)
                nc.scalar.activation(a[i][:], psP[:, 3], ACT.Sigmoid, bias=two_c[:]).then_inc(gates_ready, 1)
                nc.scalar.activation(g[i][:], psP[:, 4], ACT.Sigmoid).then_inc(gates_ready, 1)
                nc.scalar.copy(q[i][:], psP[:, 0]).then_inc(proj_read, 1)
                nc.scalar.copy(v[i][:], psP[:, 2]).then_inc(proj_read, 1)

            prep(0)
            for b in range(B):
                if b + 1 < B:
                    prep(b + 1)
                act.wait_ge(q_turned, b + 1)
                nc.scalar.copy(qrT[:], psA[0:H, 256:256 + S]).then_inc(qrT_ready, 1)
                act.wait_ge(h2_turned, b + 1)
                nc.scalar.activation(h2T[:], psA[:, 0:S], ACT.Copy, scale=n2[:]).then_inc(h2T_ready, 1)
                act.wait_ge(fc_ready, b + 1)
                nc.scalar.activation(sT[:], psC[:], ACT.Silu).then_inc(silu_ready, 1)


def layer_sign_linear(m, pre):
    nc = m.nc
    LIMIT = 100.0
    with ExitStack() as es:
        sb, ps, sem = allocators(nc, es, pre)
        wT, scale, bias = sb("wT", [P, D]), sb("scale", [P, D]), sb("bias", [P, D])
        w = Norm(sb)
        h, hT, y = sb("h", [P, TB, D]), sb("hT", [P, S]), sb("y", [P, TB, D])
        psT, psY = ps("psT", [P, S]), ps("psY", [P, TB, D])
        loaded, w_signed, var_ready, rstd_ready = sem("loaded"), sem("w_signed"), sem("var_ready"), sem("rstd_ready")
        h_ready, turned, hT_ready, y_ready, dve_chain = (sem("h_ready"), sem("turned"), sem("hT_ready"),
                                                          sem("y_ready"), sem("dve_chain"))
        y_done = sem("y_done")
        block = es.enter_context(nc.Block())

        @block.sync
        def _(sp):
            sp.dma_start(wT[:], m.dram[f"{pre}_weights"]).then_inc(loaded, 16)
            sp.dma_start(scale[:], rows(m.dram[f"{pre}_scale"]).to_broadcast((P, D))).then_inc(loaded, 16)
            sp.dma_start(bias[:], rows(m.dram[f"{pre}_bias"]).to_broadcast((P, D))).then_inc(loaded, 16)

        @block.gpsimd
        def _(pool):
            with pool.Fori(0, B) as b:
                pool.wait_ge(var_ready, b + 1)
                pool_rsqrt(nc, m, w).then_inc(rstd_ready, 1)

        @block.vector
        def _(dve):
            STEPS = 2 * TB + 9
            dve.wait_ge(loaded, 48)
            nc.vector.tensor_scalar(wT[:], wT[:], 0.0, 2.0, ALU.is_ge, ALU.mult).then_inc(w_signed, 1)
            dve.wait_ge(w_signed, 1)
            nc.vector.tensor_scalar(wT[:], wT[:], 1.0, None, ALU.subtract).then_inc(w_signed, 1)
            with dve.Fori(0, B) as b:
                link = Links(dve, dve_chain, b * STEPS)
                dve_moments(nc, link, w, [m.x[:, b, t] for t in range(TB)], D, LN_EPS).then_inc(var_ready, 1)
                dve.wait_ge(rstd_ready, b + 1)
                for t in range(TB):
                    nc.vector.tensor_scalar(h[:, t], m.x[:, b, t], w.mean[:, t:t + 1], w.rstd[:, t:t + 1], ALU.subtract, ALU.mult).then_inc(h_ready, 1)
                dve.wait_ge(y_ready, b + 1)
                bc = lambda a: a[:, None, :].to_broadcast((P, TB, D))
                link(nc.vector.tensor_tensor(y[:], psY[:], bc(scale[:]), ALU.mult))
                link(nc.vector.tensor_tensor(y[:], y[:], bc(bias[:]), ALU.add))
                link(nc.vector.tensor_scalar(y[:], y[:], -LIMIT, LIMIT, ALU.max, ALU.min))
                for t in range(TB):
                    link(nc.vector.tensor_tensor(m.x[:, b, t], m.x[:, b, t], y[:, t], ALU.add))
                assert link.n == STEPS, link.n

        @block.tensor
        def _(pe):
            pe.wait_ge(w_signed, 2)
            with pe.Fori(0, B) as b:
                pe.wait_ge(h_ready, TB * b + TB)
                for t in range(TB):
                    ins = nc.tensor.transpose(psT[:, t * P:(t + 1) * P], h[:, t], m.ident[:])
                ins.then_inc(turned, 1)
                pe.wait_ge(hT_ready, b + 1)
                for t in range(TB):
                    ins = nc.tensor.matmul(psY[:, t], hT[:, t * P:(t + 1) * P], wT[:], start=True, stop=True)
                ins.then_inc(y_ready, 1)

        @block.scalar
        def _(act):
            with act.Fori(0, B) as b:
                act.wait_ge(turned, b + 1)
                nc.scalar.copy(hT[:], psT[:]).then_inc(hT_ready, 1)


def layer_moe_top8(m, pre):
    nc = m.nc
    d = m.dram
    E, F, TOP = 64, 64, 8
    EG = 8
    NGR = E // EG
    BK = EG * F // P
    with ExitStack() as es:
        sb, ps, sem = allocators(nc, es, pre)
        wup, wdn = sb("wup", [P, E, F]), sb("wdn", [P, E // 2, D])
        sup, sdn, cen, ebias = sb("sup", [P, F]), sb("sdn", [F, D]), sb("cen", [P, E]), sb("ebias", [P, E])
        w = Norm(sb)
        h, hT = sb("h", [P, TB, D]), [sb(f"hT{i}", [P, S]) for i in range(2)]
        aff, bia, top8, rest = sb("aff", [P, TB, E]), sb("bia", [P, TB, E]), sb("top8", [P, TB, 8]), sb("rest", [P, TB, E])
        sig, cw, wsum = sb("sig", [P, TB, E]), [sb(f"cw{i}", [P, TB, E]) for i in range(2)], sb("wsum", [P, TB])
        act_s, wt_s, fT = [sb(f"act{i}", [P, EG * F]) for i in range(3)], [sb(f"wt{i}", [P, EG * F]) for i in range(3)], [sb(f"fT{i}", [P, BK, P]) for i in range(3)]
        shT = [sb(f"shT{i}", [F, S]) for i in range(2)]
        psU, psF = [ps(f"psU{i}", [P, EG * F]) for i in range(2)], [ps(f"psF{i}", [P, BK * P]) for i in range(2)]
        psY = [ps(f"psY{i}", [P, 512]) for i in range(2)]
        psM, psH = ps("psM", [P, 512]), ps("psH", [P, 512])
        names = ("loaded", "dve_chain", "var_ready", "rstd_ready", "h_ready", "turned", "hT_ready", "aff_ready", "aff_copied",
                 "sig_ready", "cw_ready", "up_ready", "silu_ready", "weighted", "f_turned", "fT_ready", "down_done", "sh_up",
                 "sh_silu", "x_done")
        (loaded, dve_chain, var_ready, rstd_ready, h_ready, turned, hT_ready, aff_ready, aff_copied,
         sig_ready, cw_ready, up_ready, silu_ready, weighted, f_turned, fT_ready, down_done, sh_up,
         sh_silu, x_done) = (sem(n) for n in names)
        block = es.enter_context(nc.Block())
        LT, LD = 2, 3
        NG = NT * NGR

        @block.sync
        def _(sp):
            for dst, src in ((sup[:], d[f"{pre}_Ws_up"]), (sdn[:], d[f"{pre}_Ws_down"]), (cen[:], d[f"{pre}_centroids"]),
                             (ebias[:], rows(d[f"{pre}_expert_biases"]).to_broadcast((P, E)))):
                sp.dma_start(dst, src).then_inc(loaded, 16)
            for q in range(4):
                c = slice(q * E // 4, (q + 1) * E // 4)
                sp.dma_start(wup[:, c], d[f"{pre}_W_up"][c].rearrange("e d f -> d e f")).then_inc(loaded, 16)
            sp.dma_start(wdn[:], d[f"{pre}_W_down"].rearrange("(n e) f d -> (e f) n d", e=2)).then_inc(loaded, 16)

        @block.gpsimd
        def _(pool):
            for b in range(B):
                pool.wait_ge(var_ready, b + 1)
                pool_rsqrt(nc, m, w).then_inc(rstd_ready, 1)

        @block.vector
        def _(dve):
            link = Links(dve, dve_chain)
            dve.wait_ge(loaded, 16 * 9)

            def norm(b):
                dve_moments(nc, link, w, [m.x[:, b, t] for t in range(TB)], D, LN_EPS).then_inc(var_ready, 1)
                dve.wait_ge(rstd_ready, b + 1)
                wait(dve, turned, b)
                for t in range(TB):
                    nc.vector.tensor_scalar(h[:, t], m.x[:, b, t], w.mean[:, t:t + 1], w.rstd[:, t:t + 1], ALU.subtract, ALU.mult).then_inc(h_ready, 1)

            def route_a(b):
                dve.wait_ge(aff_ready, b + 1)
                wait(dve, sig_ready, b)
                nc.vector.tensor_copy(aff[:], psM[:, 256:256 + TB * E].rearrange("p (t e) -> p t e", t=TB)).then_inc(aff_copied, 1)
                dve.wait_ge(aff_copied, b + 1)
                link(nc.vector.tensor_tensor(bia[:], aff[:], ebias[:, None, :].to_broadcast((P, TB, E)), ALU.add))
                for t in range(TB):
                    link.mark(nc.vector.max(top8[:, t], bia[:, t]))
                link.wait()
                for t in range(TB):
                    link.mark(nc.vector.match_replace(rest[:, t], top8[:, t], bia[:, t], -3.0e38))
                link.wait()

            def route_b(b):
                link(nc.vector.tensor_tensor(rest[:], rest[:], bia[:], ALU.not_equal))
                dve.wait_ge(sig_ready, b + 1)
                c = cw[b % 2]
                link(nc.vector.tensor_tensor(c[:], sig[:], rest[:], ALU.mult))
                link(nc.vector.reduce_sum(wsum[:], c[:], AX.X))
                link(nc.vector.tensor_scalar(wsum[:], wsum[:], 1e-8, None, ALU.add))
                link(nc.vector.reciprocal(wsum[:], wsum[:]))
                nc.vector.tensor_tensor(c[:], c[:], wsum[:, :, None].to_broadcast((P, TB, E)), ALU.mult).then_inc(cw_ready, 1)

            def weigh(n):
                tile, g = n // NGR, n % NGR
                b, t = tile // TB, tile % TB
                dve.wait_ge(silu_ready, n + 1)
                if g == 0 and t == 0:
                    dve.wait_ge(cw_ready, b + 1)
                wait(dve, f_turned, n - 2)
                e = g * EG
                nc.vector.tensor_tensor(wt_s[n % 3][:].rearrange("p (e f) -> p e f", f=F), act_s[n % 3][:].rearrange("p (e f) -> p e f", f=F),
                                        cw[b % 2][:, t, e:e + EG, None].to_broadcast((P, EG, F)), ALU.mult).then_inc(weighted, 1)

            def update(tile):
                b, t = tile // TB, tile % TB
                dve.wait_ge(down_done, NGR * (tile + 1))
                nc.vector.tensor_tensor(m.x[:, b, t], m.x[:, b, t], psY[tile % 2][:, 0:D], ALU.add).then_inc(x_done, 1)

            norm(0)
            route_a(0)
            route_b(0)
            for n in range(NG):
                tile, g = n // NGR, n % NGR
                b, t = tile // TB, tile % TB
                weigh(n)
                if t == 0 and g == 1 and b + 1 < B:
                    norm(b + 1)
                if t == 1 and g == 2 and b + 1 < B:
                    route_a(b + 1)
                if t == 1 and g == 4 and b + 1 < B:
                    route_b(b + 1)
                if g == 5 and tile >= 1:
                    update(tile - 1)
            update(NT - 1)

        @block.tensor
        def _(pe):
            pe.wait_ge(loaded, 16 * 9)

            def turn(b):
                pe.wait_ge(h_ready, TB * (b + 1))
                wait(pe, hT_ready, b)
                for t in range(TB):
                    ins = nc.tensor.transpose(psM[:, t * P:(t + 1) * P], h[:, t], m.ident[:])
                ins.then_inc(turned, 1)

            def affinities(b):
                pe.wait_ge(hT_ready, b + 1)
                wait(pe, aff_copied, b)
                for t in range(TB):
                    ins = nc.tensor.matmul(psM[:, 256 + t * E:256 + (t + 1) * E], hT[b % 2][:, t * P:(t + 1) * P], cen[:], start=True, stop=True)
                ins.then_inc(aff_ready, 1)

            def up(n):
                tile, g = n // NGR, n % NGR
                b, t = tile // TB, tile % TB
                wait(pe, silu_ready, n - 1)
                nc.tensor.matmul(psU[n % 2][:], hT[b % 2][:, t * P:(t + 1) * P], wup[:, g * EG:(g + 1) * EG].rearrange("p e f -> p (e f)"),
                                 start=True, stop=True).then_inc(up_ready, 1)

            def shared_up(b):
                wait(pe, sh_silu, b)
                nc.tensor.matmul(psH[0:F, 0:S], sup[:], hT[b % 2][:], start=True, stop=True).then_inc(sh_up, 1)

            def turn_hidden(n):
                pe.wait_ge(weighted, n + 1)
                wait(pe, fT_ready, n - 1)
                for k in range(BK):
                    ins = nc.tensor.transpose(psF[n % 2][:, k * P:(k + 1) * P], wt_s[n % 3][:, k * P:(k + 1) * P], m.ident[:])
                ins.then_inc(f_turned, 1)

            def down(n):
                tile, g = n // NGR, n % NGR
                b, t = tile // TB, tile % TB
                if g == 0:
                    pe.wait_ge(sh_silu, b + 1)
                    wait(pe, x_done, tile - 1)
                    nc.tensor.matmul(psY[tile % 2][:, 0:D], shT[b % 2][:, t * P:(t + 1) * P], sdn[:], start=True, stop=False)
                pe.wait_ge(fT_ready, n + 1)
                for k in range(BK):
                    ins = nc.tensor.matmul(psY[tile % 2][:, 0:D], fT[n % 3][:, k], wdn[:, g * BK + k], start=False, stop=(g == NGR - 1 and k == BK - 1))
                ins.then_inc(down_done, 1)

            turn(0)
            affinities(0)
            shared_up(0)
            for n in range(NG + LD):
                tile, g = n // NGR, n % NGR
                b, t = tile // TB, tile % TB
                if n < NG:
                    up(n)
                    if t == 0 and g == 5 and b + 1 < B:
                        turn(b + 1)
                    if t == 1 and g == 0 and b + 1 < B:
                        affinities(b + 1)
                    if t == 1 and g == 1 and b + 1 < B:
                        shared_up(b + 1)
                if LT <= n < NG + LT:
                    turn_hidden(n - LT)
                if n >= LD:
                    down(n - LD)

        @block.scalar
        def _(act):
            def copy_h(b):
                act.wait_ge(turned, b + 1)
                wait(act, up_ready, TB * NGR * (b - 1))
                nc.scalar.copy(hT[b % 2][:], psM[:, 0:S]).then_inc(hT_ready, 1)

            def sigmoids(b):
                act.wait_ge(aff_copied, b + 1)
                wait(act, cw_ready, b)
                nc.scalar.activation(sig[:], aff[:], ACT.Sigmoid).then_inc(sig_ready, 1)

            def shared_silu(b):
                act.wait_ge(sh_up, b + 1)
                wait(act, down_done, TB * NGR * (b - 1))
                nc.scalar.activation(shT[b % 2][:], psH[0:F, 0:S], ACT.Silu).then_inc(sh_silu, 1)

            def silu(n):
                act.wait_ge(up_ready, n + 1)
                wait(act, weighted, n - 2)
                nc.scalar.activation(act_s[n % 3][:], psU[n % 2][:], ACT.Silu).then_inc(silu_ready, 1)

            def copy_turned(n):
                act.wait_ge(f_turned, n + 1)
                wait(act, down_done, n - 2)
                nc.scalar.copy(fT[n % 3][:].rearrange("p n q -> p (n q)"), psF[n % 2][:]).then_inc(fT_ready, 1)

            copy_h(0)
            sigmoids(0)
            shared_silu(0)
            for n in range(NG + LT):
                tile, g = n // NGR, n % NGR
                b, t = tile // TB, tile % TB
                if n < NG:
                    silu(n)
                    if t == 0 and g == 6 and b + 1 < B:
                        copy_h(b + 1)
                    if t == 1 and g == 3 and b + 1 < B:
                        sigmoids(b + 1)
                        shared_silu(b + 1)
                if n >= LT:
                    copy_turned(n - LT)


def layer_selected_experts(m, pre):
    nc = m.nc
    d = m.dram
    E, F, M = 8, 64, 256
    MT = M // P
    EF = E * F
    EB = EF // P
    NEG = E + 1
    with ExitStack() as es:
        sb, ps, sem = allocators(nc, es, pre)
        sw12, sw3 = sb("sw12", [P, 2 * F]), sb("sw3", [F, D])
        sb12, sb3, sg, sbeta = sb("sb12", [P, 2 * F]), sb("sb3", [P, D]), sb("sln_g", [F, 1]), sb("sln_b", [F, 1])
        wgate, bgate, ebias = sb("wgate", [P, NEG]), sb("bgate", [P, NEG]), sb("ebias", [P, E])
        ew = [sb(f"ew{i + 1}", [P, E, F]) for i in range(2)]
        eb = [sb(f"eb{i + 1}", [P, EF]) for i in range(2)]
        ew3, eb3 = sb("ew3", [P, EB, D]), sb("eb3", [E, D])
        lng, lnb = sb("lng", [P, F]), sb("lnb", [P, F])
        ib_row, it_row, id_row = sb("ib_row", [P, M], I32), sb("it_row", [P, M], I32), sb("id_row", [P, M])
        ib_col, it_col, id_col = sb("ib_col", [P, MT], I32), sb("it_col", [P, MT], I32), sb("id_col", [P, MT])
        rowf, colf = sb("rowf", [P, M]), sb("colf", [P, MT])
        tok_col, tok_row, rank = sb("tok_col", [P, NT]), sb("tok_row", [P, NT * P]), sb("rank", [P, E])
        pick, spread = sb("pick", [P, NT, M]), sb("spread", [P, MT, NT * P])
        wa, ws, we = Norm(sb, "a", NT), Norm(sb, "s", NT), Norm(sb, "e", MT * E)
        h, hT = sb("h", [P, NT, D]), sb("hT", [P, NT, P])
        x12, u, shT, so = sb("x12", [P, NT, 2 * F]), sb("u", [P, NT, F]), sb("shT", [F, NT, P]), sb("so", [P, NT, D])
        xpT = sb("xpT", [P, M])
        gl, sc, bi, oh, key = sb("gl", [P, MT, NEG]), sb("sc", [P, MT, NEG]), sb("bi", [P, MT, E]), sb("oh", [P, MT, E]), sb("key", [P, MT, E])
        top, two, mx2, wsum = sb("top", [P, MT]), sb("two", [P, MT, 2]), sb("mx2", [P, MT]), sb("wsum", [P, MT])
        e1, e2 = sb("e1", [P, MT, EF]), sb("e2", [P, MT, EF])
        zT, ohT, picked_out = sb("zT", [P, EB, M]), sb("ohT", [E, M]), sb("picked_out", [P, MT, D + 2])
        seen, cnt, rec, keep = sb("seen", [P, NT, 2]), sb("cnt", [P, NT]), sb("rec", [P, NT]), sb("keep", [P, NT])
        psT, psX, psE = [ps(f"psT{i}", [P, 512]) for i in range(2)], [ps(f"psX{i}", [P, 512]) for i in range(2)], [ps(f"psE{i}", [P, 512]) for i in range(2)]
        psG, psC = ps("psG", [P, 512]), ps("psC", [P, 512])
        names = ("loaded", "dve_chain", "pool_chain", "iota_ready", "var_ready", "rstd_ready", "h_ready", "pick_ready", "turned", "hT_ready",
                 "x12_ready", "biased", "silu_ready", "z_ready", "z_turned", "shT_ready", "shared_out", "so_ready", "gathered",
                 "xpT_ready", "gates_ready", "logits_ready", "sig_ready", "two_ready", "exp_ready", "e_ready", "e_biased", "esilu_ready", "ez_ready",
                 "ez_turned", "zT_ready", "eo_ready", "po_ready", "seen_ready", "spread_done", "x_done")
        (loaded, dve_chain, pool_chain, iota_ready, var_ready, rstd_ready, h_ready, pick_ready, turned, hT_ready,
         x12_ready, biased, silu_ready, z_ready, z_turned, shT_ready, shared_out, so_ready, gathered,
         xpT_ready, gates_ready, logits_ready, sig_ready, two_ready, exp_ready, e_ready, e_biased, esilu_ready, ez_ready,
         ez_turned, zT_ready, eo_ready, po_ready, seen_ready, spread_done, x_done) = (sem(n) for n in names)
        block = es.enter_context(nc.Block())
        col = lambda a: a.rearrange("(d a) -> d a", a=1)
        wide = lambda name, n: rows(d[f"{pre}_{name}"]).to_broadcast((P, n))
        loads = [(ib_row[:], wide("index_b", M)), (it_row[:], wide("index_t", M)),
                 (sw12[:, 0:F], d[f"{pre}_sw1"]), (sw12[:, F:], d[f"{pre}_sw2"]), (sw3[:], d[f"{pre}_sw3"]),
                 (sb12[:, 0:F], wide("sb1", F)), (sb12[:, F:], wide("sb2", F)), (sb3[:], wide("sb3", D)),
                 (sg[:], col(d[f"{pre}_s_ln_g"])), (sbeta[:], col(d[f"{pre}_s_ln_b"])),
                 (wgate[:, 0:1], d[f"{pre}_sg_w"]), (wgate[:, 1:], d[f"{pre}_eg_w"]),
                 (bgate[:, 0:1], wide("sg_b", 1)), (bgate[:, 1:], wide("eg_b", E)), (ebias[:], wide("exp_bias", E)),
                 (ew[0][:], d[f"{pre}_ew1"].rearrange("e d f -> d e f")), (ew[1][:], d[f"{pre}_ew2"].rearrange("e d f -> d e f")),
                 (eb[0][:], rows(d[f"{pre}_eb1"].rearrange("e f -> (e f)")).to_broadcast((P, EF))),
                 (eb[1][:], rows(d[f"{pre}_eb2"].rearrange("e f -> (e f)")).to_broadcast((P, EF))),
                 (ew3[:], d[f"{pre}_ew3"].rearrange("e f d -> (e f) d").rearrange("(n p) d -> p n d", p=P)), (eb3[:], d[f"{pre}_eb3"]),
                 (lng[:], wide("sel_ln_g", F)), (lnb[:], wide("sel_ln_b", F))]
        for c, name in ((ib_col, "index_b"), (it_col, "index_t")):
            loads += [(c[:, t:t + 1], col(d[f"{pre}_{name}"][t * P:(t + 1) * P])) for t in range(MT)]
        NLOAD = 16 * len(loads)

        @block.sync
        def _(sp):
            for dst, src in loads:
                sp.dma_start(dst, src).then_inc(loaded, 16)

        @block.gpsimd
        def _(pool):
            link = Links(pool, pool_chain)
            nc.gpsimd.iota(tok_col[:], pattern=[[P, NT]], base=0, channel_multiplier=1, allow_small_or_imprecise_dtypes=True).then_inc(iota_ready, 1)
            nc.gpsimd.iota(tok_row[:], pattern=[[1, NT * P]], base=0, channel_multiplier=0, allow_small_or_imprecise_dtypes=True).then_inc(iota_ready, 1)
            nc.gpsimd.iota(rank[:], pattern=[[-1, E]], base=E, channel_multiplier=0, allow_small_or_imprecise_dtypes=True).then_inc(iota_ready, 1)
            nc.gpsimd.memset(picked_out[:, :, D + 1:], 1.0).then_inc(iota_ready, 1)
            for n, ww in enumerate((wa, ws, we)):
                pool.wait_ge(var_ready, n + 1)
                pool_rsqrt(nc, m, ww, ww.n).then_inc(rstd_ready, 1)

        @block.vector
        def _(dve):
            link = Links(dve, dve_chain)
            fl = lambda a: a.rearrange("p n d -> p (n d)")
            dve_moments(nc, link, wa, [m.x[:, i // TB, i % TB] for i in range(NT)], D, LN_EPS).then_inc(var_ready, 1)
            dve.wait_ge(loaded, NLOAD)
            for b_, t_, f_, out in ((ib_row, it_row, rowf, id_row), (ib_col, it_col, colf, id_col)):
                link.mark(nc.vector.tensor_copy(f_[:], b_[:]))
                link(nc.vector.tensor_copy(out[:], t_[:]))
                link(nc.vector.scalar_tensor_tensor(out[:], f_[:], float(S), out[:], ALU.mult, ALU.add))
            dve.wait_ge(iota_ready, 4)
            dve.wait_ge(rstd_ready, 1)
            for i in range(NT):
                nc.vector.tensor_scalar(h[:, i], m.x[:, i // TB, i % TB], wa.mean[:, i:i + 1], wa.rstd[:, i:i + 1], ALU.subtract, ALU.mult).then_inc(h_ready, 1)
                nc.vector.tensor_scalar(pick[:, i], id_row[:], tok_col[:, i:i + 1], None, ALU.is_equal).then_inc(pick_ready, 1)
            for b in range(B):
                dve.wait_ge(x12_ready, b + 1)
                nc.vector.tensor_tensor(x12[:, TB * b:TB * (b + 1)], psX[b % 2][:, 0:TB * 2 * F].rearrange("p (t f) -> p t f", t=TB),
                                        sb12[:, None, :].to_broadcast((P, TB, 2 * F)), ALU.add).then_inc(biased, 1)
            dve.wait_ge(gates_ready, 1)
            nc.vector.tensor_tensor(gl[:], psC[:, 0:MT * NEG].rearrange("p (t e) -> p t e", t=MT), bgate[:, None, :].to_broadcast((P, MT, NEG)), ALU.add).then_inc(logits_ready, 1)
            for b in range(B):
                dve.wait_ge(silu_ready, b + 1)
                i = slice(TB * b, TB * (b + 1))
                link.mark(nc.vector.tensor_tensor(u[:, i], u[:, i], x12[:, i, F:], ALU.mult))
            link.wait()
            dve_moments(nc, link, ws, [u[:, i] for i in range(NT)], F, LN_EPS).then_inc(var_ready, 1)
            for t in range(MT):
                for k, e in enumerate((e1, e2)):
                    dve.wait_ge(e_ready, 2 * t + k + 1)
                    nc.vector.tensor_tensor(e[:, t], psE[k][:], eb[k][:], ALU.add).then_inc(e_biased, 1)
            dve.wait_ge(rstd_ready, 2)
            for i in range(NT):
                if i == 0:
                    link.wait()
                nc.vector.tensor_scalar(u[:, i], u[:, i], ws.mean[:, i:i + 1], ws.rstd[:, i:i + 1], ALU.subtract, ALU.mult).then_inc(z_ready, 1)
            dve.wait_ge(e_biased, 2 * MT)
            for t in range(MT):
                dve.wait_ge(esilu_ready, t + 1)
                link.mark(nc.vector.tensor_tensor(e1[:, t], e1[:, t], e2[:, t], ALU.mult))
            link.wait()
            dve_moments(nc, link, we, [e1[:, n // E, n % E * F:(n % E + 1) * F] for n in range(MT * E)], F, LN_EPS).then_inc(var_ready, 1)
            dve.wait_ge(sig_ready, 1)
            link(nc.vector.tensor_tensor(bi[:], sc[:, :, 1:], ebias[:, None, :].to_broadcast((P, MT, E)), ALU.add))
            link(nc.vector.reduce_max(top[:], bi[:], AX.X))
            link(nc.vector.tensor_tensor(oh[:], bi[:], top[:, :, None].to_broadcast((P, MT, E)), ALU.is_equal))
            link(nc.vector.tensor_tensor(key[:], oh[:], rank[:, None, :].to_broadcast((P, MT, E)), ALU.mult))
            link(nc.vector.reduce_max(top[:], key[:], AX.X))
            link(nc.vector.tensor_tensor(oh[:], key[:], top[:, :, None].to_broadcast((P, MT, E)), ALU.is_equal))
            link(nc.vector.tensor_tensor(key[:], oh[:], sc[:, :, 1:], ALU.mult))
            link.mark(nc.vector.tensor_copy(two[:, :, 0:1], sc[:, :, 0:1]))
            link(nc.vector.reduce_sum(two[:, :, 1:2], key[:], AX.X))
            link(nc.vector.reduce_max(mx2[:], two[:], AX.X))
            nc.vector.tensor_tensor(two[:], two[:], mx2[:, :, None].to_broadcast((P, MT, 2)), ALU.subtract).then_inc(two_ready, 1)
            dve.wait_ge(rstd_ready, 3)
            per = lambda a: a.rearrange("p t (e f) -> p (t e) f", f=F)
            E1 = per(e1[:])
            shape = (P, MT * E, F)
            link(nc.vector.tensor_tensor(E1, E1, we.mean[:, :, None].to_broadcast(shape), ALU.subtract))
            link(nc.vector.tensor_tensor(E1, E1, we.rstd[:, :, None].to_broadcast(shape), ALU.mult))
            link(nc.vector.tensor_tensor(E1, E1, lng[:, None, :].to_broadcast(shape), ALU.mult))
            link(nc.vector.tensor_tensor(E1, E1, lnb[:, None, :].to_broadcast(shape), ALU.add))
            nc.vector.tensor_tensor(E1, E1, fl(oh[:])[:, :, None].to_broadcast(shape), ALU.mult).then_inc(ez_ready, 1)
            for t in range(MT):
                link.mark(nc.vector.tensor_scalar(spread[:, t], tok_row[:], id_col[:, t:t + 1], None, ALU.is_equal))
            for b in range(B):
                dve.wait_ge(shared_out, b + 1)
                nc.vector.tensor_tensor(so[:, TB * b:TB * (b + 1)], psX[b % 2][:, 0:TB * D].rearrange("p (t d) -> p t d", t=TB),
                                        sb3[:, None, :].to_broadcast((P, TB, D)), ALU.add).then_inc(so_ready, 1)
            dve.wait_ge(exp_ready, 1)
            link(nc.vector.reduce_sum(wsum[:], two[:], AX.X))
            link(nc.vector.reciprocal(wsum[:], wsum[:]))
            link(nc.vector.tensor_tensor(two[:], two[:], wsum[:, :, None].to_broadcast((P, MT, 2)), ALU.mult))
            link.mark(nc.vector.tensor_copy(picked_out[:, :, D:D + 1], two[:, :, 0:1]))
            for t in range(MT):
                dve.wait_ge(eo_ready, MT)
                nc.vector.tensor_scalar(picked_out[:, t, 0:D], psC[:, 128 + t * D:128 + (t + 1) * D], two[:, t, 1:2], None, ALU.mult).then_inc(po_ready, 1)
            dve.wait_ge(seen_ready, 1)
            link(nc.vector.tensor_copy(seen[:], psG[:, 0:2 * NT].rearrange("p (i k) -> p i k", k=2)))
            link.mark(nc.vector.tensor_scalar(cnt[:], seen[:, :, 1], 1.0, None, ALU.max))
            link(nc.vector.tensor_scalar(keep[:], seen[:, :, 1], 1.0, None, ALU.min))
            link.mark(nc.vector.reciprocal(rec[:], cnt[:]))
            link(nc.vector.tensor_scalar(keep[:], keep[:], -1.0, 1.0, ALU.mult, ALU.add))
            link(nc.vector.tensor_tensor(cnt[:], seen[:, :, 0], rec[:], ALU.mult))
            link(nc.vector.tensor_tensor(keep[:], keep[:], cnt[:], ALU.add))
            dve.wait_ge(so_ready, B)
            for i in range(NT):
                x = m.x[:, i // TB, i % TB]
                link.mark(nc.vector.scalar_tensor_tensor(x, so[:, i], keep[:, i:i + 1], x, ALU.mult, ALU.add))
            link.wait()
            for i in range(NT):
                b, t = i // TB, i % TB
                dve.wait_ge(spread_done, b + 1)
                x = m.x[:, b, t]
                nc.vector.scalar_tensor_tensor(x, psE[b % 2][:, t * D:(t + 1) * D], rec[:, i:i + 1], x, ALU.mult, ALU.add).then_inc(x_done, 1)

        @block.tensor
        def _(pe):
            for b in range(B):
                pe.wait_ge(h_ready, TB * (b + 1))
                wait(pe, hT_ready, b - 1)
                for t in range(TB):
                    ins = nc.tensor.transpose(psT[b % 2][:, t * P:(t + 1) * P], h[:, TB * b + t], m.ident[:])
                ins.then_inc(turned, 1)
                pe.wait_ge(pick_ready, TB * (b + 1))
                for i in range(TB * b, TB * (b + 1)):
                    ins = nc.tensor.matmul(psG[:, 0:M], h[:, i], pick[:, i], start=(i == 0), stop=(i == NT - 1))
                if b == B - 1:
                    ins.then_inc(gathered, 1)
                if b == 0:
                    pe.wait_ge(loaded, NLOAD)
                pe.wait_ge(hT_ready, b + 1)
                wait(pe, biased, b - 1)
                for t in range(TB):
                    ins = nc.tensor.matmul(psX[b % 2][:, t * 2 * F:(t + 1) * 2 * F], hT[:, TB * b + t], sw12[:], start=True, stop=True)
                ins.then_inc(x12_ready, 1)
            pe.wait_ge(xpT_ready, 1)
            for t in range(MT):
                ins = nc.tensor.matmul(psC[:, t * NEG:(t + 1) * NEG], xpT[:, t * P:(t + 1) * P], wgate[:], start=True, stop=True)
            ins.then_inc(gates_ready, 1)
            for t in range(MT):
                for k in range(2):
                    wait(pe, e_biased, 2 * (t - 1) + k + 1)
                    nc.tensor.matmul(psE[k][:], xpT[:, t * P:(t + 1) * P], ew[k][:].rearrange("p e f -> p (e f)"), start=True, stop=True).then_inc(e_ready, 1)
            for b in range(B):
                pe.wait_ge(z_ready, TB * (b + 1))
                pe.wait_ge(hT_ready, B)
                wait(pe, shT_ready, b - 1)
                for t in range(TB):
                    ins = nc.tensor.transpose(psT[b % 2][0:F, t * P:(t + 1) * P], u[:, TB * b + t], m.ident[:])
                ins.then_inc(z_turned, 1)
                pe.wait_ge(shT_ready, b + 1)
                pe.wait_ge(biased, B)
                wait(pe, so_ready, b - 1)
                for t in range(TB):
                    ins = nc.tensor.matmul(psX[b % 2][:, t * D:(t + 1) * D], shT[:, TB * b + t], sw3[:], start=True, stop=True)
                ins.then_inc(shared_out, 1)
            pe.wait_ge(ez_ready, 1)
            pe.wait_ge(e_biased, 2 * MT)
            for t in range(MT):
                for k in range(EB):
                    nc.tensor.transpose(psE[t][:, k * P:(k + 1) * P], e1[:, t, k * P:(k + 1) * P], m.ident[:])
                pe.wait_ge(shT_ready, B)
                nc.tensor.transpose(psT[t][0:E, 0:P], oh[:, t], m.ident[:]).then_inc(ez_turned, 1)
            pe.wait_ge(logits_ready, 1)
            for t in range(MT):
                pe.wait_ge(zT_ready, t + 1)
                for k in range(EB):
                    nc.tensor.matmul(psC[:, 128 + t * D:128 + (t + 1) * D], zT[:, k, t * P:(t + 1) * P], ew3[:, k], start=(k == 0), stop=False)
                nc.tensor.matmul(psC[:, 128 + t * D:128 + (t + 1) * D], ohT[:, t * P:(t + 1) * P], eb3[:], start=False, stop=True).then_inc(eo_ready, 1)
            pe.wait_ge(po_ready, MT)
            pe.wait_ge(xpT_ready, 1)
            for i in range(NT):
                for t in range(MT):
                    ins = nc.tensor.matmul(psG[:, 2 * i:2 * (i + 1)], spread[:, t, i * P:(i + 1) * P], picked_out[:, t, D:], start=(t == 0), stop=(t == MT - 1))
            ins.then_inc(seen_ready, 1)
            for b in range(B):
                wait(pe, x_done, TB * (b - 1))
                for i in range(TB):
                    for t in range(MT):
                        c = (TB * b + i) * P
                        ins = nc.tensor.matmul(psE[b % 2][:, i * D:(i + 1) * D], spread[:, t, c:c + P], picked_out[:, t, 0:D], start=(t == 0), stop=(t == MT - 1))
                ins.then_inc(spread_done, 1)

        @block.scalar
        def _(act):
            for b in range(B):
                act.wait_ge(turned, b + 1)
                nc.scalar.copy(hT[:, TB * b:TB * (b + 1)].rearrange("p t q -> p (t q)"), psT[b % 2][:, 0:S]).then_inc(hT_ready, 1)
            act.wait_ge(gathered, 1)
            nc.scalar.copy(xpT[:], psG[:, 0:M]).then_inc(xpT_ready, 1)
            for b in range(B):
                act.wait_ge(biased, b + 1)
                i = slice(TB * b, TB * (b + 1))
                nc.scalar.activation(u[:, i], x12[:, i, 0:F], ACT.Silu).then_inc(silu_ready, 1)
            for t in range(MT):
                act.wait_ge(e_biased, 2 * t + 1)
                nc.scalar.activation(e1[:, t], e1[:, t], ACT.Silu).then_inc(esilu_ready, 1)
            act.wait_ge(logits_ready, 1)
            nc.scalar.activation(sc[:], gl[:], ACT.Sigmoid).then_inc(sig_ready, 1)
            act.wait_ge(loaded, NLOAD)
            for b in range(B):
                act.wait_ge(z_turned, b + 1)
                nc.scalar.activation(shT[:, TB * b:TB * (b + 1)].rearrange("p t q -> p (t q)"), psT[b % 2][0:F, 0:S], ACT.Identity,
                                     bias=sbeta[:], scale=sg[:]).then_inc(shT_ready, 1)
            act.wait_ge(two_ready, 1)
            nc.scalar.activation(two[:], two[:], ACT.Exp).then_inc(exp_ready, 1)
            for t in range(MT):
                act.wait_ge(ez_turned, t + 1)
                nc.scalar.copy(zT[:, :, t * P:(t + 1) * P], psE[t][:].rearrange("p (k q) -> p k q", k=EB))
                nc.scalar.copy(ohT[:, t * P:(t + 1) * P], psT[t][0:E, 0:P]).then_inc(zT_ready, 1)


def layer_attention_single(m, pre, scale, inner_norm):
    nc = m.nc
    d = m.dram
    with ExitStack() as es:
        sb, ps, sem = allocators(nc, es, pre)
        wq, wk, wv, wo = sb("wq", [P, D]), sb("wk", [DK, D]), sb("wv", [DK, D]), sb("wo", [P, D])
        bq, bk = sb("bq", [P, 1]), sb("bk", [P, 1])
        bv, bo = sb("bv", [P, D]), sb("bo", [P, D])
        w, w1, w2 = Norm(sb), Norm(sb, "1"), Norm(sb, "2", KT)
        h, hT = sb("h", [P, TB, D]), sb("hT", [P, S])
        ctx = sb("ctx", [P, 2, KT, DK]) if inner_norm else None
        ctxT = sb("ctxT", [DK, 2, SK])
        g1, b1, g2, b2 = sb("g1", [P, 1]), sb("b1", [P, 1]), sb("g2", [DK, 1]), sb("b2", [DK, 1])
        qT, kT, v = sb("qT", [P, S]), sb("kT", [P, SK]), sb("v", [P, KT, D])
        mx, negm, rsum, rinv = sb("mx", [P, TB]), sb("negm", [P, TB]), sb("rsum", [P, TB]), sb("rinv", [P, TB])
        pr, prT = sb("pr", [P, TB, SK]), sb("prT", [P, KT, S])
        oT, y = sb("oT", [P, S]), sb("y", [P, TB, D])
        psA, psK, psV, psS, psP, psO = (ps("psA", [P, 512]), ps("psK", [P, SK]), ps("psV", [P, KT, D]), ps("psS", [P, TB, SK]),
                                        ps("psP", [P, KT, S]), ps("psO", [P, S]))
        loaded, ctx_loaded = sem("loaded"), [sem("ctx_loaded0"), sem("ctx_loaded1")]
        names = ("dve_chain", "moments", "rstd", "h_ready", "turned", "hT_ready", "q_ready", "qT_ready", "ctx_turned", "ctxT_ready",
                 "c_ready", "k_ready", "kT_ready", "vp_ready", "v_ready", "s_ready", "negm_ready", "exp_ready", "p_turned",
                 "prT_ready", "o_ready", "oT_ready", "y_ready", "x_done")
        (dve_chain, moments, rstd, h_ready, turned, hT_ready, q_ready, qT_ready, ctx_turned, ctxT_ready,
         c_ready, k_ready, kT_ready, vp_ready, v_ready, s_ready, negm_ready, exp_ready, p_turned,
         prT_ready, o_ready, oT_ready, y_ready, x_done) = (sem(n) for n in names)
        block = es.enter_context(nc.Block())
        NLOAD = 12 if inner_norm else 8
        NMOM = 3 if inner_norm else 1

        @block.sync
        def _(sp):
            col = lambda a: a.rearrange("(d a) -> d a", a=1)
            loads = [(wq[:], d[f"{pre}_Wq"]), (wk[:], d[f"{pre}_Wk"]), (wv[:], d[f"{pre}_Wv"]), (wo[:], d[f"{pre}_Wo"]),
                     (bq[:], col(d[f"{pre}_bq"])), (bk[:], col(d[f"{pre}_bk"])),
                     (bv[:], rows(d[f"{pre}_bv"]).to_broadcast((P, D))), (bo[:], rows(d[f"{pre}_bo"]).to_broadcast((P, D)))]
            if inner_norm:
                loads += [(g1[:], col(d[f"{pre}_ln1_g"])), (b1[:], col(d[f"{pre}_ln1_b"])),
                          (g2[:], col(d[f"{pre}_ln2_g"])), (b2[:], col(d[f"{pre}_ln2_b"]))]
            for dst, src in loads:
                sp.dma_start(dst, src).then_inc(loaded, 16)
            for b in range(B):
                if inner_norm:
                    wait(sp, ctx_turned, b - 1)
                    sp.dma_start(ctx[:, b % 2], d["ctx_rows"][b].rearrange("(t p) c -> p t c", p=P)).then_inc(ctx_loaded[b % 2], 16)
                else:
                    wait(sp, vp_ready, b - 1)
                    sp.dma_start(ctxT[:, b % 2], d["ctx_768"][b]).then_inc(ctx_loaded[b % 2], 16)

        @block.gpsimd
        def _(pool):
            for b in range(B):
                for n, ww in enumerate((w, w1, w2)[:NMOM]):
                    pool.wait_ge(moments, NMOM * b + n + 1)
                    pool_rsqrt(nc, m, ww, ww.n).then_inc(rstd, 1)

        @block.vector
        def _(dve):
            link = Links(dve, dve_chain)
            dve.wait_ge(loaded, 16 * NLOAD)
            link(nc.vector.tensor_scalar(bq[:], bq[:], scale, None, ALU.mult))

            def normed(dst, src, ww):
                for t in range(ww.n):
                    ins = nc.vector.tensor_scalar(dst[t], src[t], ww.mean[:, t:t + 1], ww.rstd[:, t:t + 1], ALU.subtract, ALU.mult)
                    if t < ww.n - 1:
                        link.mark(ins)
                return ins

            for b in range(B):
                xs, hs = [m.x[:, b, t] for t in range(TB)], [h[:, t] for t in range(TB)]
                dve_moments(nc, link, w, xs, D, LN_EPS).then_inc(moments, 1)
                dve.wait_ge(rstd, NMOM * b + 1)
                wait(dve, turned, b)
                if inner_norm:
                    link(normed(hs, xs, w))
                    dve_moments(nc, link, w1, hs, D, LN_EPS).then_inc(moments, 1)
                    dve.wait_ge(rstd, NMOM * b + 2)
                    normed(hs, hs, w1).then_inc(h_ready, 1)
                    dve.wait_ge(ctx_loaded[b % 2], 16 * (b // 2 + 1))
                    cs = [ctx[:, b % 2, t] for t in range(KT)]
                    dve_moments(nc, link, w2, cs, DK, LN_EPS).then_inc(moments, 1)
                    dve.wait_ge(rstd, NMOM * b + 3)
                    normed(cs, cs, w2).then_inc(c_ready, 1)
                else:
                    normed(hs, xs, w).then_inc(h_ready, 1)
                dve.wait_ge(vp_ready, b + 1)
                nc.vector.tensor_tensor(v[:], psV[:], bv[:, None, :].to_broadcast((P, KT, D)), ALU.add).then_inc(v_ready, 1)
                dve.wait_ge(s_ready, b + 1)
                link(nc.vector.reduce_max(mx[:], psS[:], AX.X))
                nc.vector.tensor_scalar(negm[:], mx[:], -1.0, None, ALU.mult).then_inc(negm_ready, 1)
                dve.wait_ge(p_turned, b + 1)
                nc.vector.tensor_copy(prT[:], psP[:]).then_inc(prT_ready, 1)
                dve.wait_ge(exp_ready, TB * (b + 1))
                link(nc.vector.reciprocal(rinv[:], rsum[:]))
                dve.wait_ge(y_ready, b + 1)
                for t in range(TB):
                    link.mark(nc.vector.scalar_tensor_tensor(y[:, t], psA[:, t * D:(t + 1) * D], rinv[:, t:t + 1], bo[:], ALU.mult, ALU.add))
                link.wait()
                nc.vector.tensor_tensor(m.x[:, b], m.x[:, b], y[:], ALU.add).then_inc(x_done, 1)

        @block.tensor
        def _(pe):
            pe.wait_ge(loaded, 16 * NLOAD)
            for b in range(B):
                pe.wait_ge(h_ready, b + 1)
                wait(pe, x_done, b)
                for t in range(TB):
                    ins = nc.tensor.transpose(psA[:, t * P:(t + 1) * P], h[:, t], m.ident[:])
                ins.then_inc(turned, 1)
                if inner_norm:
                    pe.wait_ge(c_ready, b + 1)
                    for t in range(KT):
                        ins = nc.tensor.transpose(psK[0:DK, t * P:(t + 1) * P], ctx[:, b % 2, t], m.ident[:])
                    ins.then_inc(ctx_turned, 1)
                    pe.wait_ge(ctxT_ready, b + 1)
                else:
                    pe.wait_ge(ctx_loaded[b % 2], 16 * (b // 2 + 1))
                src = ctxT[:, b % 2]
                pe.wait_ge(hT_ready, b + 1)
                nc.tensor.matmul(psA[:, 0:S], wq[:], hT[:], start=True, stop=True).then_inc(q_ready, 1)
                nc.tensor.matmul(psK[:], wk[:], src, start=True, stop=True).then_inc(k_ready, 1)
                for t in range(KT):
                    ins = nc.tensor.matmul(psV[:, t], src[:, t * P:(t + 1) * P], wv[:], start=True, stop=True)
                ins.then_inc(vp_ready, 1)
                pe.wait_ge(qT_ready, b + 1)
                pe.wait_ge(kT_ready, b + 1)
                for t in range(TB):
                    ins = nc.tensor.matmul(psS[:, t], qT[:, t * P:(t + 1) * P], kT[:], start=True, stop=True)
                ins.then_inc(s_ready, 1)
                pe.wait_ge(exp_ready, TB * (b + 1))
                for k in range(KT):
                    for t in range(TB):
                        ins = nc.tensor.transpose(psP[:, k, t * P:(t + 1) * P], pr[:, t, k * P:(k + 1) * P], m.ident[:])
                ins.then_inc(p_turned, 1)
                pe.wait_ge(prT_ready, b + 1)
                pe.wait_ge(v_ready, b + 1)
                for k in range(KT):
                    ins = nc.tensor.matmul(psO[:], v[:, k], prT[:, k], start=(k == 0), stop=(k == KT - 1))
                ins.then_inc(o_ready, 1)
                pe.wait_ge(oT_ready, b + 1)
                for t in range(TB):
                    ins = nc.tensor.matmul(psA[:, t * D:(t + 1) * D], oT[:, t * P:(t + 1) * P], wo[:], start=True, stop=True)
                ins.then_inc(y_ready, 1)

        @block.scalar
        def _(act):
            act.wait_ge(dve_chain, 1)
            act.wait_ge(loaded, 16 * NLOAD)
            for b in range(B):
                act.wait_ge(turned, b + 1)
                if inner_norm:
                    nc.scalar.activation(hT[:], psA[:, 0:S], ACT.Identity, bias=b1[:], scale=g1[:]).then_inc(hT_ready, 1)
                    act.wait_ge(ctx_turned, b + 1)
                    nc.scalar.activation(ctxT[:, b % 2], psK[0:DK], ACT.Identity, bias=b2[:], scale=g2[:]).then_inc(ctxT_ready, 1)
                else:
                    nc.scalar.copy(hT[:], psA[:, 0:S]).then_inc(hT_ready, 1)
                act.wait_ge(q_ready, b + 1)
                nc.scalar.activation(qT[:], psA[:, 0:S], ACT.Identity, bias=bq[:], scale=scale).then_inc(qT_ready, 1)
                act.wait_ge(k_ready, b + 1)
                nc.scalar.activation(kT[:], psK[:], ACT.Identity, bias=bk[:]).then_inc(kT_ready, 1)
                act.wait_ge(negm_ready, b + 1)
                for t in range(TB):
                    nc.scalar.activation(pr[:, t], psS[:, t], ACT.Exp, bias=negm[:, t:t + 1], accum_out=rsum[:, t:t + 1]).then_inc(exp_ready, 1)
                act.wait_ge(o_ready, b + 1)
                nc.scalar.copy(oT[:], psO[:]).then_inc(oT_ready, 1)


def l1_attn(m):
    layer_attention_heads8(m, "L1_attn", "L1_attn_Wq", "L1_attn_Wk", "L1_attn_Wk", "L1_attn_Wo", None, None, None,
                           "L1_attn_bo", S, float(D) ** -0.5, False)


def l0_xattn(m):
    w = {v: f"L0_xattn_{v}" for v in ("Wq", "Wk", "Wv", "Wo", "bq", "bk", "bv", "bo")}
    layer_attention_heads8(m, "L0_xattn", w["Wq"], w["Wk"], w["Wv"], w["Wo"], w["bq"], w["bk"], w["bv"], w["bo"],
                           SK, 8 ** -0.5, True)


def l3_xattn(m):
    p = "L3_xattn_"
    layer_attention_heads8(m, "L3_xattn", p + "q_w", p + "v_w", p + "v_w", p + "o_w", p + "q_b", p + "v_b", p + "v_b", p + "o_b",
                           SK, 8 ** -0.5, True, head_major=True)


STACK = {8: lambda m: layer_selected_experts(m, "L2_ffn"), 6: lambda m: layer_attention_heads64(m, "L2_attn", True), 9: lambda m: layer_attention_heads64(m, "L3_attn", False),
         0: lambda m: layer_gated_recurrence(m, "L0_attn"), 2: lambda m: layer_moe_top8(m, "L0_ffn"), 4: lambda m: layer_attention_single(m, "L1_xattn", 0.25, False), 7: lambda m: layer_attention_single(m, "L2_xattn", float(D) ** -0.5, True),
         5: lambda m: layer_fp4_mlp(m, "L1_ffn"), 11: lambda m: layer_sign_linear(m, "L3_ffn"), 3: l1_attn, 1: l0_xattn, 10: l3_xattn}


HOST_TRANSPOSED = {"L3_ffn_weights", "L3_xattn_q_w", "L3_xattn_v_w", "L3_xattn_o_w", "L0_attn_in_proj_w",
                   "L0_attn_out_proj_w", "L0_attn_fc_w", "L0_attn_proj_w", "L0_ffn_centroids", "L2_ffn_sw1", "L2_ffn_sw2",
                   "L2_ffn_sw3", "L2_ffn_sg_w", "L2_ffn_eg_w", "L3_attn_w_down_q", "L3_attn_w_down_kv", "L3_attn_w_up_q",
                   "L3_attn_w_up_k", "L3_attn_w_up_v", "L3_attn_w_out"}


def build(nc, dram, out):
    with ExitStack() as ctx:
        m = Model(nc, dram, out, ctx)
        setup(m)
        for n in LAYERS:
            STACK[n](m)
        finish(m)


def rotary_tables(tokens, width):
    inv = 1.0 / 10000.0 ** (np.arange(0, width, 2, dtype=np.float32) / width)
    angle = np.outer(np.arange(tokens, dtype=np.float32), inv)
    pick = lambda v: np.concatenate([v, v], -1)[:, ::2]
    cos, sin = (np.repeat(pick(f(angle)).T, 2, axis=0).astype(np.float32) for f in (np.cos, np.sin))
    sign = np.where(np.arange(width) % 2 == 0, -1.0, 1.0).astype(np.float32)[:, None]
    return np.tile(cos, (2, 1)), np.tile(sin * sign, (2, 1))


def kernel(**inputs):
    import concourse.bacc as bacc
    from concourse.bass_utils import run_bass_kernel_spmd as run

    nc = bacc.Bacc("TRN2", target_bir_lowering=False, num_devices=1)
    arrays, dram = {}, {}
    for name, value in inputs.items():
        a = np.asarray(value)
        if name in HOST_TRANSPOSED:
            a = a.T
        if name == "ctx_768":
            dram["ctx_rows"] = nc.dram_tensor("in_ctx_rows", a.shape, mybir.dt.from_np(a.dtype), kind="ExternalInput").ap()
            arrays["in_ctx_rows"] = np.ascontiguousarray(a)
        if name == "ctx_768" or name in ("L2_ffn_ew1", "L2_ffn_ew2", "L2_ffn_ew3"):
            a = a.transpose(0, 2, 1)
        a = np.ascontiguousarray(a)
        arrays[f"in_{name}"] = a
        dram[name] = nc.dram_tensor(f"in_{name}", a.shape, mybir.dt.from_np(a.dtype), kind="ExternalInput").ap()
    def extra(name, a):
        arrays[f"in_{name}"] = a = np.ascontiguousarray(a)
        dram[name] = nc.dram_tensor(f"in_{name}", a.shape, mybir.dt.from_np(a.dtype), kind="ExternalInput").ap()

    for v in "qk":
        a = arrays[f"in_L3_attn_w_up_{v}"]
        extra(f"up_{v}_swapped", a.reshape(a.shape[0], -1, 2)[:, :, ::-1].reshape(a.shape))
    cos, sin = rotary_tables(S, 64)
    extra("rope_cos", cos)
    extra("rope_sin", sin)
    out = nc.dram_tensor("out", (B, S, D), F32, kind="ExternalOutput").ap()
    build(nc, dram, out)
    return run(nc, [arrays], core_ids=[0]).results[0]["out"]
```

```python
import numpy as np
import concourse.bass as bass
from concourse import mybir
from contextlib import ExitStack

F32 = mybir.dt.float32
BF16 = mybir.dt.bfloat16
I32 = mybir.dt.int32
ALU = mybir.AluOpType
ACT = mybir.ActivationFunctionType
AX = mybir.AxisListType

LAYERS = [0, 1, 2, 3, 4, 5, 6, 7, 8, 9, 10, 11]

B, S, D = 8, 256, 128
P = 128
TB = S // P
NT = B * TB
SK, DK = 512, 96
KT = SK // P
LN_EPS = 1e-5


class Links:

    def __init__(self, eng, sem, base=0):
        self.eng, self.sem, self.base, self.n = eng, sem, base, 0

    def mark(self, ins):
        ins.then_inc(self.sem, 1)
        self.n += 1

    def wait(self):
        self.eng.wait_ge(self.sem, self.base + self.n)

    def __call__(self, ins):
        self.mark(ins)
        self.wait()


class Model:

    def __init__(self, nc, dram, out, ctx):
        self.nc, self.dram, self.out, self.ctx = nc, dram, out, ctx
        self.x_stored = ctx.enter_context(nc.semaphore("x_stored"))
        self.x = self.sb("x", [P, B, TB, D], F32)
        self.ident = self.sb("ident", [P, P], F32)
        self.identb = self.sb("identb", [P, P], BF16)
        self.half = self.sb("minus_half", [P, 64], F32)

    def sb(self, name, shape, dt=F32):
        return self.ctx.enter_context(self.nc.sbuf_tensor(name, shape, dt))


def rows(ap):
    return ap.rearrange("(a d) -> a d", a=1)


def setup(m):
    nc = m.nc
    with ExitStack() as es:
        _, _, sem = allocators(nc, es, "setup")
        x_loaded, pool_chain = sem("x_loaded"), sem("pool_chain")
        block = es.enter_context(nc.Block())

        @block.sync
        def _(sp):
            for b in range(B):
                sp.dma_start(m.x[:, b], m.dram["x"][b].rearrange("(t p) d -> p t d", p=P)).then_inc(x_loaded, 16)
            sp.wait_ge(x_loaded, 16 * B)

        @block.gpsimd
        def _(pool):
            link = Links(pool, pool_chain)
            link(nc.gpsimd.memset(m.half[:], -0.5))
            link(nc.gpsimd.memset(m.ident[:], 0.0))
            link(nc.gpsimd.affine_select(out=m.ident[:], in_=m.ident[:], compare_op=ALU.not_equal, fill=1.0,
                                         base=0, pattern=[[-1, P]], channel_multiplier=1))
            link(nc.gpsimd.tensor_copy(m.identb[:], m.ident[:]))


def finish(m):
    nc = m.nc
    x_stored = m.x_stored
    with nc.Block() as block:

        @block.sync
        def _(sp):
            for b in range(B):
                sp.dma_start(m.out[b].rearrange("(t p) d -> p t d", p=P), m.x[:, b]).then_inc(x_stored, 16)
            sp.wait_ge(x_stored, 16 * B)


def wait(eng, sem, count):
    if not isinstance(count, int) or count > 0:
        eng.wait_ge(sem, count)


class Norm:

    def __init__(self, sb, tag="", n=TB):
        self.n = n
        self.stats = sb(f"stats{tag}", [P, n, 6])
        self.s, self.d, self.m2, self.q = (sb(f"{v}{tag}", [P, n]) for v in ("msum", "mdif", "m2", "msq"))
        self.mean, self.veps, self.rstd = (sb(f"{v}{tag}", [P, n]) for v in ("mean", "veps", "rstd"))


def dve_moments(nc, link, w, xs, width, eps):
    for t, x in enumerate(xs):
        link.mark(nc.vector.bn_stats(w.stats[:, t], x))
    link.wait()
    n = len(xs)
    me, mo, ve, vo = w.stats[:, 0:n, 1], w.stats[:, 0:n, 4], w.stats[:, 0:n, 2], w.stats[:, 0:n, 5]
    link.mark(nc.vector.tensor_tensor(w.s[:, 0:n], me, mo, ALU.add))
    link.mark(nc.vector.tensor_tensor(w.d[:, 0:n], me, mo, ALU.subtract))
    link(nc.vector.tensor_tensor(w.m2[:, 0:n], ve, vo, ALU.add))
    link.mark(nc.vector.tensor_scalar(w.mean[:, 0:n], w.s[:, 0:n], 0.5, None, ALU.mult))
    link.mark(nc.vector.tensor_tensor(w.q[:, 0:n], w.d[:, 0:n], w.d[:, 0:n], ALU.mult))
    link(nc.vector.tensor_scalar(w.m2[:, 0:n], w.m2[:, 0:n], 1.0 / width, eps, ALU.mult, ALU.add))
    return nc.vector.scalar_tensor_tensor(w.veps[:, 0:n], w.q[:, 0:n], 0.25, w.m2[:, 0:n], ALU.mult, ALU.add)


def dve_square_mean(nc, link, w, xs, width, eps):
    for t, x in enumerate(xs):
        link.mark(nc.vector.bn_stats(w.stats[:, t], x))
    link.wait()
    n = len(xs)
    me, mo, ve, vo = w.stats[:, 0:n, 1], w.stats[:, 0:n, 4], w.stats[:, 0:n, 2], w.stats[:, 0:n, 5]
    link.mark(nc.vector.tensor_tensor(w.s[:, 0:n], me, me, ALU.mult))
    link.mark(nc.vector.tensor_tensor(w.d[:, 0:n], mo, mo, ALU.mult))
    link(nc.vector.tensor_tensor(w.m2[:, 0:n], ve, vo, ALU.add))
    link.mark(nc.vector.tensor_tensor(w.q[:, 0:n], w.s[:, 0:n], w.d[:, 0:n], ALU.add))
    link(nc.vector.tensor_scalar(w.m2[:, 0:n], w.m2[:, 0:n], 1.0 / width, eps, ALU.mult, ALU.add))
    return nc.vector.scalar_tensor_tensor(w.veps[:, 0:n], w.q[:, 0:n], 0.5, w.m2[:, 0:n], ALU.mult, ALU.add)


def pool_rsqrt(nc, m, w, n=TB):
    return nc.gpsimd.tensor_tensor(w.rstd[:, 0:n], w.veps[:, 0:n], m.half[:, 0:n], ALU.pow)


def allocators(nc, es, pre):
    sems = []

    def clear():
        nc.clear_and_free_semaphores(sems)
        nc.all_engine_barrier()

    es.callback(clear)

    def sem(name):
        sems.append(nc.alloc_semaphore(name=f"{pre}_{name}"))
        return sems[-1]

    sb = lambda name, shape, dt=F32: es.enter_context(nc.sbuf_tensor(f"{pre}_{name}", shape, dt))
    ps = lambda name, shape, dt=F32: es.enter_context(nc.psum_tensor(f"{pre}_{name}", shape, dt))
    return sb, ps, sem


def layer_attention_heads64(m, pre, causal):
    nc = m.nc
    d = m.dram
    H, DH, NPAIR, LAT = 16, 64, 8, 64
    VW = DH + 1
    EPS_SUM = 1e-8 if causal else 0.0
    SCALE = DH ** -0.5
    with ExitStack() as es:
        sb, ps, sem = allocators(nc, es, pre)
        KW = D if causal else LAT
        wq, wk, wv = sb("wq", [P, H * DH]), sb("wk", [P, H * DH]), sb("wv", [P, H * DH])
        if not causal:
            wqs, wks = sb("wqs", [P, H * DH]), sb("wks", [P, H * DH])
            wdq, wdkv, gain, shift = sb("wdq", [P, LAT]), sb("wdkv", [P, LAT]), sb("gain", [P, 1]), sb("shift", [P, 1])
            cosT, sinT = sb("cosT", [P, S]), sb("sinT", [P, S])
            cT, w2 = sb("cT", [P, 2, S]), Norm(sb, "2")
            rotc, rots = ([sb(f"{v}{i}", [P, 2, S]) for i in range(2)] for v in ("rotc", "rots"))
        wo = sb("wo", [P, NPAIR, D])
        bo = sb("bo", [P, D]) if causal else None
        mask = sb("mask", [P, P]) if causal else None
        w = Norm(sb)
        h, hi, hT = [sb(f"hn{i}", [P, TB, D]) for i in range(3)], sb("hi", [P, TB, D]), sb("hT", [P, S])
        qT, kT = [sb(f"q{i}", [P, H, S]) for i in range(2)], [sb(f"k{i}", [P, NPAIR, S]) for i in range(2)]
        V = [sb(f"V{i}", [P, TB, H, VW]) for i in range(2)]
        mx, negm = sb("mx", [P, 4, TB]), sb("negm", [P, 4, TB])
        pr = [sb(f"pr{i}", [P, TB, S]) for i in range(3)]
        prT = [sb(f"prT{i}", [P, 2 * S]) for i in range(3)]
        ao, aoT, rinv = [sb(f"ao{i}", [P, TB, H, DH]) for i in range(2)], sb("aoT", [P, NPAIR, S]), sb("rinv", [P, 4])
        y = sb("y", [P, TB, D])
        psA = [ps(f"psA{i}", [P, 2, S]) for i in range(2)]
        psS, psO = ([ps(f"{v}{i}", [P, TB, S]) for i in range(2)] for v in ("psS", "psO"))
        psT = [ps(f"psT{i}", [P, 2 * S]) for i in range(2)]
        names = ("loaded", "consts", "pool_chain", "dve_chain", "moments", "rstd", "h_ready",
                 "proj_ready", "rotated", "s_ready", "negm_ready", "exp_ready", "masked", "p_turned", "prT_ready", "pv_done",
                 "ao_ready", "x_added")
        (loaded, consts, pool_chain, dve_chain, moments, rstd, h_ready,
         proj_ready, rotated, s_ready, negm_ready, exp_ready, masked, p_turned, prT_ready, pv_done,
         ao_ready, x_added) = (sem(n) for n in names)
        bank_read = [sem(f"bank_read{i}") for i in range(2)]
        block = es.enter_context(nc.Block())
        NMOM = 1 if causal else 2
        NQK = NPAIR * (1 if causal else 2)
        NV = TB * 2
        NPJ = NQK + NV
        LT, LV, LN_ = 2, 3, 4
        NH = B * H
        FIRST_P, FIRST_A, SLOT_O = 3, LN_ + 1, LN_ + 6

        def prep_jobs(b):
            return [("T", b, 0)] + ([] if causal else [("C", b, 0)]) + [("P", b, j) for j in range(NPJ)]

        slots = [[] for _ in range(NH + H)]
        for b in range(B):
            if b + 1 < B:
                heads = prep_jobs(b + 1)
                slots[b * H + 1].append(heads.pop(0))
                if not causal:
                    slots[b * H + 2].append(heads.pop(0))
                for j, job in enumerate(heads):
                    slots[b * H + FIRST_P + j * (H - FIRST_P) // NPJ].append(job)
            for q in range(4):
                slots[(b + 1) * H + FIRST_A + q].append(("A", b, q))
            slots[(b + 1) * H + SLOT_O].append(("O", b, 0))
        place = {job: n for n, job in enumerate(prep_jobs(0) + [job for jobs in slots for job in jobs])}

        def await_read(eng, job):
            n = place[job]
            eng.wait_ge(bank_read[n % 2], n // 2 + 1)

        def await_bank(eng, job):
            n = place[job]
            wait(eng, bank_read[n % 2], n // 2)

        blocks = [(0, 0), (0, 1), (1, 1)] if causal else [(0, 0), (0, 1), (1, 0), (1, 1)]
        WB = len(blocks) * P
        loads = []
        if causal:
            loads = [(wq[:], d[f"{pre}_Wq"]), (wk[:], d[f"{pre}_Wkv"][:, 0:H * DH]), (wv[:], d[f"{pre}_Wkv"][:, H * DH:2 * H * DH]),
                     (wo[:], d[f"{pre}_Wo"].rearrange("(n p) c -> p n c", p=P)), (bo[:], rows(d[f"{pre}_bo"]).to_broadcast((P, D)))]
        else:
            loads = [(wq[0:KW], d[f"{pre}_w_up_q"]), (wk[0:KW], d[f"{pre}_w_up_k"]), (wv[0:KW], d[f"{pre}_w_up_v"]),
                     (wo[:], d[f"{pre}_w_out"].rearrange("(n p) c -> p n c", p=P)),
                     (wqs[0:KW], d["up_q_swapped"]), (wks[0:KW], d["up_k_swapped"]), (wdq[:], d[f"{pre}_w_down_q"]), (wdkv[:], d[f"{pre}_w_down_kv"]),
                     (gain[:], d[f"{pre}_ln_scale"].rearrange("(d a) -> d a", a=1)), (shift[:], d[f"{pre}_ln_bias"].rearrange("(d a) -> d a", a=1)),
                     (cosT[:], d["rope_cos"]), (sinT[:], d["rope_sin"])]

        @block.sync
        def _(sp):
            for dst, src in loads:
                sp.dma_start(dst, src).then_inc(loaded, 16)

        @block.gpsimd
        def _(pool):
            link = Links(pool, pool_chain)
            for i in range(2):
                link(nc.gpsimd.memset(V[i][:], 1.0))
                for r in range(2):
                    rest = qT[i][(1 - r) * DH:(2 - r) * DH].rearrange("p (n r) c -> p n r c", r=2)[:, :, r]
                    link(nc.gpsimd.memset(rest, 0.0))
            if not causal:
                for z in (wq, wk, wv, wqs, wks, cT):
                    link(nc.gpsimd.memset(z[LAT:], 0.0))
                nc.gpsimd.sem_inc(consts, 1)
            if causal:
                link(nc.gpsimd.memset(mask[:], 1.0))
                nc.gpsimd.affine_select(out=mask[:], in_=mask[:], compare_op=ALU.is_ge, fill=0.0, base=0,
                                        pattern=[[-1, P]], channel_multiplier=1).then_inc(consts, 1)

            def prep(b):
                pool.wait_ge(moments, NMOM * b + 1)
                pool_rsqrt(nc, m, w).then_inc(rstd, 1)
                if not causal:
                    pool.wait_ge(moments, NMOM * b + 2)
                    pool_rsqrt(nc, m, w2).then_inc(rstd, 1)

            def rotate(b):
                for j in range(NPAIR):
                    n = b * NPAIR + j
                    await_read(pool, ("P", b, 2 * j))
                    await_read(pool, ("P", b, 2 * j + 1))
                    wait(pool, pv_done, H * (b - 1))
                    for r in range(2):
                        c = slice(r * DH, (r + 1) * DH)
                        link(nc.gpsimd.tensor_tensor(qT[b % 2][c, 2 * j + r], rotc[j % 2][c, 0], rots[j % 2][c, 0], ALU.add))
                    link(nc.gpsimd.tensor_tensor(kT[b % 2][:, j], rotc[j % 2][:, 1], rots[j % 2][:, 1], ALU.add))
                    nc.gpsimd.sem_inc(rotated, 1)

            def mask_probs(n):
                pool.wait_ge(exp_ready, n + 1)
                for t in range(TB):
                    z = pr[n % 3][:, t, t * P:(t + 1) * P]
                    nc.gpsimd.tensor_tensor(z, z, mask[:], ALU.mult).then_inc(masked, 1)

            if causal:
                pool.wait_ge(consts, 1)
            prep(0)
            if not causal:
                rotate(0)
            for b in range(B):
                if b + 1 < B:
                    prep(b + 1)
                    if not causal:
                        rotate(b + 1)
                if causal:
                    for hd in range(H):
                        mask_probs(b * H + hd)

        @block.vector
        def _(dve):
            link = Links(dve, dve_chain)
            dve.wait_ge(loaded, 16 * len(loads))
            dve.wait_ge(consts, 1)

            def norm(b):
                xs, hs = [m.x[:, b, t] for t in range(TB)], [h[b % 3][:, t] for t in range(TB)]
                dve_moments(nc, link, w, xs, D, LN_EPS).then_inc(moments, 1)
                dve.wait_ge(rstd, NMOM * b + 1)
                if b >= 1:
                    await_read(dve, ("T", b - 1, 0))
                if not causal and b >= 3:
                    dve.wait_ge(x_added, b - 2)
                for t in range(TB):
                    ins = nc.vector.tensor_scalar(hs[t], xs[t], w.mean[:, t:t + 1], w.rstd[:, t:t + 1], ALU.subtract, ALU.mult)
                    if causal:
                        ins.then_inc(h_ready, 1)
                    else:
                        link.mark(ins)
                if not causal:
                    link.wait()
                    dve_moments(nc, link, w2, hs, D, LN_EPS).then_inc(moments, 1)
                    dve.wait_ge(rstd, NMOM * b + 2)
                    for t in range(TB):
                        nc.vector.tensor_scalar(hi[:, t], hs[t], w2.mean[:, t:t + 1], w2.rstd[:, t:t + 1], ALU.subtract, ALU.mult).then_inc(h_ready, 1)

            def read(job):
                kind, b, j = job
                bank, free = psA[place[job] % 2], bank_read[place[job] % 2]
                if not (kind == "O" or kind == "P" and (j >= NQK or not causal)):
                    return
                dve.wait_ge(proj_ready, place[job] + 1)
                if kind == "O":
                    other = bo[:, None, :].to_broadcast((P, TB, D)) if causal else h[b % 3][:]
                    nc.vector.tensor_tensor(y[:], bank[:, 0].rearrange("p (t d) -> p t d", t=TB), other, ALU.add).then_inc(free, 1)
                    await_read(dve, job)
                    nc.vector.tensor_tensor(m.x[:, b], m.x[:, b], y[:], ALU.add).then_inc(x_added, 1)
                elif j < NQK:
                    pair, swapped = j // 2, j % 2
                    wait(dve, rotated, b * NPAIR + pair - 1)
                    dst, tab = (rots[pair % 2], sinT) if swapped else (rotc[pair % 2], cosT)
                    nc.vector.tensor_tensor(dst[:], bank[:], tab[:, None, :].to_broadcast((P, 2, S)), ALU.mult).then_inc(free, 1)
                else:
                    t, half = (j - NQK) // 2, (j - NQK) % 2
                    wait(dve, pv_done, H * (b - 1))
                    nc.vector.tensor_copy(V[b % 2][:, t, half * 8:half * 8 + 8, 0:DH],
                                          bank[:].rearrange("p a (c e) -> p (a c) e", e=DH)).then_inc(free, 1)

            def maximum(n):
                dve.wait_ge(s_ready, n + 1)
                wait(dve, exp_ready, n - 3)
                link(nc.vector.reduce_max(mx[:, n % 4], psS[n % 2][:], AX.X))
                nc.vector.tensor_scalar(negm[:, n % 4], mx[:, n % 4], -SCALE, None, ALU.mult).then_inc(negm_ready, 1)

            def copy_turned(n):
                dve.wait_ge(p_turned, n + 1)
                wait(dve, pv_done, n - 2)
                nc.vector.tensor_copy(prT[n % 3][:, 0:WB], psT[n % 2][:, 0:WB]).then_inc(prT_ready, 1)

            def normalise(n):
                b, hd = n // H, n % H
                dve.wait_ge(pv_done, n + 1)
                if hd == 0 and b >= 2:
                    await_read(dve, ("A", b - 2, 2))
                    await_read(dve, ("A", b - 2, 3))
                r = rinv[:, 2 * (n % 2):2 * (n % 2) + 2]
                link(nc.vector.tensor_scalar(r, psO[n % 2][:, :, DH], EPS_SUM, None, ALU.add))
                link(nc.vector.reciprocal(r, r))
                nc.vector.tensor_tensor(ao[b % 2][:, :, hd], psO[n % 2][:, :, 0:DH], r[:, :, None].to_broadcast((P, TB, DH)), ALU.mult).then_inc(ao_ready, 1)

            norm(0)
            for job in prep_jobs(0):
                read(job)
            for n in range(NH + H):
                if n % H == 0 and n // H + 1 < B:
                    norm(n // H + 1)
                if n < NH:
                    maximum(n)
                if 0 <= n - LT < NH:
                    copy_turned(n - LT)
                for job in slots[n]:
                    read(job)
                if 0 <= n - LN_ < NH:
                    normalise(n - LN_)

        @block.tensor
        def _(pe):
            pe.wait_ge(loaded, 16 * len(loads))
            pe.wait_ge(consts, 1)

            def run(job):
                kind, b, j = job
                bank = psA[place[job] % 2]
                if kind == "T":
                    pe.wait_ge(h_ready, TB * (b + 1))
                elif kind == "A" and j == 0:
                    pe.wait_ge(ao_ready, H * (b + 1))
                elif kind == "C" or kind == "P" and j == 0:
                    await_read(pe, ("T", b, 0) if kind == "C" or causal else ("C", b, 0))
                elif kind == "O":
                    await_read(pe, ("A", b, 2))
                    await_read(pe, ("A", b, 3))
                await_bank(pe, job)
                if kind == "T":
                    src = h[b % 3] if causal else hi
                    for t in range(TB):
                        ins = nc.tensor.transpose(bank[:, 0, t * P:(t + 1) * P], src[:, t], m.ident[:])
                elif kind == "C":
                    nc.tensor.matmul(bank[0:LAT, 0], wdq[:], hT[:], start=True, stop=True)
                    ins = nc.tensor.matmul(bank[0:LAT, 1], wdkv[:], hT[:], start=True, stop=True)
                elif kind == "P" and j < NQK:
                    pair = j if causal else j // 2
                    c = slice(pair * P, (pair + 1) * P)
                    mats = (wq, wk) if causal or j % 2 == 0 else (wqs, wks)
                    for i, mat in enumerate(mats):
                        ins = nc.tensor.matmul(bank[:, i], mat[:, c], hT[:] if causal else cT[:, i], start=True, stop=True)
                elif kind == "P":
                    t, half = (j - NQK) // 2, (j - NQK) % 2
                    lhs = hT[:, t * P:(t + 1) * P] if causal else cT[:, 1, t * P:(t + 1) * P]
                    ins = nc.tensor.matmul(bank[:].rearrange("p a c -> p (a c)"), lhs, wv[:, half * 512:(half + 1) * 512], start=True, stop=True)
                elif kind == "A":
                    for i in range(2):
                        for t in range(TB):
                            pair = 2 * j + i
                            ins = nc.tensor.transpose(bank[:, i, t * P:(t + 1) * P], ao[b % 2][:, t, 2 * pair:2 * pair + 2].rearrange("p h e -> p (h e)"), m.ident[:])
                else:
                    for t in range(TB):
                        for pair in range(NPAIR):
                            ins = nc.tensor.matmul(bank[:, 0, t * D:(t + 1) * D], aoT[:, pair, t * P:(t + 1) * P], wo[:, pair], start=(pair == 0), stop=(pair == NPAIR - 1))
                ins.then_inc(proj_ready, 1)

            def scores(n):
                b, hd = n // H, n % H
                wait(pe, exp_ready, n - 1)
                if hd == 0:
                    if causal:
                        await_read(pe, ("P", b, NQK - 2))
                        await_read(pe, ("P", b, NQK - 1))
                        pe.wait_ge(rotated, 2 * NQK * (b + 1))
                    else:
                        pe.wait_ge(rotated, NPAIR * (b + 1))
                for t in range(TB):
                    ins = nc.tensor.matmul(psS[n % 2][:, t], qT[b % 2][:, hd, t * P:(t + 1) * P], kT[b % 2][:, hd // 2], start=True, stop=True)
                ins.then_inc(s_ready, 1)

            def turn_probs(n):
                if causal:
                    pe.wait_ge(masked, TB * (n + 1))
                else:
                    pe.wait_ge(exp_ready, n + 1)
                wait(pe, prT_ready, n - 1)
                for i, (k, t) in enumerate(blocks):
                    ins = nc.tensor.transpose(psT[n % 2][:, i * P:(i + 1) * P], pr[n % 3][:, t, k * P:(k + 1) * P], m.ident[:])
                ins.then_inc(p_turned, 1)

            def values(n):
                b, hd = n // H, n % H
                pe.wait_ge(prT_ready, n + 1)
                if hd == 0:
                    await_read(pe, ("P", b, NPJ - 2))
                    await_read(pe, ("P", b, NPJ - 1))
                wait(pe, ao_ready, n - 1)
                for t in range(TB):
                    mine = [(i, k) for i, (k, tt) in enumerate(blocks) if tt == t]
                    for i, k in mine:
                        ins = nc.tensor.matmul(psO[n % 2][:, t, 0:VW], prT[n % 3][:, i * P:(i + 1) * P], V[b % 2][:, k, hd], start=(i == mine[0][0]), stop=(i == mine[-1][0]))
                ins.then_inc(pv_done, 1)

            for job in prep_jobs(0):
                run(job)
            for n in range(NH + H):
                if n < NH:
                    scores(n)
                if 0 <= n - LT < NH:
                    turn_probs(n - LT)
                for job in slots[n]:
                    run(job)
                if 0 <= n - LV < NH:
                    values(n - LV)

        @block.scalar
        def _(act):
            act.wait_ge(loaded, 16 * len(loads))
            act.wait_ge(consts, 1)

            def read(job):
                kind, b, j = job
                bank, free = psA[place[job] % 2], bank_read[place[job] % 2]
                if kind == "O" or kind == "P" and (j >= NQK or not causal):
                    return
                act.wait_ge(proj_ready, place[job] + 1)
                if kind == "T":
                    if causal:
                        nc.scalar.copy(hT[:], bank[:, 0]).then_inc(free, 1)
                    else:
                        nc.scalar.activation(hT[:], bank[:, 0], ACT.Identity, bias=shift[:], scale=gain[:]).then_inc(free, 1)
                elif kind == "C":
                    nc.scalar.copy(cT[0:LAT], bank[0:LAT]).then_inc(free, 1)
                elif kind == "P":
                    wait(act, pv_done, H * (b - 1))
                    for r in range(2):
                        c = slice(r * DH, (r + 1) * DH)
                        nc.scalar.copy(qT[b % 2][c, 2 * j + r], bank[c, 0]).then_inc(rotated, 1)
                    nc.scalar.copy(kT[b % 2][:, j], bank[:, 1]).then_inc(free, 1)
                else:
                    nc.scalar.copy(aoT[:, 2 * j:2 * j + 2], bank[:]).then_inc(free, 1)

            def exps(n):
                act.wait_ge(negm_ready, n + 1)
                wait(act, p_turned, n - 2)
                for t in range(TB):
                    width = (t + 1) * P if causal else S
                    ins = nc.scalar.activation(pr[n % 3][:, t, 0:width], psS[n % 2][:, t, 0:width], ACT.Exp, bias=negm[:, n % 4, t:t + 1], scale=SCALE)
                ins.then_inc(exp_ready, 1)

            for job in prep_jobs(0):
                read(job)
            for n in range(NH + H):
                if n < NH:
                    exps(n)
                for job in slots[n]:
                    read(job)


def layer_attention_heads8(m, pre, wq, wk, wv, wo, bq, bk, bv, bo, keys, scale, from_ctx, head_major=False, clamp=None):
    nc = m.nc
    H, DH = 16, 8
    PARTS = 3
    PAIR = PARTS * PARTS * DH
    MAXROW = 96
    NKT = keys // P
    NU = NKT // 2
    HG, HW = 4, 32
    NG = H // HG
    CK = DK if from_ctx else D
    SPB = keys // 256
    NREG = 2 * PARTS * PARTS
    k_on_dve = keys == S
    LW = 1
    NPS, NPT = 3, 6
    NSU = H * SPB
    LAST_S = 12
    T_H, T_Q, T_K, T_V, T_O, T_Y, T_M = 2, 3, 4, 5, 8, 9, 12
    s_until = [min(NSU, -(-(hd + 1) * NSU // LAST_S)) for hd in range(H)]
    s_units = [list(range(s_until[hd - 1] if hd else 0, s_until[hd])) for hd in range(H)]
    with ExitStack() as es:
        sb, ps, sem = allocators(nc, es, pre)
        wq_s, wk_s, wv_s, wo_s = sb("wq", [P, D]), sb("wk", [CK, D]), sb("wv", [CK, D]), sb("wo", [P, D])
        bq_s, bk_s = sb("bq", [P, 1]), sb("bk", [P, 1])
        bv_s, bo_s = sb("bv", [P, D]), sb("bo", [P, D])
        ctxT = sb("ctxT", [CK, 2, keys]) if from_ctx else None
        w = Norm(sb)
        h, hT = sb("h", [P, TB, D]), sb("hT", [P, S])
        qf, kf = sb("qf", [P, S]), sb("kf", [P, keys])
        qs, ks = sb("qs", [P, PARTS, S], BF16), sb("ks", [P, PARTS, keys], BF16)
        QR = [sb(f"QR{i}", [P, H, S], BF16) for i in range(3)]
        KR = [sb(f"KR{i}", [P, H, keys], BF16) for i in range(3)]
        V = [sb(f"V{i}", [P, NKT, H, HW]) for i in range(3)]
        mx = sb("mx", [P, TB, H])
        negm, mp = sb("negm", [H, S]), sb("mp", [H, PARTS, S], BF16)
        PT = [sb(f"PT{i}", [P, 2, S]) for i in range(NPT)]
        ot = [sb(f"ot{i}", [P, S]) for i in range(2)]
        rinv, ao, aoT = sb("rinv", [P, TB, HG]), sb("ao", [P, 2, TB, H, DH]), sb("aoT", [P, S])
        ao2 = sb("ao2", [P, TB, D]) if head_major else None
        y = sb("y", [P, TB, D])
        floor, floor_w = (sb("floor", [H, S]), [sb(f"floor_w{i}", [P, H, S]) for i in range(2)]) if clamp else (None, None)
        minus_clamp = sb("minus_clamp", [H, 1]) if clamp else None
        f_dram = nc.dram_tensor(f"{pre}_staged_floor", (H, S), F32, kind="Internal").ap() if clamp else None
        psS = [ps(f"psS{i}", [P, 512]) for i in range(2)]
        psT = [ps(f"psT{i}", [P, 2, S]) for i in range(NPS)]
        psO, psOT, psM = ps("psO", [P, 2, S]), ps("psOT", [P, TB, HG, HW]), ps("psM", [P, 512])
        q_dram = nc.dram_tensor(f"{pre}_q_parts", (PARTS, P, S), BF16, kind="Internal").ap()
        k_dram = nc.dram_tensor(f"{pre}_k_parts", (PARTS, P, keys), BF16, kind="Internal").ap()
        m_dram = nc.dram_tensor(f"{pre}_m_parts", (PARTS, H, S), BF16, kind="Internal").ap()
        o_dram = nc.dram_tensor(f"{pre}_o_heads", (H, S, DH), F32, kind="Internal").ap() if head_major else None
        names = ("loaded", "bias_scaled", "rows_set", "clamp_set", "negm_ready", "floor_ready", "floor_staged", "floor_spread", "clamped", "dve_chain", "pool_chain", "var_ready", "rstd_ready", "h_ready", "turned",
                 "hT_ready", "q_proj", "qf_ready", "k_proj", "kf_ready", "v_proj", "v_ready", "q_split", "k_split", "q_staged",
                 "k_staged", "m_staged", "regrouped", "s_ready", "s_used", "mx_turned", "m_split", "m_rows", "st_ready",
                 "exp_ready", "pv_done", "ot_ready", "group_turned", "ao_ready", "o_staged", "ao_back", "ao_turned", "aoT_ready",
                 "out_ready", "x_done")
        (loaded, bias_scaled, rows_set, clamp_set, negm_ready, floor_ready, floor_staged, floor_spread, clamped, dve_chain, pool_chain, var_ready, rstd_ready, h_ready, turned,
         hT_ready, q_proj, qf_ready, k_proj, kf_ready, v_proj, v_ready, q_split, k_split, q_staged,
         k_staged, m_staged, regrouped, s_ready, s_used, mx_turned, m_split, m_rows, st_ready,
         exp_ready, pv_done, ot_ready, group_turned, ao_ready, o_staged, ao_back, ao_turned, aoT_ready,
         out_ready, x_done) = (sem(n) for n in names)
        ctx_loaded = [sem("ctx_loaded0"), sem("ctx_loaded1")]
        block = es.enter_context(nc.Block())
        NLOAD = 8 if bq is not None else 5

        @block.sync
        def _(sp):
            loads = [(wq_s[:], m.dram[wq]), (wk_s[:], m.dram[wk]), (wv_s[:], m.dram[wv]), (wo_s[:], m.dram[wo]),
                     (bo_s[:], rows(m.dram[bo]).to_broadcast((P, D)))]
            if bq is not None:
                loads += [(bq_s[:], m.dram[bq].rearrange("(d a) -> d a", a=1)), (bk_s[:], m.dram[bk].rearrange("(d a) -> d a", a=1)),
                          (bv_s[:], rows(m.dram[bv]).to_broadcast((P, D)))]
            for dst, src in loads:
                sp.dma_start(dst, src).then_inc(loaded, 16)

            def load_ctx(b):
                if from_ctx:
                    wait(sp, v_proj, b - 1)
                    sp.dma_start(ctxT[:, b % 2], m.dram["ctx_768"][b]).then_inc(ctx_loaded[b % 2], 16)

            def regroup(b):
                wait(sp, st_ready, NU * H * (b - 2))
                wait(sp, regrouped, 16 * NREG * b)
                if b < 3:
                    sp.wait_ge(rows_set, 2 * (b + 1))
                sp.wait_ge(q_split, b + 1)
                sp.dma_start(q_dram.rearrange("i p c -> p i c"), qs[:]).then_inc(q_staged, 16)
                sp.wait_ge(k_split, b + 1)
                sp.dma_start(k_dram.rearrange("i p c -> p i c"), ks[:]).then_inc(k_staged, 16)
                sp.wait_ge(q_staged, 16 * (b + 1))
                for i in range(PARTS):
                    for j in range(PARTS):
                        r = (i * PARTS + j) * DH
                        sp.dma_start(QR[b % 3][r:r + DH], q_dram[i].rearrange("(h d) c -> d h c", d=DH)).then_inc(regrouped, 16)
                sp.wait_ge(k_staged, 16 * (b + 1))
                for i in range(PARTS):
                    for j in range(PARTS):
                        r = (i * PARTS + j) * DH
                        sp.dma_start(KR[b % 3][r:r + DH], k_dram[j].rearrange("(h d) c -> d h c", d=DH)).then_inc(regrouped, 16)

            def reread(b):
                if head_major:
                    sp.wait_ge(ao_ready, NG * (b + 1))
                    for t in range(TB):
                        sp.dma_start(o_dram[:, t * P:(t + 1) * P].rearrange("h q d -> q h d"), ao[:, b % 2, t]).then_inc(o_staged, 16)
                    sp.wait_ge(o_staged, 16 * TB * (b + 1))
                    wait(sp, ao_turned, b)
                    flat = o_dram.rearrange("h (l r) d -> (h l) (r d)", r=D // DH)
                    sp.dma_start(ao2[:], flat.rearrange("(t p) c -> p t c", p=P)).then_inc(ao_back, 16)

            load_ctx(0)
            load_ctx(1)
            regroup(0)
            regroup(1)
            for b in range(B):
                if b + 2 < B:
                    load_ctx(b + 2)
                if b >= 1:
                    reread(b - 1)
                if b + 2 < B:
                    regroup(b + 2)
            reread(B - 1)

        def split(eng, link, src, parts):
            link(eng.tensor_copy(parts[:, 0], src[:]))
            link(eng.tensor_tensor(src[:], src[:], parts[:, 0], ALU.subtract))
            link(eng.tensor_copy(parts[:, 1], src[:]))
            link(eng.tensor_tensor(src[:], src[:], parts[:, 1], ALU.subtract))
            return eng.tensor_copy(parts[:, 2], src[:])

        @block.gpsimd
        def _(pool):
            link = Links(pool, pool_chain)

            def fixed_rows(i):
                nc.gpsimd.memset(KR[i][:], 1.0).then_inc(rows_set, 1)
                nc.gpsimd.memset(QR[i][:], 0.0).then_inc(rows_set, 1)

            if clamp:
                nc.gpsimd.memset(minus_clamp[:], -clamp).then_inc(clamp_set, 1)
            fixed_rows(0)

            for b in range(B):
                pool.wait_ge(var_ready, b + 1)
                pool_rsqrt(nc, m, w).then_inc(rstd_ready, 1)
                pool.wait_ge(qf_ready, b + 1)
                wait(pool, q_staged, 16 * b)
                split(nc.gpsimd, link, qf, qs).then_inc(q_split, 1)
                if not k_on_dve:
                    pool.wait_ge(kf_ready, b + 1)
                    wait(pool, k_staged, 16 * b)
                    split(nc.gpsimd, link, kf, ks).then_inc(k_split, 1)
                if b == 1:
                    fixed_rows(1)
                    fixed_rows(2)

        @block.vector
        def _(dve):
            link = Links(dve, dve_chain)

            def moments(b):
                dve_moments(nc, link, w, [m.x[:, b, t] for t in range(TB)], D, LN_EPS).then_inc(var_ready, 1)

            def norm(b):
                dve.wait_ge(rstd_ready, b + 1)
                wait(dve, turned, b)
                for t in range(TB):
                    nc.vector.tensor_scalar(h[:, t], m.x[:, b, t], w.mean[:, t:t + 1], w.rstd[:, t:t + 1], ALU.subtract, ALU.mult).then_inc(h_ready, 1)

            def split_k(b):
                if k_on_dve:
                    dve.wait_ge(kf_ready, b + 1)
                    wait(dve, k_staged, 16 * b)
                    split(nc.vector, link, kf, ks).then_inc(k_split, 1)

            def values(b):
                dve.wait_ge(v_proj, b + 1)
                wait(dve, pv_done, H * (b - 2))
                for t in range(NKT):
                    src = psM[:, t * D:(t + 1) * D].rearrange("p (h d) -> p h d", d=DH)
                    if bq is not None:
                        nc.vector.tensor_tensor(V[b % 3][:, t, :, 0:DH], src, bv_s[:].rearrange("p (h d) -> p h d", d=DH), ALU.add).then_inc(v_ready, 1)
                    else:
                        nc.vector.tensor_copy(V[b % 3][:, t, :, 0:DH], src).then_inc(v_ready, 1)

            def maxima(b, unit):
                n = b * NSU + unit
                hd, u = unit // SPB, unit % SPB
                dve.wait_ge(s_ready, n + 1)
                if unit == 0:
                    wait(dve, mx_turned, b)
                if SPB == 2:
                    nc.vector.reduce_max(mx[:, u, hd:hd + 1], psS[n % 2][:], AX.X).then_inc(s_used, 1)
                else:
                    nc.vector.reduce_max(mx[:, :, hd], psS[n % 2][:].rearrange("p (t k) -> p t k", t=TB), AX.X).then_inc(s_used, 1)

            def clamp_probs(n):
                b, hd = n // NU // H, n // NU % H
                dve.wait_ge(exp_ready, n + 1)
                if n % (NU * H) == 0:
                    dve.wait_ge(floor_spread, 16 * (b + 1))
                at = PT[n % NPT][:]
                nc.vector.scalar_tensor_tensor(at, at, 1.0, floor_w[b % 2][:, hd, None, :].to_broadcast((P, 2, S)), ALU.min, ALU.max).then_inc(clamped, 1)

            def split_max(b):
                dve.wait_ge(mx_turned, b + 1)
                wait(dve, m_staged, 16 * b)
                if clamp:
                    wait(dve, floor_ready, b)
                    link(nc.vector.tensor_scalar(negm[:], psM[0:H, 0:S], clamp, -clamp, ALU.min, ALU.max))
                    nc.vector.tensor_scalar(negm[:], negm[:], -1.0, None, ALU.mult).then_inc(negm_ready, 1)
                    dve.wait_ge(negm_ready, b + 1)
                else:
                    link(nc.vector.tensor_scalar(negm[:], psM[0:H, 0:S], -1.0, None, ALU.mult))
                link(nc.vector.tensor_copy(mp[:, 0], negm[:]))
                if clamp:
                    dve.wait_ge(floor_ready, b + 1)
                link(nc.vector.tensor_tensor(negm[:], negm[:], mp[:, 0], ALU.subtract))
                link(nc.vector.tensor_copy(mp[:, 1], negm[:]))
                link(nc.vector.tensor_tensor(negm[:], negm[:], mp[:, 1], ALU.subtract))
                nc.vector.tensor_copy(mp[:, 2], negm[:]).then_inc(m_split, 1)

            def normalise(g):
                b, hg = g // NG, g % NG
                dve.wait_ge(group_turned, g + 1)
                link(nc.vector.reciprocal(rinv[:], psOT[:, :, :, DH]))
                if hg == 0:
                    if head_major:
                        wait(dve, o_staged, 16 * TB * (b - 1))
                    else:
                        wait(dve, ao_turned, b - 1)
                nc.vector.tensor_tensor(ao[:, b % 2, :, hg * HG:(hg + 1) * HG, :], psOT[:, :, :, 0:DH],
                                        rinv[:][:, :, :, None].to_broadcast((P, TB, HG, DH)), ALU.mult).then_inc(ao_ready, 1)

            def update(b):
                dve.wait_ge(out_ready, b + 1)
                link(nc.vector.tensor_tensor(y[:], psM[:, 0:S].rearrange("p (t d) -> p t d", t=TB), bo_s[:, None, :].to_broadcast((P, TB, D)), ALU.add))
                nc.vector.tensor_tensor(m.x[:, b], m.x[:, b], y[:], ALU.add).then_inc(x_done, 1)

            moments(0)
            for i in range(3):
                link(nc.vector.memset(V[i][:], 1.0))
            dve.wait_ge(loaded, 16 * NLOAD)
            if bq is not None:
                nc.vector.tensor_scalar(bq_s[:], bq_s[:], scale, None, ALU.mult).then_inc(bias_scaled, 1)
            norm(0)
            split_k(0)
            values(0)
            moments(1)
            norm(1)
            split_k(1)
            values(1)
            for unit in range(NSU):
                maxima(0, unit)
            split_max(0)
            for b in range(B):
                for hd in range(H):
                    n = b * H + hd
                    if hd == 0 and b + 2 < B:
                        moments(b + 2)
                    if b + 1 < B:
                        for unit in s_units[hd]:
                            maxima(b + 1, unit)
                    if clamp:
                        for u in range(NU):
                            clamp_probs(n * NU + u)
                    if hd == 1 and b + 2 < B:
                        norm(b + 2)
                    if n >= 6 and n % HG == 2:
                        normalise(n // HG - 1)
                    if hd == T_V and b + 2 < B:
                        split_k(b + 2)
                        values(b + 2)
                    if hd == T_Y and b >= 1:
                        update(b - 1)
                    if hd == T_M and b + 1 < B:
                        split_max(b + 1)
            normalise(B * NG - 1)
            update(B - 1)

        @block.tensor
        def _(pe):
            pe.wait_ge(loaded, 16 * NLOAD)

            def turn(b):
                pe.wait_ge(h_ready, TB * (b + 1))
                for t in range(TB):
                    ins = nc.tensor.transpose(psM[:, t * P:(t + 1) * P], h[:, t], m.ident[:])
                ins.then_inc(turned, 1)

            def project_q(b):
                pe.wait_ge(hT_ready, b + 1)
                nc.tensor.matmul(psM[:, 0:S], wq_s[:], hT[:], start=True, stop=True).then_inc(q_proj, 1)

            def kv_source(b):
                return ctxT[:, b % 2] if from_ctx else hT[:]

            def project_k(b):
                if from_ctx:
                    pe.wait_ge(ctx_loaded[b % 2], 16 * (b // 2 + 1))
                pe.wait_ge(qf_ready, b + 1)
                nc.tensor.matmul(psM[:, 0:keys], wk_s[:], kv_source(b), start=True, stop=True).then_inc(k_proj, 1)

            def project_v(b):
                pe.wait_ge(kf_ready, b + 1)
                for t in range(NKT):
                    ins = nc.tensor.matmul(psM[:, t * D:(t + 1) * D], kv_source(b)[:, t * P:(t + 1) * P], wv_s[:], start=True, stop=True)
                ins.then_inc(v_proj, 1)

            def scores(b, unit):
                n = b * NSU + unit
                hd = unit // SPB
                if unit == 0:
                    pe.wait_ge(regrouped, 16 * NREG * (b + 1))
                wait(pe, s_used, n - 1)
                tiles = [unit % SPB] if SPB == 2 else range(TB)
                for i, t in enumerate(tiles):
                    ins = nc.tensor.matmul(psS[n % 2][:, i * keys:(i + 1) * keys], QR[b % 3][0:MAXROW, hd, t * P:(t + 1) * P], KR[b % 3][0:MAXROW, hd, :], start=True, stop=True)
                ins.then_inc(s_ready, 1)

            def turn_max(b):
                pe.wait_ge(s_used, H * SPB * (b + 1))
                for t in range(TB):
                    ins = nc.tensor.transpose(psM[0:H, t * P:(t + 1) * P], mx[:, t], m.ident[:])
                ins.then_inc(mx_turned, 1)

            def scores_turned(b, hd, u):
                if hd == 0 and u == 0:
                    pe.wait_ge(m_rows, 16 * (b + 1))
                n = (b * H + hd) * NU + u
                wait(pe, exp_ready, n - NPS + 1)
                for k in range(2):
                    kt = 2 * u + k
                    ins = nc.tensor.matmul(psT[n % NPS][:, k], KR[b % 3][:, hd, kt * P:(kt + 1) * P], QR[b % 3][:, hd, :], start=True, stop=True)
                ins.then_inc(st_ready, 1)

            def weigh(b, hd):
                g = (b * H + hd) // HG
                if hd == 0:
                    pe.wait_ge(v_ready, NKT * (b + 1))
                if hd % HG == 0:
                    wait(pe, ot_ready, g)
                for u in range(NU):
                    n = (b * H + hd) * NU + u
                    pe.wait_ge(clamped if clamp else exp_ready, n + 1)
                    for k in range(2):
                        kt = 2 * u + k
                        r = hd % HG * HW
                        ins = nc.tensor.matmul(psO[r:r + HW, g % 2], V[b % 3][:, kt, hd], PT[n % NPT][:, k], start=(kt == 0), stop=(kt == NKT - 1))
                ins.then_inc(pv_done, 1)

            def turn_group(g):
                pe.wait_ge(ot_ready, g + 1)
                wait(pe, ao_ready, g)
                for t in range(TB):
                    ins = nc.tensor.transpose(psOT[:, t].rearrange("p h w -> p (h w)"), ot[g % 2][:, t * P:(t + 1) * P], m.ident[:])
                ins.then_inc(group_turned, 1)

            def turn_out(b):
                if head_major:
                    pe.wait_ge(ao_back, 16 * (b + 1))
                else:
                    pe.wait_ge(ao_ready, NG * (b + 1))
                for t in range(TB):
                    src = ao2[:, t] if head_major else ao[:, b % 2, t].rearrange("p h d -> p (h d)")
                    ins = nc.tensor.transpose(psM[:, t * P:(t + 1) * P], src, m.ident[:])
                ins.then_inc(ao_turned, 1)

            def project_out(b):
                pe.wait_ge(aoT_ready, b + 1)
                for t in range(TB):
                    ins = nc.tensor.matmul(psM[:, t * D:(t + 1) * D], aoT[:, t * P:(t + 1) * P], wo_s[:], start=True, stop=True)
                ins.then_inc(out_ready, 1)

            for b in range(2):
                wait(pe, v_ready, NKT * b)
                turn(b)
                project_q(b)
                project_k(b)
                project_v(b)
            for unit in range(NSU):
                scores(0, unit)
            pe.wait_ge(v_ready, NKT * 2)
            turn_max(0)
            for b in range(B):
                for hd in range(H):
                    n = b * H + hd
                    more = b + 2 < B
                    if hd == T_H and more:
                        pe.wait_ge(m_split, b + 1)
                        turn(b + 2)
                    if hd == T_Q and more:
                        project_q(b + 2)
                    if hd == T_K and more:
                        project_k(b + 2)
                    if hd == T_V and more:
                        project_v(b + 2)
                    if hd == T_O and b >= 1:
                        if more:
                            pe.wait_ge(v_ready, NKT * (b + 3))
                        else:
                            pe.wait_ge(m_split, b + 1)
                        turn_out(b - 1)
                    if hd == T_Y and b >= 1:
                        project_out(b - 1)
                    if hd == T_M and b + 1 < B:
                        wait(pe, x_done, b)
                        if b == 0:
                            pe.wait_ge(v_ready, NKT * 3)
                        turn_max(b + 1)
                    if n >= 6 and n % HG == 2:
                        turn_group(n // HG - 1)
                    units = list(s_units[hd]) if b + 1 < B else []
                    for u in range(NU):
                        if units:
                            scores(b + 1, units.pop(0))
                        scores_turned(b, hd, u)
                    for unit in units:
                        scores(b + 1, unit)
                    if n >= LW:
                        weigh((n - LW) // H, (n - LW) % H)
            for hd in range(H - LW, H):
                weigh(B - 1, hd)
            turn_group(B * NG - 1)
            turn_out(B - 1)
            project_out(B - 1)

        @block.scalar
        def _(act):
            if bq is not None:
                act.wait_ge(bias_scaled, 1)

            def copy_h(b):
                act.wait_ge(turned, b + 1)
                nc.scalar.copy(hT[:], psM[:, 0:S]).then_inc(hT_ready, 1)

            def copy_q(b):
                act.wait_ge(q_proj, b + 1)
                wait(act, q_split, b)
                nc.scalar.activation(qf[:], psM[:, 0:S], ACT.Identity, bias=bq_s[:] if bq is not None else 0.0, scale=scale).then_inc(qf_ready, 1)

            def copy_k(b):
                act.wait_ge(k_proj, b + 1)
                wait(act, k_split, b)
                nc.scalar.activation(kf[:], psM[:, 0:keys], ACT.Identity, bias=bk_s[:] if bq is not None else 0.0).then_inc(kf_ready, 1)

            def copy_group(g):
                act.wait_ge(pv_done, HG * (g + 1))
                wait(act, group_turned, g - 1)
                nc.scalar.copy(ot[g % 2][:], psO[:, g % 2]).then_inc(ot_ready, 1)

            def copy_out(b):
                act.wait_ge(ao_turned, b + 1)
                nc.scalar.copy(aoT[:], psM[:, 0:S]).then_inc(aoT_ready, 1)

            def floors(b):
                if clamp:
                    act.wait_ge(negm_ready, b + 1)
                    wait(act, floor_staged, 16 * b)
                    nc.scalar.activation(floor[:], negm[:], ACT.Exp, bias=minus_clamp[:]).then_inc(floor_ready, 1)

            def stage_max(b):
                act.wait_ge(m_split, b + 1)
                nc.scalar.dma_start(m_dram.rearrange("i h c -> h i c"), mp[:]).then_inc(m_staged, 16)
                if clamp:
                    act.wait_ge(floor_ready, b + 1)
                    wait(act, floor_spread, 16 * b)
                    nc.scalar.dma_start(f_dram, floor[:]).then_inc(floor_staged, 16)

            def max_rows(b):
                act.wait_ge(m_staged, 16 * (b + 1))
                nc.scalar.dma_start(QR[b % 3][MAXROW:MAXROW + PARTS], m_dram).then_inc(m_rows, 16)
                if clamp:
                    act.wait_ge(floor_staged, 16 * (b + 1))
                    wait(act, clamped, NU * H * (b - 1))
                    nc.scalar.dma_start(floor_w[b % 2][:].rearrange("p h s -> p (h s)"),
                                        rows(f_dram.rearrange("h s -> (h s)")).to_broadcast((P, H * S))).then_inc(floor_spread, 16)

            if clamp:
                act.wait_ge(clamp_set, 1)
            for b in range(2):
                copy_h(b)
                copy_q(b)
                copy_k(b)
            floors(0)
            stage_max(0)
            max_rows(0)
            for b in range(B):
                for hd in range(H):
                    more = b + 2 < B
                    if hd == T_H and more:
                        copy_h(b + 2)
                    if hd == T_Q and more:
                        copy_q(b + 2)
                    if hd == T_K and more:
                        copy_k(b + 2)
                    if hd == T_O and b >= 1:
                        copy_out(b - 1)
                    if (b * H + hd) % HG == 1 and b * H + hd >= 5:
                        copy_group((b * H + hd) // HG - 1)
                    for u in range(NU):
                        n = (b * H + hd) * NU + u
                        act.wait_ge(st_ready, n + 1)
                        wait(act, pv_done, (n - NPT) // NU + 1)
                        nc.scalar.activation(PT[n % NPT][:], psT[n % NPS][:], ACT.Exp).then_inc(exp_ready, 1)
                    if hd == T_M and b + 1 < B:
                        floors(b + 1)
                    if hd == T_M + 1 and b + 1 < B:
                        stage_max(b + 1)
                    if hd == T_M + 2 and b + 1 < B:
                        max_rows(b + 1)
            copy_group(B * NG - 1)
            copy_out(B - 1)


def layer_fp4_mlp(m, pre):
    nc = m.nc
    d = m.dram
    BLK, FI = 16, 352
    CH = [(0, 128), (128, 128), (256, 96)]
    REST = CH[2][1]
    with ExitStack() as es:
        sb, ps, sem = allocators(nc, es, pre)
        WU, WD, WALL = 3 * D, 6 * D, 6 * D + FI
        wall = sb("wall", [P, WALL])
        wguT, wdT = sb("wguT", [P, 2, FI]), sb("wdT", [P, 3, D])
        w = Norm(sb, "", NT)
        h, f = sb("h", [P, NT, D]), sb("f", [P, NT, FI])
        hT, g = [sb(f"hT{i}", [P, S]) for i in range(2)], [sb(f"g{i}", [P, TB, FI]) for i in range(2)]
        fT = sb("fT", [P, 3, S])
        HALF, GRP = NT // 2, 2 * TB
        fl = lambda v: v.rearrange("p t d -> p (t d)")
        groups = [(fl(h[:, 0:HALF]), HALF * D), (wall[:], WALL), (fl(h[:, HALF:]), HALF * D)]
        groups += [(fl(f[:, GRP * k:GRP * (k + 1)]), GRP * FI) for k in range(NT // GRP)]
        RING, WIDE = 3, max(n for _, n in groups)
        mag, sg = ([sb(f"{v}{i}", [P, WIDE]) for i in range(RING)] for v in ("mag", "sg"))
        lev, low = sb("lev", [P, WIDE]), sb("low", [P, WIDE])
        bmax, bscale, binv, bhalf = ([sb(f"{v}{i}", [P, WIDE // BLK]) for i in range(RING)] for v in ("bmax", "bscale", "binv", "bhalf"))
        psA, psG, psU, psF, psY = ps("psA", [P, 512]), ps("psG", [P, TB, 512]), ps("psU", [P, TB, 512]), ps("psF", [P, 2, 512]), ps("psY", [P, TB, D])
        names = ("loaded", "zeroed", "dve_chain", "w_turned", "wT_ready", "moments", "rstd", "h_ready", "parted", "scaled",
                 "normed", "quantised", "turned", "hT_ready", "gu_ready", "silu_ready", "f_ready", "f_turned", "fT_ready", "y_ready", "x_done")
        (loaded, zeroed, dve_chain, w_turned, wT_ready, moments, rstd, h_ready, parted, scaled,
         normed, quantised, turned, hT_ready, gu_ready, silu_ready, f_ready, f_turned, fT_ready, y_ready, x_done) = (sem(n) for n in names)
        block = es.enter_context(nc.Block())
        NLOAD = 7
        F0 = 3

        @block.sync
        def _(sp):
            sp.wait_ge(zeroed, 1)
            for n, (c, k) in enumerate(CH):
                sp.dma_start(wall[0:k, n * D:(n + 1) * D], d[f"{pre}_w_gate"][c:c + k]).then_inc(loaded, 16)
                sp.dma_start(wall[0:k, WU + n * D:WU + (n + 1) * D], d[f"{pre}_w_up"][c:c + k]).then_inc(loaded, 16)
            sp.dma_start(wall[:, WD:], d[f"{pre}_w_down"]).then_inc(loaded, 16)

        @block.gpsimd
        def _(pool):
            nc.gpsimd.memset(wall[:], 0.0).then_inc(zeroed, 1)
            pool.wait_ge(moments, 1)
            pool_rsqrt(nc, m, w, NT).then_inc(rstd, 1)
            for p, (_, width) in enumerate(groups):
                i, nb = p % RING, width // BLK
                blocks = lambda v: v[:, 0:width].rearrange("p (n e) -> p n e", e=BLK)
                wide = lambda v: v[:, 0:nb][:, :, None].to_broadcast((P, nb, BLK))
                pool.wait_ge(scaled, p + 1)
                nc.gpsimd.tensor_tensor(blocks(mag[i]), blocks(mag[i]), wide(binv[i]), ALU.mult).then_inc(normed, 1)
                nc.gpsimd.tensor_tensor(blocks(sg[i]), blocks(sg[i]), wide(bhalf[i]), ALU.mult).then_inc(normed, 1)

        @block.vector
        def _(dve):
            link = Links(dve, dve_chain)

            def scales(p):
                i, width = p % RING, groups[p][1]
                nb = width // BLK
                dve.wait_ge(parted, 2 * (p + 1))
                link(nc.vector.tensor_reduce(bmax[i][:, 0:nb], mag[i][:, 0:width].rearrange("p (n e) -> p n e", e=BLK), AX.X, ALU.max))
                link(nc.vector.tensor_scalar(bscale[i][:, 0:nb], bmax[i][:, 0:nb], 1.0 / 6.0, 1e-12, ALU.mult, ALU.max))
                link.mark(nc.vector.tensor_scalar(bhalf[i][:, 0:nb], bscale[i][:, 0:nb], 0.5, None, ALU.mult))
                link(nc.vector.reciprocal(binv[i][:, 0:nb], bscale[i][:, 0:nb]))
                nc.vector.sem_inc(scaled, 1)

            def levels(p, between=None):
                i, (a, width) = p % RING, groups[p]
                M, L, C, G = mag[i][:, 0:width], lev[:, 0:width], low[:, 0:width], sg[i][:, 0:width]
                dve.wait_ge(normed, 2 * p + 1)
                link.mark(nc.vector.tensor_scalar(C, M, 0.25, None, ALU.is_gt))
                link(nc.vector.tensor_scalar(L, M, 5.0, 2.0, ALU.is_gt, ALU.mult))
                link(nc.vector.scalar_tensor_tensor(L, M, 3.5, L, ALU.is_gt, ALU.add))
                link(nc.vector.scalar_tensor_tensor(L, M, 2.5, L, ALU.is_gt, ALU.add))
                if between is not None:
                    between()
                link(nc.vector.scalar_tensor_tensor(L, L, 2.0, C, ALU.mult, ALU.add))
                for mid in (0.75, 1.25, 1.75):
                    link(nc.vector.scalar_tensor_tensor(L, M, mid, L, ALU.is_gt, ALU.add))
                dve.wait_ge(normed, 2 * p + 2)
                nc.vector.tensor_tensor(a, L, G, ALU.mult).then_inc(quantised, 1)
                dve.wait_ge(quantised, p + 1)

            def gate(b):
                dve.wait_ge(silu_ready, b + 1)
                nc.vector.tensor_tensor(f[:, TB * b:TB * (b + 1)], g[b % 2][:], psU[:, :, 0:FI], ALU.mult).then_inc(f_ready, 1)

            def update(b):
                dve.wait_ge(y_ready, b + 1)
                nc.vector.tensor_tensor(m.x[:, b], m.x[:, b], psY[:], ALU.add).then_inc(x_done, 1)

            xs = [m.x[:, i // TB, i % TB] for i in range(NT)]
            dve_moments(nc, link, w, xs, D, LN_EPS).then_inc(moments, 1)
            dve.wait_ge(rstd, 1)
            for i in range(NT):
                nc.vector.tensor_scalar(h[:, i], xs[i], w.mean[:, i:i + 1], w.rstd[:, i:i + 1], ALU.subtract, ALU.mult).then_inc(h_ready, 1)
            scales(0)
            scales(1)
            levels(0)
            scales(2)
            levels(1)
            levels(2, lambda: gate(0))
            gate(1)
            scales(F0)
            gate(2)
            gate(3)
            scales(F0 + 1)
            levels(F0, lambda: gate(4))
            gate(5)
            scales(F0 + 2)
            levels(F0 + 1, lambda: gate(6))
            gate(7)
            scales(F0 + 3)
            update(0)
            update(1)
            levels(F0 + 2, lambda: update(2))
            update(3)
            levels(F0 + 3, lambda: update(4))
            update(5)
            update(6)
            update(7)

        @block.tensor
        def _(pe):
            pe.wait_ge(quantised, 2)
            for n, (c, k) in enumerate(CH):
                nc.tensor.transpose(psG[:, 0, c:c + k], wall[0:k, n * D:(n + 1) * D], m.ident[0:k, 0:k])
                nc.tensor.transpose(psG[:, 1, c:c + k], wall[0:k, WU + n * D:WU + (n + 1) * D], m.ident[0:k, 0:k])
                ins = nc.tensor.transpose(psU[0:k, 0, n * D:(n + 1) * D], wall[:, WD + c:WD + c + k], m.ident[:])
            ins.then_inc(w_turned, 1)

            def turn(b):
                pe.wait_ge(quantised, 1 if b < B // 2 else 3)
                wait(pe, hT_ready, b)
                for t in range(TB):
                    ins = nc.tensor.transpose(psA[:, t * P:(t + 1) * P], h[:, TB * b + t], m.ident[:])
                ins.then_inc(turned, 1)

            def up(b):
                pe.wait_ge(hT_ready, b + 1)
                wait(pe, f_ready, b)
                for t in range(TB):
                    nc.tensor.matmul(psG[:, t, 0:FI], hT[b % 2][:, t * P:(t + 1) * P], wguT[:, 0], start=True, stop=True)
                    ins = nc.tensor.matmul(psU[:, t, 0:FI], hT[b % 2][:, t * P:(t + 1) * P], wguT[:, 1], start=True, stop=True)
                ins.then_inc(gu_ready, 1)

            def down(b):
                pe.wait_ge(quantised, F0 + b // 2 + 1)
                wait(pe, fT_ready, 2 * b)
                for n, (c, k) in enumerate(CH):
                    for t in range(TB):
                        at = psF[0:k, n // 2, (n % 2) * S + t * P:(n % 2) * S + (t + 1) * P]
                        ins = nc.tensor.transpose(at, f[:, TB * b + t, c:c + k], m.ident[:])
                ins.then_inc(f_turned, 1)
                pe.wait_ge(fT_ready, 2 * (b + 1))
                wait(pe, x_done, b)
                for t in range(TB):
                    for n, (c, k) in enumerate(CH):
                        ins = nc.tensor.matmul(psY[:, t], fT[0:k, n, t * P:(t + 1) * P], wdT[0:k, n], start=(n == 0), stop=(n == 2))
                ins.then_inc(y_ready, 1)

            turn(0)
            pe.wait_ge(wT_ready, 3)
            for b in range(B):
                if b + 1 < B:
                    turn(b + 1)
                up(b)
            for b in range(B):
                down(b)

        @block.scalar
        def _(act):
            def part(p):
                i, (a, width) = p % RING, groups[p]
                wait(act, quantised, p - RING + 1)
                nc.scalar.activation(mag[i][:, 0:width], a, ACT.Abs).then_inc(parted, 1)
                nc.scalar.activation(sg[i][:, 0:width], a, ACT.Sign).then_inc(parted, 1)

            def copy_h(b):
                act.wait_ge(turned, b + 1)
                wait(act, gu_ready, b - 1)
                nc.scalar.copy(hT[b % 2][:], psA[:, 0:S]).then_inc(hT_ready, 1)

            act.wait_ge(h_ready, HALF)
            part(0)
            act.wait_ge(loaded, 16 * NLOAD)
            part(1)
            act.wait_ge(h_ready, NT)
            part(2)
            act.wait_ge(w_turned, 1)
            nc.scalar.copy(wguT[:], psG[:, :, 0:FI]).then_inc(wT_ready, 1)
            nc.scalar.copy(wdT[:, 0:2], psU[:, 0, 0:2 * D].rearrange("p (n d) -> p n d", n=2)).then_inc(wT_ready, 1)
            nc.scalar.copy(wdT[0:REST, 2], psU[0:REST, 0, 2 * D:3 * D]).then_inc(wT_ready, 1)
            copy_h(0)
            for b in range(B):
                if b + 1 < B:
                    copy_h(b + 1)
                act.wait_ge(gu_ready, b + 1)
                wait(act, f_ready, b - 1)
                nc.scalar.activation(g[b % 2][:], psG[:, :, 0:FI], ACT.Silu).then_inc(silu_ready, 1)
                if b % 2 == 1:
                    act.wait_ge(f_ready, b + 1)
                    part(F0 + b // 2)
            for b in range(B):
                act.wait_ge(f_turned, b + 1)
                wait(act, y_ready, b)
                nc.scalar.copy(fT[:, 0:2], psF[:, 0].rearrange("p (n s) -> p n s", n=2)).then_inc(fT_ready, 1)
                nc.scalar.copy(fT[0:REST, 2], psF[0:REST, 1, 0:S]).then_inc(fT_ready, 1)


def layer_gated_recurrence(m, pre):
    nc = m.nc
    H, DH, CHUNK, FC = 16, 8, 64, 512
    NC = S // CHUNK
    RES = float(1.0 / np.sqrt(2.0))
    EPS_Q = float(np.finfo(np.float32).eps)
    EPS_X = 1e-6
    with ExitStack() as es:
        sb, ps, sem = allocators(nc, es, pre)
        wi, wo, wf, wp = sb("wi", [P, 5 * D]), sb("wo", [P, D]), sb("wf", [P, FC]), sb("wp", [P, FC // P, D])
        n1, n2 = sb("n1", [P, 1]), sb("n2", [P, 1])
        headsum, headexp = sb("headsum", [P, H]), sb("headexp", [H, P])
        go, begin = sb("go", [P, S]), sb("begin", [P, S])
        w, w1, w3 = Norm(sb), Norm(sb, "1"), Norm(sb, "3")
        h, h1, hT = [sb(f"hn{i}", [P, TB, D]) for i in range(2)], sb("h1", [P, TB, D]), sb("hT", [P, S])
        two = lambda v: [sb(f"{v}{i}", [P, S]) for i in range(2)]
        q, k, v, a, g, q2 = two("q"), two("k"), two("v"), two("a"), two("g"), two("q2")
        two_c = sb("two", [P, 1])
        qms, qrs, qrT = sb("qms", [P, TB * H]), sb("qrs", [P, TB * H]), sb("qrT", [H, S])
        u, a0, a1, pref, rec, acc, st, yT = (sb(n, [P, S]) for n in ("u", "a_go", "a_begin", "pref", "rec", "acc", "st", "yT"))
        hm, h2, h2T, sT, y = sb("hm", [P, TB, D]), sb("h2", [P, TB, D]), sb("h2T", [P, S]), sb("sT", [P, FC // P, S]), sb("y", [P, TB, D])
        psA, psP, psB, psC, psD = ps("psA", [P, 512]), ps("psP", [P, 6, S]), ps("psB", [P, 512]), ps("psC", [P, FC // P, S]), ps("psD", [P, TB, D])
        names = ("loaded", "consts", "pool_chain", "dve_chain", "moments", "rstd", "h_ready", "turned", "hT_ready", "proj_ready", "proj_read",
                 "q2_ready", "qs_ready", "qms_ready", "qrs_ready", "q_turned", "qrT_ready", "q_spread", "clipped", "started",
                 "u_ready", "y_ready", "mix_ready", "m3", "rstd3", "h2_ready", "h2_turned", "h2T_ready", "fc_ready", "silu_ready", "mlp_ready", "x_done",
                 "gates_ready")
        (loaded, consts, pool_chain, dve_chain, moments, rstd, h_ready, turned, hT_ready, proj_ready, proj_read,
         q2_ready, qs_ready, qms_ready, qrs_ready, q_turned, qrT_ready, q_spread, clipped, started,
         u_ready, y_ready, mix_ready, m3, rstd3, h2_ready, h2_turned, h2T_ready, fc_ready, silu_ready, mlp_ready, x_done,
         gates_ready) = (sem(n) for n in names)
        block = es.enter_context(nc.Block())
        NLOAD = 6

        @block.sync
        def _(sp):
            col = lambda ap: ap.rearrange("(d a) -> d a", a=1)
            for dst, src in ((wi[:], m.dram[f"{pre}_in_proj_w"]), (wo[:], m.dram[f"{pre}_out_proj_w"]), (wf[:], m.dram[f"{pre}_fc_w"]),
                             (wp[:], m.dram[f"{pre}_proj_w"].rearrange("(c p) d -> p c d", p=P)),
                             (n1[:], col(m.dram[f"{pre}_norm1_w"])), (n2[:], col(m.dram[f"{pre}_norm2_w"]))):
                sp.dma_start(dst, src).then_inc(loaded, 16)

        @block.gpsimd
        def _(pool):
            link = Links(pool, pool_chain)

            def band(t, keep, steps):
                link(nc.gpsimd.memset(t[:], keep))
                for base, mult, step in steps:
                    link(nc.gpsimd.affine_select(out=t[:], in_=t[:], compare_op=ALU.is_ge, fill=0.0, base=base,
                                                 pattern=[[step, t.shape[1]]], channel_multiplier=mult))

            band(headsum, 1.0 / DH, [(0, 1, -DH), (DH - 1, -1, DH)])
            band(headexp, 1.0, [(0, -DH, 1), (DH - 1, DH, -1)])
            link(nc.gpsimd.memset(two_c[:], 2.0))
            link(nc.gpsimd.memset(go[:], 1.0))
            link(nc.gpsimd.memset(begin[:], 0.0))
            link(nc.gpsimd.memset(go[:, 0:S:CHUNK], 0.0))
            nc.gpsimd.memset(begin[:, 0:S:CHUNK], 1.0).then_inc(consts, 1)
            pool.wait_ge(consts, 1)

            def prep(b):
                pool.wait_ge(moments, 2 * b + 1)
                pool_rsqrt(nc, m, w).then_inc(rstd, 1)
                pool.wait_ge(moments, 2 * b + 2)
                pool_rsqrt(nc, m, w1).then_inc(rstd, 1)

            prep(0)
            for b in range(B):
                i = b % 2
                if b + 1 < B:
                    prep(b + 1)
                pool.wait_ge(gates_ready, 3 * (b + 1))
                pool.wait_ge(proj_read, 2 * (b + 1))
                wait(pool, y_ready, b)
                nc.gpsimd.tensor_tensor(u[:], k[i][:], v[i][:], ALU.mult).then_inc(u_ready, 1)
                pool.wait_ge(clipped, b + 1)
                nc.gpsimd.tensor_tensor(a0[:], a[i][:], go[:], ALU.mult).then_inc(started, 1)
                nc.gpsimd.tensor_tensor(a1[:], a[i][:], begin[:], ALU.mult).then_inc(started, 1)
                pool.wait_ge(qms_ready, b + 1)
                nc.gpsimd.tensor_tensor(qrs[:], qms[:], m.half[:, 0:TB * H], ALU.pow).then_inc(qrs_ready, 1)
                pool.wait_ge(m3, b + 1)
                pool_rsqrt(nc, m, w3).then_inc(rstd3, 1)

        @block.vector
        def _(dve):
            link = Links(dve, dve_chain)
            dve.wait_ge(loaded, 16 * NLOAD)
            dve.wait_ge(consts, 1)

            def prep(b):
                xs, hs = [m.x[:, b, t] for t in range(TB)], [h[b % 2][:, t] for t in range(TB)]
                dve_moments(nc, link, w, xs, D, LN_EPS).then_inc(moments, 1)
                dve.wait_ge(rstd, 2 * b + 1)
                for t in range(TB):
                    link.mark(nc.vector.tensor_scalar(hs[t], xs[t], w.mean[:, t:t + 1], w.rstd[:, t:t + 1], ALU.subtract, ALU.mult))
                link.wait()
                dve_square_mean(nc, link, w1, hs, D, EPS_X).then_inc(moments, 1)
                dve.wait_ge(rstd, 2 * b + 2)
                wait(dve, turned, b)
                for t in range(TB):
                    nc.vector.tensor_scalar(h1[:, t], hs[t], w1.rstd[:, t:t + 1], None, ALU.mult).then_inc(h_ready, 1)

            prep(0)
            for b in range(B):
                i = b % 2
                dve.wait_ge(gates_ready, 3 * (b + 1))
                nc.vector.tensor_scalar(a[i][:], a[i][:], 0.6, 0.9995, ALU.max, ALU.min).then_inc(clipped, 1)
                dve.wait_ge(qs_ready, b + 1)
                nc.vector.tensor_scalar(qms[:], psB[:, 0:TB * H], EPS_Q, None, ALU.add).then_inc(qms_ready, 1)
                if b + 1 < B:
                    prep(b + 1)
                dve.wait_ge(started, 2 * (b + 1))
                link(nc.vector.tensor_tensor_scan(pref[:], a0[:], a1[:], 0.0, ALU.mult, ALU.add))
                link(nc.vector.tensor_scalar(rec[:], pref[:], 1e-6, None, ALU.max))
                link(nc.vector.reciprocal(rec[:], rec[:]))
                dve.wait_ge(u_ready, b + 1)
                link(nc.vector.tensor_tensor(rec[:], u[:], rec[:], ALU.mult))
                link(nc.vector.tensor_tensor_scan(acc[:], go[:], rec[:], 0.0, ALU.mult, ALU.add))
                link(nc.vector.tensor_tensor(st[:, 0:CHUNK], pref[:, 0:CHUNK], acc[:, 0:CHUNK], ALU.mult))
                for c in range(1, NC):
                    z = slice(c * CHUNK, (c + 1) * CHUNK)
                    link(nc.vector.scalar_tensor_tensor(st[:, z], acc[:, z], st[:, c * CHUNK - 1:c * CHUNK], pref[:, z], ALU.add, ALU.mult))
                dve.wait_ge(proj_read, 2 * (b + 1))
                link(nc.vector.tensor_tensor(st[:], st[:], q[i][:], ALU.mult))
                dve.wait_ge(q_spread, b + 1)
                link(nc.vector.tensor_tensor(st[:], st[:], psB[:, 0:S], ALU.mult))
                link(nc.vector.tensor_tensor(st[:], st[:], v[i][:], ALU.subtract))
                link(nc.vector.tensor_tensor(st[:], st[:], g[i][:], ALU.mult))
                nc.vector.tensor_tensor(yT[:], st[:], v[i][:], ALU.add).then_inc(y_ready, 1)
                dve.wait_ge(mix_ready, b + 1)
                link(nc.vector.scalar_tensor_tensor(hm[:], psB[:, 0:S].rearrange("p (t d) -> p t d", t=TB), RES, h[i][:], ALU.mult, ALU.add))
                dve_square_mean(nc, link, w3, [hm[:, t] for t in range(TB)], D, EPS_X).then_inc(m3, 1)
                dve.wait_ge(rstd3, b + 1)
                for t in range(TB):
                    nc.vector.tensor_scalar(h2[:, t], hm[:, t], w3.rstd[:, t:t + 1], None, ALU.mult).then_inc(h2_ready, 1)
                dve.wait_ge(mlp_ready, b + 1)
                link(nc.vector.scalar_tensor_tensor(y[:], psD[:], RES, hm[:], ALU.mult, ALU.add))
                nc.vector.tensor_tensor(m.x[:, b], m.x[:, b], y[:], ALU.add).then_inc(x_done, 1)

        @block.tensor
        def _(pe):
            pe.wait_ge(loaded, 16 * NLOAD)
            pe.wait_ge(consts, 1)

            def prep(b):
                pe.wait_ge(h_ready, TB * (b + 1))
                for t in range(TB):
                    ins = nc.tensor.transpose(psA[:, t * P:(t + 1) * P], h1[:, t], m.ident[:])
                ins.then_inc(turned, 1)
                pe.wait_ge(hT_ready, b + 1)
                wait(pe, proj_read, 2 * b)
                wait(pe, gates_ready, 3 * b)
                wait(pe, q2_ready, b)
                for j in range(5):
                    ins = nc.tensor.matmul(psP[:, j], wi[:, j * D:(j + 1) * D], hT[:], start=True, stop=True)
                ins.then_inc(proj_ready, 1)

            prep(0)
            for b in range(B):
                i = b % 2
                pe.wait_ge(q2_ready, b + 1)
                for t in range(TB):
                    ins = nc.tensor.matmul(psB[:, t * H:(t + 1) * H], q2[i][:, t * P:(t + 1) * P], headsum[:], start=True, stop=True)
                ins.then_inc(qs_ready, 1)
                if b + 1 < B:
                    prep(b + 1)
                pe.wait_ge(qrs_ready, b + 1)
                for t in range(TB):
                    ins = nc.tensor.transpose(psA[0:H, 256 + t * P:256 + (t + 1) * P], qrs[:, t * H:(t + 1) * H], m.ident[:])
                ins.then_inc(q_turned, 1)
                pe.wait_ge(qrT_ready, b + 1)
                nc.tensor.matmul(psB[:, 0:S], headexp[:], qrT[:], start=True, stop=True).then_inc(q_spread, 1)
                pe.wait_ge(y_ready, b + 1)
                for t in range(TB):
                    ins = nc.tensor.matmul(psB[:, t * D:(t + 1) * D], yT[:, t * P:(t + 1) * P], wo[:], start=True, stop=True)
                ins.then_inc(mix_ready, 1)
                pe.wait_ge(h2_ready, TB * (b + 1))
                for t in range(TB):
                    ins = nc.tensor.transpose(psA[:, t * P:(t + 1) * P], h2[:, t], m.ident[:])
                ins.then_inc(h2_turned, 1)
                pe.wait_ge(h2T_ready, b + 1)
                for c in range(FC // P):
                    ins = nc.tensor.matmul(psC[:, c], wf[:, c * P:(c + 1) * P], h2T[:], start=True, stop=True)
                ins.then_inc(fc_ready, 1)
                pe.wait_ge(silu_ready, b + 1)
                for t in range(TB):
                    for c in range(FC // P):
                        ins = nc.tensor.matmul(psD[:, t], sT[:, c, t * P:(t + 1) * P], wp[:, c], start=(c == 0), stop=(c == FC // P - 1))
                ins.then_inc(mlp_ready, 1)

        @block.scalar
        def _(act):
            act.wait_ge(loaded, 16 * NLOAD)
            act.wait_ge(consts, 1)

            def prep(b):
                i = b % 2
                act.wait_ge(turned, b + 1)
                nc.scalar.activation(hT[:], psA[:, 0:S], ACT.Copy, scale=n1[:]).then_inc(hT_ready, 1)
                act.wait_ge(proj_ready, b + 1)
                wait(act, y_ready, b - 1)
                nc.scalar.activation(q2[i][:], psP[:, 0], ACT.Square).then_inc(q2_ready, 1)
                nc.scalar.activation(k[i][:], psP[:, 1], ACT.Tanh).then_inc(gates_ready, 1)
                nc.scalar.activation(a[i][:], psP[:, 3], ACT.Sigmoid, bias=two_c[:]).then_inc(gates_ready, 1)
                nc.scalar.activation(g[i][:], psP[:, 4], ACT.Sigmoid).then_inc(gates_ready, 1)
                nc.scalar.copy(q[i][:], psP[:, 0]).then_inc(proj_read, 1)
                nc.scalar.copy(v[i][:], psP[:, 2]).then_inc(proj_read, 1)

            prep(0)
            for b in range(B):
                if b + 1 < B:
                    prep(b + 1)
                act.wait_ge(q_turned, b + 1)
                nc.scalar.copy(qrT[:], psA[0:H, 256:256 + S]).then_inc(qrT_ready, 1)
                act.wait_ge(h2_turned, b + 1)
                nc.scalar.activation(h2T[:], psA[:, 0:S], ACT.Copy, scale=n2[:]).then_inc(h2T_ready, 1)
                act.wait_ge(fc_ready, b + 1)
                nc.scalar.activation(sT[:], psC[:], ACT.Silu).then_inc(silu_ready, 1)


def layer_sign_linear(m, pre):
    nc = m.nc
    LIMIT = 100.0
    with ExitStack() as es:
        sb, ps, sem = allocators(nc, es, pre)
        wT, scale, bias = sb("wT", [P, D]), sb("scale", [P, D]), sb("bias", [P, D])
        w = Norm(sb)
        h, hT, y = sb("h", [P, TB, D]), sb("hT", [P, S]), sb("y", [P, TB, D])
        psT, psY = ps("psT", [P, S]), ps("psY", [P, TB, D])
        loaded, w_signed, var_ready, rstd_ready = sem("loaded"), sem("w_signed"), sem("var_ready"), sem("rstd_ready")
        h_ready, turned, hT_ready, y_ready, dve_chain = (sem("h_ready"), sem("turned"), sem("hT_ready"),
                                                          sem("y_ready"), sem("dve_chain"))
        y_done = sem("y_done")
        block = es.enter_context(nc.Block())

        @block.sync
        def _(sp):
            sp.dma_start(wT[:], m.dram[f"{pre}_weights"]).then_inc(loaded, 16)
            sp.dma_start(scale[:], rows(m.dram[f"{pre}_scale"]).to_broadcast((P, D))).then_inc(loaded, 16)
            sp.dma_start(bias[:], rows(m.dram[f"{pre}_bias"]).to_broadcast((P, D))).then_inc(loaded, 16)

        @block.gpsimd
        def _(pool):
            with pool.Fori(0, B) as b:
                pool.wait_ge(var_ready, b + 1)
                pool_rsqrt(nc, m, w).then_inc(rstd_ready, 1)

        @block.vector
        def _(dve):
            STEPS = 2 * TB + 9
            dve.wait_ge(loaded, 48)
            nc.vector.tensor_scalar(wT[:], wT[:], 0.0, 2.0, ALU.is_ge, ALU.mult).then_inc(w_signed, 1)
            dve.wait_ge(w_signed, 1)
            nc.vector.tensor_scalar(wT[:], wT[:], 1.0, None, ALU.subtract).then_inc(w_signed, 1)
            with dve.Fori(0, B) as b:
                link = Links(dve, dve_chain, b * STEPS)
                dve_moments(nc, link, w, [m.x[:, b, t] for t in range(TB)], D, LN_EPS).then_inc(var_ready, 1)
                dve.wait_ge(rstd_ready, b + 1)
                for t in range(TB):
                    nc.vector.tensor_scalar(h[:, t], m.x[:, b, t], w.mean[:, t:t + 1], w.rstd[:, t:t + 1], ALU.subtract, ALU.mult).then_inc(h_ready, 1)
                dve.wait_ge(y_ready, b + 1)
                bc = lambda a: a[:, None, :].to_broadcast((P, TB, D))
                link(nc.vector.tensor_tensor(y[:], psY[:], bc(scale[:]), ALU.mult))
                link(nc.vector.tensor_tensor(y[:], y[:], bc(bias[:]), ALU.add))
                link(nc.vector.tensor_scalar(y[:], y[:], -LIMIT, LIMIT, ALU.max, ALU.min))
                for t in range(TB):
                    link(nc.vector.tensor_tensor(m.x[:, b, t], m.x[:, b, t], y[:, t], ALU.add))
                assert link.n == STEPS, link.n

        @block.tensor
        def _(pe):
            pe.wait_ge(w_signed, 2)
            with pe.Fori(0, B) as b:
                pe.wait_ge(h_ready, TB * b + TB)
                for t in range(TB):
                    ins = nc.tensor.transpose(psT[:, t * P:(t + 1) * P], h[:, t], m.ident[:])
                ins.then_inc(turned, 1)
                pe.wait_ge(hT_ready, b + 1)
                for t in range(TB):
                    ins = nc.tensor.matmul(psY[:, t], hT[:, t * P:(t + 1) * P], wT[:], start=True, stop=True)
                ins.then_inc(y_ready, 1)

        @block.scalar
        def _(act):
            with act.Fori(0, B) as b:
                act.wait_ge(turned, b + 1)
                nc.scalar.copy(hT[:], psT[:]).then_inc(hT_ready, 1)


def layer_moe_top8(m, pre):
    nc = m.nc
    d = m.dram
    E, F, TOP = 64, 64, 8
    EG = 8
    NGR = E // EG
    BK = EG * F // P
    with ExitStack() as es:
        sb, ps, sem = allocators(nc, es, pre)
        wup, wdn = sb("wup", [P, E, F]), sb("wdn", [P, E // 2, D])
        sup, sdn, cen, ebias = sb("sup", [P, F]), sb("sdn", [F, D]), sb("cen", [P, E]), sb("ebias", [P, E])
        w = Norm(sb)
        h, hT = sb("h", [P, TB, D]), [sb(f"hT{i}", [P, S]) for i in range(2)]
        aff, bia, top8, rest = sb("aff", [P, TB, E]), sb("bia", [P, TB, E]), sb("top8", [P, TB, 8]), sb("rest", [P, TB, E])
        sig, cw, wsum = sb("sig", [P, TB, E]), [sb(f"cw{i}", [P, TB, E]) for i in range(2)], sb("wsum", [P, TB])
        act_s, wt_s, fT = [sb(f"act{i}", [P, EG * F]) for i in range(3)], [sb(f"wt{i}", [P, EG * F]) for i in range(3)], [sb(f"fT{i}", [P, BK, P]) for i in range(3)]
        shT = [sb(f"shT{i}", [F, S]) for i in range(2)]
        psU, psF = [ps(f"psU{i}", [P, EG * F]) for i in range(2)], [ps(f"psF{i}", [P, BK * P]) for i in range(2)]
        psY = [ps(f"psY{i}", [P, 512]) for i in range(2)]
        psM, psH = ps("psM", [P, 512]), ps("psH", [P, 512])
        names = ("loaded", "dve_chain", "var_ready", "rstd_ready", "h_ready", "turned", "hT_ready", "aff_ready", "aff_copied",
                 "sig_ready", "cw_ready", "up_ready", "silu_ready", "weighted", "f_turned", "fT_ready", "down_done", "sh_up",
                 "sh_silu", "x_done")
        (loaded, dve_chain, var_ready, rstd_ready, h_ready, turned, hT_ready, aff_ready, aff_copied,
         sig_ready, cw_ready, up_ready, silu_ready, weighted, f_turned, fT_ready, down_done, sh_up,
         sh_silu, x_done) = (sem(n) for n in names)
        block = es.enter_context(nc.Block())
        LT, LD = 2, 3
        NG = NT * NGR

        @block.sync
        def _(sp):
            for dst, src in ((sup[:], d[f"{pre}_Ws_up"]), (sdn[:], d[f"{pre}_Ws_down"]), (cen[:], d[f"{pre}_centroids"]),
                             (ebias[:], rows(d[f"{pre}_expert_biases"]).to_broadcast((P, E)))):
                sp.dma_start(dst, src).then_inc(loaded, 16)
            for q in range(4):
                c = slice(q * E // 4, (q + 1) * E // 4)
                sp.dma_start(wup[:, c], d[f"{pre}_W_up"][c].rearrange("e d f -> d e f")).then_inc(loaded, 16)
            sp.dma_start(wdn[:], d[f"{pre}_W_down"].rearrange("(n e) f d -> (e f) n d", e=2)).then_inc(loaded, 16)

        @block.gpsimd
        def _(pool):
            for b in range(B):
                pool.wait_ge(var_ready, b + 1)
                pool_rsqrt(nc, m, w).then_inc(rstd_ready, 1)

        @block.vector
        def _(dve):
            link = Links(dve, dve_chain)
            dve.wait_ge(loaded, 16 * 9)

            def norm(b):
                dve_moments(nc, link, w, [m.x[:, b, t] for t in range(TB)], D, LN_EPS).then_inc(var_ready, 1)
                dve.wait_ge(rstd_ready, b + 1)
                wait(dve, turned, b)
                for t in range(TB):
                    nc.vector.tensor_scalar(h[:, t], m.x[:, b, t], w.mean[:, t:t + 1], w.rstd[:, t:t + 1], ALU.subtract, ALU.mult).then_inc(h_ready, 1)

            def route_a(b):
                dve.wait_ge(aff_ready, b + 1)
                wait(dve, sig_ready, b)
                nc.vector.tensor_copy(aff[:], psM[:, 256:256 + TB * E].rearrange("p (t e) -> p t e", t=TB)).then_inc(aff_copied, 1)
                dve.wait_ge(aff_copied, b + 1)
                link(nc.vector.tensor_tensor(bia[:], aff[:], ebias[:, None, :].to_broadcast((P, TB, E)), ALU.add))
                for t in range(TB):
                    link.mark(nc.vector.max(top8[:, t], bia[:, t]))
                link.wait()
                for t in range(TB):
                    link.mark(nc.vector.match_replace(rest[:, t], top8[:, t], bia[:, t], -3.0e38))
                link.wait()

            def route_b(b):
                link(nc.vector.tensor_tensor(rest[:], rest[:], bia[:], ALU.not_equal))
                dve.wait_ge(sig_ready, b + 1)
                c = cw[b % 2]
                link(nc.vector.tensor_tensor(c[:], sig[:], rest[:], ALU.mult))
                link(nc.vector.reduce_sum(wsum[:], c[:], AX.X))
                link(nc.vector.tensor_scalar(wsum[:], wsum[:], 1e-8, None, ALU.add))
                link(nc.vector.reciprocal(wsum[:], wsum[:]))
                nc.vector.tensor_tensor(c[:], c[:], wsum[:, :, None].to_broadcast((P, TB, E)), ALU.mult).then_inc(cw_ready, 1)

            def weigh(n):
                tile, g = n // NGR, n % NGR
                b, t = tile // TB, tile % TB
                dve.wait_ge(silu_ready, n + 1)
                if g == 0 and t == 0:
                    dve.wait_ge(cw_ready, b + 1)
                wait(dve, f_turned, n - 2)
                e = g * EG
                nc.vector.tensor_tensor(wt_s[n % 3][:].rearrange("p (e f) -> p e f", f=F), act_s[n % 3][:].rearrange("p (e f) -> p e f", f=F),
                                        cw[b % 2][:, t, e:e + EG, None].to_broadcast((P, EG, F)), ALU.mult).then_inc(weighted, 1)

            def update(tile):
                b, t = tile // TB, tile % TB
                dve.wait_ge(down_done, NGR * (tile + 1))
                nc.vector.tensor_tensor(m.x[:, b, t], m.x[:, b, t], psY[tile % 2][:, 0:D], ALU.add).then_inc(x_done, 1)

            norm(0)
            route_a(0)
            route_b(0)
            for n in range(NG):
                tile, g = n // NGR, n % NGR
                b, t = tile // TB, tile % TB
                weigh(n)
                if t == 0 and g == 1 and b + 1 < B:
                    norm(b + 1)
                if t == 1 and g == 2 and b + 1 < B:
                    route_a(b + 1)
                if t == 1 and g == 4 and b + 1 < B:
                    route_b(b + 1)
                if g == 5 and tile >= 1:
                    update(tile - 1)
            update(NT - 1)

        @block.tensor
        def _(pe):
            pe.wait_ge(loaded, 16 * 9)

            def turn(b):
                pe.wait_ge(h_ready, TB * (b + 1))
                wait(pe, hT_ready, b)
                for t in range(TB):
                    ins = nc.tensor.transpose(psM[:, t * P:(t + 1) * P], h[:, t], m.ident[:])
                ins.then_inc(turned, 1)

            def affinities(b):
                pe.wait_ge(hT_ready, b + 1)
                wait(pe, aff_copied, b)
                for t in range(TB):
                    ins = nc.tensor.matmul(psM[:, 256 + t * E:256 + (t + 1) * E], hT[b % 2][:, t * P:(t + 1) * P], cen[:], start=True, stop=True)
                ins.then_inc(aff_ready, 1)

            def up(n):
                tile, g = n // NGR, n % NGR
                b, t = tile // TB, tile % TB
                wait(pe, silu_ready, n - 1)
                nc.tensor.matmul(psU[n % 2][:], hT[b % 2][:, t * P:(t + 1) * P], wup[:, g * EG:(g + 1) * EG].rearrange("p e f -> p (e f)"),
                                 start=True, stop=True).then_inc(up_ready, 1)

            def shared_up(b):
                wait(pe, sh_silu, b)
                nc.tensor.matmul(psH[0:F, 0:S], sup[:], hT[b % 2][:], start=True, stop=True).then_inc(sh_up, 1)

            def turn_hidden(n):
                pe.wait_ge(weighted, n + 1)
                wait(pe, fT_ready, n - 1)
                for k in range(BK):
                    ins = nc.tensor.transpose(psF[n % 2][:, k * P:(k + 1) * P], wt_s[n % 3][:, k * P:(k + 1) * P], m.ident[:])
                ins.then_inc(f_turned, 1)

            def down(n):
                tile, g = n // NGR, n % NGR
                b, t = tile // TB, tile % TB
                if g == 0:
                    pe.wait_ge(sh_silu, b + 1)
                    wait(pe, x_done, tile - 1)
                    nc.tensor.matmul(psY[tile % 2][:, 0:D], shT[b % 2][:, t * P:(t + 1) * P], sdn[:], start=True, stop=False)
                pe.wait_ge(fT_ready, n + 1)
                for k in range(BK):
                    ins = nc.tensor.matmul(psY[tile % 2][:, 0:D], fT[n % 3][:, k], wdn[:, g * BK + k], start=False, stop=(g == NGR - 1 and k == BK - 1))
                ins.then_inc(down_done, 1)

            turn(0)
            affinities(0)
            shared_up(0)
            for n in range(NG + LD):
                tile, g = n // NGR, n % NGR
                b, t = tile // TB, tile % TB
                if n < NG:
                    up(n)
                    if t == 0 and g == 5 and b + 1 < B:
                        turn(b + 1)
                    if t == 1 and g == 0 and b + 1 < B:
                        affinities(b + 1)
                    if t == 1 and g == 1 and b + 1 < B:
                        shared_up(b + 1)
                if LT <= n < NG + LT:
                    turn_hidden(n - LT)
                if n >= LD:
                    down(n - LD)

        @block.scalar
        def _(act):
            def copy_h(b):
                act.wait_ge(turned, b + 1)
                wait(act, up_ready, TB * NGR * (b - 1))
                nc.scalar.copy(hT[b % 2][:], psM[:, 0:S]).then_inc(hT_ready, 1)

            def sigmoids(b):
                act.wait_ge(aff_copied, b + 1)
                wait(act, cw_ready, b)
                nc.scalar.activation(sig[:], aff[:], ACT.Sigmoid).then_inc(sig_ready, 1)

            def shared_silu(b):
                act.wait_ge(sh_up, b + 1)
                wait(act, down_done, TB * NGR * (b - 1))
                nc.scalar.activation(shT[b % 2][:], psH[0:F, 0:S], ACT.Silu).then_inc(sh_silu, 1)

            def silu(n):
                act.wait_ge(up_ready, n + 1)
                wait(act, weighted, n - 2)
                nc.scalar.activation(act_s[n % 3][:], psU[n % 2][:], ACT.Silu).then_inc(silu_ready, 1)

            def copy_turned(n):
                act.wait_ge(f_turned, n + 1)
                wait(act, down_done, n - 2)
                nc.scalar.copy(fT[n % 3][:].rearrange("p n q -> p (n q)"), psF[n % 2][:]).then_inc(fT_ready, 1)

            copy_h(0)
            sigmoids(0)
            shared_silu(0)
            for n in range(NG + LT):
                tile, g = n // NGR, n % NGR
                b, t = tile // TB, tile % TB
                if n < NG:
                    silu(n)
                    if t == 0 and g == 6 and b + 1 < B:
                        copy_h(b + 1)
                    if t == 1 and g == 3 and b + 1 < B:
                        sigmoids(b + 1)
                        shared_silu(b + 1)
                if n >= LT:
                    copy_turned(n - LT)


def layer_selected_experts(m, pre):
    nc = m.nc
    d = m.dram
    E, F, M = 8, 64, 256
    MT = M // P
    EF = E * F
    EB = EF // P
    NEG = E + 1
    with ExitStack() as es:
        sb, ps, sem = allocators(nc, es, pre)
        sw12, sw3 = sb("sw12", [P, 2 * F]), sb("sw3", [F, D])
        sb12, sb3, sg, sbeta = sb("sb12", [P, 2 * F]), sb("sb3", [P, D]), sb("sln_g", [F, 1]), sb("sln_b", [F, 1])
        wgate, bgate, ebias = sb("wgate", [P, NEG]), sb("bgate", [P, NEG]), sb("ebias", [P, E])
        ew = [sb(f"ew{i + 1}", [P, E, F]) for i in range(2)]
        eb = [sb(f"eb{i + 1}", [P, EF]) for i in range(2)]
        ew3, eb3 = sb("ew3", [P, EB, D]), sb("eb3", [E, D])
        lng, lnb = sb("lng", [P, F]), sb("lnb", [P, F])
        ib_row, it_row, id_row = sb("ib_row", [P, M], I32), sb("it_row", [P, M], I32), sb("id_row", [P, M])
        ib_col, it_col, id_col = sb("ib_col", [P, MT], I32), sb("it_col", [P, MT], I32), sb("id_col", [P, MT])
        rowf, colf = sb("rowf", [P, M]), sb("colf", [P, MT])
        tok_col, tok_row, rank = sb("tok_col", [P, NT]), sb("tok_row", [P, NT * P]), sb("rank", [P, E])
        pick, spread = sb("pick", [P, NT, M]), sb("spread", [P, MT, NT * P])
        wa, ws, we = Norm(sb, "a", NT), Norm(sb, "s", NT), Norm(sb, "e", MT * E)
        h, hT = sb("h", [P, NT, D]), sb("hT", [P, NT, P])
        x12, u, shT, so = sb("x12", [P, NT, 2 * F]), sb("u", [P, NT, F]), sb("shT", [F, NT, P]), sb("so", [P, NT, D])
        xpT = sb("xpT", [P, M])
        gl, sc, bi, oh, key = sb("gl", [P, MT, NEG]), sb("sc", [P, MT, NEG]), sb("bi", [P, MT, E]), sb("oh", [P, MT, E]), sb("key", [P, MT, E])
        top, two, mx2, wsum = sb("top", [P, MT]), sb("two", [P, MT, 2]), sb("mx2", [P, MT]), sb("wsum", [P, MT])
        e1, e2 = sb("e1", [P, MT, EF]), sb("e2", [P, MT, EF])
        zT, ohT, picked_out = sb("zT", [P, EB, M]), sb("ohT", [E, M]), sb("picked_out", [P, MT, D + 2])
        seen, cnt, rec, keep = sb("seen", [P, NT, 2]), sb("cnt", [P, NT]), sb("rec", [P, NT]), sb("keep", [P, NT])
        psT, psX, psE = [ps(f"psT{i}", [P, 512]) for i in range(2)], [ps(f"psX{i}", [P, 512]) for i in range(2)], [ps(f"psE{i}", [P, 512]) for i in range(2)]
        psG, psC = ps("psG", [P, 512]), ps("psC", [P, 512])
        names = ("loaded", "dve_chain", "pool_chain", "iota_ready", "var_ready", "rstd_ready", "h_ready", "pick_ready", "turned", "hT_ready",
                 "x12_ready", "biased", "silu_ready", "z_ready", "z_turned", "shT_ready", "shared_out", "so_ready", "gathered",
                 "xpT_ready", "gates_ready", "logits_ready", "sig_ready", "two_ready", "exp_ready", "e_ready", "e_biased", "esilu_ready", "ez_ready",
                 "ez_turned", "zT_ready", "eo_ready", "po_ready", "seen_ready", "spread_done", "x_done")
        (loaded, dve_chain, pool_chain, iota_ready, var_ready, rstd_ready, h_ready, pick_ready, turned, hT_ready,
         x12_ready, biased, silu_ready, z_ready, z_turned, shT_ready, shared_out, so_ready, gathered,
         xpT_ready, gates_ready, logits_ready, sig_ready, two_ready, exp_ready, e_ready, e_biased, esilu_ready, ez_ready,
         ez_turned, zT_ready, eo_ready, po_ready, seen_ready, spread_done, x_done) = (sem(n) for n in names)
        block = es.enter_context(nc.Block())
        col = lambda a: a.rearrange("(d a) -> d a", a=1)
        wide = lambda name, n: rows(d[f"{pre}_{name}"]).to_broadcast((P, n))
        loads = [(ib_row[:], wide("index_b", M)), (it_row[:], wide("index_t", M)),
                 (sw12[:, 0:F], d[f"{pre}_sw1"]), (sw12[:, F:], d[f"{pre}_sw2"]), (sw3[:], d[f"{pre}_sw3"]),
                 (sb12[:, 0:F], wide("sb1", F)), (sb12[:, F:], wide("sb2", F)), (sb3[:], wide("sb3", D)),
                 (sg[:], col(d[f"{pre}_s_ln_g"])), (sbeta[:], col(d[f"{pre}_s_ln_b"])),
                 (wgate[:, 0:1], d[f"{pre}_sg_w"]), (wgate[:, 1:], d[f"{pre}_eg_w"]),
                 (bgate[:, 0:1], wide("sg_b", 1)), (bgate[:, 1:], wide("eg_b", E)), (ebias[:], wide("exp_bias", E)),
                 (ew[0][:], d[f"{pre}_ew1"].rearrange("e d f -> d e f")), (ew[1][:], d[f"{pre}_ew2"].rearrange("e d f -> d e f")),
                 (eb[0][:], rows(d[f"{pre}_eb1"].rearrange("e f -> (e f)")).to_broadcast((P, EF))),
                 (eb[1][:], rows(d[f"{pre}_eb2"].rearrange("e f -> (e f)")).to_broadcast((P, EF))),
                 (ew3[:], d[f"{pre}_ew3"].rearrange("e f d -> (e f) d").rearrange("(n p) d -> p n d", p=P)), (eb3[:], d[f"{pre}_eb3"]),
                 (lng[:], wide("sel_ln_g", F)), (lnb[:], wide("sel_ln_b", F))]
        for c, name in ((ib_col, "index_b"), (it_col, "index_t")):
            loads += [(c[:, t:t + 1], col(d[f"{pre}_{name}"][t * P:(t + 1) * P])) for t in range(MT)]
        NLOAD = 16 * len(loads)

        @block.sync
        def _(sp):
            for dst, src in loads:
                sp.dma_start(dst, src).then_inc(loaded, 16)

        @block.gpsimd
        def _(pool):
            link = Links(pool, pool_chain)
            nc.gpsimd.iota(tok_col[:], pattern=[[P, NT]], base=0, channel_multiplier=1, allow_small_or_imprecise_dtypes=True).then_inc(iota_ready, 1)
            nc.gpsimd.iota(tok_row[:], pattern=[[1, NT * P]], base=0, channel_multiplier=0, allow_small_or_imprecise_dtypes=True).then_inc(iota_ready, 1)
            nc.gpsimd.iota(rank[:], pattern=[[-1, E]], base=E, channel_multiplier=0, allow_small_or_imprecise_dtypes=True).then_inc(iota_ready, 1)
            nc.gpsimd.memset(picked_out[:, :, D + 1:], 1.0).then_inc(iota_ready, 1)
            for n, ww in enumerate((wa, ws, we)):
                pool.wait_ge(var_ready, n + 1)
                pool_rsqrt(nc, m, ww, ww.n).then_inc(rstd_ready, 1)

        @block.vector
        def _(dve):
            link = Links(dve, dve_chain)
            fl = lambda a: a.rearrange("p n d -> p (n d)")
            dve_moments(nc, link, wa, [m.x[:, i // TB, i % TB] for i in range(NT)], D, LN_EPS).then_inc(var_ready, 1)
            dve.wait_ge(loaded, NLOAD)
            for b_, t_, f_, out in ((ib_row, it_row, rowf, id_row), (ib_col, it_col, colf, id_col)):
                link.mark(nc.vector.tensor_copy(f_[:], b_[:]))
                link(nc.vector.tensor_copy(out[:], t_[:]))
                link(nc.vector.scalar_tensor_tensor(out[:], f_[:], float(S), out[:], ALU.mult, ALU.add))
            dve.wait_ge(iota_ready, 4)
            dve.wait_ge(rstd_ready, 1)
            for i in range(NT):
                nc.vector.tensor_scalar(h[:, i], m.x[:, i // TB, i % TB], wa.mean[:, i:i + 1], wa.rstd[:, i:i + 1], ALU.subtract, ALU.mult).then_inc(h_ready, 1)
                nc.vector.tensor_scalar(pick[:, i], id_row[:], tok_col[:, i:i + 1], None, ALU.is_equal).then_inc(pick_ready, 1)
            for b in range(B):
                dve.wait_ge(x12_ready, b + 1)
                nc.vector.tensor_tensor(x12[:, TB * b:TB * (b + 1)], psX[b % 2][:, 0:TB * 2 * F].rearrange("p (t f) -> p t f", t=TB),
                                        sb12[:, None, :].to_broadcast((P, TB, 2 * F)), ALU.add).then_inc(biased, 1)
            dve.wait_ge(gates_ready, 1)
            nc.vector.tensor_tensor(gl[:], psC[:, 0:MT * NEG].rearrange("p (t e) -> p t e", t=MT), bgate[:, None, :].to_broadcast((P, MT, NEG)), ALU.add).then_inc(logits_ready, 1)
            for b in range(B):
                dve.wait_ge(silu_ready, b + 1)
                i = slice(TB * b, TB * (b + 1))
                link.mark(nc.vector.tensor_tensor(u[:, i], u[:, i], x12[:, i, F:], ALU.mult))
            link.wait()
            dve_moments(nc, link, ws, [u[:, i] for i in range(NT)], F, LN_EPS).then_inc(var_ready, 1)
            for t in range(MT):
                for k, e in enumerate((e1, e2)):
                    dve.wait_ge(e_ready, 2 * t + k + 1)
                    nc.vector.tensor_tensor(e[:, t], psE[k][:], eb[k][:], ALU.add).then_inc(e_biased, 1)
            dve.wait_ge(rstd_ready, 2)
            for i in range(NT):
                if i == 0:
                    link.wait()
                nc.vector.tensor_scalar(u[:, i], u[:, i], ws.mean[:, i:i + 1], ws.rstd[:, i:i + 1], ALU.subtract, ALU.mult).then_inc(z_ready, 1)
            dve.wait_ge(e_biased, 2 * MT)
            for t in range(MT):
                dve.wait_ge(esilu_ready, t + 1)
                link.mark(nc.vector.tensor_tensor(e1[:, t], e1[:, t], e2[:, t], ALU.mult))
            link.wait()
            dve_moments(nc, link, we, [e1[:, n // E, n % E * F:(n % E + 1) * F] for n in range(MT * E)], F, LN_EPS).then_inc(var_ready, 1)
            dve.wait_ge(sig_ready, 1)
            link(nc.vector.tensor_tensor(bi[:], sc[:, :, 1:], ebias[:, None, :].to_broadcast((P, MT, E)), ALU.add))
            link(nc.vector.reduce_max(top[:], bi[:], AX.X))
            link(nc.vector.tensor_tensor(oh[:], bi[:], top[:, :, None].to_broadcast((P, MT, E)), ALU.is_equal))
            link(nc.vector.tensor_tensor(key[:], oh[:], rank[:, None, :].to_broadcast((P, MT, E)), ALU.mult))
            link(nc.vector.reduce_max(top[:], key[:], AX.X))
            link(nc.vector.tensor_tensor(oh[:], key[:], top[:, :, None].to_broadcast((P, MT, E)), ALU.is_equal))
            link(nc.vector.tensor_tensor(key[:], oh[:], sc[:, :, 1:], ALU.mult))
            link.mark(nc.vector.tensor_copy(two[:, :, 0:1], sc[:, :, 0:1]))
            link(nc.vector.reduce_sum(two[:, :, 1:2], key[:], AX.X))
            link(nc.vector.reduce_max(mx2[:], two[:], AX.X))
            nc.vector.tensor_tensor(two[:], two[:], mx2[:, :, None].to_broadcast((P, MT, 2)), ALU.subtract).then_inc(two_ready, 1)
            dve.wait_ge(rstd_ready, 3)
            per = lambda a: a.rearrange("p t (e f) -> p (t e) f", f=F)
            E1 = per(e1[:])
            shape = (P, MT * E, F)
            link(nc.vector.tensor_tensor(E1, E1, we.mean[:, :, None].to_broadcast(shape), ALU.subtract))
            link(nc.vector.tensor_tensor(E1, E1, we.rstd[:, :, None].to_broadcast(shape), ALU.mult))
            link(nc.vector.tensor_tensor(E1, E1, lng[:, None, :].to_broadcast(shape), ALU.mult))
            link(nc.vector.tensor_tensor(E1, E1, lnb[:, None, :].to_broadcast(shape), ALU.add))
            nc.vector.tensor_tensor(E1, E1, fl(oh[:])[:, :, None].to_broadcast(shape), ALU.mult).then_inc(ez_ready, 1)
            for t in range(MT):
                link.mark(nc.vector.tensor_scalar(spread[:, t], tok_row[:], id_col[:, t:t + 1], None, ALU.is_equal))
            for b in range(B):
                dve.wait_ge(shared_out, b + 1)
                nc.vector.tensor_tensor(so[:, TB * b:TB * (b + 1)], psX[b % 2][:, 0:TB * D].rearrange("p (t d) -> p t d", t=TB),
                                        sb3[:, None, :].to_broadcast((P, TB, D)), ALU.add).then_inc(so_ready, 1)
            dve.wait_ge(exp_ready, 1)
            link(nc.vector.reduce_sum(wsum[:], two[:], AX.X))
            link(nc.vector.reciprocal(wsum[:], wsum[:]))
            link(nc.vector.tensor_tensor(two[:], two[:], wsum[:, :, None].to_broadcast((P, MT, 2)), ALU.mult))
            link.mark(nc.vector.tensor_copy(picked_out[:, :, D:D + 1], two[:, :, 0:1]))
            for t in range(MT):
                dve.wait_ge(eo_ready, MT)
                nc.vector.tensor_scalar(picked_out[:, t, 0:D], psC[:, 128 + t * D:128 + (t + 1) * D], two[:, t, 1:2], None, ALU.mult).then_inc(po_ready, 1)
            dve.wait_ge(seen_ready, 1)
            link(nc.vector.tensor_copy(seen[:], psG[:, 0:2 * NT].rearrange("p (i k) -> p i k", k=2)))
            link.mark(nc.vector.tensor_scalar(cnt[:], seen[:, :, 1], 1.0, None, ALU.max))
            link(nc.vector.tensor_scalar(keep[:], seen[:, :, 1], 1.0, None, ALU.min))
            link.mark(nc.vector.reciprocal(rec[:], cnt[:]))
            link(nc.vector.tensor_scalar(keep[:], keep[:], -1.0, 1.0, ALU.mult, ALU.add))
            link(nc.vector.tensor_tensor(cnt[:], seen[:, :, 0], rec[:], ALU.mult))
            link(nc.vector.tensor_tensor(keep[:], keep[:], cnt[:], ALU.add))
            dve.wait_ge(so_ready, B)
            for i in range(NT):
                x = m.x[:, i // TB, i % TB]
                link.mark(nc.vector.scalar_tensor_tensor(x, so[:, i], keep[:, i:i + 1], x, ALU.mult, ALU.add))
            link.wait()
            for i in range(NT):
                b, t = i // TB, i % TB
                dve.wait_ge(spread_done, b + 1)
                x = m.x[:, b, t]
                nc.vector.scalar_tensor_tensor(x, psE[b % 2][:, t * D:(t + 1) * D], rec[:, i:i + 1], x, ALU.mult, ALU.add).then_inc(x_done, 1)

        @block.tensor
        def _(pe):
            for b in range(B):
                pe.wait_ge(h_ready, TB * (b + 1))
                wait(pe, hT_ready, b - 1)
                for t in range(TB):
                    ins = nc.tensor.transpose(psT[b % 2][:, t * P:(t + 1) * P], h[:, TB * b + t], m.ident[:])
                ins.then_inc(turned, 1)
                pe.wait_ge(pick_ready, TB * (b + 1))
                for i in range(TB * b, TB * (b + 1)):
                    ins = nc.tensor.matmul(psG[:, 0:M], h[:, i], pick[:, i], start=(i == 0), stop=(i == NT - 1))
                if b == B - 1:
                    ins.then_inc(gathered, 1)
                if b == 0:
                    pe.wait_ge(loaded, NLOAD)
                pe.wait_ge(hT_ready, b + 1)
                wait(pe, biased, b - 1)
                for t in range(TB):
                    ins = nc.tensor.matmul(psX[b % 2][:, t * 2 * F:(t + 1) * 2 * F], hT[:, TB * b + t], sw12[:], start=True, stop=True)
                ins.then_inc(x12_ready, 1)
            pe.wait_ge(xpT_ready, 1)
            for t in range(MT):
                ins = nc.tensor.matmul(psC[:, t * NEG:(t + 1) * NEG], xpT[:, t * P:(t + 1) * P], wgate[:], start=True, stop=True)
            ins.then_inc(gates_ready, 1)
            for t in range(MT):
                for k in range(2):
                    wait(pe, e_biased, 2 * (t - 1) + k + 1)
                    nc.tensor.matmul(psE[k][:], xpT[:, t * P:(t + 1) * P], ew[k][:].rearrange("p e f -> p (e f)"), start=True, stop=True).then_inc(e_ready, 1)
            for b in range(B):
                pe.wait_ge(z_ready, TB * (b + 1))
                pe.wait_ge(hT_ready, B)
                wait(pe, shT_ready, b - 1)
                for t in range(TB):
                    ins = nc.tensor.transpose(psT[b % 2][0:F, t * P:(t + 1) * P], u[:, TB * b + t], m.ident[:])
                ins.then_inc(z_turned, 1)
                pe.wait_ge(shT_ready, b + 1)
                pe.wait_ge(biased, B)
                wait(pe, so_ready, b - 1)
                for t in range(TB):
                    ins = nc.tensor.matmul(psX[b % 2][:, t * D:(t + 1) * D], shT[:, TB * b + t], sw3[:], start=True, stop=True)
                ins.then_inc(shared_out, 1)
            pe.wait_ge(ez_ready, 1)
            pe.wait_ge(e_biased, 2 * MT)
            for t in range(MT):
                for k in range(EB):
                    nc.tensor.transpose(psE[t][:, k * P:(k + 1) * P], e1[:, t, k * P:(k + 1) * P], m.ident[:])
                pe.wait_ge(shT_ready, B)
                nc.tensor.transpose(psT[t][0:E, 0:P], oh[:, t], m.ident[:]).then_inc(ez_turned, 1)
            pe.wait_ge(logits_ready, 1)
            for t in range(MT):
                pe.wait_ge(zT_ready, t + 1)
                for k in range(EB):
                    nc.tensor.matmul(psC[:, 128 + t * D:128 + (t + 1) * D], zT[:, k, t * P:(t + 1) * P], ew3[:, k], start=(k == 0), stop=False)
                nc.tensor.matmul(psC[:, 128 + t * D:128 + (t + 1) * D], ohT[:, t * P:(t + 1) * P], eb3[:], start=False, stop=True).then_inc(eo_ready, 1)
            pe.wait_ge(po_ready, MT)
            pe.wait_ge(xpT_ready, 1)
            for i in range(NT):
                for t in range(MT):
                    ins = nc.tensor.matmul(psG[:, 2 * i:2 * (i + 1)], spread[:, t, i * P:(i + 1) * P], picked_out[:, t, D:], start=(t == 0), stop=(t == MT - 1))
            ins.then_inc(seen_ready, 1)
            for b in range(B):
                wait(pe, x_done, TB * (b - 1))
                for i in range(TB):
                    for t in range(MT):
                        c = (TB * b + i) * P
                        ins = nc.tensor.matmul(psE[b % 2][:, i * D:(i + 1) * D], spread[:, t, c:c + P], picked_out[:, t, 0:D], start=(t == 0), stop=(t == MT - 1))
                ins.then_inc(spread_done, 1)

        @block.scalar
        def _(act):
            for b in range(B):
                act.wait_ge(turned, b + 1)
                nc.scalar.copy(hT[:, TB * b:TB * (b + 1)].rearrange("p t q -> p (t q)"), psT[b % 2][:, 0:S]).then_inc(hT_ready, 1)
            act.wait_ge(gathered, 1)
            nc.scalar.copy(xpT[:], psG[:, 0:M]).then_inc(xpT_ready, 1)
            for b in range(B):
                act.wait_ge(biased, b + 1)
                i = slice(TB * b, TB * (b + 1))
                nc.scalar.activation(u[:, i], x12[:, i, 0:F], ACT.Silu).then_inc(silu_ready, 1)
            for t in range(MT):
                act.wait_ge(e_biased, 2 * t + 1)
                nc.scalar.activation(e1[:, t], e1[:, t], ACT.Silu).then_inc(esilu_ready, 1)
            act.wait_ge(logits_ready, 1)
            nc.scalar.activation(sc[:], gl[:], ACT.Sigmoid).then_inc(sig_ready, 1)
            act.wait_ge(loaded, NLOAD)
            for b in range(B):
                act.wait_ge(z_turned, b + 1)
                nc.scalar.activation(shT[:, TB * b:TB * (b + 1)].rearrange("p t q -> p (t q)"), psT[b % 2][0:F, 0:S], ACT.Identity,
                                     bias=sbeta[:], scale=sg[:]).then_inc(shT_ready, 1)
            act.wait_ge(two_ready, 1)
            nc.scalar.activation(two[:], two[:], ACT.Exp).then_inc(exp_ready, 1)
            for t in range(MT):
                act.wait_ge(ez_turned, t + 1)
                nc.scalar.copy(zT[:, :, t * P:(t + 1) * P], psE[t][:].rearrange("p (k q) -> p k q", k=EB))
                nc.scalar.copy(ohT[:, t * P:(t + 1) * P], psT[t][0:E, 0:P]).then_inc(zT_ready, 1)


def layer_attention_single(m, pre, scale, inner_norm):
    nc = m.nc
    d = m.dram
    NC = B * KT
    with ExitStack() as es:
        sb, ps, sem = allocators(nc, es, pre)
        wq, wk, wv, wo = sb("wq", [P, D]), sb("wk", [DK, D]), sb("wv", [DK, D]), sb("wo", [P, D])
        bq, bk = sb("bq", [P, 1]), sb("bk", [P, 1])
        bv, bo = sb("bv", [P, D]), sb("bo", [P, D])
        w, w1 = Norm(sb, "", NT), Norm(sb, "1", NT)
        w2 = Norm(sb, "2", NC) if inner_norm else None
        h = sb("h", [P, NT, D])
        hT = [sb(f"hT{i}", [P, S]) for i in range(2)]
        ctx = sb("ctx", [P, B, KT, DK]) if inner_norm else None
        ctxT = [sb(f"ctxT{i}", [DK, SK]) for i in range(2)]
        g1, b1, g2, b2 = sb("g1", [P, 1]), sb("b1", [P, 1]), sb("g2", [DK, 1]), sb("b2", [DK, 1])
        qT, kT, v = sb("qT", [P, B, S]), sb("kT", [P, B, SK]), sb("v", [P, B, KT, D])
        RING = 4
        mx, negm, rsum, rinv = (sb(n, [P, RING]) for n in ("mx", "negm", "rsum", "rinv"))
        pr, prT = [sb(f"pr{i}", [P, SK]) for i in range(3)], [sb(f"prT{i}", [P, KT * P]) for i in range(2)]
        oT, y = [sb(f"oT{i}", [P, P]) for i in range(2)], sb("y", [P, D])
        psA, psS, psP, psO = ([ps(f"{n}{i}", [P, 512]) for i in range(2)] for n in ("psA", "psS", "psP", "psO"))
        names = ("loaded", "ctx_loaded", "dve_chain", "bias_scaled", "moments", "rstd", "h_ready", "turned", "hT_ready", "q_ready", "qT_ready",
                 "c_ready", "ctx_turned", "ctxT_ready", "k_ready", "kT_ready", "vp_ready", "v_ready", "s_ready", "negm_ready", "exp_ready",
                 "p_turned", "prT_ready", "o_ready", "oT_ready", "y_ready", "y_read")
        (loaded, ctx_loaded, dve_chain, bias_scaled, moments, rstd, h_ready, turned, hT_ready, q_ready, qT_ready,
         c_ready, ctx_turned, ctxT_ready, k_ready, kT_ready, vp_ready, v_ready, s_ready, negm_ready, exp_ready,
         p_turned, prT_ready, o_ready, oT_ready, y_ready, y_read) = (sem(n) for n in names)
        block = es.enter_context(nc.Block())
        NLOAD = 12 if inner_norm else 8
        LT, LV, LY = 2, 3, 4
        norms = (w, w1, w2) if inner_norm else (w,)

        @block.sync
        def _(sp):
            col = lambda a: a.rearrange("(d a) -> d a", a=1)
            loads = [(wq[:], d[f"{pre}_Wq"]), (wk[:], d[f"{pre}_Wk"]), (wv[:], d[f"{pre}_Wv"]), (wo[:], d[f"{pre}_Wo"]),
                     (bq[:], col(d[f"{pre}_bq"])), (bk[:], col(d[f"{pre}_bk"])),
                     (bv[:], rows(d[f"{pre}_bv"]).to_broadcast((P, D))), (bo[:], rows(d[f"{pre}_bo"]).to_broadcast((P, D)))]
            if inner_norm:
                loads += [(g1[:], col(d[f"{pre}_ln1_g"])), (b1[:], col(d[f"{pre}_ln1_b"])),
                          (g2[:], col(d[f"{pre}_ln2_g"])), (b2[:], col(d[f"{pre}_ln2_b"]))]
                for b in range(B):
                    sp.dma_start(ctx[:, b], d["ctx_rows"][b].rearrange("(t p) c -> p t c", p=P)).then_inc(ctx_loaded, 16)
            for dst, src in loads:
                sp.dma_start(dst, src).then_inc(loaded, 16)
            if not inner_norm:
                for b in range(B):
                    wait(sp, vp_ready, b - 1)
                    wait(sp, ctx_loaded, 16 * b)
                    sp.dma_start(ctxT[b % 2][:], d["ctx_768"][b]).then_inc(ctx_loaded, 16)

        @block.gpsimd
        def _(pool):
            for n, ww in enumerate(norms):
                pool.wait_ge(moments, n + 1)
                pool_rsqrt(nc, m, ww, ww.n).then_inc(rstd, 1)

        @block.vector
        def _(dve):
            link = Links(dve, dve_chain)

            def normed(dst, src, ww, t, done):
                nc.vector.tensor_scalar(dst, src, ww.mean[:, t:t + 1], ww.rstd[:, t:t + 1], ALU.subtract, ALU.mult).then_inc(done, 1)

            xs, hs = [m.x[:, i // TB, i % TB] for i in range(NT)], [h[:, i] for i in range(NT)]
            dve_moments(nc, link, w, xs, D, LN_EPS).then_inc(moments, 1)
            dve.wait_ge(rstd, 1)
            if inner_norm:
                for i in range(NT):
                    normed(hs[i], xs[i], w, i, link.sem)
                link.n += NT
                link.wait()
                dve_moments(nc, link, w1, hs, D, LN_EPS).then_inc(moments, 1)
                dve.wait_ge(ctx_loaded, 16 * B)
                cs = [ctx[:, i // KT, i % KT] for i in range(NC)]
                dve_moments(nc, link, w2, cs, DK, LN_EPS).then_inc(moments, 1)
                dve.wait_ge(rstd, 3)
                for b in range(B):
                    for i in range(b * TB, (b + 1) * TB):
                        normed(hs[i], hs[i], w1, i, h_ready)
                    for i in range(b * KT, (b + 1) * KT):
                        normed(cs[i], cs[i], w2, i, c_ready)
            else:
                for i in range(NT):
                    normed(hs[i], xs[i], w, i, h_ready)
            dve.wait_ge(loaded, 16 * NLOAD)
            nc.vector.tensor_scalar(bq[:], bq[:], scale, None, ALU.mult).then_inc(bias_scaled, 1)
            for b in range(B):
                dve.wait_ge(vp_ready, b + 1)
                nc.vector.tensor_tensor(v[:, b], psP[b % 2][:].rearrange("p (t d) -> p t d", t=KT), bv[:, None, :].to_broadcast((P, KT, D)), ALU.add).then_inc(v_ready, 1)

            def maximum(n):
                dve.wait_ge(s_ready, n + 1)
                c = slice(n % RING, n % RING + 1)
                wait(dve, exp_ready, n - RING + 1)
                link(nc.vector.reduce_max(mx[:, c], psS[n % 2][:], AX.X))
                nc.vector.tensor_scalar(negm[:, c], mx[:, c], -1.0, None, ALU.mult).then_inc(negm_ready, 1)

            def copy_turned(n):
                dve.wait_ge(p_turned, n + 1)
                wait(dve, o_ready, n - 1)
                nc.vector.tensor_copy(prT[n % 2][:], psP[n % 2][:]).then_inc(prT_ready, 1)

            def update(n):
                dve.wait_ge(y_ready, n + 1)
                c = slice(n % RING, n % RING + 1)
                link(nc.vector.reciprocal(rinv[:, c], rsum[:, c]))
                nc.vector.scalar_tensor_tensor(y[:], psA[n % 2][:, 0:D], rinv[:, c], bo[:], ALU.mult, ALU.add).then_inc(y_read, 1)
                dve.wait_ge(y_read, n + 1)
                link(nc.vector.tensor_tensor(xs[n], xs[n], y[:], ALU.add))

            for n in range(NT + LY):
                if n < NT:
                    maximum(n)
                if 0 <= n - LT < NT:
                    copy_turned(n - LT)
                if 0 <= n - LY:
                    update(n - LY)

        @block.tensor
        def _(pe):
            pe.wait_ge(loaded, 16 * NLOAD)
            for b in range(B):
                i = b % 2
                pe.wait_ge(h_ready, TB * (b + 1))
                wait(pe, qT_ready, b - 1)
                for t in range(TB):
                    ins = nc.tensor.transpose(psA[i][:, t * P:(t + 1) * P], h[:, TB * b + t], m.ident[:])
                ins.then_inc(turned, 1)
                if inner_norm:
                    pe.wait_ge(c_ready, KT * (b + 1))
                    wait(pe, ctxT_ready, b - 1)
                    for t in range(KT):
                        ins = nc.tensor.transpose(psO[i][0:DK, t * P:(t + 1) * P], ctx[:, b, t], m.ident[:])
                    ins.then_inc(ctx_turned, 1)
                pe.wait_ge(hT_ready, b + 1)
                nc.tensor.matmul(psA[i][:, S:2 * S], wq[:], hT[i][:], start=True, stop=True).then_inc(q_ready, 1)
                if inner_norm:
                    pe.wait_ge(ctxT_ready, b + 1)
                else:
                    pe.wait_ge(ctx_loaded, 16 * (b + 1))
                wait(pe, kT_ready, b - 1)
                nc.tensor.matmul(psS[i][:], wk[:], ctxT[i][:], start=True, stop=True).then_inc(k_ready, 1)
                wait(pe, v_ready, b - 1)
                for t in range(KT):
                    ins = nc.tensor.matmul(psP[i][:, t * P:(t + 1) * P], ctxT[i][:, t * P:(t + 1) * P], wv[:], start=True, stop=True)
                ins.then_inc(vp_ready, 1)

            def scores(n):
                wait(pe, exp_ready, n - 1)
                nc.tensor.matmul(psS[n % 2][:], qT[:, n // TB, n % TB * P:(n % TB + 1) * P], kT[:, n // TB], start=True, stop=True).then_inc(s_ready, 1)

            def turn_probs(n):
                pe.wait_ge(exp_ready, n + 1)
                wait(pe, prT_ready, n - 1)
                for k in range(KT):
                    ins = nc.tensor.transpose(psP[n % 2][:, k * P:(k + 1) * P], pr[n % 3][:, k * P:(k + 1) * P], m.ident[:])
                ins.then_inc(p_turned, 1)

            def values(n):
                pe.wait_ge(prT_ready, n + 1)
                wait(pe, oT_ready, n - 1)
                for k in range(KT):
                    ins = nc.tensor.matmul(psO[n % 2][:, 0:P], v[:, n // TB, k], prT[n % 2][:, k * P:(k + 1) * P], start=(k == 0), stop=(k == KT - 1))
                ins.then_inc(o_ready, 1)

            def project_out(n):
                pe.wait_ge(oT_ready, n + 1)
                wait(pe, y_read, n - 1)
                nc.tensor.matmul(psA[n % 2][:, 0:D], oT[n % 2][:], wo[:], start=True, stop=True).then_inc(y_ready, 1)

            pe.wait_ge(qT_ready, B)
            pe.wait_ge(kT_ready, B)
            pe.wait_ge(v_ready, B)
            for n in range(NT + LY):
                if n < NT:
                    scores(n)
                if 0 <= n - LT < NT:
                    turn_probs(n - LT)
                if 0 <= n - LV < NT:
                    values(n - LV)
                if 0 <= n - LY:
                    project_out(n - LY)

        @block.scalar
        def _(act):
            act.wait_ge(loaded, 16 * NLOAD)
            act.wait_ge(bias_scaled, 1)
            for b in range(B):
                i = b % 2
                act.wait_ge(turned, b + 1)
                wait(act, q_ready, b - 1)
                if inner_norm:
                    nc.scalar.activation(hT[i][:], psA[i][:, 0:S], ACT.Identity, bias=b1[:], scale=g1[:]).then_inc(hT_ready, 1)
                    act.wait_ge(ctx_turned, b + 1)
                    wait(act, vp_ready, b - 1)
                    nc.scalar.activation(ctxT[i][:], psO[i][0:DK], ACT.Identity, bias=b2[:], scale=g2[:]).then_inc(ctxT_ready, 1)
                else:
                    nc.scalar.copy(hT[i][:], psA[i][:, 0:S]).then_inc(hT_ready, 1)
                act.wait_ge(q_ready, b + 1)
                nc.scalar.activation(qT[:, b], psA[i][:, S:2 * S], ACT.Identity, bias=bq[:], scale=scale).then_inc(qT_ready, 1)
                act.wait_ge(k_ready, b + 1)
                nc.scalar.activation(kT[:, b], psS[i][:], ACT.Identity, bias=bk[:]).then_inc(kT_ready, 1)

            def exponential(n):
                act.wait_ge(negm_ready, n + 1)
                wait(act, p_turned, n - 2)
                wait(act, y_read, n - RING + 1)
                nc.scalar.activation(pr[n % 3][:], psS[n % 2][:], ACT.Exp, bias=negm[:, n % RING:n % RING + 1],
                                     accum_out=rsum[:, n % RING:n % RING + 1]).then_inc(exp_ready, 1)

            def copy_out(n):
                act.wait_ge(o_ready, n + 1)
                wait(act, y_ready, n - 1)
                nc.scalar.copy(oT[n % 2][:], psO[n % 2][:, 0:P]).then_inc(oT_ready, 1)

            for n in range(NT + LV):
                if n < NT:
                    exponential(n)
                if 0 <= n - LV:
                    copy_out(n - LV)


def l1_attn(m):
    layer_attention_heads8(m, "L1_attn", "L1_attn_Wq", "L1_attn_Wk", "L1_attn_Wk", "L1_attn_Wo", None, None, None,
                           "L1_attn_bo", S, float(D) ** -0.5, False)


def l0_xattn(m):
    w = {v: f"L0_xattn_{v}" for v in ("Wq", "Wk", "Wv", "Wo", "bq", "bk", "bv", "bo")}
    layer_attention_heads8(m, "L0_xattn", w["Wq"], w["Wk"], w["Wv"], w["Wo"], w["bq"], w["bk"], w["bv"], w["bo"],
                           SK, 8 ** -0.5, True, clamp=1e4)


def l3_xattn(m):
    p = "L3_xattn_"
    layer_attention_heads8(m, "L3_xattn", p + "q_w", p + "v_w", p + "v_w", p + "o_w", p + "q_b", p + "v_b", p + "v_b", p + "o_b",
                           SK, 8 ** -0.5, True, head_major=True)


STACK = {8: lambda m: layer_selected_experts(m, "L2_ffn"), 6: lambda m: layer_attention_heads64(m, "L2_attn", True), 9: lambda m: layer_attention_heads64(m, "L3_attn", False),
         0: lambda m: layer_gated_recurrence(m, "L0_attn"), 2: lambda m: layer_moe_top8(m, "L0_ffn"), 4: lambda m: layer_attention_single(m, "L1_xattn", 0.25, False), 7: lambda m: layer_attention_single(m, "L2_xattn", float(D) ** -0.5, True),
         5: lambda m: layer_fp4_mlp(m, "L1_ffn"), 11: lambda m: layer_sign_linear(m, "L3_ffn"), 3: l1_attn, 1: l0_xattn, 10: l3_xattn}


HOST_TRANSPOSED = {"L3_ffn_weights", "L3_xattn_q_w", "L3_xattn_v_w", "L3_xattn_o_w", "L0_attn_in_proj_w",
                   "L0_attn_out_proj_w", "L0_attn_fc_w", "L0_attn_proj_w", "L0_ffn_centroids", "L2_ffn_sw1", "L2_ffn_sw2",
                   "L2_ffn_sw3", "L2_ffn_sg_w", "L2_ffn_eg_w", "L3_attn_w_down_q", "L3_attn_w_down_kv", "L3_attn_w_up_q",
                   "L3_attn_w_up_k", "L3_attn_w_up_v", "L3_attn_w_out"}


def build(nc, dram, out):
    with ExitStack() as ctx:
        m = Model(nc, dram, out, ctx)
        setup(m)
        for n in LAYERS:
            STACK[n](m)
        finish(m)


def rotary_tables(tokens, width):
    inv = 1.0 / 10000.0 ** (np.arange(0, width, 2, dtype=np.float32) / width)
    angle = np.outer(np.arange(tokens, dtype=np.float32), inv)
    pick = lambda v: np.concatenate([v, v], -1)[:, ::2]
    cos, sin = (np.repeat(pick(f(angle)).T, 2, axis=0).astype(np.float32) for f in (np.cos, np.sin))
    sign = np.where(np.arange(width) % 2 == 0, -1.0, 1.0).astype(np.float32)[:, None]
    return np.tile(cos, (2, 1)), np.tile(sin * sign, (2, 1))


def kernel(**inputs):
    import concourse.bacc as bacc
    from concourse.bass_utils import run_bass_kernel_spmd as run

    nc = bacc.Bacc("TRN2", target_bir_lowering=False, num_devices=1)
    arrays, dram = {}, {}
    for name, value in inputs.items():
        a = np.asarray(value)
        if name in HOST_TRANSPOSED:
            a = a.T
        if name == "ctx_768":
            dram["ctx_rows"] = nc.dram_tensor("in_ctx_rows", a.shape, mybir.dt.from_np(a.dtype), kind="ExternalInput").ap()
            arrays["in_ctx_rows"] = np.ascontiguousarray(a)
        if name == "ctx_768" or name in ("L2_ffn_ew1", "L2_ffn_ew2", "L2_ffn_ew3"):
            a = a.transpose(0, 2, 1)
        a = np.ascontiguousarray(a)
        arrays[f"in_{name}"] = a
        dram[name] = nc.dram_tensor(f"in_{name}", a.shape, mybir.dt.from_np(a.dtype), kind="ExternalInput").ap()
    def extra(name, a):
        arrays[f"in_{name}"] = a = np.ascontiguousarray(a)
        dram[name] = nc.dram_tensor(f"in_{name}", a.shape, mybir.dt.from_np(a.dtype), kind="ExternalInput").ap()

    for v in "qk":
        a = arrays[f"in_L3_attn_w_up_{v}"]
        extra(f"up_{v}_swapped", a.reshape(a.shape[0], -1, 2)[:, :, ::-1].reshape(a.shape))
    cos, sin = rotary_tables(S, 64)
    extra("rope_cos", cos)
    extra("rope_sin", sin)
    out = nc.dram_tensor("out", (B, S, D), F32, kind="ExternalOutput").ap()
    build(nc, dram, out)
    return run(nc, [arrays], core_ids=[0]).results[0]["out"]
```

```python
import numpy as np
import concourse.bass as bass
from concourse import mybir
from contextlib import ExitStack

F32 = mybir.dt.float32
BF16 = mybir.dt.bfloat16
I32 = mybir.dt.int32
ALU = mybir.AluOpType
ACT = mybir.ActivationFunctionType
AX = mybir.AxisListType

LAYERS = [0, 1, 2, 3, 4, 5, 6, 7, 8, 9, 10, 11]

B, S, D = 8, 256, 128
P = 128
TB = S // P
NT = B * TB
SK, DK = 512, 96
KT = SK // P
LN_EPS = 1e-5


class Links:

    def __init__(self, eng, sem, base=0):
        self.eng, self.sem, self.base, self.n = eng, sem, base, 0

    def mark(self, ins):
        ins.then_inc(self.sem, 1)
        self.n += 1

    def wait(self):
        self.eng.wait_ge(self.sem, self.base + self.n)

    def __call__(self, ins):
        self.mark(ins)
        self.wait()


class Model:

    def __init__(self, nc, dram, out, ctx):
        self.nc, self.dram, self.out, self.ctx = nc, dram, out, ctx
        self.x_stored = ctx.enter_context(nc.semaphore("x_stored"))
        self.x = self.sb("x", [P, B, TB, D], F32)
        self.ident = self.sb("ident", [P, P], F32)
        self.identb = self.sb("identb", [P, P], BF16)
        self.half = self.sb("minus_half", [P, 64], F32)

    def sb(self, name, shape, dt=F32):
        return self.ctx.enter_context(self.nc.sbuf_tensor(name, shape, dt))


def rows(ap):
    return ap.rearrange("(a d) -> a d", a=1)


def setup(m):
    nc = m.nc
    with ExitStack() as es:
        _, _, sem = allocators(nc, es, "setup")
        x_loaded, pool_chain = sem("x_loaded"), sem("pool_chain")
        block = es.enter_context(nc.Block())

        @block.sync
        def _(sp):
            for b in range(B):
                sp.dma_start(m.x[:, b], m.dram["x"][b].rearrange("(t p) d -> p t d", p=P)).then_inc(x_loaded, 16)
            sp.wait_ge(x_loaded, 16 * B)

        @block.gpsimd
        def _(pool):
            link = Links(pool, pool_chain)
            link(nc.gpsimd.memset(m.half[:], -0.5))
            link(nc.gpsimd.memset(m.ident[:], 0.0))
            link(nc.gpsimd.affine_select(out=m.ident[:], in_=m.ident[:], compare_op=ALU.not_equal, fill=1.0,
                                         base=0, pattern=[[-1, P]], channel_multiplier=1))
            link(nc.gpsimd.tensor_copy(m.identb[:], m.ident[:]))


def finish(m):
    nc = m.nc
    x_stored = m.x_stored
    with nc.Block() as block:

        @block.sync
        def _(sp):
            for b in range(B):
                sp.dma_start(m.out[b].rearrange("(t p) d -> p t d", p=P), m.x[:, b]).then_inc(x_stored, 16)
            sp.wait_ge(x_stored, 16 * B)


def wait(eng, sem, count):
    if not isinstance(count, int) or count > 0:
        eng.wait_ge(sem, count)


class Norm:

    def __init__(self, sb, tag="", n=TB):
        self.n = n
        self.stats = sb(f"stats{tag}", [P, n, 6])
        self.s, self.d, self.m2, self.q = (sb(f"{v}{tag}", [P, n]) for v in ("msum", "mdif", "m2", "msq"))
        self.mean, self.veps, self.rstd = (sb(f"{v}{tag}", [P, n]) for v in ("mean", "veps", "rstd"))


def dve_moments(nc, link, w, xs, width, eps):
    for t, x in enumerate(xs):
        link.mark(nc.vector.bn_stats(w.stats[:, t], x))
    link.wait()
    n = len(xs)
    me, mo, ve, vo = w.stats[:, 0:n, 1], w.stats[:, 0:n, 4], w.stats[:, 0:n, 2], w.stats[:, 0:n, 5]
    link.mark(nc.vector.tensor_tensor(w.s[:, 0:n], me, mo, ALU.add))
    link.mark(nc.vector.tensor_tensor(w.d[:, 0:n], me, mo, ALU.subtract))
    link(nc.vector.tensor_tensor(w.m2[:, 0:n], ve, vo, ALU.add))
    link.mark(nc.vector.tensor_scalar(w.mean[:, 0:n], w.s[:, 0:n], 0.5, None, ALU.mult))
    link.mark(nc.vector.tensor_tensor(w.q[:, 0:n], w.d[:, 0:n], w.d[:, 0:n], ALU.mult))
    link(nc.vector.tensor_scalar(w.m2[:, 0:n], w.m2[:, 0:n], 1.0 / width, eps, ALU.mult, ALU.add))
    return nc.vector.scalar_tensor_tensor(w.veps[:, 0:n], w.q[:, 0:n], 0.25, w.m2[:, 0:n], ALU.mult, ALU.add)


def dve_square_mean(nc, link, w, xs, width, eps):
    for t, x in enumerate(xs):
        link.mark(nc.vector.bn_stats(w.stats[:, t], x))
    link.wait()
    n = len(xs)
    me, mo, ve, vo = w.stats[:, 0:n, 1], w.stats[:, 0:n, 4], w.stats[:, 0:n, 2], w.stats[:, 0:n, 5]
    link.mark(nc.vector.tensor_tensor(w.s[:, 0:n], me, me, ALU.mult))
    link.mark(nc.vector.tensor_tensor(w.d[:, 0:n], mo, mo, ALU.mult))
    link(nc.vector.tensor_tensor(w.m2[:, 0:n], ve, vo, ALU.add))
    link.mark(nc.vector.tensor_tensor(w.q[:, 0:n], w.s[:, 0:n], w.d[:, 0:n], ALU.add))
    link(nc.vector.tensor_scalar(w.m2[:, 0:n], w.m2[:, 0:n], 1.0 / width, eps, ALU.mult, ALU.add))
    return nc.vector.scalar_tensor_tensor(w.veps[:, 0:n], w.q[:, 0:n], 0.5, w.m2[:, 0:n], ALU.mult, ALU.add)


def pool_rsqrt(nc, m, w, n=TB):
    return nc.gpsimd.tensor_tensor(w.rstd[:, 0:n], w.veps[:, 0:n], m.half[:, 0:n], ALU.pow)


def allocators(nc, es, pre):
    sems = []

    def clear():
        nc.clear_and_free_semaphores(sems)
        nc.all_engine_barrier()

    es.callback(clear)

    def sem(name):
        sems.append(nc.alloc_semaphore(name=f"{pre}_{name}"))
        return sems[-1]

    sb = lambda name, shape, dt=F32: es.enter_context(nc.sbuf_tensor(f"{pre}_{name}", shape, dt))
    ps = lambda name, shape, dt=F32: es.enter_context(nc.psum_tensor(f"{pre}_{name}", shape, dt))
    return sb, ps, sem


def layer_attention_heads64(m, pre, causal):
    nc = m.nc
    d = m.dram
    H, DH, NPAIR, LAT = 16, 64, 8, 64
    VW = DH + 1
    EPS_SUM = 1e-8 if causal else 0.0
    SCALE = DH ** -0.5
    with ExitStack() as es:
        sb, ps, sem = allocators(nc, es, pre)
        KW = D if causal else LAT
        wq, wk, wv = sb("wq", [P, H * DH]), sb("wk", [P, H * DH]), sb("wv", [P, H * DH])
        if not causal:
            wqs, wks = sb("wqs", [P, H * DH]), sb("wks", [P, H * DH])
            wdq, wdkv, gain, shift = sb("wdq", [P, LAT]), sb("wdkv", [P, LAT]), sb("gain", [P, 1]), sb("shift", [P, 1])
            cosT, sinT = sb("cosT", [P, S]), sb("sinT", [P, S])
            cT, w2 = sb("cT", [P, 2, S]), Norm(sb, "2")
            rotc, rots = ([sb(f"{v}{i}", [P, 2, S]) for i in range(2)] for v in ("rotc", "rots"))
        wo = sb("wo", [P, NPAIR, D])
        bo = sb("bo", [P, D]) if causal else None
        mask = sb("mask", [P, P]) if causal else None
        w = Norm(sb)
        h, hi, hT = [sb(f"hn{i}", [P, TB, D]) for i in range(3)], sb("hi", [P, TB, D]), sb("hT", [P, S])
        qT, kT = [sb(f"q{i}", [P, H, S]) for i in range(2)], [sb(f"k{i}", [P, NPAIR, S]) for i in range(2)]
        V = [sb(f"V{i}", [P, TB, H, VW]) for i in range(2)]
        mx, negm = sb("mx", [P, 4, TB]), sb("negm", [P, 4, TB])
        pr = [sb(f"pr{i}", [P, TB, S]) for i in range(3)]
        prT = [sb(f"prT{i}", [P, 2 * S]) for i in range(3)]
        ao, aoT, rinv = [sb(f"ao{i}", [P, TB, H, DH]) for i in range(2)], sb("aoT", [P, NPAIR, S]), sb("rinv", [P, 4])
        y = sb("y", [P, TB, D])
        psA = [ps(f"psA{i}", [P, 2, S]) for i in range(2)]
        psS, psO = ([ps(f"{v}{i}", [P, TB, S]) for i in range(2)] for v in ("psS", "psO"))
        psT = [ps(f"psT{i}", [P, 2 * S]) for i in range(2)]
        names = ("loaded", "consts", "rows_zeroed", "pool_chain", "dve_chain", "moments", "rstd", "h_ready",
                 "proj_ready", "rotated", "s_ready", "negm_ready", "exp_ready", "masked", "p_turned", "prT_ready", "pv_done",
                 "ao_ready", "x_added")
        (loaded, consts, rows_zeroed, pool_chain, dve_chain, moments, rstd, h_ready,
         proj_ready, rotated, s_ready, negm_ready, exp_ready, masked, p_turned, prT_ready, pv_done,
         ao_ready, x_added) = (sem(n) for n in names)
        bank_read = [sem(f"bank_read{i}") for i in range(2)]
        block = es.enter_context(nc.Block())
        NMOM = 1 if causal else 2
        NQK = NPAIR * (1 if causal else 2)
        NV = TB * 2
        NPJ = NQK + NV
        LT, LV, LN_ = 2, 3, 4
        NH = B * H
        FIRST_P, FIRST_A, SLOT_O = 3, LN_ + 1, LN_ + 6

        def prep_jobs(b):
            return [("T", b, 0)] + ([] if causal else [("C", b, 0)]) + [("P", b, j) for j in range(NPJ)]

        slots = [[] for _ in range(NH + H)]
        for b in range(B):
            if b + 1 < B:
                heads = prep_jobs(b + 1)
                slots[b * H + 1].append(heads.pop(0))
                if not causal:
                    slots[b * H + 2].append(heads.pop(0))
                for j, job in enumerate(heads):
                    slots[b * H + FIRST_P + j * (H - FIRST_P) // NPJ].append(job)
            for q in range(4):
                slots[(b + 1) * H + FIRST_A + q].append(("A", b, q))
            slots[(b + 1) * H + SLOT_O].append(("O", b, 0))
        place = {job: n for n, job in enumerate(prep_jobs(0) + [job for jobs in slots for job in jobs])}

        def await_read(eng, job):
            n = place[job]
            eng.wait_ge(bank_read[n % 2], n // 2 + 1)

        def await_bank(eng, job):
            n = place[job]
            wait(eng, bank_read[n % 2], n // 2)

        blocks = [(0, 0), (0, 1), (1, 1)] if causal else [(0, 0), (0, 1), (1, 0), (1, 1)]
        WB = len(blocks) * P
        loads = []
        if causal:
            loads = [(wq[:], d[f"{pre}_Wq"]), (wk[:], d[f"{pre}_Wkv"][:, 0:H * DH]), (wv[:], d[f"{pre}_Wkv"][:, H * DH:2 * H * DH]),
                     (wo[:], d[f"{pre}_Wo"].rearrange("(n p) c -> p n c", p=P)), (bo[:], rows(d[f"{pre}_bo"]).to_broadcast((P, D)))]
        else:
            loads = [(wq[0:KW], d[f"{pre}_w_up_q"]), (wk[0:KW], d[f"{pre}_w_up_k"]), (wv[0:KW], d[f"{pre}_w_up_v"]),
                     (wo[:], d[f"{pre}_w_out"].rearrange("(n p) c -> p n c", p=P)),
                     (wqs[0:KW], d["up_q_swapped"]), (wks[0:KW], d["up_k_swapped"]), (wdq[:], d[f"{pre}_w_down_q"]), (wdkv[:], d[f"{pre}_w_down_kv"]),
                     (gain[:], d[f"{pre}_ln_scale"].rearrange("(d a) -> d a", a=1)), (shift[:], d[f"{pre}_ln_bias"].rearrange("(d a) -> d a", a=1)),
                     (cosT[:], d["rope_cos"]), (sinT[:], d["rope_sin"])]

        @block.sync
        def _(sp):
            for dst, src in loads:
                sp.dma_start(dst, src).then_inc(loaded, 16)

        @block.gpsimd
        def _(pool):
            link = Links(pool, pool_chain)

            def fills(i):
                link(nc.gpsimd.memset(V[i][:], 1.0))
                for r in range(2):
                    rest = qT[i][(1 - r) * DH:(2 - r) * DH].rearrange("p (n r) c -> p n r c", r=2)[:, :, r]
                    link(nc.gpsimd.memset(rest, 0.0))
                nc.gpsimd.sem_inc(consts, 1)

            def prep(b):
                pool.wait_ge(moments, NMOM * b + 1)
                pool_rsqrt(nc, m, w).then_inc(rstd, 1)
                if not causal:
                    pool.wait_ge(moments, NMOM * b + 2)
                    pool_rsqrt(nc, m, w2).then_inc(rstd, 1)

            def rotate(b):
                for j in range(NPAIR):
                    n = b * NPAIR + j
                    await_read(pool, ("P", b, 2 * j))
                    await_read(pool, ("P", b, 2 * j + 1))
                    wait(pool, pv_done, H * (b - 1))
                    for r in range(2):
                        c = slice(r * DH, (r + 1) * DH)
                        link(nc.gpsimd.tensor_tensor(qT[b % 2][c, 2 * j + r], rotc[j % 2][c, 0], rots[j % 2][c, 0], ALU.add))
                    link(nc.gpsimd.tensor_tensor(kT[b % 2][:, j], rotc[j % 2][:, 1], rots[j % 2][:, 1], ALU.add))
                    nc.gpsimd.sem_inc(rotated, 1)

            def mask_probs(n):
                pool.wait_ge(exp_ready, n + 1)
                for t in range(TB):
                    z = pr[n % 3][:, t, t * P:(t + 1) * P]
                    nc.gpsimd.tensor_tensor(z, z, mask[:], ALU.mult).then_inc(masked, 1)

            fills(0)
            prep(0)
            if causal:
                link(nc.gpsimd.memset(mask[:], 1.0))
                link(nc.gpsimd.affine_select(out=mask[:], in_=mask[:], compare_op=ALU.is_ge, fill=0.0, base=0,
                                             pattern=[[-1, P]], channel_multiplier=1))
            fills(1)
            if not causal:
                rotate(0)
            for b in range(B):
                if b + 1 < B:
                    prep(b + 1)
                    if not causal:
                        rotate(b + 1)
                if causal:
                    for hd in range(H):
                        mask_probs(b * H + hd)

        @block.vector
        def _(dve):
            link = Links(dve, dve_chain)
            if not causal:
                for z in (wq, wk, wv, wqs, wks, cT):
                    link(nc.vector.memset(z[LAT:], 0.0))
                nc.vector.sem_inc(rows_zeroed, 1)

            def norm(b):
                xs, hs = [m.x[:, b, t] for t in range(TB)], [h[b % 3][:, t] for t in range(TB)]
                dve_moments(nc, link, w, xs, D, LN_EPS).then_inc(moments, 1)
                dve.wait_ge(rstd, NMOM * b + 1)
                if b >= 1:
                    await_read(dve, ("T", b - 1, 0))
                if not causal and b >= 3:
                    dve.wait_ge(x_added, b - 2)
                for t in range(TB):
                    ins = nc.vector.tensor_scalar(hs[t], xs[t], w.mean[:, t:t + 1], w.rstd[:, t:t + 1], ALU.subtract, ALU.mult)
                    if causal:
                        ins.then_inc(h_ready, 1)
                    else:
                        link.mark(ins)
                if not causal:
                    link.wait()
                    dve_moments(nc, link, w2, hs, D, LN_EPS).then_inc(moments, 1)
                    dve.wait_ge(rstd, NMOM * b + 2)
                    for t in range(TB):
                        nc.vector.tensor_scalar(hi[:, t], hs[t], w2.mean[:, t:t + 1], w2.rstd[:, t:t + 1], ALU.subtract, ALU.mult).then_inc(h_ready, 1)

            def read(job):
                kind, b, j = job
                bank, free = psA[place[job] % 2], bank_read[place[job] % 2]
                if not (kind == "O" or kind == "P" and (j >= NQK or not causal)):
                    return
                dve.wait_ge(proj_ready, place[job] + 1)
                if kind == "O":
                    other = bo[:, None, :].to_broadcast((P, TB, D)) if causal else h[b % 3][:]
                    nc.vector.tensor_tensor(y[:], bank[:, 0].rearrange("p (t d) -> p t d", t=TB), other, ALU.add).then_inc(free, 1)
                    await_read(dve, job)
                    nc.vector.tensor_tensor(m.x[:, b], m.x[:, b], y[:], ALU.add).then_inc(x_added, 1)
                elif j < NQK:
                    pair, swapped = j // 2, j % 2
                    wait(dve, rotated, b * NPAIR + pair - 1)
                    dst, tab = (rots[pair % 2], sinT) if swapped else (rotc[pair % 2], cosT)
                    nc.vector.tensor_tensor(dst[:], bank[:], tab[:, None, :].to_broadcast((P, 2, S)), ALU.mult).then_inc(free, 1)
                else:
                    t, half = (j - NQK) // 2, (j - NQK) % 2
                    if b == 1:
                        dve.wait_ge(consts, 2)
                    wait(dve, pv_done, H * (b - 1))
                    nc.vector.tensor_copy(V[b % 2][:, t, half * 8:half * 8 + 8, 0:DH],
                                          bank[:].rearrange("p a (c e) -> p (a c) e", e=DH)).then_inc(free, 1)

            def maximum(n):
                dve.wait_ge(s_ready, n + 1)
                wait(dve, exp_ready, n - 3)
                link(nc.vector.reduce_max(mx[:, n % 4], psS[n % 2][:], AX.X))
                nc.vector.tensor_scalar(negm[:, n % 4], mx[:, n % 4], -SCALE, None, ALU.mult).then_inc(negm_ready, 1)

            def copy_turned(n):
                dve.wait_ge(p_turned, n + 1)
                wait(dve, pv_done, n - 2)
                nc.vector.tensor_copy(prT[n % 3][:, 0:WB], psT[n % 2][:, 0:WB]).then_inc(prT_ready, 1)

            def normalise(n):
                b, hd = n // H, n % H
                dve.wait_ge(pv_done, n + 1)
                if hd == 0 and b >= 2:
                    await_read(dve, ("A", b - 2, 2))
                    await_read(dve, ("A", b - 2, 3))
                r = rinv[:, 2 * (n % 2):2 * (n % 2) + 2]
                link(nc.vector.tensor_scalar(r, psO[n % 2][:, :, DH], EPS_SUM, None, ALU.add))
                link(nc.vector.reciprocal(r, r))
                nc.vector.tensor_tensor(ao[b % 2][:, :, hd], psO[n % 2][:, :, 0:DH], r[:, :, None].to_broadcast((P, TB, DH)), ALU.mult).then_inc(ao_ready, 1)

            norm(0)
            dve.wait_ge(loaded, 16 * len(loads))
            dve.wait_ge(consts, 1)
            for job in prep_jobs(0):
                read(job)
            for n in range(NH + H):
                if n % H == 0 and n // H + 1 < B:
                    norm(n // H + 1)
                if n < NH:
                    maximum(n)
                if 0 <= n - LN_ < NH:
                    normalise(n - LN_)
                if 0 <= n - LT < NH:
                    copy_turned(n - LT)
                for job in slots[n]:
                    read(job)

        @block.tensor
        def _(pe):
            pe.wait_ge(loaded, 16 * len(loads))
            pe.wait_ge(consts, 1)
            if not causal:
                pe.wait_ge(rows_zeroed, 1)

            def run(job):
                kind, b, j = job
                bank = psA[place[job] % 2]
                if kind == "T":
                    pe.wait_ge(h_ready, TB * (b + 1))
                elif kind == "A" and j == 0:
                    pe.wait_ge(ao_ready, H * (b + 1))
                elif kind == "C" or kind == "P" and j == 0:
                    await_read(pe, ("T", b, 0) if kind == "C" or causal else ("C", b, 0))
                elif kind == "O":
                    await_read(pe, ("A", b, 2))
                    await_read(pe, ("A", b, 3))
                await_bank(pe, job)
                if kind == "T":
                    src = h[b % 3] if causal else hi
                    for t in range(TB):
                        ins = nc.tensor.transpose(bank[:, 0, t * P:(t + 1) * P], src[:, t], m.ident[:])
                elif kind == "C":
                    nc.tensor.matmul(bank[0:LAT, 0], wdq[:], hT[:], start=True, stop=True)
                    ins = nc.tensor.matmul(bank[0:LAT, 1], wdkv[:], hT[:], start=True, stop=True)
                elif kind == "P" and j < NQK:
                    pair = j if causal else j // 2
                    c = slice(pair * P, (pair + 1) * P)
                    mats = (wq, wk) if causal or j % 2 == 0 else (wqs, wks)
                    for i, mat in enumerate(mats):
                        ins = nc.tensor.matmul(bank[:, i], mat[:, c], hT[:] if causal else cT[:, i], start=True, stop=True)
                elif kind == "P":
                    t, half = (j - NQK) // 2, (j - NQK) % 2
                    lhs = hT[:, t * P:(t + 1) * P] if causal else cT[:, 1, t * P:(t + 1) * P]
                    ins = nc.tensor.matmul(bank[:].rearrange("p a c -> p (a c)"), lhs, wv[:, half * 512:(half + 1) * 512], start=True, stop=True)
                elif kind == "A":
                    for i in range(2):
                        for t in range(TB):
                            pair = 2 * j + i
                            ins = nc.tensor.transpose(bank[:, i, t * P:(t + 1) * P], ao[b % 2][:, t, 2 * pair:2 * pair + 2].rearrange("p h e -> p (h e)"), m.ident[:])
                else:
                    for t in range(TB):
                        for pair in range(NPAIR):
                            ins = nc.tensor.matmul(bank[:, 0, t * D:(t + 1) * D], aoT[:, pair, t * P:(t + 1) * P], wo[:, pair], start=(pair == 0), stop=(pair == NPAIR - 1))
                ins.then_inc(proj_ready, 1)

            def scores(n):
                b, hd = n // H, n % H
                wait(pe, exp_ready, n - 1)
                if n == H:
                    pe.wait_ge(consts, 2)
                if hd == 0:
                    if causal:
                        await_read(pe, ("P", b, NQK - 2))
                        await_read(pe, ("P", b, NQK - 1))
                        pe.wait_ge(rotated, 2 * NQK * (b + 1))
                    else:
                        pe.wait_ge(rotated, NPAIR * (b + 1))
                for t in range(TB):
                    ins = nc.tensor.matmul(psS[n % 2][:, t], qT[b % 2][:, hd, t * P:(t + 1) * P], kT[b % 2][:, hd // 2], start=True, stop=True)
                ins.then_inc(s_ready, 1)

            def turn_probs(n):
                if causal:
                    pe.wait_ge(masked, TB * (n + 1))
                else:
                    pe.wait_ge(exp_ready, n + 1)
                wait(pe, prT_ready, n - 1)
                for i, (k, t) in enumerate(blocks):
                    ins = nc.tensor.transpose(psT[n % 2][:, i * P:(i + 1) * P], pr[n % 3][:, t, k * P:(k + 1) * P], m.ident[:])
                ins.then_inc(p_turned, 1)

            def values(n):
                b, hd = n // H, n % H
                pe.wait_ge(prT_ready, n + 1)
                if hd == 0:
                    await_read(pe, ("P", b, NPJ - 2))
                    await_read(pe, ("P", b, NPJ - 1))
                wait(pe, ao_ready, n - 1)
                for t in range(TB):
                    mine = [(i, k) for i, (k, tt) in enumerate(blocks) if tt == t]
                    for i, k in mine:
                        ins = nc.tensor.matmul(psO[n % 2][:, t, 0:VW], prT[n % 3][:, i * P:(i + 1) * P], V[b % 2][:, k, hd], start=(i == mine[0][0]), stop=(i == mine[-1][0]))
                ins.then_inc(pv_done, 1)

            for job in prep_jobs(0):
                run(job)
            for n in range(NH + H):
                if n < NH:
                    scores(n)
                if 0 <= n - LT < NH:
                    turn_probs(n - LT)
                if 0 <= n - LV < NH:
                    values(n - LV)
                for job in slots[n]:
                    run(job)

        @block.scalar
        def _(act):
            act.wait_ge(loaded, 16 * len(loads))
            act.wait_ge(consts, 1)

            def read(job):
                kind, b, j = job
                bank, free = psA[place[job] % 2], bank_read[place[job] % 2]
                if kind == "O" or kind == "P" and (j >= NQK or not causal):
                    return
                act.wait_ge(proj_ready, place[job] + 1)
                if kind == "T":
                    if causal:
                        nc.scalar.copy(hT[:], bank[:, 0]).then_inc(free, 1)
                    else:
                        nc.scalar.activation(hT[:], bank[:, 0], ACT.Identity, bias=shift[:], scale=gain[:]).then_inc(free, 1)
                elif kind == "C":
                    nc.scalar.copy(cT[0:LAT], bank[0:LAT]).then_inc(free, 1)
                elif kind == "P":
                    if b == 1:
                        act.wait_ge(consts, 2)
                    wait(act, pv_done, H * (b - 1))
                    for r in range(2):
                        c = slice(r * DH, (r + 1) * DH)
                        nc.scalar.copy(qT[b % 2][c, 2 * j + r], bank[c, 0]).then_inc(rotated, 1)
                    nc.scalar.copy(kT[b % 2][:, j], bank[:, 1]).then_inc(free, 1)
                else:
                    nc.scalar.copy(aoT[:, 2 * j:2 * j + 2], bank[:]).then_inc(free, 1)

            def exps(n):
                act.wait_ge(negm_ready, n + 1)
                wait(act, p_turned, n - 2)
                for t in range(TB):
                    width = (t + 1) * P if causal else S
                    ins = nc.scalar.activation(pr[n % 3][:, t, 0:width], psS[n % 2][:, t, 0:width], ACT.Exp, bias=negm[:, n % 4, t:t + 1], scale=SCALE)
                ins.then_inc(exp_ready, 1)

            for job in prep_jobs(0):
                read(job)
            for n in range(NH + H):
                if n < NH:
                    exps(n)
                for job in slots[n]:
                    read(job)


def layer_attention_heads8(m, pre, wq, wk, wv, wo, bq, bk, bv, bo, keys, scale, from_ctx, head_major=False, clamp=None):
    nc = m.nc
    H, DH = 16, 8
    PARTS = 3
    PAIR = PARTS * PARTS * DH
    MAXROW = 96
    NKT = keys // P
    NU = NKT // 2
    HG, HW = 4, 32
    NG = H // HG
    CK = DK if from_ctx else D
    SPB = keys // 256
    NREG = 2 * PARTS * PARTS
    k_on_dve = keys == S
    LW = 2 if clamp else 1
    LG = HG + LW
    NPS, NPT = 3, 8
    NSU = H * SPB
    LAST_S = 11
    T_H, T_Q, T_K, T_V, T_O, T_Y, T_M = 2, 3, 4, 5, 8, 9, 11
    s_until = [min(NSU, -(-(hd + 1) * NSU // LAST_S)) for hd in range(H)]
    s_units = [list(range(s_until[hd - 1] if hd else 0, s_until[hd])) for hd in range(H)]
    with ExitStack() as es:
        sb, ps, sem = allocators(nc, es, pre)
        wq_s, wk_s, wv_s, wo_s = sb("wq", [P, D]), sb("wk", [CK, D]), sb("wv", [CK, D]), sb("wo", [P, D])
        bq_s, bk_s = sb("bq", [P, 1]), sb("bk", [P, 1])
        bv_s, bo_s = sb("bv", [P, D]), sb("bo", [P, D])
        ctxT = sb("ctxT", [CK, 2, keys]) if from_ctx else None
        w = Norm(sb)
        h, hT = sb("h", [P, TB, D]), sb("hT", [P, S])
        qf, kf = sb("qf", [P, S]), sb("kf", [P, keys])
        qs, ks = sb("qs", [P, PARTS, S], BF16), sb("ks", [P, PARTS, keys], BF16)
        QR = [sb(f"QR{i}", [P, H, S], BF16) for i in range(3)]
        KR = [sb(f"KR{i}", [P, H, keys], BF16) for i in range(3)]
        V = [sb(f"V{i}", [P, NKT, H, HW]) for i in range(3)]
        mx = sb("mx", [P, TB, H])
        negm, mp = sb("negm", [H, S]), sb("mp", [H, PARTS, S], BF16)
        PT = [sb(f"PT{i}", [P, 2, S]) for i in range(NPT)]
        ot = [sb(f"ot{i}", [P, S]) for i in range(2)]
        rinv, ao, aoT = sb("rinv", [P, TB, HG]), sb("ao", [P, 2, TB, H, DH]), sb("aoT", [P, S])
        ao2 = sb("ao2", [P, TB, D]) if head_major else None
        y = sb("y", [P, TB, D])
        floor, floor_w = (sb("floor", [H, S]), [sb(f"floor_w{i}", [P, H, S]) for i in range(2)]) if clamp else (None, None)
        minus_clamp = sb("minus_clamp", [H, 1]) if clamp else None
        f_dram = nc.dram_tensor(f"{pre}_staged_floor", (H, S), F32, kind="Internal").ap() if clamp else None
        psS = [ps(f"psS{i}", [P, 512]) for i in range(2)]
        psT = [ps(f"psT{i}", [P, 2, S]) for i in range(NPS)]
        psO, psOT, psM = ps("psO", [P, 2, S]), ps("psOT", [P, TB, HG, HW]), ps("psM", [P, 512])
        q_dram = nc.dram_tensor(f"{pre}_q_parts", (PARTS, P, S), BF16, kind="Internal").ap()
        k_dram = nc.dram_tensor(f"{pre}_k_parts", (PARTS, P, keys), BF16, kind="Internal").ap()
        m_dram = nc.dram_tensor(f"{pre}_m_parts", (PARTS, H, S), BF16, kind="Internal").ap()
        o_dram = nc.dram_tensor(f"{pre}_o_heads", (H, S, DH), F32, kind="Internal").ap() if head_major else None
        names = ("loaded", "bias_scaled", "rows_set", "clamp_set", "negm_ready", "floor_ready", "floor_staged", "floor_spread", "clamped", "dve_chain", "pool_chain", "var_ready", "rstd_ready", "h_ready", "turned",
                 "hT_ready", "q_proj", "qf_ready", "k_proj", "kf_ready", "v_proj", "v_ready", "q_split", "k_split", "q_staged",
                 "k_staged", "m_staged", "regrouped", "s_ready", "s_used", "mx_turned", "m_split", "m_rows", "st_ready",
                 "exp_ready", "pv_done", "ot_ready", "group_turned", "ao_ready", "o_staged", "ao_back", "ao_turned", "aoT_ready",
                 "out_ready", "x_done")
        (loaded, bias_scaled, rows_set, clamp_set, negm_ready, floor_ready, floor_staged, floor_spread, clamped, dve_chain, pool_chain, var_ready, rstd_ready, h_ready, turned,
         hT_ready, q_proj, qf_ready, k_proj, kf_ready, v_proj, v_ready, q_split, k_split, q_staged,
         k_staged, m_staged, regrouped, s_ready, s_used, mx_turned, m_split, m_rows, st_ready,
         exp_ready, pv_done, ot_ready, group_turned, ao_ready, o_staged, ao_back, ao_turned, aoT_ready,
         out_ready, x_done) = (sem(n) for n in names)
        ctx_loaded = [sem("ctx_loaded0"), sem("ctx_loaded1")]
        block = es.enter_context(nc.Block())
        NLOAD = 8 if bq is not None else 5

        @block.sync
        def _(sp):
            loads = [(wq_s[:], m.dram[wq]), (wk_s[:], m.dram[wk]), (wv_s[:], m.dram[wv]), (wo_s[:], m.dram[wo]),
                     (bo_s[:], rows(m.dram[bo]).to_broadcast((P, D)))]
            if bq is not None:
                loads += [(bq_s[:], m.dram[bq].rearrange("(d a) -> d a", a=1)), (bk_s[:], m.dram[bk].rearrange("(d a) -> d a", a=1)),
                          (bv_s[:], rows(m.dram[bv]).to_broadcast((P, D)))]
            for dst, src in loads:
                sp.dma_start(dst, src).then_inc(loaded, 16)

            def load_ctx(b):
                if from_ctx:
                    wait(sp, v_proj, b - 1)
                    sp.dma_start(ctxT[:, b % 2], m.dram["ctx_768"][b]).then_inc(ctx_loaded[b % 2], 16)

            def regroup(b):
                wait(sp, st_ready, NU * H * (b - 2))
                wait(sp, regrouped, 16 * NREG * b)
                if b < 3:
                    sp.wait_ge(rows_set, 2 * (b + 1))
                sp.wait_ge(q_split, b + 1)
                sp.dma_start(q_dram.rearrange("i p c -> p i c"), qs[:]).then_inc(q_staged, 16)
                sp.wait_ge(k_split, b + 1)
                sp.dma_start(k_dram.rearrange("i p c -> p i c"), ks[:]).then_inc(k_staged, 16)
                sp.wait_ge(q_staged, 16 * (b + 1))
                for i in range(PARTS):
                    for j in range(PARTS):
                        r = (i * PARTS + j) * DH
                        sp.dma_start(QR[b % 3][r:r + DH], q_dram[i].rearrange("(h d) c -> d h c", d=DH)).then_inc(regrouped, 16)
                sp.wait_ge(k_staged, 16 * (b + 1))
                for i in range(PARTS):
                    for j in range(PARTS):
                        r = (i * PARTS + j) * DH
                        sp.dma_start(KR[b % 3][r:r + DH], k_dram[j].rearrange("(h d) c -> d h c", d=DH)).then_inc(regrouped, 16)

            def reread(b):
                if head_major:
                    sp.wait_ge(ao_ready, NG * (b + 1))
                    for t in range(TB):
                        sp.dma_start(o_dram[:, t * P:(t + 1) * P].rearrange("h q d -> q h d"), ao[:, b % 2, t]).then_inc(o_staged, 16)
                    sp.wait_ge(o_staged, 16 * TB * (b + 1))
                    wait(sp, ao_turned, b)
                    flat = o_dram.rearrange("h (l r) d -> (h l) (r d)", r=D // DH)
                    sp.dma_start(ao2[:], flat.rearrange("(t p) c -> p t c", p=P)).then_inc(ao_back, 16)

            load_ctx(0)
            load_ctx(1)
            regroup(0)
            regroup(1)
            for b in range(B):
                if b + 2 < B:
                    load_ctx(b + 2)
                if b >= 1:
                    reread(b - 1)
                if b + 2 < B:
                    regroup(b + 2)
            reread(B - 1)

        def split(eng, link, src, parts):
            link(eng.tensor_copy(parts[:, 0], src[:]))
            link(eng.tensor_tensor(src[:], src[:], parts[:, 0], ALU.subtract))
            link(eng.tensor_copy(parts[:, 1], src[:]))
            link(eng.tensor_tensor(src[:], src[:], parts[:, 1], ALU.subtract))
            return eng.tensor_copy(parts[:, 2], src[:])

        @block.gpsimd
        def _(pool):
            link = Links(pool, pool_chain)

            def fixed_rows(i):
                nc.gpsimd.memset(KR[i][:], 1.0).then_inc(rows_set, 1)
                nc.gpsimd.memset(QR[i][:], 0.0).then_inc(rows_set, 1)

            if clamp:
                nc.gpsimd.memset(minus_clamp[:], -clamp).then_inc(clamp_set, 1)
            fixed_rows(0)

            for b in range(B):
                pool.wait_ge(var_ready, b + 1)
                pool_rsqrt(nc, m, w).then_inc(rstd_ready, 1)
                pool.wait_ge(qf_ready, b + 1)
                wait(pool, q_staged, 16 * b)
                split(nc.gpsimd, link, qf, qs).then_inc(q_split, 1)
                if not k_on_dve:
                    pool.wait_ge(kf_ready, b + 1)
                    wait(pool, k_staged, 16 * b)
                    split(nc.gpsimd, link, kf, ks).then_inc(k_split, 1)
                if b == 1:
                    fixed_rows(1)
                    fixed_rows(2)

        @block.vector
        def _(dve):
            link = Links(dve, dve_chain)

            def moments(b):
                dve_moments(nc, link, w, [m.x[:, b, t] for t in range(TB)], D, LN_EPS).then_inc(var_ready, 1)

            def norm(b):
                dve.wait_ge(rstd_ready, b + 1)
                wait(dve, turned, b)
                for t in range(TB):
                    nc.vector.tensor_scalar(h[:, t], m.x[:, b, t], w.mean[:, t:t + 1], w.rstd[:, t:t + 1], ALU.subtract, ALU.mult).then_inc(h_ready, 1)

            def split_k(b):
                if k_on_dve:
                    dve.wait_ge(kf_ready, b + 1)
                    wait(dve, k_staged, 16 * b)
                    split(nc.vector, link, kf, ks).then_inc(k_split, 1)

            def values(b):
                dve.wait_ge(v_proj, b + 1)
                wait(dve, pv_done, H * (b - 2))
                for t in range(NKT):
                    src = psM[:, t * D:(t + 1) * D].rearrange("p (h d) -> p h d", d=DH)
                    if bq is not None:
                        nc.vector.tensor_tensor(V[b % 3][:, t, :, 0:DH], src, bv_s[:].rearrange("p (h d) -> p h d", d=DH), ALU.add).then_inc(v_ready, 1)
                    else:
                        nc.vector.tensor_copy(V[b % 3][:, t, :, 0:DH], src).then_inc(v_ready, 1)

            def maxima(b, unit):
                n = b * NSU + unit
                hd, u = unit // SPB, unit % SPB
                dve.wait_ge(s_ready, n + 1)
                if unit == 0:
                    wait(dve, mx_turned, b)
                if SPB == 2:
                    nc.vector.reduce_max(mx[:, u, hd:hd + 1], psS[n % 2][:], AX.X).then_inc(s_used, 1)
                else:
                    nc.vector.reduce_max(mx[:, :, hd], psS[n % 2][:].rearrange("p (t k) -> p t k", t=TB), AX.X).then_inc(s_used, 1)

            def clamp_probs(n):
                b, hd = n // NU // H, n // NU % H
                dve.wait_ge(exp_ready, n + 1)
                if n % (NU * H) == 0:
                    dve.wait_ge(floor_spread, 16 * (b + 1))
                at = PT[n % NPT][:]
                nc.vector.scalar_tensor_tensor(at, at, 1.0, floor_w[b % 2][:, hd, None, :].to_broadcast((P, 2, S)), ALU.min, ALU.max).then_inc(clamped, 1)

            def split_max(b):
                dve.wait_ge(mx_turned, b + 1)
                wait(dve, m_staged, 16 * b)
                if clamp:
                    wait(dve, floor_ready, b)
                    link(nc.vector.tensor_scalar(negm[:], psM[0:H, 0:S], clamp, -clamp, ALU.min, ALU.max))
                    nc.vector.tensor_scalar(negm[:], negm[:], -1.0, None, ALU.mult).then_inc(negm_ready, 1)
                    dve.wait_ge(negm_ready, b + 1)
                else:
                    link(nc.vector.tensor_scalar(negm[:], psM[0:H, 0:S], -1.0, None, ALU.mult))
                link(nc.vector.tensor_copy(mp[:, 0], negm[:]))
                if clamp:
                    dve.wait_ge(floor_ready, b + 1)
                link(nc.vector.tensor_tensor(negm[:], negm[:], mp[:, 0], ALU.subtract))
                link(nc.vector.tensor_copy(mp[:, 1], negm[:]))
                link(nc.vector.tensor_tensor(negm[:], negm[:], mp[:, 1], ALU.subtract))
                nc.vector.tensor_copy(mp[:, 2], negm[:]).then_inc(m_split, 1)

            def normalise(g):
                b, hg = g // NG, g % NG
                dve.wait_ge(group_turned, g + 1)
                link(nc.vector.reciprocal(rinv[:], psOT[:, :, :, DH]))
                if hg == 0:
                    if head_major:
                        wait(dve, o_staged, 16 * TB * (b - 1))
                    else:
                        wait(dve, ao_turned, b - 1)
                nc.vector.tensor_tensor(ao[:, b % 2, :, hg * HG:(hg + 1) * HG, :], psOT[:, :, :, 0:DH],
                                        rinv[:][:, :, :, None].to_broadcast((P, TB, HG, DH)), ALU.mult).then_inc(ao_ready, 1)

            def update(b):
                dve.wait_ge(out_ready, b + 1)
                link(nc.vector.tensor_tensor(y[:], psM[:, 0:S].rearrange("p (t d) -> p t d", t=TB), bo_s[:, None, :].to_broadcast((P, TB, D)), ALU.add))
                nc.vector.tensor_tensor(m.x[:, b], m.x[:, b], y[:], ALU.add).then_inc(x_done, 1)

            moments(0)
            for i in range(3):
                link(nc.vector.memset(V[i][:], 1.0))
            dve.wait_ge(loaded, 16 * NLOAD)
            if bq is not None:
                nc.vector.tensor_scalar(bq_s[:], bq_s[:], scale, None, ALU.mult).then_inc(bias_scaled, 1)
            norm(0)
            split_k(0)
            values(0)
            moments(1)
            norm(1)
            split_k(1)
            values(1)
            for unit in range(NSU):
                maxima(0, unit)
            split_max(0)
            for b in range(B):
                for hd in range(H):
                    n = b * H + hd
                    if hd == 0 and b + 2 < B:
                        moments(b + 2)
                    if b + 1 < B:
                        for unit in s_units[hd]:
                            maxima(b + 1, unit)
                    if clamp and n >= 1:
                        for u in range(NU):
                            clamp_probs((n - 1) * NU + u)
                    if hd == 1 and b + 2 < B:
                        norm(b + 2)
                    if n > LG and (n - LG - 1) % HG == 0:
                        normalise((n - LG - 1) // HG)
                    if hd == T_V and b + 2 < B:
                        split_k(b + 2)
                        values(b + 2)
                    if hd == T_Y and b >= 1:
                        update(b - 1)
                    if hd == T_M and b + 1 < B:
                        split_max(b + 1)
            for u in range(NU if clamp else 0):
                clamp_probs((B * H - 1) * NU + u)
            normalise(B * NG - 1)
            update(B - 1)

        @block.tensor
        def _(pe):
            pe.wait_ge(loaded, 16 * NLOAD)

            def turn(b):
                pe.wait_ge(h_ready, TB * (b + 1))
                for t in range(TB):
                    ins = nc.tensor.transpose(psM[:, t * P:(t + 1) * P], h[:, t], m.ident[:])
                ins.then_inc(turned, 1)

            def project_q(b):
                pe.wait_ge(hT_ready, b + 1)
                nc.tensor.matmul(psM[:, 0:S], wq_s[:], hT[:], start=True, stop=True).then_inc(q_proj, 1)

            def kv_source(b):
                return ctxT[:, b % 2] if from_ctx else hT[:]

            def project_k(b):
                if from_ctx:
                    pe.wait_ge(ctx_loaded[b % 2], 16 * (b // 2 + 1))
                pe.wait_ge(qf_ready, b + 1)
                nc.tensor.matmul(psM[:, 0:keys], wk_s[:], kv_source(b), start=True, stop=True).then_inc(k_proj, 1)

            def project_v(b):
                pe.wait_ge(kf_ready, b + 1)
                for t in range(NKT):
                    ins = nc.tensor.matmul(psM[:, t * D:(t + 1) * D], kv_source(b)[:, t * P:(t + 1) * P], wv_s[:], start=True, stop=True)
                ins.then_inc(v_proj, 1)

            def scores(b, unit):
                n = b * NSU + unit
                hd = unit // SPB
                if unit == 0:
                    pe.wait_ge(regrouped, 16 * NREG * (b + 1))
                wait(pe, s_used, n - 1)
                tiles = [unit % SPB] if SPB == 2 else range(TB)
                for i, t in enumerate(tiles):
                    ins = nc.tensor.matmul(psS[n % 2][:, i * keys:(i + 1) * keys], QR[b % 3][0:MAXROW, hd, t * P:(t + 1) * P], KR[b % 3][0:MAXROW, hd, :], start=True, stop=True)
                ins.then_inc(s_ready, 1)

            def turn_max(b):
                pe.wait_ge(s_used, H * SPB * (b + 1))
                for t in range(TB):
                    ins = nc.tensor.transpose(psM[0:H, t * P:(t + 1) * P], mx[:, t], m.ident[:])
                ins.then_inc(mx_turned, 1)

            def scores_turned(b, hd, u):
                if hd == 0 and u == 0:
                    pe.wait_ge(m_rows, 16 * (b + 1))
                n = (b * H + hd) * NU + u
                wait(pe, exp_ready, n - NPS + 1)
                for k in range(2):
                    kt = 2 * u + k
                    ins = nc.tensor.matmul(psT[n % NPS][:, k], KR[b % 3][:, hd, kt * P:(kt + 1) * P], QR[b % 3][:, hd, :], start=True, stop=True)
                ins.then_inc(st_ready, 1)

            def weigh(b, hd):
                g = (b * H + hd) // HG
                if hd == 0:
                    pe.wait_ge(v_ready, NKT * (b + 1))
                if hd % HG == 0:
                    wait(pe, ot_ready, g)
                for u in range(NU):
                    n = (b * H + hd) * NU + u
                    pe.wait_ge(clamped if clamp else exp_ready, n + 1)
                    for k in range(2):
                        kt = 2 * u + k
                        r = hd % HG * HW
                        ins = nc.tensor.matmul(psO[r:r + HW, g % 2], V[b % 3][:, kt, hd], PT[n % NPT][:, k], start=(kt == 0), stop=(kt == NKT - 1))
                ins.then_inc(pv_done, 1)

            def turn_group(g):
                pe.wait_ge(ot_ready, g + 1)
                wait(pe, ao_ready, g)
                for t in range(TB):
                    ins = nc.tensor.transpose(psOT[:, t].rearrange("p h w -> p (h w)"), ot[g % 2][:, t * P:(t + 1) * P], m.ident[:])
                ins.then_inc(group_turned, 1)

            def turn_out(b):
                if head_major:
                    pe.wait_ge(ao_back, 16 * (b + 1))
                else:
                    pe.wait_ge(ao_ready, NG * (b + 1))
                for t in range(TB):
                    src = ao2[:, t] if head_major else ao[:, b % 2, t].rearrange("p h d -> p (h d)")
                    ins = nc.tensor.transpose(psM[:, t * P:(t + 1) * P], src, m.ident[:])
                ins.then_inc(ao_turned, 1)

            def project_out(b):
                pe.wait_ge(aoT_ready, b + 1)
                for t in range(TB):
                    ins = nc.tensor.matmul(psM[:, t * D:(t + 1) * D], aoT[:, t * P:(t + 1) * P], wo_s[:], start=True, stop=True)
                ins.then_inc(out_ready, 1)

            for b in range(2):
                wait(pe, v_ready, NKT * b)
                turn(b)
                project_q(b)
                project_k(b)
                project_v(b)
            for unit in range(NSU):
                scores(0, unit)
            pe.wait_ge(v_ready, NKT * 2)
            turn_max(0)
            for b in range(B):
                for hd in range(H):
                    n = b * H + hd
                    more = b + 2 < B
                    if hd == T_H and more:
                        pe.wait_ge(m_split, b + 1)
                        turn(b + 2)
                    if hd == T_Q and more:
                        project_q(b + 2)
                    if hd == T_K and more:
                        project_k(b + 2)
                    if hd == T_V and more:
                        project_v(b + 2)
                    if hd == T_O and b >= 1:
                        if more:
                            pe.wait_ge(v_ready, NKT * (b + 3))
                        else:
                            pe.wait_ge(m_split, b + 1)
                        turn_out(b - 1)
                    if hd == T_Y and b >= 1:
                        project_out(b - 1)
                    if hd == T_M and b + 1 < B:
                        wait(pe, x_done, b)
                        if b == 0:
                            pe.wait_ge(v_ready, NKT * 3)
                        turn_max(b + 1)
                    if n > LG and (n - LG - 1) % HG == 0:
                        turn_group((n - LG - 1) // HG)
                    units = list(s_units[hd]) if b + 1 < B else []
                    for u in range(NU):
                        if units:
                            scores(b + 1, units.pop(0))
                        scores_turned(b, hd, u)
                    for unit in units:
                        scores(b + 1, unit)
                    if n >= LW:
                        weigh((n - LW) // H, (n - LW) % H)
            for hd in range(H - LW, H):
                weigh(B - 1, hd)
            turn_group(B * NG - 1)
            turn_out(B - 1)
            project_out(B - 1)

        @block.scalar
        def _(act):
            if bq is not None:
                act.wait_ge(bias_scaled, 1)

            def copy_h(b):
                act.wait_ge(turned, b + 1)
                nc.scalar.copy(hT[:], psM[:, 0:S]).then_inc(hT_ready, 1)

            def copy_q(b):
                act.wait_ge(q_proj, b + 1)
                wait(act, q_split, b)
                nc.scalar.activation(qf[:], psM[:, 0:S], ACT.Identity, bias=bq_s[:] if bq is not None else 0.0, scale=scale).then_inc(qf_ready, 1)

            def copy_k(b):
                act.wait_ge(k_proj, b + 1)
                wait(act, k_split, b)
                nc.scalar.activation(kf[:], psM[:, 0:keys], ACT.Identity, bias=bk_s[:] if bq is not None else 0.0).then_inc(kf_ready, 1)

            def copy_group(g):
                act.wait_ge(pv_done, HG * (g + 1))
                wait(act, group_turned, g - 1)
                nc.scalar.copy(ot[g % 2][:], psO[:, g % 2]).then_inc(ot_ready, 1)

            def copy_out(b):
                act.wait_ge(ao_turned, b + 1)
                nc.scalar.copy(aoT[:], psM[:, 0:S]).then_inc(aoT_ready, 1)

            def floors(b):
                if clamp:
                    act.wait_ge(negm_ready, b + 1)
                    wait(act, floor_staged, 16 * b)
                    nc.scalar.activation(floor[:], negm[:], ACT.Exp, bias=minus_clamp[:]).then_inc(floor_ready, 1)

            def stage_max(b):
                act.wait_ge(m_split, b + 1)
                nc.scalar.dma_start(m_dram.rearrange("i h c -> h i c"), mp[:]).then_inc(m_staged, 16)
                if clamp:
                    act.wait_ge(floor_ready, b + 1)
                    wait(act, floor_spread, 16 * b)
                    nc.scalar.dma_start(f_dram, floor[:]).then_inc(floor_staged, 16)

            def max_rows(b):
                act.wait_ge(m_staged, 16 * (b + 1))
                nc.scalar.dma_start(QR[b % 3][MAXROW:MAXROW + PARTS], m_dram).then_inc(m_rows, 16)
                if clamp:
                    act.wait_ge(floor_staged, 16 * (b + 1))
                    wait(act, clamped, NU * H * (b - 1))
                    nc.scalar.dma_start(floor_w[b % 2][:].rearrange("p h s -> p (h s)"),
                                        rows(f_dram.rearrange("h s -> (h s)")).to_broadcast((P, H * S))).then_inc(floor_spread, 16)

            if clamp:
                act.wait_ge(clamp_set, 1)
            for b in range(2):
                copy_h(b)
                copy_q(b)
                copy_k(b)
            floors(0)
            stage_max(0)
            max_rows(0)
            for b in range(B):
                for hd in range(H):
                    more = b + 2 < B
                    if hd == T_H and more:
                        copy_h(b + 2)
                    if hd == T_Q and more:
                        copy_q(b + 2)
                    if hd == T_K and more:
                        copy_k(b + 2)
                    if hd == T_O and b >= 1:
                        copy_out(b - 1)
                    n = b * H + hd
                    if n >= LG and (n - LG) % HG == 0:
                        copy_group((n - LG) // HG)
                    for u in range(NU):
                        n = (b * H + hd) * NU + u
                        act.wait_ge(st_ready, n + 1)
                        wait(act, pv_done, (n - NPT) // NU + 1)
                        nc.scalar.activation(PT[n % NPT][:], psT[n % NPS][:], ACT.Exp).then_inc(exp_ready, 1)
                    if hd == T_M and b + 1 < B:
                        floors(b + 1)
                    if hd == T_M + 1 and b + 1 < B:
                        stage_max(b + 1)
                    if hd == T_M + 2 and b + 1 < B:
                        max_rows(b + 1)
            copy_group(B * NG - 1)
            copy_out(B - 1)


def layer_fp4_mlp(m, pre):
    nc = m.nc
    d = m.dram
    BLK, FI = 16, 352
    CH = [(0, 128), (128, 128), (256, 96)]
    REST = CH[2][1]
    with ExitStack() as es:
        sb, ps, sem = allocators(nc, es, pre)
        WU, WD, WALL = 3 * D, 6 * D, 6 * D + FI
        wall = sb("wall", [P, WALL])
        wguT, wdT = sb("wguT", [P, 2, FI]), sb("wdT", [P, 3, D])
        w = Norm(sb, "", NT)
        h, f = sb("h", [P, NT, D]), sb("f", [P, NT, FI])
        hT, g = [sb(f"hT{i}", [P, S]) for i in range(2)], [sb(f"g{i}", [P, TB, FI]) for i in range(2)]
        fT = sb("fT", [P, 3, S])
        HALF, GRP = NT // 2, 2 * TB
        fl = lambda v: v.rearrange("p t d -> p (t d)")
        groups = [(fl(h[:, 0:HALF]), HALF * D), (wall[:], WALL), (fl(h[:, HALF:]), HALF * D)]
        groups += [(fl(f[:, GRP * k:GRP * (k + 1)]), GRP * FI) for k in range(NT // GRP)]
        RING, WIDE = 3, max(n for _, n in groups)
        mag, sg = ([sb(f"{v}{i}", [P, WIDE]) for i in range(RING)] for v in ("mag", "sg"))
        lev, low = sb("lev", [P, WIDE]), sb("low", [P, WIDE])
        bmax, bscale, binv, bhalf = ([sb(f"{v}{i}", [P, WIDE // BLK]) for i in range(RING)] for v in ("bmax", "bscale", "binv", "bhalf"))
        psA, psG, psU, psF, psY = ps("psA", [P, 512]), ps("psG", [P, TB, 512]), ps("psU", [P, TB, 512]), ps("psF", [P, 2, 512]), ps("psY", [P, TB, D])
        names = ("loaded", "zeroed", "dve_chain", "w_turned", "wT_ready", "moments", "rstd", "h_ready", "parted", "scaled",
                 "normed", "quantised", "turned", "hT_ready", "gu_ready", "silu_ready", "f_ready", "f_turned", "fT_ready", "y_ready", "x_done")
        (loaded, zeroed, dve_chain, w_turned, wT_ready, moments, rstd, h_ready, parted, scaled,
         normed, quantised, turned, hT_ready, gu_ready, silu_ready, f_ready, f_turned, fT_ready, y_ready, x_done) = (sem(n) for n in names)
        block = es.enter_context(nc.Block())
        NLOAD = 7
        F0 = 3

        @block.sync
        def _(sp):
            sp.wait_ge(zeroed, 1)
            for n, (c, k) in enumerate(CH):
                sp.dma_start(wall[0:k, n * D:(n + 1) * D], d[f"{pre}_w_gate"][c:c + k]).then_inc(loaded, 16)
                sp.dma_start(wall[0:k, WU + n * D:WU + (n + 1) * D], d[f"{pre}_w_up"][c:c + k]).then_inc(loaded, 16)
            sp.dma_start(wall[:, WD:], d[f"{pre}_w_down"]).then_inc(loaded, 16)

        @block.gpsimd
        def _(pool):
            nc.gpsimd.memset(wall[:], 0.0).then_inc(zeroed, 1)
            pool.wait_ge(moments, 1)
            pool_rsqrt(nc, m, w, NT).then_inc(rstd, 1)
            for p, (_, width) in enumerate(groups):
                i, nb = p % RING, width // BLK
                blocks = lambda v: v[:, 0:width].rearrange("p (n e) -> p n e", e=BLK)
                wide = lambda v: v[:, 0:nb][:, :, None].to_broadcast((P, nb, BLK))
                pool.wait_ge(scaled, p + 1)
                nc.gpsimd.tensor_tensor(blocks(mag[i]), blocks(mag[i]), wide(binv[i]), ALU.mult).then_inc(normed, 1)
                nc.gpsimd.tensor_tensor(blocks(sg[i]), blocks(sg[i]), wide(bhalf[i]), ALU.mult).then_inc(normed, 1)

        @block.vector
        def _(dve):
            link = Links(dve, dve_chain)

            def scales(p):
                i, width = p % RING, groups[p][1]
                nb = width // BLK
                dve.wait_ge(parted, 2 * (p + 1))
                link(nc.vector.tensor_reduce(bmax[i][:, 0:nb], mag[i][:, 0:width].rearrange("p (n e) -> p n e", e=BLK), AX.X, ALU.max))
                link(nc.vector.tensor_scalar(bscale[i][:, 0:nb], bmax[i][:, 0:nb], 1.0 / 6.0, 1e-12, ALU.mult, ALU.max))
                link.mark(nc.vector.tensor_scalar(bhalf[i][:, 0:nb], bscale[i][:, 0:nb], 0.5, None, ALU.mult))
                link(nc.vector.reciprocal(binv[i][:, 0:nb], bscale[i][:, 0:nb]))
                nc.vector.sem_inc(scaled, 1)

            def levels(p, between=None):
                i, (a, width) = p % RING, groups[p]
                M, L, C, G = mag[i][:, 0:width], lev[:, 0:width], low[:, 0:width], sg[i][:, 0:width]
                dve.wait_ge(normed, 2 * p + 1)
                link.mark(nc.vector.tensor_scalar(C, M, 0.25, None, ALU.is_gt))
                link(nc.vector.tensor_scalar(L, M, 5.0, 2.0, ALU.is_gt, ALU.mult))
                link(nc.vector.scalar_tensor_tensor(L, M, 3.5, L, ALU.is_gt, ALU.add))
                link(nc.vector.scalar_tensor_tensor(L, M, 2.5, L, ALU.is_gt, ALU.add))
                if between is not None:
                    between()
                link(nc.vector.scalar_tensor_tensor(L, L, 2.0, C, ALU.mult, ALU.add))
                for mid in (0.75, 1.25, 1.75):
                    link(nc.vector.scalar_tensor_tensor(L, M, mid, L, ALU.is_gt, ALU.add))
                dve.wait_ge(normed, 2 * p + 2)
                nc.vector.tensor_tensor(a, L, G, ALU.mult).then_inc(quantised, 1)
                dve.wait_ge(quantised, p + 1)

            def gate(b):
                dve.wait_ge(silu_ready, b + 1)
                nc.vector.tensor_tensor(f[:, TB * b:TB * (b + 1)], g[b % 2][:], psU[:, :, 0:FI], ALU.mult).then_inc(f_ready, 1)

            def update(b):
                dve.wait_ge(y_ready, b + 1)
                nc.vector.tensor_tensor(m.x[:, b], m.x[:, b], psY[:], ALU.add).then_inc(x_done, 1)

            xs = [m.x[:, i // TB, i % TB] for i in range(NT)]
            dve_moments(nc, link, w, xs, D, LN_EPS).then_inc(moments, 1)
            dve.wait_ge(rstd, 1)
            for i in range(NT):
                nc.vector.tensor_scalar(h[:, i], xs[i], w.mean[:, i:i + 1], w.rstd[:, i:i + 1], ALU.subtract, ALU.mult).then_inc(h_ready, 1)
            scales(0)
            scales(1)
            levels(0)
            scales(2)
            levels(1)
            levels(2, lambda: gate(0))
            gate(1)
            scales(F0)
            gate(2)
            gate(3)
            scales(F0 + 1)
            levels(F0, lambda: gate(4))
            gate(5)
            scales(F0 + 2)
            levels(F0 + 1, lambda: gate(6))
            gate(7)
            scales(F0 + 3)
            update(0)
            update(1)
            levels(F0 + 2, lambda: update(2))
            update(3)
            levels(F0 + 3, lambda: update(4))
            update(5)
            update(6)
            update(7)

        @block.tensor
        def _(pe):
            pe.wait_ge(quantised, 2)
            for n, (c, k) in enumerate(CH):
                nc.tensor.transpose(psG[:, 0, c:c + k], wall[0:k, n * D:(n + 1) * D], m.ident[0:k, 0:k])
                nc.tensor.transpose(psG[:, 1, c:c + k], wall[0:k, WU + n * D:WU + (n + 1) * D], m.ident[0:k, 0:k])
                ins = nc.tensor.transpose(psU[0:k, 0, n * D:(n + 1) * D], wall[:, WD + c:WD + c + k], m.ident[:])
            ins.then_inc(w_turned, 1)

            def turn(b):
                pe.wait_ge(quantised, 1 if b < B // 2 else 3)
                wait(pe, hT_ready, b)
                for t in range(TB):
                    ins = nc.tensor.transpose(psA[:, t * P:(t + 1) * P], h[:, TB * b + t], m.ident[:])
                ins.then_inc(turned, 1)

            def up(b):
                pe.wait_ge(hT_ready, b + 1)
                wait(pe, f_ready, b)
                for t in range(TB):
                    nc.tensor.matmul(psG[:, t, 0:FI], hT[b % 2][:, t * P:(t + 1) * P], wguT[:, 0], start=True, stop=True)
                    ins = nc.tensor.matmul(psU[:, t, 0:FI], hT[b % 2][:, t * P:(t + 1) * P], wguT[:, 1], start=True, stop=True)
                ins.then_inc(gu_ready, 1)

            def down(b):
                pe.wait_ge(quantised, F0 + b // 2 + 1)
                wait(pe, fT_ready, 2 * b)
                for n, (c, k) in enumerate(CH):
                    for t in range(TB):
                        at = psF[0:k, n // 2, (n % 2) * S + t * P:(n % 2) * S + (t + 1) * P]
                        ins = nc.tensor.transpose(at, f[:, TB * b + t, c:c + k], m.ident[:])
                ins.then_inc(f_turned, 1)
                pe.wait_ge(fT_ready, 2 * (b + 1))
                wait(pe, x_done, b)
                for t in range(TB):
                    for n, (c, k) in enumerate(CH):
                        ins = nc.tensor.matmul(psY[:, t], fT[0:k, n, t * P:(t + 1) * P], wdT[0:k, n], start=(n == 0), stop=(n == 2))
                ins.then_inc(y_ready, 1)

            turn(0)
            pe.wait_ge(wT_ready, 3)
            for b in range(B):
                if b + 1 < B:
                    turn(b + 1)
                up(b)
            for b in range(B):
                down(b)

        @block.scalar
        def _(act):
            def part(p):
                i, (a, width) = p % RING, groups[p]
                wait(act, quantised, p - RING + 1)
                nc.scalar.activation(mag[i][:, 0:width], a, ACT.Abs).then_inc(parted, 1)
                nc.scalar.activation(sg[i][:, 0:width], a, ACT.Sign).then_inc(parted, 1)

            def copy_h(b):
                act.wait_ge(turned, b + 1)
                wait(act, gu_ready, b - 1)
                nc.scalar.copy(hT[b % 2][:], psA[:, 0:S]).then_inc(hT_ready, 1)

            act.wait_ge(h_ready, HALF)
            part(0)
            act.wait_ge(loaded, 16 * NLOAD)
            part(1)
            act.wait_ge(h_ready, NT)
            part(2)
            act.wait_ge(w_turned, 1)
            nc.scalar.copy(wguT[:], psG[:, :, 0:FI]).then_inc(wT_ready, 1)
            nc.scalar.copy(wdT[:, 0:2], psU[:, 0, 0:2 * D].rearrange("p (n d) -> p n d", n=2)).then_inc(wT_ready, 1)
            nc.scalar.copy(wdT[0:REST, 2], psU[0:REST, 0, 2 * D:3 * D]).then_inc(wT_ready, 1)
            copy_h(0)
            for b in range(B):
                if b + 1 < B:
                    copy_h(b + 1)
                act.wait_ge(gu_ready, b + 1)
                wait(act, f_ready, b - 1)
                nc.scalar.activation(g[b % 2][:], psG[:, :, 0:FI], ACT.Silu).then_inc(silu_ready, 1)
                if b % 2 == 1:
                    act.wait_ge(f_ready, b + 1)
                    part(F0 + b // 2)
            for b in range(B):
                act.wait_ge(f_turned, b + 1)
                wait(act, y_ready, b)
                nc.scalar.copy(fT[:, 0:2], psF[:, 0].rearrange("p (n s) -> p n s", n=2)).then_inc(fT_ready, 1)
                nc.scalar.copy(fT[0:REST, 2], psF[0:REST, 1, 0:S]).then_inc(fT_ready, 1)


def layer_gated_recurrence(m, pre):
    nc = m.nc
    d = m.dram
    H, DH, CHUNK, FC = 16, 8, 64, 512
    NC, NF = S // CHUNK, FC // P
    RES = float(1.0 / np.sqrt(2.0))
    EPS_Q = float(np.finfo(np.float32).eps)
    EPS_X = 1e-6
    GT, NG = 4, NT // 4
    HT, NH, W = NT // 2, 2, NT // 2 * P
    HB = B // 2
    PROJ = 5
    with ExitStack() as es:
        sb, ps, sem = allocators(nc, es, pre)
        wi, wo, wf, wp = sb("wi", [P, PROJ * D]), sb("wo", [P, D]), sb("wf", [P, FC]), sb("wp", [P, NF, D])
        n1, n2, two_c = sb("n1", [P, 1]), sb("n2", [P, 1]), sb("two", [P, 1])
        headsum, headexp = sb("headsum", [P, H]), sb("headexp", [H, P])
        go = sb("go", [P, W])
        w, w1, w3 = Norm(sb, "", NT), Norm(sb, "1", NT), Norm(sb, "3", HT)
        h, h1 = sb("h", [P, NT, D]), sb("h1", [P, NT, D])
        hT = [sb(f"hT{i}", [P, GT * P]) for i in range(2)]
        q, k, v, a, g, q2, gv = (sb(n, [P, NT * P]) for n in ("q", "k", "v", "a", "g", "q2", "gv"))
        qms, qrs, qrT = sb("qms", [P, NT * H]), sb("qrs", [P, NT * H]), sb("qrT", [H, W])
        first, pref, rec, acc, st, yT = (sb(n, [P, W]) for n in ("first", "pref", "rec", "acc", "st", "yT"))
        hm, h2, h2T = sb("hm", [P, NT, D]), sb("h2", [P, HT, D]), sb("h2T", [P, W])
        sT, y = [sb(f"sT{i}", [P, NF, GT * P]) for i in range(2)], sb("y", [P, GT, D])
        psA, psR, psQ = ps("psA", [P, 2, 512]), ps("psR", [P, 2, 512]), ps("psQ", [P, 512])
        psP = [ps(f"psP{i}", [P, 512]) for i in range(3)]
        names = ("loaded", "consts", "pool_chain", "dve_chain", "moments", "rstd", "h_ready", "turned", "hT_ready", "proj_ready", "proj_read",
                 "qs_ready", "qms_ready", "rms_ready", "qrs_ready", "q_turned", "qrT_ready", "q_spread",
                 "y_ready", "mix_ready", "hm_ready", "h2_ready", "h2_turned", "h2T_ready", "fc_ready", "silu_ready", "mlp_ready", "mlp_read")
        (loaded, consts, pool_chain, dve_chain, moments, rstd, h_ready, turned, hT_ready, proj_ready, proj_read,
         qs_ready, qms_ready, rms_ready, qrs_ready, q_turned, qrT_ready, q_spread,
         y_ready, mix_ready, hm_ready, h2_ready, h2_turned, h2T_ready, fc_ready, silu_ready, mlp_ready, mlp_read) = (sem(n) for n in names)
        block = es.enter_context(nc.Block())
        NLOAD = 6
        half = lambda t, i: t[:, i * W:(i + 1) * W]
        READS = PROJ

        @block.sync
        def _(sp):
            col = lambda ap: ap.rearrange("(d a) -> d a", a=1)
            for dst, src in ((wi[:], d[f"{pre}_in_proj_w"]), (n1[:], col(d[f"{pre}_norm1_w"])), (wo[:], d[f"{pre}_out_proj_w"]),
                             (wf[:], d[f"{pre}_fc_w"]), (wp[:], d[f"{pre}_proj_w"].rearrange("(c p) d -> p c d", p=P)),
                             (n2[:], col(d[f"{pre}_norm2_w"]))):
                sp.dma_start(dst, src).then_inc(loaded, 16)

        @block.gpsimd
        def _(pool):
            link = Links(pool, pool_chain)

            def band(t, keep, steps):
                link(nc.gpsimd.memset(t[:], keep))
                for base, mult, step in steps:
                    link(nc.gpsimd.affine_select(out=t[:], in_=t[:], compare_op=ALU.is_ge, fill=0.0, base=base,
                                                 pattern=[[step, t.shape[1]]], channel_multiplier=mult))

            band(headsum, 1.0 / DH, [(0, 1, -DH), (DH - 1, -1, DH)])
            band(headexp, 1.0, [(0, -DH, 1), (DH - 1, DH, -1)])
            link(nc.gpsimd.memset(two_c[:], 2.0))
            link(nc.gpsimd.memset(first[:], 0.0))
            link(nc.gpsimd.memset(go[:], 1.0))
            nc.gpsimd.memset(go[:, 0:W:CHUNK], 0.0).then_inc(consts, 1)
            for n, ww in enumerate((w, w1)):
                pool.wait_ge(moments, n + 1)
                pool_rsqrt(nc, m, ww, NT).then_inc(rstd, 1)

            for i in range(NH):
                pool.wait_ge(moments, i + 3)
                pool_rsqrt(nc, m, w3, HT).then_inc(rstd, 1)

        @block.vector
        def _(dve):
            link = Links(dve, dve_chain)
            xs, hs = [m.x[:, i // TB, i % TB] for i in range(NT)], [h[:, i] for i in range(NT)]
            dve_moments(nc, link, w, xs, D, LN_EPS).then_inc(moments, 1)
            dve.wait_ge(rstd, 1)
            for i in range(NT):
                link.mark(nc.vector.tensor_scalar(hs[i], xs[i], w.mean[:, i:i + 1], w.rstd[:, i:i + 1], ALU.subtract, ALU.mult))
            link.wait()
            dve_square_mean(nc, link, w1, hs, D, EPS_X).then_inc(moments, 1)
            dve.wait_ge(rstd, 2)
            for i in range(NT):
                nc.vector.tensor_scalar(h1[:, i], hs[i], w1.rstd[:, i:i + 1], None, ALU.mult).then_inc(h_ready, 1)
            dve.wait_ge(consts, 1)

            def products(i):
                dve.wait_ge(proj_read, READS * NG // NH * (i + 1))
                link.mark(nc.vector.tensor_tensor(half(gv, i), half(g, i), half(v, i), ALU.mult))
                link.mark(nc.vector.tensor_tensor(half(k, i), half(k, i), half(v, i), ALU.mult))
                link(nc.vector.tensor_tensor(half(q, i), half(g, i), half(q, i), ALU.mult))
                link.mark(nc.vector.tensor_tensor(half(gv, i), half(v, i), half(gv, i), ALU.subtract))
                dve.wait_ge(qs_ready, i + 1)
                z = slice(i * HT * H, (i + 1) * HT * H)
                nc.vector.tensor_scalar(qms[:, z], psQ[:, z], EPS_Q, None, ALU.add).then_inc(qms_ready, 1)

            def inverse(i):
                z = slice(i * HT * H, (i + 1) * HT * H)
                dve.wait_ge(rms_ready, i + 1)
                nc.vector.reciprocal(qrs[:, z], qrs[:, z]).then_inc(qrs_ready, 1)

            def prefixes(i):
                A = half(a, i)
                link(nc.vector.tensor_scalar(A, A, 0.6, 0.9995, ALU.max, ALU.min))
                link(nc.vector.tensor_copy(first[:, 0:W:CHUNK], a[:, i * W:(i + 1) * W:CHUNK]))
                link(nc.vector.memset(a[:, i * W:(i + 1) * W:CHUNK], 0.0))
                link(nc.vector.tensor_tensor_scan(pref[:], A, first[:], 0.0, ALU.mult, ALU.add))
                link(nc.vector.tensor_scalar(rec[:], pref[:], 1e-6, None, ALU.max))

            def states(i):
                link(nc.vector.reciprocal(rec[:], rec[:]))
                link(nc.vector.tensor_tensor(rec[:], half(k, i), rec[:], ALU.mult))
                link(nc.vector.tensor_tensor_scan(acc[:], go[:], rec[:], 0.0, ALU.mult, ALU.add))
                view = lambda t: t[:].rearrange("p (b n c) -> p b n c", b=HB, n=NC)
                ST, AC, PR = view(st), view(acc), view(pref)
                link(nc.vector.tensor_tensor(ST[:, :, 0], PR[:, :, 0], AC[:, :, 0], ALU.mult))
                for c in range(1, NC):
                    link(nc.vector.tensor_tensor(ST[:, :, c], AC[:, :, c], ST[:, :, c - 1, CHUNK - 1:CHUNK].to_broadcast((P, HB, CHUNK)), ALU.add))
                    link(nc.vector.tensor_tensor(ST[:, :, c], ST[:, :, c], PR[:, :, c], ALU.mult))
                link(nc.vector.tensor_tensor(st[:], st[:], half(q, i), ALU.mult))
                dve.wait_ge(q_spread, i + 1)
                link(nc.vector.tensor_tensor(st[:], st[:], psR[:].rearrange("p a c -> p (a c)"), ALU.mult))
                wait(dve, mix_ready, i)
                nc.vector.tensor_tensor(yT[:], st[:], half(gv, i), ALU.add).then_inc(y_ready, 1)

            def after_mixer(i):
                dve.wait_ge(mix_ready, i + 1)
                t = slice(i * HT, (i + 1) * HT)
                nc.vector.scalar_tensor_tensor(hm[:, t], psA[:].rearrange("p a (t d) -> p (a t) d", d=D), RES, h[:, t], ALU.mult, ALU.add).then_inc(hm_ready, 1)
                dve.wait_ge(hm_ready, i + 1)
                dve_square_mean(nc, link, w3, [hm[:, i * HT + j] for j in range(HT)], D, EPS_X).then_inc(moments, 1)
                dve.wait_ge(rstd, 3 + i)
                wait(dve, h2_turned, i)
                for j in range(HT):
                    nc.vector.tensor_scalar(h2[:, j], hm[:, i * HT + j], w3.rstd[:, j:j + 1], None, ALU.mult).then_inc(h2_ready, 1)

            def update(n):
                dve.wait_ge(mlp_ready, n + 1)
                nc.vector.scalar_tensor_tensor(y[:], psQ[:].rearrange("p (t d) -> p t d", d=D), RES, hm[:, n * GT:(n + 1) * GT], ALU.mult, ALU.add).then_inc(mlp_read, 1)
                dve.wait_ge(mlp_read, n + 1)
                bs = slice(n * GT // TB, (n + 1) * GT // TB)
                link(nc.vector.tensor_tensor(m.x[:, bs], m.x[:, bs], y[:].rearrange("p (b t) d -> p b t d", t=TB), ALU.add))

            products(0)
            prefixes(0)
            inverse(0)
            states(0)
            products(1)
            prefixes(1)
            inverse(1)
            after_mixer(0)
            states(1)
            update(0)
            after_mixer(1)
            for n in range(1, NG):
                update(n)

        @block.tensor
        def _(pe):
            pe.wait_ge(loaded, 16 * NLOAD)
            def project(n):
                pe.wait_ge(h_ready, GT * (n + 1))
                wait(pe, hT_ready, n - 1)
                for t in range(GT):
                    ins = nc.tensor.transpose(psA[:, n % 2, t * P:(t + 1) * P], h1[:, n * GT + t], m.ident[:])
                ins.then_inc(turned, 1)
                pe.wait_ge(hT_ready, n + 1)
                for j in range(PROJ):
                    job = n * PROJ + j
                    wait(pe, proj_read, job - 2)
                    nc.tensor.matmul(psP[job % 3][:], wi[:, j * D:(j + 1) * D], hT[n % 2][:], start=True, stop=True).then_inc(proj_ready, 1)
            def squares(i):
                pe.wait_ge(consts, 1)
                pe.wait_ge(proj_read, READS * NG // NH * (i + 1))
                wait(pe, qms_ready, i)
                for t in range(i * HT, (i + 1) * HT):
                    ins = nc.tensor.matmul(psQ[:, t * H:(t + 1) * H], q2[:, t * P:(t + 1) * P], headsum[:], start=True, stop=True)
                ins.then_inc(qs_ready, 1)

            def spread(i):
                pe.wait_ge(qrs_ready, i + 1)
                wait(pe, y_ready, i)
                for t in range(HT):
                    ins = nc.tensor.transpose(psR[0:H, t // GT, t % GT * P:(t % GT + 1) * P], qrs[:, (i * HT + t) * H:(i * HT + t + 1) * H], m.ident[:])
                ins.then_inc(q_turned, 1)
                pe.wait_ge(qrT_ready, i + 1)
                for c in range(2):
                    ins = nc.tensor.matmul(psR[:, c], headexp[:], qrT[:, c * 512:(c + 1) * 512], start=True, stop=True)
                ins.then_inc(q_spread, 1)

            def mix(i):
                pe.wait_ge(y_ready, i + 1)
                wait(pe, h2T_ready, i)
                for t in range(HT):
                    ins = nc.tensor.matmul(psA[:, t // GT, t % GT * P:(t % GT + 1) * P], yT[:, t * P:(t + 1) * P], wo[:], start=True, stop=True)
                ins.then_inc(mix_ready, 1)

            def turn(i):
                pe.wait_ge(h2_ready, HT * (i + 1))
                pe.wait_ge(hm_ready, i + 1)
                for t in range(HT):
                    ins = nc.tensor.transpose(psA[:, t // GT, t % GT * P:(t % GT + 1) * P], h2[:, t], m.ident[:])
                ins.then_inc(h2_turned, 1)

            def fc(n):
                pe.wait_ge(h2T_ready, n // 2 + 1)
                for c in range(NF):
                    job = n * NF + c
                    wait(pe, silu_ready, job - 2)
                    nc.tensor.matmul(psP[job % 3][:], wf[:, c * P:(c + 1) * P], h2T[:, n % 2 * 512:(n % 2 + 1) * 512], start=True, stop=True).then_inc(fc_ready, 1)

            def down(n):
                pe.wait_ge(silu_ready, NF * (n + 1))
                wait(pe, mlp_read, n)
                for t in range(GT):
                    for c in range(NF):
                        ins = nc.tensor.matmul(psQ[:, t * D:(t + 1) * D], sT[n % 2][:, c, t * P:(t + 1) * P], wp[:, c], start=(c == 0), stop=(c == NF - 1))
                ins.then_inc(mlp_ready, 1)

            for n in range(NG):
                project(n)
                if n % 2 == 1:
                    squares(n // 2)
                if n == NG // 2:
                    spread(0)
            mix(0)
            spread(1)
            turn(0)
            fc(0)
            down(0)
            fc(1)
            mix(1)
            down(1)
            turn(1)
            fc(2)
            down(2)
            fc(3)
            down(3)

        @block.scalar
        def _(act):
            act.wait_ge(loaded, 16 * NLOAD)
            act.wait_ge(consts, 1)
            def project(n):
                z = slice(n * 512, (n + 1) * 512)
                act.wait_ge(turned, n + 1)
                wait(act, proj_ready, PROJ * (n - 1))
                nc.scalar.activation(hT[n % 2][:], psA[:, n % 2], ACT.Copy, scale=n1[:]).then_inc(hT_ready, 1)
                bank = lambda j: psP[(n * PROJ + j) % 3][:]
                for j, (dst, func) in enumerate(((q2, ACT.Square), (k, ACT.Tanh), (v, ACT.Copy), (a, ACT.Sigmoid), (g, ACT.Sigmoid))):
                    act.wait_ge(proj_ready, n * PROJ + j + 1)
                    if j == 0:
                        nc.scalar.activation(q[:, z], bank(j), ACT.Copy)
                    if j == 3:
                        nc.scalar.activation(dst[:, z], bank(j), func, bias=two_c[:]).then_inc(proj_read, 1)
                    else:
                        nc.scalar.activation(dst[:, z], bank(j), func).then_inc(proj_read, 1)

            def root(i):
                z = slice(i * HT * H, (i + 1) * HT * H)
                act.wait_ge(qms_ready, i + 1)
                nc.scalar.activation(qrs[:, z], qms[:, z], ACT.Sqrt).then_inc(rms_ready, 1)

            def copy_q(i):
                act.wait_ge(q_turned, i + 1)
                wait(act, q_spread, i)
                nc.scalar.copy(qrT[:], psR[0:H].rearrange("p a c -> p (a c)")).then_inc(qrT_ready, 1)

            def copy_h2(i):
                act.wait_ge(h2_turned, i + 1)
                wait(act, fc_ready, 2 * NF * i)
                nc.scalar.activation(h2T[:], psA[:].rearrange("p a c -> p (a c)"), ACT.Copy, scale=n2[:]).then_inc(h2T_ready, 1)

            def silu(n):
                for c in range(NF):
                    job = n * NF + c
                    act.wait_ge(fc_ready, job + 1)
                    wait(act, mlp_ready, n - 1)
                    nc.scalar.activation(sT[n % 2][:, c], psP[job % 3][:], ACT.Silu).then_inc(silu_ready, 1)

            for n in range(NG):
                project(n)
                if n == NG // 2 - 1:
                    root(0)
                if n == NG // 2:
                    copy_q(0)
            root(1)
            copy_q(1)
            for i in range(NH):
                copy_h2(i)
                silu(2 * i)
                silu(2 * i + 1)


def layer_sign_linear(m, pre):
    nc = m.nc
    LIMIT = 100.0
    with ExitStack() as es:
        sb, ps, sem = allocators(nc, es, pre)
        wT, scale, bias = sb("wT", [P, D]), sb("scale", [P, D]), sb("bias", [P, D])
        w = Norm(sb)
        h, hT, y = sb("h", [P, TB, D]), sb("hT", [P, S]), sb("y", [P, TB, D])
        psT, psY = ps("psT", [P, S]), ps("psY", [P, TB, D])
        loaded, w_signed, var_ready, rstd_ready = sem("loaded"), sem("w_signed"), sem("var_ready"), sem("rstd_ready")
        h_ready, turned, hT_ready, y_ready, dve_chain = (sem("h_ready"), sem("turned"), sem("hT_ready"),
                                                          sem("y_ready"), sem("dve_chain"))
        y_done = sem("y_done")
        block = es.enter_context(nc.Block())

        @block.sync
        def _(sp):
            sp.dma_start(wT[:], m.dram[f"{pre}_weights"]).then_inc(loaded, 16)
            sp.dma_start(scale[:], rows(m.dram[f"{pre}_scale"]).to_broadcast((P, D))).then_inc(loaded, 16)
            sp.dma_start(bias[:], rows(m.dram[f"{pre}_bias"]).to_broadcast((P, D))).then_inc(loaded, 16)

        @block.gpsimd
        def _(pool):
            with pool.Fori(0, B) as b:
                pool.wait_ge(var_ready, b + 1)
                pool_rsqrt(nc, m, w).then_inc(rstd_ready, 1)

        @block.vector
        def _(dve):
            STEPS = 2 * TB + 9
            dve.wait_ge(loaded, 48)
            nc.vector.tensor_scalar(wT[:], wT[:], 0.0, 2.0, ALU.is_ge, ALU.mult).then_inc(w_signed, 1)
            dve.wait_ge(w_signed, 1)
            nc.vector.tensor_scalar(wT[:], wT[:], 1.0, None, ALU.subtract).then_inc(w_signed, 1)
            with dve.Fori(0, B) as b:
                link = Links(dve, dve_chain, b * STEPS)
                dve_moments(nc, link, w, [m.x[:, b, t] for t in range(TB)], D, LN_EPS).then_inc(var_ready, 1)
                dve.wait_ge(rstd_ready, b + 1)
                for t in range(TB):
                    nc.vector.tensor_scalar(h[:, t], m.x[:, b, t], w.mean[:, t:t + 1], w.rstd[:, t:t + 1], ALU.subtract, ALU.mult).then_inc(h_ready, 1)
                dve.wait_ge(y_ready, b + 1)
                bc = lambda a: a[:, None, :].to_broadcast((P, TB, D))
                link(nc.vector.tensor_tensor(y[:], psY[:], bc(scale[:]), ALU.mult))
                link(nc.vector.tensor_tensor(y[:], y[:], bc(bias[:]), ALU.add))
                link(nc.vector.tensor_scalar(y[:], y[:], -LIMIT, LIMIT, ALU.max, ALU.min))
                for t in range(TB):
                    link(nc.vector.tensor_tensor(m.x[:, b, t], m.x[:, b, t], y[:, t], ALU.add))
                assert link.n == STEPS, link.n

        @block.tensor
        def _(pe):
            pe.wait_ge(w_signed, 2)
            with pe.Fori(0, B) as b:
                pe.wait_ge(h_ready, TB * b + TB)
                for t in range(TB):
                    ins = nc.tensor.transpose(psT[:, t * P:(t + 1) * P], h[:, t], m.ident[:])
                ins.then_inc(turned, 1)
                pe.wait_ge(hT_ready, b + 1)
                for t in range(TB):
                    ins = nc.tensor.matmul(psY[:, t], hT[:, t * P:(t + 1) * P], wT[:], start=True, stop=True)
                ins.then_inc(y_ready, 1)

        @block.scalar
        def _(act):
            with act.Fori(0, B) as b:
                act.wait_ge(turned, b + 1)
                nc.scalar.copy(hT[:], psT[:]).then_inc(hT_ready, 1)


def layer_moe_top8(m, pre):
    nc = m.nc
    d = m.dram
    E, F, TOP = 64, 64, 8
    EG = 8
    NGR = E // EG
    BK = EG * F // P
    with ExitStack() as es:
        sb, ps, sem = allocators(nc, es, pre)
        wup, wdn = sb("wup", [P, E, F]), sb("wdn", [P, E // 2, D])
        sup, sdn, cen, ebias = sb("sup", [P, F]), sb("sdn", [F, D]), sb("cen", [P, E]), sb("ebias", [P, E])
        w = Norm(sb)
        h, hT = sb("h", [P, TB, D]), [sb(f"hT{i}", [P, S]) for i in range(2)]
        aff, bia, top8, rest = sb("aff", [P, TB, E]), sb("bia", [P, TB, E]), sb("top8", [P, TB, 8]), sb("rest", [P, TB, E])
        sig, cw, wsum = sb("sig", [P, TB, E]), [sb(f"cw{i}", [P, TB, E]) for i in range(2)], sb("wsum", [P, TB])
        act_s, wt_s, fT = [sb(f"act{i}", [P, EG * F]) for i in range(3)], [sb(f"wt{i}", [P, EG * F]) for i in range(3)], [sb(f"fT{i}", [P, BK, P]) for i in range(3)]
        shT = [sb(f"shT{i}", [F, S]) for i in range(2)]
        psU, psF = [ps(f"psU{i}", [P, EG * F]) for i in range(2)], [ps(f"psF{i}", [P, BK * P]) for i in range(2)]
        psY = [ps(f"psY{i}", [P, 512]) for i in range(2)]
        psM, psH = ps("psM", [P, 512]), ps("psH", [P, 512])
        names = ("loaded", "dve_chain", "var_ready", "rstd_ready", "h_ready", "turned", "hT_ready", "aff_ready", "aff_copied",
                 "sig_ready", "cw_ready", "up_ready", "silu_ready", "weighted", "f_turned", "fT_ready", "down_done", "sh_up",
                 "sh_silu", "x_done")
        (loaded, dve_chain, var_ready, rstd_ready, h_ready, turned, hT_ready, aff_ready, aff_copied,
         sig_ready, cw_ready, up_ready, silu_ready, weighted, f_turned, fT_ready, down_done, sh_up,
         sh_silu, x_done) = (sem(n) for n in names)
        up_loaded, down_loaded = [sem(f"up_loaded{q}") for q in range(4)], sem("down_loaded")
        block = es.enter_context(nc.Block())
        LT, LD = 2, 3
        NG = NT * NGR

        @block.sync
        def _(sp):
            for dst, src in ((sup[:], d[f"{pre}_Ws_up"]), (sdn[:], d[f"{pre}_Ws_down"]), (cen[:], d[f"{pre}_centroids"]),
                             (ebias[:], rows(d[f"{pre}_expert_biases"]).to_broadcast((P, E)))):
                sp.dma_start(dst, src).then_inc(loaded, 16)
            for q in range(4):
                c = slice(q * E // 4, (q + 1) * E // 4)
                sp.dma_start(wup[:, c], d[f"{pre}_W_up"][c].rearrange("e d f -> d e f")).then_inc(up_loaded[q], 16)
            sp.dma_start(wdn[:], d[f"{pre}_W_down"].rearrange("(n e) f d -> (e f) n d", e=2)).then_inc(down_loaded, 16)

        @block.gpsimd
        def _(pool):
            for b in range(B):
                pool.wait_ge(var_ready, b + 1)
                pool_rsqrt(nc, m, w).then_inc(rstd_ready, 1)

        @block.vector
        def _(dve):
            link = Links(dve, dve_chain)

            def norm(b):
                dve_moments(nc, link, w, [m.x[:, b, t] for t in range(TB)], D, LN_EPS).then_inc(var_ready, 1)
                dve.wait_ge(rstd_ready, b + 1)
                wait(dve, turned, b)
                for t in range(TB):
                    nc.vector.tensor_scalar(h[:, t], m.x[:, b, t], w.mean[:, t:t + 1], w.rstd[:, t:t + 1], ALU.subtract, ALU.mult).then_inc(h_ready, 1)

            def route_a(b):
                dve.wait_ge(aff_ready, b + 1)
                wait(dve, sig_ready, b)
                nc.vector.tensor_copy(aff[:], psM[:, 256:256 + TB * E].rearrange("p (t e) -> p t e", t=TB)).then_inc(aff_copied, 1)
                dve.wait_ge(aff_copied, b + 1)
                link(nc.vector.tensor_tensor(bia[:], aff[:], ebias[:, None, :].to_broadcast((P, TB, E)), ALU.add))
                for t in range(TB):
                    link.mark(nc.vector.max(top8[:, t], bia[:, t]))
                link.wait()
                for t in range(TB):
                    link.mark(nc.vector.match_replace(rest[:, t], top8[:, t], bia[:, t], -3.0e38))
                link.wait()

            def route_b(b):
                link(nc.vector.tensor_tensor(rest[:], rest[:], bia[:], ALU.not_equal))
                dve.wait_ge(sig_ready, b + 1)
                c = cw[b % 2]
                link(nc.vector.tensor_tensor(c[:], sig[:], rest[:], ALU.mult))
                link(nc.vector.reduce_sum(wsum[:], c[:], AX.X))
                link(nc.vector.tensor_scalar(wsum[:], wsum[:], 1e-8, None, ALU.add))
                link(nc.vector.reciprocal(wsum[:], wsum[:]))
                nc.vector.tensor_tensor(c[:], c[:], wsum[:, :, None].to_broadcast((P, TB, E)), ALU.mult).then_inc(cw_ready, 1)

            def weigh(n):
                tile, g = n // NGR, n % NGR
                b, t = tile // TB, tile % TB
                dve.wait_ge(silu_ready, n + 1)
                if g == 0 and t == 0:
                    dve.wait_ge(cw_ready, b + 1)
                wait(dve, f_turned, n - 2)
                e = g * EG
                nc.vector.tensor_tensor(wt_s[n % 3][:].rearrange("p (e f) -> p e f", f=F), act_s[n % 3][:].rearrange("p (e f) -> p e f", f=F),
                                        cw[b % 2][:, t, e:e + EG, None].to_broadcast((P, EG, F)), ALU.mult).then_inc(weighted, 1)

            def update(tile):
                b, t = tile // TB, tile % TB
                dve.wait_ge(down_done, NGR * (tile + 1))
                nc.vector.tensor_tensor(m.x[:, b, t], m.x[:, b, t], psY[tile % 2][:, 0:D], ALU.add).then_inc(x_done, 1)

            norm(0)
            dve.wait_ge(loaded, 16 * 4)
            route_a(0)
            route_b(0)
            for n in range(NG):
                tile, g = n // NGR, n % NGR
                b, t = tile // TB, tile % TB
                weigh(n)
                if t == 0 and g == 1 and b + 1 < B:
                    norm(b + 1)
                if t == 1 and g == 2 and b + 1 < B:
                    route_a(b + 1)
                if t == 1 and g == 4 and b + 1 < B:
                    route_b(b + 1)
                if g == 5 and tile >= 1:
                    update(tile - 1)
            update(NT - 1)

        @block.tensor
        def _(pe):
            pe.wait_ge(loaded, 16 * 4)

            def turn(b):
                pe.wait_ge(h_ready, TB * (b + 1))
                wait(pe, hT_ready, b)
                for t in range(TB):
                    ins = nc.tensor.transpose(psM[:, t * P:(t + 1) * P], h[:, t], m.ident[:])
                ins.then_inc(turned, 1)

            def affinities(b):
                pe.wait_ge(hT_ready, b + 1)
                wait(pe, aff_copied, b)
                for t in range(TB):
                    ins = nc.tensor.matmul(psM[:, 256 + t * E:256 + (t + 1) * E], hT[b % 2][:, t * P:(t + 1) * P], cen[:], start=True, stop=True)
                ins.then_inc(aff_ready, 1)

            def up(n):
                tile, g = n // NGR, n % NGR
                b, t = tile // TB, tile % TB
                wait(pe, silu_ready, n - 1)
                if n < NGR and n % 2 == 0:
                    pe.wait_ge(up_loaded[n // 2], 16)
                nc.tensor.matmul(psU[n % 2][:], hT[b % 2][:, t * P:(t + 1) * P], wup[:, g * EG:(g + 1) * EG].rearrange("p e f -> p (e f)"),
                                 start=True, stop=True).then_inc(up_ready, 1)

            def shared_up(b):
                wait(pe, sh_silu, b)
                nc.tensor.matmul(psH[0:F, 0:S], sup[:], hT[b % 2][:], start=True, stop=True).then_inc(sh_up, 1)

            def turn_hidden(n):
                pe.wait_ge(weighted, n + 1)
                wait(pe, fT_ready, n - 1)
                for k in range(BK):
                    ins = nc.tensor.transpose(psF[n % 2][:, k * P:(k + 1) * P], wt_s[n % 3][:, k * P:(k + 1) * P], m.ident[:])
                ins.then_inc(f_turned, 1)

            def down(n):
                tile, g = n // NGR, n % NGR
                b, t = tile // TB, tile % TB
                if g == 0:
                    pe.wait_ge(sh_silu, b + 1)
                    wait(pe, x_done, tile - 1)
                    nc.tensor.matmul(psY[tile % 2][:, 0:D], shT[b % 2][:, t * P:(t + 1) * P], sdn[:], start=True, stop=False)
                if n == 0:
                    pe.wait_ge(down_loaded, 16)
                pe.wait_ge(fT_ready, n + 1)
                for k in range(BK):
                    ins = nc.tensor.matmul(psY[tile % 2][:, 0:D], fT[n % 3][:, k], wdn[:, g * BK + k], start=False, stop=(g == NGR - 1 and k == BK - 1))
                ins.then_inc(down_done, 1)

            turn(0)
            affinities(0)
            shared_up(0)
            for n in range(NG + LD):
                tile, g = n // NGR, n % NGR
                b, t = tile // TB, tile % TB
                if n < NG:
                    up(n)
                    if t == 0 and g == 5 and b + 1 < B:
                        turn(b + 1)
                    if t == 1 and g == 0 and b + 1 < B:
                        affinities(b + 1)
                    if t == 1 and g == 1 and b + 1 < B:
                        shared_up(b + 1)
                if LT <= n < NG + LT:
                    turn_hidden(n - LT)
                if n >= LD:
                    down(n - LD)

        @block.scalar
        def _(act):
            def copy_h(b):
                act.wait_ge(turned, b + 1)
                wait(act, up_ready, TB * NGR * (b - 1))
                nc.scalar.copy(hT[b % 2][:], psM[:, 0:S]).then_inc(hT_ready, 1)

            def sigmoids(b):
                act.wait_ge(aff_copied, b + 1)
                wait(act, cw_ready, b)
                nc.scalar.activation(sig[:], aff[:], ACT.Sigmoid).then_inc(sig_ready, 1)

            def shared_silu(b):
                act.wait_ge(sh_up, b + 1)
                wait(act, down_done, TB * NGR * (b - 1))
                nc.scalar.activation(shT[b % 2][:], psH[0:F, 0:S], ACT.Silu).then_inc(sh_silu, 1)

            def silu(n):
                act.wait_ge(up_ready, n + 1)
                wait(act, weighted, n - 2)
                nc.scalar.activation(act_s[n % 3][:], psU[n % 2][:], ACT.Silu).then_inc(silu_ready, 1)

            def copy_turned(n):
                act.wait_ge(f_turned, n + 1)
                wait(act, down_done, n - 2)
                nc.scalar.copy(fT[n % 3][:].rearrange("p n q -> p (n q)"), psF[n % 2][:]).then_inc(fT_ready, 1)

            copy_h(0)
            sigmoids(0)
            shared_silu(0)
            for n in range(NG + LT):
                tile, g = n // NGR, n % NGR
                b, t = tile // TB, tile % TB
                if n < NG:
                    silu(n)
                    if t == 0 and g == 6 and b + 1 < B:
                        copy_h(b + 1)
                    if t == 1 and g == 3 and b + 1 < B:
                        sigmoids(b + 1)
                        shared_silu(b + 1)
                if n >= LT:
                    copy_turned(n - LT)


def layer_selected_experts(m, pre):
    nc = m.nc
    d = m.dram
    E, F, M = 8, 64, 256
    MT = M // P
    EF = E * F
    EB = EF // P
    NEG = E + 1
    with ExitStack() as es:
        sb, ps, sem = allocators(nc, es, pre)
        sw12, sw3 = sb("sw12", [P, 2 * F]), sb("sw3", [F, D])
        sb12, sb3, sg, sbeta = sb("sb12", [P, 2 * F]), sb("sb3", [P, D]), sb("sln_g", [F, 1]), sb("sln_b", [F, 1])
        wgate, bgate, ebias = sb("wgate", [P, NEG]), sb("bgate", [P, NEG]), sb("ebias", [P, E])
        ew = [sb(f"ew{i + 1}", [P, E, F]) for i in range(2)]
        eb = [sb(f"eb{i + 1}", [P, EF]) for i in range(2)]
        ew3, eb3 = sb("ew3", [P, EB, D]), sb("eb3", [E, D])
        lng, lnb = sb("lng", [P, F]), sb("lnb", [P, F])
        ib_row, it_row, id_row = sb("ib_row", [P, M], I32), sb("it_row", [P, M], I32), sb("id_row", [P, M])
        ib_col, it_col, id_col = sb("ib_col", [P, MT], I32), sb("it_col", [P, MT], I32), sb("id_col", [P, MT])
        rowf, colf = sb("rowf", [P, M]), sb("colf", [P, MT])
        tok_col, tok_row, rank = sb("tok_col", [P, NT]), sb("tok_row", [P, NT * P]), sb("rank", [P, E])
        pick, spread = sb("pick", [P, NT, M]), sb("spread", [P, MT, NT * P])
        wa, ws, we = Norm(sb, "a", NT), Norm(sb, "s", NT), Norm(sb, "e", MT * E)
        h, hT = sb("h", [P, NT, D]), sb("hT", [P, NT, P])
        x12, u, shT, so = sb("x12", [P, NT, 2 * F]), sb("u", [P, NT, F]), sb("shT", [F, NT, P]), sb("so", [P, NT, D])
        xpT = sb("xpT", [P, M])
        gl, sc, bi, oh, key = sb("gl", [P, MT, NEG]), sb("sc", [P, MT, NEG]), sb("bi", [P, MT, E]), sb("oh", [P, MT, E]), sb("key", [P, MT, E])
        top, two, mx2, wsum = sb("top", [P, MT]), sb("two", [P, MT, 2]), sb("mx2", [P, MT]), sb("wsum", [P, MT])
        e1, e2 = sb("e1", [P, MT, EF]), sb("e2", [P, MT, EF])
        zT, ohT, picked_out = sb("zT", [P, EB, M]), sb("ohT", [E, M]), sb("picked_out", [P, MT, D + 2])
        seen, cnt, rec, keep = sb("seen", [P, NT, 2]), sb("cnt", [P, NT]), sb("rec", [P, NT]), sb("keep", [P, NT])
        psT, psX, psE = [ps(f"psT{i}", [P, 512]) for i in range(2)], [ps(f"psX{i}", [P, 512]) for i in range(2)], [ps(f"psE{i}", [P, 512]) for i in range(2)]
        psG, psC = ps("psG", [P, 512]), ps("psC", [P, 512])
        names = ("loaded", "dve_chain", "pool_chain", "iota_ready", "var_ready", "rstd_ready", "h_ready", "pick_ready", "turned", "hT_ready",
                 "x12_ready", "biased", "silu_ready", "z_ready", "z_turned", "shT_ready", "shared_out", "so_ready", "gathered",
                 "xpT_ready", "gates_ready", "logits_ready", "sig_ready", "two_ready", "exp_ready", "e_ready", "e_biased", "esilu_ready", "ez_ready",
                 "ez_turned", "zT_ready", "eo_ready", "po_ready", "seen_ready", "spread_done", "x_done")
        (loaded, dve_chain, pool_chain, iota_ready, var_ready, rstd_ready, h_ready, pick_ready, turned, hT_ready,
         x12_ready, biased, silu_ready, z_ready, z_turned, shT_ready, shared_out, so_ready, gathered,
         xpT_ready, gates_ready, logits_ready, sig_ready, two_ready, exp_ready, e_ready, e_biased, esilu_ready, ez_ready,
         ez_turned, zT_ready, eo_ready, po_ready, seen_ready, spread_done, x_done) = (sem(n) for n in names)
        block = es.enter_context(nc.Block())
        col = lambda a: a.rearrange("(d a) -> d a", a=1)
        wide = lambda name, n: rows(d[f"{pre}_{name}"]).to_broadcast((P, n))
        loads = [(ib_row[:], wide("index_b", M)), (it_row[:], wide("index_t", M)),
                 (sw12[:, 0:F], d[f"{pre}_sw1"]), (sw12[:, F:], d[f"{pre}_sw2"]), (sw3[:], d[f"{pre}_sw3"]),
                 (sb12[:, 0:F], wide("sb1", F)), (sb12[:, F:], wide("sb2", F)), (sb3[:], wide("sb3", D)),
                 (sg[:], col(d[f"{pre}_s_ln_g"])), (sbeta[:], col(d[f"{pre}_s_ln_b"])),
                 (wgate[:, 0:1], d[f"{pre}_sg_w"]), (wgate[:, 1:], d[f"{pre}_eg_w"]),
                 (bgate[:, 0:1], wide("sg_b", 1)), (bgate[:, 1:], wide("eg_b", E)), (ebias[:], wide("exp_bias", E)),
                 (ew[0][:], d[f"{pre}_ew1"].rearrange("e d f -> d e f")), (ew[1][:], d[f"{pre}_ew2"].rearrange("e d f -> d e f")),
                 (eb[0][:], rows(d[f"{pre}_eb1"].rearrange("e f -> (e f)")).to_broadcast((P, EF))),
                 (eb[1][:], rows(d[f"{pre}_eb2"].rearrange("e f -> (e f)")).to_broadcast((P, EF))),
                 (ew3[:], d[f"{pre}_ew3"].rearrange("e f d -> (e f) d").rearrange("(n p) d -> p n d", p=P)), (eb3[:], d[f"{pre}_eb3"]),
                 (lng[:], wide("sel_ln_g", F)), (lnb[:], wide("sel_ln_b", F))]
        for c, name in ((ib_col, "index_b"), (it_col, "index_t")):
            loads += [(c[:, t:t + 1], col(d[f"{pre}_{name}"][t * P:(t + 1) * P])) for t in range(MT)]
        NLOAD = 16 * len(loads)

        @block.sync
        def _(sp):
            for dst, src in loads:
                sp.dma_start(dst, src).then_inc(loaded, 16)

        @block.gpsimd
        def _(pool):
            link = Links(pool, pool_chain)
            nc.gpsimd.iota(tok_col[:], pattern=[[P, NT]], base=0, channel_multiplier=1, allow_small_or_imprecise_dtypes=True).then_inc(iota_ready, 1)
            nc.gpsimd.iota(tok_row[:], pattern=[[1, NT * P]], base=0, channel_multiplier=0, allow_small_or_imprecise_dtypes=True).then_inc(iota_ready, 1)
            nc.gpsimd.iota(rank[:], pattern=[[-1, E]], base=E, channel_multiplier=0, allow_small_or_imprecise_dtypes=True).then_inc(iota_ready, 1)
            nc.gpsimd.memset(picked_out[:, :, D + 1:], 1.0).then_inc(iota_ready, 1)
            for n, ww in enumerate((wa, ws, we)):
                pool.wait_ge(var_ready, n + 1)
                pool_rsqrt(nc, m, ww, ww.n).then_inc(rstd_ready, 1)

        @block.vector
        def _(dve):
            link = Links(dve, dve_chain)
            fl = lambda a: a.rearrange("p n d -> p (n d)")
            dve_moments(nc, link, wa, [m.x[:, i // TB, i % TB] for i in range(NT)], D, LN_EPS).then_inc(var_ready, 1)
            dve.wait_ge(loaded, NLOAD)
            for b_, t_, f_, out in ((ib_row, it_row, rowf, id_row), (ib_col, it_col, colf, id_col)):
                link.mark(nc.vector.tensor_copy(f_[:], b_[:]))
                link(nc.vector.tensor_copy(out[:], t_[:]))
                link(nc.vector.scalar_tensor_tensor(out[:], f_[:], float(S), out[:], ALU.mult, ALU.add))
            dve.wait_ge(iota_ready, 4)
            dve.wait_ge(rstd_ready, 1)
            for i in range(NT):
                nc.vector.tensor_scalar(h[:, i], m.x[:, i // TB, i % TB], wa.mean[:, i:i + 1], wa.rstd[:, i:i + 1], ALU.subtract, ALU.mult).then_inc(h_ready, 1)
                nc.vector.tensor_scalar(pick[:, i], id_row[:], tok_col[:, i:i + 1], None, ALU.is_equal).then_inc(pick_ready, 1)
            for b in range(B):
                dve.wait_ge(x12_ready, b + 1)
                nc.vector.tensor_tensor(x12[:, TB * b:TB * (b + 1)], psX[b % 2][:, 0:TB * 2 * F].rearrange("p (t f) -> p t f", t=TB),
                                        sb12[:, None, :].to_broadcast((P, TB, 2 * F)), ALU.add).then_inc(biased, 1)
            dve.wait_ge(gates_ready, 1)
            nc.vector.tensor_tensor(gl[:], psC[:, 0:MT * NEG].rearrange("p (t e) -> p t e", t=MT), bgate[:, None, :].to_broadcast((P, MT, NEG)), ALU.add).then_inc(logits_ready, 1)
            for b in range(B):
                dve.wait_ge(silu_ready, b + 1)
                i = slice(TB * b, TB * (b + 1))
                link.mark(nc.vector.tensor_tensor(u[:, i], u[:, i], x12[:, i, F:], ALU.mult))
            link.wait()
            dve_moments(nc, link, ws, [u[:, i] for i in range(NT)], F, LN_EPS).then_inc(var_ready, 1)
            for t in range(MT):
                for k, e in enumerate((e1, e2)):
                    dve.wait_ge(e_ready, 2 * t + k + 1)
                    nc.vector.tensor_tensor(e[:, t], psE[k][:], eb[k][:], ALU.add).then_inc(e_biased, 1)
            dve.wait_ge(rstd_ready, 2)
            for i in range(NT):
                if i == 0:
                    link.wait()
                nc.vector.tensor_scalar(u[:, i], u[:, i], ws.mean[:, i:i + 1], ws.rstd[:, i:i + 1], ALU.subtract, ALU.mult).then_inc(z_ready, 1)
            dve.wait_ge(e_biased, 2 * MT)
            for t in range(MT):
                dve.wait_ge(esilu_ready, t + 1)
                link.mark(nc.vector.tensor_tensor(e1[:, t], e1[:, t], e2[:, t], ALU.mult))
            link.wait()
            dve_moments(nc, link, we, [e1[:, n // E, n % E * F:(n % E + 1) * F] for n in range(MT * E)], F, LN_EPS).then_inc(var_ready, 1)
            dve.wait_ge(sig_ready, 1)
            link(nc.vector.tensor_tensor(bi[:], sc[:, :, 1:], ebias[:, None, :].to_broadcast((P, MT, E)), ALU.add))
            link(nc.vector.reduce_max(top[:], bi[:], AX.X))
            link(nc.vector.tensor_tensor(oh[:], bi[:], top[:, :, None].to_broadcast((P, MT, E)), ALU.is_equal))
            link(nc.vector.tensor_tensor(key[:], oh[:], rank[:, None, :].to_broadcast((P, MT, E)), ALU.mult))
            link(nc.vector.reduce_max(top[:], key[:], AX.X))
            link(nc.vector.tensor_tensor(oh[:], key[:], top[:, :, None].to_broadcast((P, MT, E)), ALU.is_equal))
            link(nc.vector.tensor_tensor(key[:], oh[:], sc[:, :, 1:], ALU.mult))
            link.mark(nc.vector.tensor_copy(two[:, :, 0:1], sc[:, :, 0:1]))
            link(nc.vector.reduce_sum(two[:, :, 1:2], key[:], AX.X))
            link(nc.vector.reduce_max(mx2[:], two[:], AX.X))
            nc.vector.tensor_tensor(two[:], two[:], mx2[:, :, None].to_broadcast((P, MT, 2)), ALU.subtract).then_inc(two_ready, 1)
            dve.wait_ge(rstd_ready, 3)
            per = lambda a: a.rearrange("p t (e f) -> p (t e) f", f=F)
            E1 = per(e1[:])
            shape = (P, MT * E, F)
            link(nc.vector.tensor_tensor(E1, E1, we.mean[:, :, None].to_broadcast(shape), ALU.subtract))
            link(nc.vector.tensor_tensor(E1, E1, we.rstd[:, :, None].to_broadcast(shape), ALU.mult))
            link(nc.vector.tensor_tensor(E1, E1, lng[:, None, :].to_broadcast(shape), ALU.mult))
            link(nc.vector.tensor_tensor(E1, E1, lnb[:, None, :].to_broadcast(shape), ALU.add))
            nc.vector.tensor_tensor(E1, E1, fl(oh[:])[:, :, None].to_broadcast(shape), ALU.mult).then_inc(ez_ready, 1)
            for t in range(MT):
                link.mark(nc.vector.tensor_scalar(spread[:, t], tok_row[:], id_col[:, t:t + 1], None, ALU.is_equal))
            for b in range(B):
                dve.wait_ge(shared_out, b + 1)
                nc.vector.tensor_tensor(so[:, TB * b:TB * (b + 1)], psX[b % 2][:, 0:TB * D].rearrange("p (t d) -> p t d", t=TB),
                                        sb3[:, None, :].to_broadcast((P, TB, D)), ALU.add).then_inc(so_ready, 1)
            dve.wait_ge(exp_ready, 1)
            link(nc.vector.reduce_sum(wsum[:], two[:], AX.X))
            link(nc.vector.reciprocal(wsum[:], wsum[:]))
            link(nc.vector.tensor_tensor(two[:], two[:], wsum[:, :, None].to_broadcast((P, MT, 2)), ALU.mult))
            link.mark(nc.vector.tensor_copy(picked_out[:, :, D:D + 1], two[:, :, 0:1]))
            for t in range(MT):
                dve.wait_ge(eo_ready, MT)
                nc.vector.tensor_scalar(picked_out[:, t, 0:D], psC[:, 128 + t * D:128 + (t + 1) * D], two[:, t, 1:2], None, ALU.mult).then_inc(po_ready, 1)
            dve.wait_ge(seen_ready, 1)
            link(nc.vector.tensor_copy(seen[:], psG[:, 0:2 * NT].rearrange("p (i k) -> p i k", k=2)))
            link.mark(nc.vector.tensor_scalar(cnt[:], seen[:, :, 1], 1.0, None, ALU.max))
            link(nc.vector.tensor_scalar(keep[:], seen[:, :, 1], 1.0, None, ALU.min))
            link.mark(nc.vector.reciprocal(rec[:], cnt[:]))
            link(nc.vector.tensor_scalar(keep[:], keep[:], -1.0, 1.0, ALU.mult, ALU.add))
            link(nc.vector.tensor_tensor(cnt[:], seen[:, :, 0], rec[:], ALU.mult))
            link(nc.vector.tensor_tensor(keep[:], keep[:], cnt[:], ALU.add))
            dve.wait_ge(so_ready, B)
            for i in range(NT):
                x = m.x[:, i // TB, i % TB]
                link.mark(nc.vector.scalar_tensor_tensor(x, so[:, i], keep[:, i:i + 1], x, ALU.mult, ALU.add))
            link.wait()
            for i in range(NT):
                b, t = i // TB, i % TB
                dve.wait_ge(spread_done, b + 1)
                x = m.x[:, b, t]
                nc.vector.scalar_tensor_tensor(x, psE[b % 2][:, t * D:(t + 1) * D], rec[:, i:i + 1], x, ALU.mult, ALU.add).then_inc(x_done, 1)

        @block.tensor
        def _(pe):
            for b in range(B):
                pe.wait_ge(h_ready, TB * (b + 1))
                wait(pe, hT_ready, b - 1)
                for t in range(TB):
                    ins = nc.tensor.transpose(psT[b % 2][:, t * P:(t + 1) * P], h[:, TB * b + t], m.ident[:])
                ins.then_inc(turned, 1)
                pe.wait_ge(pick_ready, TB * (b + 1))
                for i in range(TB * b, TB * (b + 1)):
                    ins = nc.tensor.matmul(psG[:, 0:M], h[:, i], pick[:, i], start=(i == 0), stop=(i == NT - 1))
                if b == B - 1:
                    ins.then_inc(gathered, 1)
                if b == 0:
                    pe.wait_ge(loaded, NLOAD)
                pe.wait_ge(hT_ready, b + 1)
                wait(pe, biased, b - 1)
                for t in range(TB):
                    ins = nc.tensor.matmul(psX[b % 2][:, t * 2 * F:(t + 1) * 2 * F], hT[:, TB * b + t], sw12[:], start=True, stop=True)
                ins.then_inc(x12_ready, 1)
            pe.wait_ge(xpT_ready, 1)
            for t in range(MT):
                ins = nc.tensor.matmul(psC[:, t * NEG:(t + 1) * NEG], xpT[:, t * P:(t + 1) * P], wgate[:], start=True, stop=True)
            ins.then_inc(gates_ready, 1)
            for t in range(MT):
                for k in range(2):
                    wait(pe, e_biased, 2 * (t - 1) + k + 1)
                    nc.tensor.matmul(psE[k][:], xpT[:, t * P:(t + 1) * P], ew[k][:].rearrange("p e f -> p (e f)"), start=True, stop=True).then_inc(e_ready, 1)
            for b in range(B):
                pe.wait_ge(z_ready, TB * (b + 1))
                pe.wait_ge(hT_ready, B)
                wait(pe, shT_ready, b - 1)
                for t in range(TB):
                    ins = nc.tensor.transpose(psT[b % 2][0:F, t * P:(t + 1) * P], u[:, TB * b + t], m.ident[:])
                ins.then_inc(z_turned, 1)
                pe.wait_ge(shT_ready, b + 1)
                pe.wait_ge(biased, B)
                wait(pe, so_ready, b - 1)
                for t in range(TB):
                    ins = nc.tensor.matmul(psX[b % 2][:, t * D:(t + 1) * D], shT[:, TB * b + t], sw3[:], start=True, stop=True)
                ins.then_inc(shared_out, 1)
            pe.wait_ge(ez_ready, 1)
            pe.wait_ge(e_biased, 2 * MT)
            for t in range(MT):
                for k in range(EB):
                    nc.tensor.transpose(psE[t][:, k * P:(k + 1) * P], e1[:, t, k * P:(k + 1) * P], m.ident[:])
                pe.wait_ge(shT_ready, B)
                nc.tensor.transpose(psT[t][0:E, 0:P], oh[:, t], m.ident[:]).then_inc(ez_turned, 1)
            pe.wait_ge(logits_ready, 1)
            for t in range(MT):
                pe.wait_ge(zT_ready, t + 1)
                for k in range(EB):
                    nc.tensor.matmul(psC[:, 128 + t * D:128 + (t + 1) * D], zT[:, k, t * P:(t + 1) * P], ew3[:, k], start=(k == 0), stop=False)
                nc.tensor.matmul(psC[:, 128 + t * D:128 + (t + 1) * D], ohT[:, t * P:(t + 1) * P], eb3[:], start=False, stop=True).then_inc(eo_ready, 1)
            pe.wait_ge(po_ready, MT)
            pe.wait_ge(xpT_ready, 1)
            for i in range(NT):
                for t in range(MT):
                    ins = nc.tensor.matmul(psG[:, 2 * i:2 * (i + 1)], spread[:, t, i * P:(i + 1) * P], picked_out[:, t, D:], start=(t == 0), stop=(t == MT - 1))
            ins.then_inc(seen_ready, 1)
            for b in range(B):
                wait(pe, x_done, TB * (b - 1))
                for i in range(TB):
                    for t in range(MT):
                        c = (TB * b + i) * P
                        ins = nc.tensor.matmul(psE[b % 2][:, i * D:(i + 1) * D], spread[:, t, c:c + P], picked_out[:, t, 0:D], start=(t == 0), stop=(t == MT - 1))
                ins.then_inc(spread_done, 1)

        @block.scalar
        def _(act):
            for b in range(B):
                act.wait_ge(turned, b + 1)
                nc.scalar.copy(hT[:, TB * b:TB * (b + 1)].rearrange("p t q -> p (t q)"), psT[b % 2][:, 0:S]).then_inc(hT_ready, 1)
            act.wait_ge(gathered, 1)
            nc.scalar.copy(xpT[:], psG[:, 0:M]).then_inc(xpT_ready, 1)
            for b in range(B):
                act.wait_ge(biased, b + 1)
                i = slice(TB * b, TB * (b + 1))
                nc.scalar.activation(u[:, i], x12[:, i, 0:F], ACT.Silu).then_inc(silu_ready, 1)
            for t in range(MT):
                act.wait_ge(e_biased, 2 * t + 1)
                nc.scalar.activation(e1[:, t], e1[:, t], ACT.Silu).then_inc(esilu_ready, 1)
            act.wait_ge(logits_ready, 1)
            nc.scalar.activation(sc[:], gl[:], ACT.Sigmoid).then_inc(sig_ready, 1)
            act.wait_ge(loaded, NLOAD)
            for b in range(B):
                act.wait_ge(z_turned, b + 1)
                nc.scalar.activation(shT[:, TB * b:TB * (b + 1)].rearrange("p t q -> p (t q)"), psT[b % 2][0:F, 0:S], ACT.Identity,
                                     bias=sbeta[:], scale=sg[:]).then_inc(shT_ready, 1)
            act.wait_ge(two_ready, 1)
            nc.scalar.activation(two[:], two[:], ACT.Exp).then_inc(exp_ready, 1)
            for t in range(MT):
                act.wait_ge(ez_turned, t + 1)
                nc.scalar.copy(zT[:, :, t * P:(t + 1) * P], psE[t][:].rearrange("p (k q) -> p k q", k=EB))
                nc.scalar.copy(ohT[:, t * P:(t + 1) * P], psT[t][0:E, 0:P]).then_inc(zT_ready, 1)


def layer_attention_single(m, pre, scale, inner_norm):
    nc = m.nc
    d = m.dram
    NC = B * KT
    with ExitStack() as es:
        sb, ps, sem = allocators(nc, es, pre)
        wq, wk, wv, wo = sb("wq", [P, D]), sb("wk", [DK, D]), sb("wv", [DK, D]), sb("wo", [P, D])
        bq, bk = sb("bq", [P, 1]), sb("bk", [P, 1])
        bv, bo = sb("bv", [P, D]), sb("bo", [P, D])
        w, w1 = Norm(sb, "", NT), Norm(sb, "1", NT)
        w2 = Norm(sb, "2", NC) if inner_norm else None
        h = sb("h", [P, NT, D])
        hT = [sb(f"hT{i}", [P, S]) for i in range(2)]
        ctx = sb("ctx", [P, B, KT, DK]) if inner_norm else None
        ctxT = [sb(f"ctxT{i}", [DK, SK]) for i in range(2)]
        g1, b1, g2, b2 = sb("g1", [P, 1]), sb("b1", [P, 1]), sb("g2", [DK, 1]), sb("b2", [DK, 1])
        qT, kT, v = sb("qT", [P, B, S]), sb("kT", [P, B, SK]), sb("v", [P, B, KT, D])
        RING = 4
        mx, negm, rsum, rinv = (sb(n, [P, RING]) for n in ("mx", "negm", "rsum", "rinv"))
        pr, prT = [sb(f"pr{i}", [P, SK]) for i in range(3)], [sb(f"prT{i}", [P, KT * P]) for i in range(2)]
        oT, y = [sb(f"oT{i}", [P, P]) for i in range(2)], sb("y", [P, D])
        psA, psS, psP, psO = ([ps(f"{n}{i}", [P, 512]) for i in range(2)] for n in ("psA", "psS", "psP", "psO"))
        names = ("loaded", "ctx_loaded", "dve_chain", "bias_scaled", "moments", "rstd", "h_ready", "turned", "hT_ready", "q_ready", "qT_ready",
                 "c_ready", "ctx_turned", "ctxT_ready", "k_ready", "kT_ready", "vp_ready", "v_ready", "s_ready", "negm_ready", "exp_ready",
                 "p_turned", "prT_ready", "o_ready", "oT_ready", "y_ready", "y_read")
        (loaded, ctx_loaded, dve_chain, bias_scaled, moments, rstd, h_ready, turned, hT_ready, q_ready, qT_ready,
         c_ready, ctx_turned, ctxT_ready, k_ready, kT_ready, vp_ready, v_ready, s_ready, negm_ready, exp_ready,
         p_turned, prT_ready, o_ready, oT_ready, y_ready, y_read) = (sem(n) for n in names)
        block = es.enter_context(nc.Block())
        NLOAD = 12 if inner_norm else 8
        LT, LV, LY = 2, 3, 4
        norms = (w, w1, w2) if inner_norm else (w,)

        @block.sync
        def _(sp):
            col = lambda a: a.rearrange("(d a) -> d a", a=1)
            loads = [(wq[:], d[f"{pre}_Wq"]), (wk[:], d[f"{pre}_Wk"]), (wv[:], d[f"{pre}_Wv"]), (wo[:], d[f"{pre}_Wo"]),
                     (bq[:], col(d[f"{pre}_bq"])), (bk[:], col(d[f"{pre}_bk"])),
                     (bv[:], rows(d[f"{pre}_bv"]).to_broadcast((P, D))), (bo[:], rows(d[f"{pre}_bo"]).to_broadcast((P, D)))]
            if inner_norm:
                loads += [(g1[:], col(d[f"{pre}_ln1_g"])), (b1[:], col(d[f"{pre}_ln1_b"])),
                          (g2[:], col(d[f"{pre}_ln2_g"])), (b2[:], col(d[f"{pre}_ln2_b"]))]
                for b in range(B):
                    sp.dma_start(ctx[:, b], d["ctx_rows"][b].rearrange("(t p) c -> p t c", p=P)).then_inc(ctx_loaded, 16)
            for dst, src in loads:
                sp.dma_start(dst, src).then_inc(loaded, 16)
            if not inner_norm:
                for b in range(B):
                    wait(sp, vp_ready, b - 1)
                    wait(sp, ctx_loaded, 16 * b)
                    sp.dma_start(ctxT[b % 2][:], d["ctx_768"][b]).then_inc(ctx_loaded, 16)

        @block.gpsimd
        def _(pool):
            for n, ww in enumerate(norms):
                pool.wait_ge(moments, n + 1)
                pool_rsqrt(nc, m, ww, ww.n).then_inc(rstd, 1)

        @block.vector
        def _(dve):
            link = Links(dve, dve_chain)

            def normed(dst, src, ww, t, done):
                nc.vector.tensor_scalar(dst, src, ww.mean[:, t:t + 1], ww.rstd[:, t:t + 1], ALU.subtract, ALU.mult).then_inc(done, 1)

            xs, hs = [m.x[:, i // TB, i % TB] for i in range(NT)], [h[:, i] for i in range(NT)]
            dve_moments(nc, link, w, xs, D, LN_EPS).then_inc(moments, 1)
            dve.wait_ge(rstd, 1)
            if inner_norm:
                for i in range(NT):
                    normed(hs[i], xs[i], w, i, link.sem)
                link.n += NT
                link.wait()
                dve_moments(nc, link, w1, hs, D, LN_EPS).then_inc(moments, 1)
                dve.wait_ge(ctx_loaded, 16 * B)
                cs = [ctx[:, i // KT, i % KT] for i in range(NC)]
                dve_moments(nc, link, w2, cs, DK, LN_EPS).then_inc(moments, 1)
                dve.wait_ge(rstd, 2)
                for i in range(NT):
                    normed(hs[i], hs[i], w1, i, h_ready)
                dve.wait_ge(rstd, 3)
                for i in range(NC):
                    normed(cs[i], cs[i], w2, i, c_ready)
            else:
                for i in range(NT):
                    normed(hs[i], xs[i], w, i, h_ready)
            dve.wait_ge(loaded, 16 * NLOAD)
            nc.vector.tensor_scalar(bq[:], bq[:], scale, None, ALU.mult).then_inc(bias_scaled, 1)
            for b in range(B):
                dve.wait_ge(vp_ready, b + 1)
                nc.vector.tensor_tensor(v[:, b], psP[b % 2][:].rearrange("p (t d) -> p t d", t=KT), bv[:, None, :].to_broadcast((P, KT, D)), ALU.add).then_inc(v_ready, 1)

            def maximum(n):
                dve.wait_ge(s_ready, n + 1)
                c = slice(n % RING, n % RING + 1)
                wait(dve, exp_ready, n - RING + 1)
                link(nc.vector.reduce_max(mx[:, c], psS[n % 2][:], AX.X))
                nc.vector.tensor_scalar(negm[:, c], mx[:, c], -1.0, None, ALU.mult).then_inc(negm_ready, 1)

            def copy_turned(n):
                dve.wait_ge(p_turned, n + 1)
                wait(dve, o_ready, n - 1)
                nc.vector.tensor_copy(prT[n % 2][:], psP[n % 2][:]).then_inc(prT_ready, 1)

            def update(n):
                dve.wait_ge(y_ready, n + 1)
                c = slice(n % RING, n % RING + 1)
                link(nc.vector.reciprocal(rinv[:, c], rsum[:, c]))
                nc.vector.scalar_tensor_tensor(y[:], psA[n % 2][:, 0:D], rinv[:, c], bo[:], ALU.mult, ALU.add).then_inc(y_read, 1)
                dve.wait_ge(y_read, n + 1)
                link(nc.vector.tensor_tensor(xs[n], xs[n], y[:], ALU.add))

            for n in range(NT + LY):
                if n < NT:
                    maximum(n)
                if 0 <= n - LT < NT:
                    copy_turned(n - LT)
                if 0 <= n - LY:
                    update(n - LY)

        @block.tensor
        def _(pe):
            pe.wait_ge(loaded, 16 * NLOAD)
            for b in range(B):
                i = b % 2
                pe.wait_ge(h_ready, TB * (b + 1))
                wait(pe, qT_ready, b - 1)
                for t in range(TB):
                    ins = nc.tensor.transpose(psA[i][:, t * P:(t + 1) * P], h[:, TB * b + t], m.ident[:])
                ins.then_inc(turned, 1)
                if inner_norm:
                    pe.wait_ge(c_ready, KT * (b + 1))
                    wait(pe, ctxT_ready, b - 1)
                    for t in range(KT):
                        ins = nc.tensor.transpose(psO[i][0:DK, t * P:(t + 1) * P], ctx[:, b, t], m.ident[:])
                    ins.then_inc(ctx_turned, 1)
                pe.wait_ge(hT_ready, b + 1)
                nc.tensor.matmul(psA[i][:, S:2 * S], wq[:], hT[i][:], start=True, stop=True).then_inc(q_ready, 1)
                if inner_norm:
                    pe.wait_ge(ctxT_ready, b + 1)
                else:
                    pe.wait_ge(ctx_loaded, 16 * (b + 1))
                wait(pe, kT_ready, b - 1)
                nc.tensor.matmul(psS[i][:], wk[:], ctxT[i][:], start=True, stop=True).then_inc(k_ready, 1)
                wait(pe, v_ready, b - 1)
                for t in range(KT):
                    ins = nc.tensor.matmul(psP[i][:, t * P:(t + 1) * P], ctxT[i][:, t * P:(t + 1) * P], wv[:], start=True, stop=True)
                ins.then_inc(vp_ready, 1)

            def scores(n):
                wait(pe, exp_ready, n - 1)
                nc.tensor.matmul(psS[n % 2][:], qT[:, n // TB, n % TB * P:(n % TB + 1) * P], kT[:, n // TB], start=True, stop=True).then_inc(s_ready, 1)

            def turn_probs(n):
                pe.wait_ge(exp_ready, n + 1)
                wait(pe, prT_ready, n - 1)
                for k in range(KT):
                    ins = nc.tensor.transpose(psP[n % 2][:, k * P:(k + 1) * P], pr[n % 3][:, k * P:(k + 1) * P], m.ident[:])
                ins.then_inc(p_turned, 1)

            def values(n):
                pe.wait_ge(prT_ready, n + 1)
                wait(pe, oT_ready, n - 1)
                for k in range(KT):
                    ins = nc.tensor.matmul(psO[n % 2][:, 0:P], v[:, n // TB, k], prT[n % 2][:, k * P:(k + 1) * P], start=(k == 0), stop=(k == KT - 1))
                ins.then_inc(o_ready, 1)

            def project_out(n):
                pe.wait_ge(oT_ready, n + 1)
                wait(pe, y_read, n - 1)
                nc.tensor.matmul(psA[n % 2][:, 0:D], oT[n % 2][:], wo[:], start=True, stop=True).then_inc(y_ready, 1)

            pe.wait_ge(qT_ready, B)
            pe.wait_ge(kT_ready, B)
            pe.wait_ge(v_ready, B)
            for n in range(NT + LY):
                if n < NT:
                    scores(n)
                if 0 <= n - LT < NT:
                    turn_probs(n - LT)
                if 0 <= n - LV < NT:
                    values(n - LV)
                if 0 <= n - LY:
                    project_out(n - LY)

        @block.scalar
        def _(act):
            act.wait_ge(loaded, 16 * NLOAD)
            act.wait_ge(bias_scaled, 1)
            for b in range(B):
                i = b % 2
                act.wait_ge(turned, b + 1)
                wait(act, q_ready, b - 1)
                if inner_norm:
                    nc.scalar.activation(hT[i][:], psA[i][:, 0:S], ACT.Identity, bias=b1[:], scale=g1[:]).then_inc(hT_ready, 1)
                    act.wait_ge(ctx_turned, b + 1)
                    wait(act, vp_ready, b - 1)
                    nc.scalar.activation(ctxT[i][:], psO[i][0:DK], ACT.Identity, bias=b2[:], scale=g2[:]).then_inc(ctxT_ready, 1)
                else:
                    nc.scalar.copy(hT[i][:], psA[i][:, 0:S]).then_inc(hT_ready, 1)
                act.wait_ge(q_ready, b + 1)
                nc.scalar.activation(qT[:, b], psA[i][:, S:2 * S], ACT.Identity, bias=bq[:], scale=scale).then_inc(qT_ready, 1)
                act.wait_ge(k_ready, b + 1)
                nc.scalar.activation(kT[:, b], psS[i][:], ACT.Identity, bias=bk[:]).then_inc(kT_ready, 1)

            def exponential(n):
                act.wait_ge(negm_ready, n + 1)
                wait(act, p_turned, n - 2)
                wait(act, y_read, n - RING + 1)
                nc.scalar.activation(pr[n % 3][:], psS[n % 2][:], ACT.Exp, bias=negm[:, n % RING:n % RING + 1],
                                     accum_out=rsum[:, n % RING:n % RING + 1]).then_inc(exp_ready, 1)

            def copy_out(n):
                act.wait_ge(o_ready, n + 1)
                wait(act, y_ready, n - 1)
                nc.scalar.copy(oT[n % 2][:], psO[n % 2][:, 0:P]).then_inc(oT_ready, 1)

            for n in range(NT + LV):
                if n < NT:
                    exponential(n)
                if 0 <= n - LV:
                    copy_out(n - LV)


def l1_attn(m):
    layer_attention_heads8(m, "L1_attn", "L1_attn_Wq", "L1_attn_Wk", "L1_attn_Wk", "L1_attn_Wo", None, None, None,
                           "L1_attn_bo", S, float(D) ** -0.5, False)


def l0_xattn(m):
    w = {v: f"L0_xattn_{v}" for v in ("Wq", "Wk", "Wv", "Wo", "bq", "bk", "bv", "bo")}
    layer_attention_heads8(m, "L0_xattn", w["Wq"], w["Wk"], w["Wv"], w["Wo"], w["bq"], w["bk"], w["bv"], w["bo"],
                           SK, 8 ** -0.5, True, clamp=1e4)


def l3_xattn(m):
    p = "L3_xattn_"
    layer_attention_heads8(m, "L3_xattn", p + "q_w", p + "v_w", p + "v_w", p + "o_w", p + "q_b", p + "v_b", p + "v_b", p + "o_b",
                           SK, 8 ** -0.5, True, head_major=True)


STACK = {8: lambda m: layer_selected_experts(m, "L2_ffn"), 6: lambda m: layer_attention_heads64(m, "L2_attn", True), 9: lambda m: layer_attention_heads64(m, "L3_attn", False),
         0: lambda m: layer_gated_recurrence(m, "L0_attn"), 2: lambda m: layer_moe_top8(m, "L0_ffn"), 4: lambda m: layer_attention_single(m, "L1_xattn", 0.25, False), 7: lambda m: layer_attention_single(m, "L2_xattn", float(D) ** -0.5, True),
         5: lambda m: layer_fp4_mlp(m, "L1_ffn"), 11: lambda m: layer_sign_linear(m, "L3_ffn"), 3: l1_attn, 1: l0_xattn, 10: l3_xattn}


HOST_TRANSPOSED = {"L3_ffn_weights", "L3_xattn_q_w", "L3_xattn_v_w", "L3_xattn_o_w", "L0_attn_in_proj_w",
                   "L0_attn_out_proj_w", "L0_attn_fc_w", "L0_attn_proj_w", "L0_ffn_centroids", "L2_ffn_sw1", "L2_ffn_sw2",
                   "L2_ffn_sw3", "L2_ffn_sg_w", "L2_ffn_eg_w", "L3_attn_w_down_q", "L3_attn_w_down_kv", "L3_attn_w_up_q",
                   "L3_attn_w_up_k", "L3_attn_w_up_v", "L3_attn_w_out"}


def build(nc, dram, out):
    with ExitStack() as ctx:
        m = Model(nc, dram, out, ctx)
        setup(m)
        for n in LAYERS:
            STACK[n](m)
        finish(m)


def rotary_tables(tokens, width):
    inv = 1.0 / 10000.0 ** (np.arange(0, width, 2, dtype=np.float32) / width)
    angle = np.outer(np.arange(tokens, dtype=np.float32), inv)
    pick = lambda v: np.concatenate([v, v], -1)[:, ::2]
    cos, sin = (np.repeat(pick(f(angle)).T, 2, axis=0).astype(np.float32) for f in (np.cos, np.sin))
    sign = np.where(np.arange(width) % 2 == 0, -1.0, 1.0).astype(np.float32)[:, None]
    return np.tile(cos, (2, 1)), np.tile(sin * sign, (2, 1))


def kernel(**inputs):
    import concourse.bacc as bacc
    from concourse.bass_utils import run_bass_kernel_spmd as run

    nc = bacc.Bacc("TRN2", target_bir_lowering=False, num_devices=1)
    arrays, dram = {}, {}
    for name, value in inputs.items():
        a = np.asarray(value)
        if name in HOST_TRANSPOSED:
            a = a.T
        if name == "ctx_768":
            dram["ctx_rows"] = nc.dram_tensor("in_ctx_rows", a.shape, mybir.dt.from_np(a.dtype), kind="ExternalInput").ap()
            arrays["in_ctx_rows"] = np.ascontiguousarray(a)
        if name == "ctx_768" or name in ("L2_ffn_ew1", "L2_ffn_ew2", "L2_ffn_ew3"):
            a = a.transpose(0, 2, 1)
        a = np.ascontiguousarray(a)
        arrays[f"in_{name}"] = a
        dram[name] = nc.dram_tensor(f"in_{name}", a.shape, mybir.dt.from_np(a.dtype), kind="ExternalInput").ap()
    def extra(name, a):
        arrays[f"in_{name}"] = a = np.ascontiguousarray(a)
        dram[name] = nc.dram_tensor(f"in_{name}", a.shape, mybir.dt.from_np(a.dtype), kind="ExternalInput").ap()

    for v in "qk":
        a = arrays[f"in_L3_attn_w_up_{v}"]
        extra(f"up_{v}_swapped", a.reshape(a.shape[0], -1, 2)[:, :, ::-1].reshape(a.shape))
    cos, sin = rotary_tables(S, 64)
    extra("rope_cos", cos)
    extra("rope_sin", sin)
    out = nc.dram_tensor("out", (B, S, D), F32, kind="ExternalOutput").ap()
    build(nc, dram, out)
    return run(nc, [arrays], core_ids=[0]).results[0]["out"]
```
